# Optimizing a Trainium2 kernel written in Bass

```python
import numpy as np
import jax
import jax.numpy as jnp

def _softmax(x, axis=-1):
    return jax.nn.softmax(x, axis=axis)

def _gelu(x):
    return jax.nn.gelu(x, approximate=True)

def _silu(x):
    return jax.nn.silu(x)

def _sigmoid(x):
    return jax.nn.sigmoid(x)

def _layernorm(x, axis=-1, eps=1e-05):
    m = jnp.mean(x, axis=axis, keepdims=True)
    v = jnp.var(x, axis=axis, keepdims=True)
    return (x - m) / jnp.sqrt(v + eps)

def _scatter_add(tgt, idx, src, axis=0):
    return tgt.at[idx].add(src)

def _segment_sum(src, seg, n):
    return jax.ops.segment_sum(src, seg, n)
kernel_name = 'mk_lm_tower_d4_tok_ids512_r4_46eee4'

def setup_inputs(seed: int=0):
    np.random.seed(seed)
    _w = jnp.asarray

    def _rec_inputs():
        import jax
        import jax.numpy as jnp
        _rk = jax.random.key(seed)
        x = jax.random.randint(jax.random.fold_in(_rk, 1), (2, 1024), 0, 121, jnp.int32)
        return x
    x = _rec_inputs()

    def _L0_tok_setup():
        import jax, jax.numpy as jnp
        import numpy as np
        import math
        D_MODEL = 128
        HIDDEN = 64
        FEATURE_DIM = 37
        MAX_TOKEN_ID = 120
        SPECIAL_IDS = np.array([0, 107, 108, 109], dtype=np.int64)

        def gelu_approx(x):
            c = math.sqrt(2.0 / math.pi)
            return 0.5 * x * (1.0 + jnp.tanh(c * (x + 0.044715 * x * x * x)))
        key = jax.random.key(seed)
        k1, k2, k3, k4, k5, k6, k7 = jax.random.split(key, 7)
        B, S = (16, 2048)
        token_ids = jax.random.randint(k1, (B, S), 0, MAX_TOKEN_ID + 1)
        feature_table = jax.random.normal(k2, (MAX_TOKEN_ID + 1, FEATURE_DIM), dtype=jnp.float32)
        special_embed = jax.random.normal(k3, (len(SPECIAL_IDS), D_MODEL), dtype=jnp.float32)
        W1 = jax.random.normal(k4, (FEATURE_DIM, HIDDEN), dtype=jnp.float32) / math.sqrt(FEATURE_DIM)
        b1 = jax.random.normal(k5, (HIDDEN,), dtype=jnp.float32) * 0.01
        W2 = jax.random.normal(k6, (HIDDEN, D_MODEL), dtype=jnp.float32) / math.sqrt(HIDDEN)
        b2 = jax.random.normal(k7, (D_MODEL,), dtype=jnp.float32) * 0.01
        return {'feature_table': feature_table, 'special_embed': special_embed, 'W1': W1, 'b1': b1, 'W2': W2, 'b2': b2, 'token_ids': token_ids}
    _L0_tok_all = _L0_tok_setup()
    _L0_tok_in = {k: v for k, v in _L0_tok_all.items() if k in ('feature_table', 'special_embed', 'W1', 'b1', 'W2', 'b2')}
    del _L0_tok_all

    def _L0_attn_setup():
        import jax, jax.numpy as jnp
        import numpy as np
        B, N, D = (4, 512, 128)
        key = jax.random.key(seed)
        ks = jax.random.split(key, 7)
        s = 1.0 / np.sqrt(D)
        return {'x': jax.random.normal(ks[0], (B, N, D), dtype=jnp.float32), 'Wq': jax.random.uniform(ks[1], (D, D), jnp.float32, -s, s), 'bq': jax.random.uniform(ks[2], (D,), jnp.float32, -s, s), 'Wk': jax.random.uniform(ks[3], (D, D), jnp.float32, -s, s), 'bk': jax.random.uniform(ks[4], (D,), jnp.float32, -s, s), 'Wv': jax.random.uniform(ks[5], (D, D), jnp.float32, -s, s), 'bv': jax.random.uniform(ks[6], (D,), jnp.float32, -s, s)}
    _L0_attn_all = _L0_attn_setup()
    _L0_attn_in = {k: v for k, v in _L0_attn_all.items() if k in ('Wq', 'bq', 'Wk', 'bk', 'Wv', 'bv')}
    del _L0_attn_all

    def _L0_ffn_setup():
        import jax, jax.numpy as jnp
        import numpy as np

        def _haar_dwt2(x):
            a = x[:, ::2, ::2]
            b = x[:, ::2, 1::2]
            c = x[:, 1::2, ::2]
            d = x[:, 1::2, 1::2]
            ll = (a + b + c + d) * 0.5
            lh = (a + b - c - d) * 0.5
            hl = (a - b + c - d) * 0.5
            hh = (a - b - c + d) * 0.5
            return (ll, lh, hl, hh)

        def _haar_idwt2(ll, lh, hl, hh):
            a = (ll + lh + hl + hh) * 0.5
            b = (ll + lh - hl - hh) * 0.5
            c = (ll - lh + hl - hh) * 0.5
            d = (ll - lh - hl + hh) * 0.5
            B, H2, W2 = ll.shape
            out = jnp.zeros((B, 2 * H2, 2 * W2), ll.dtype)
            out = out.at[:, ::2, ::2].set(a)
            out = out.at[:, ::2, 1::2].set(b)
            out = out.at[:, 1::2, ::2].set(c)
            out = out.at[:, 1::2, 1::2].set(d)
            return out

        def _interp_linear_last(x, m):
            n = x.shape[-1]
            pos = jnp.linspace(0.0, 1.0, m, dtype=x.dtype) * (n - 1)
            i0 = jnp.clip(jnp.floor(pos).astype(jnp.int32), 0, n - 2)
            w = pos - i0.astype(x.dtype)
            return x[..., i0] * (1.0 - w) + x[..., i0 + 1] * w
        key = jax.random.key(seed)
        k0, k1, k2 = jax.random.split(key, 3)
        b, f, c, hidden = (128, 64, 128, 512)
        x = jax.random.normal(k0, (b, f, c), dtype=jnp.float32)
        fc1_w = jax.random.normal(k1, (hidden, c), dtype=jnp.float32) * 0.02
        fc1_b = jnp.zeros((hidden,), dtype=jnp.float32)
        fc2_w = jax.random.normal(k2, (c // 2, hidden), dtype=jnp.float32) * 0.02
        fc2_b = jnp.zeros((c // 2,), dtype=jnp.float32)
        return {'x': x, 'fc1_w': fc1_w, 'fc1_b': fc1_b, 'fc2_w': fc2_w, 'fc2_b': fc2_b}
    _L0_ffn_all = _L0_ffn_setup()
    _L0_ffn_in = {k: v for k, v in _L0_ffn_all.items() if k in ('fc1_w', 'fc1_b', 'fc2_w', 'fc2_b')}
    del _L0_ffn_all

    def _L1_attn_setup():
        import jax, jax.numpy as jnp
        import numpy as np
        import math
        H, D, DEG = (8, 64, 2)
        GATE_BIAS = 6.906768

        def _rope(x, sin, cos):
            x1, x2 = (x[..., ::2], x[..., 1::2])
            s = sin[None, :, None, :]
            c = cos[None, :, None, :]
            even = x1 * c - x2 * s
            odd = x2 * c + x1 * s
            return jnp.stack([even, odd], axis=-1).reshape(x.shape)

        def _forward(x, w_attn, w_proj):
            B, T, C = x.shape
            h, d, deg = (H, D, DEG)
            hd = h * d
            scale = 1.0 / math.sqrt(d)
            qkvg = x @ w_attn
            q = qkvg[..., :hd].reshape(B, T, h, d)
            k = qkvg[..., hd:2 * hd].reshape(B, T, h, d)
            v = qkvg[..., 2 * hd:3 * hd].reshape(B, T, h, d)
            log_g = jax.nn.log_sigmoid(GATE_BIAS + qkvg[..., 3 * hd:].astype(jnp.float32))
            pos = jnp.arange(T, dtype=jnp.float32)
            div = 2.0 * math.pi / float(T) ** (jnp.arange(0, d, 2, dtype=jnp.float32) / d)
            ang = pos[:, None] * div[None, :]
            sin, cos = (jnp.sin(ang), jnp.cos(ang))
            q = _rope(q, sin, cos)
            k = _rope(k, sin, cos)
            L = jnp.cumsum(log_g, axis=1).transpose(0, 2, 1)
            qk = jnp.einsum('bthd,bshd->bhts', q, k) * scale
            log_gate = L[:, :, :, None] - L[:, :, None, :]
            causal = jnp.tril(jnp.ones((T, T), dtype=bool))
            scores = jnp.where(causal, qk ** deg * jnp.exp(log_gate), 0.0)
            denom = jnp.maximum(scores.sum(-1, keepdims=True), 1e-06)
            y = jnp.einsum('bhts,bshd->bthd', scores / denom, v)
            return y.reshape(B, T, hd) @ w_proj
        key = jax.random.key(seed)
        k1, k2, k3 = jax.random.split(key, 3)
        B, T, C = (2, 512, 128)
        x = jax.random.normal(k1, (B, T, C), dtype=jnp.float32)
        w_attn = jax.random.normal(k2, (C, 3 * H * D + H), dtype=jnp.float32) * 0.02
        w_proj = jax.random.normal(k3, (H * D, C), dtype=jnp.float32) * 0.02
        return {'x': x, 'w_attn': w_attn, 'w_proj': w_proj}
    _L1_attn_all = _L1_attn_setup()
    _L1_attn_in = {k: v for k, v in _L1_attn_all.items() if k in ('w_attn', 'w_proj')}
    del _L1_attn_all

    def _L1_ffn_setup():
        import jax, jax.numpy as jnp
        import numpy as np
        D = 128
        E = 8
        K = 2
        EXP = 4
        LN_EPS = 1e-05
        key = jax.random.key(seed)
        ks = jax.random.split(key, 8)
        B, T = (8, 512)
        Dh = D * EXP
        x = jax.random.normal(ks[0], (B, T, D), dtype=jnp.float32)
        ln_g = jnp.ones((D,), dtype=jnp.float32)
        ln_b = jnp.zeros((D,), dtype=jnp.float32)
        lim_r = np.sqrt(6.0 / (D + E)).astype(np.float32)
        w_r = jax.random.uniform(ks[1], (E, D), dtype=jnp.float32, minval=-lim_r, maxval=lim_r)
        b_r = jnp.zeros((E,), dtype=jnp.float32)
        lim1 = np.sqrt(6.0 / (D + Dh)).astype(np.float32)
        W1 = jax.random.uniform(ks[2], (E, D, Dh), dtype=jnp.float32, minval=-lim1, maxval=lim1)
        b1 = jnp.zeros((E, Dh), dtype=jnp.float32)
        W2 = jax.random.uniform(ks[3], (E, Dh, D), dtype=jnp.float32, minval=-lim1, maxval=lim1)
        b2 = jnp.zeros((E, D), dtype=jnp.float32)
        return {'x': x, 'ln_g': ln_g, 'ln_b': ln_b, 'w_r': w_r, 'b_r': b_r, 'W1': W1, 'b1': b1, 'W2': W2, 'b2': b2}
    _L1_ffn_all = _L1_ffn_setup()
    _L1_ffn_in = {k: v for k, v in _L1_ffn_all.items() if k in ('ln_g', 'ln_b', 'w_r', 'b_r', 'W1', 'b1', 'W2', 'b2')}
    del _L1_ffn_all

    def _L2_attn_setup():
        import jax, jax.numpy as jnp
        import numpy as np
        H = 8
        W = 64
        SHIFT = True
        DIM = 128
        SCALE = (DIM // H) ** (-0.5)
        key = jax.random.key(seed)
        k1, k2, k3, k4 = jax.random.split(key, 4)
        x = jax.random.normal(k1, (8, 1024, DIM), dtype=jnp.float32)
        w_qkv = jax.random.normal(k2, (3 * DIM, DIM), dtype=jnp.float32) * 0.02
        w_proj = jax.random.normal(k3, (DIM, DIM), dtype=jnp.float32) * 0.02
        b_proj = jax.random.normal(k4, (DIM,), dtype=jnp.float32) * 0.02
        return {'x': x, 'w_qkv': w_qkv, 'w_proj': w_proj, 'b_proj': b_proj}
    _L2_attn_all = _L2_attn_setup()
    _L2_attn_in = {k: v for k, v in _L2_attn_all.items() if k in ('w_qkv', 'w_proj', 'b_proj')}
    del _L2_attn_all

    def _L2_ffn_setup():
        import jax, jax.numpy as jnp
        import numpy as np
        from jax import lax
        N, M, DIM, HEADS, TOPK = (4, 512, 128, 8, 16)

        def _split_heads(t, h):
            n, m, c = t.shape
            return t.reshape(n, m, h, c // h).transpose(0, 2, 1, 3).reshape(n * h, m, c // h)
        key = jax.random.key(seed)
        ks = jax.random.split(key, 7)
        f = lambda k, s, sc=1.0: jax.random.normal(k, s, dtype=jnp.float32) * sc
        return {'x': f(ks[0], (N, M, DIM)), 'pos_w': f(ks[1], (DIM, 1, 3), 0.1), 'pos_b': f(ks[2], (DIM,), 0.02), 'qkv_w': f(ks[3], (3 * DIM, DIM), 0.02), 'qkv_b': f(ks[4], (3 * DIM,), 0.02), 'wo_w': f(ks[5], (DIM, DIM), 0.02), 'wo_b': f(ks[6], (DIM,), 0.02)}
    _L2_ffn_all = _L2_ffn_setup()
    _L2_ffn_in = {k: v for k, v in _L2_ffn_all.items() if k in ('pos_w', 'pos_b', 'qkv_w', 'qkv_b', 'wo_w', 'wo_b')}
    del _L2_ffn_all

    def _L3_attn_setup():
        import jax, jax.numpy as jnp
        import numpy as np
        B_, L_, H_, P_ = (8, 1024, 128, 64)
        DT_MIN, DT_MAX = (0.001, 0.1)

        def _scan_ssm(Lambda_bar, Bu):
            A = jnp.broadcast_to(Lambda_bar, Bu.shape)

            def binop(e_i, e_j):
                a_i, b_i = e_i
                a_j, b_j = e_j
                return (a_j * a_i, a_j * b_i + b_j)
            _, xs = jax.lax.associative_scan(binop, (A, Bu))
            return xs

        def _reference_tuple_inner(input_sequence, Lambda_re, Lambda_im, B, C, D, log_step):
            Lambda = (Lambda_re + 1j * Lambda_im).astype(jnp.complex64)
            B_tilde = (B[..., 0] + 1j * B[..., 1]).astype(jnp.complex64)
            C_tilde = (C[..., 0] + 1j * C[..., 1]).astype(jnp.complex64)
            step = jnp.exp(log_step)
            Lambda_bar = jnp.exp(Lambda * step)
            B_bar = (1.0 / Lambda * (Lambda_bar - 1.0))[:, None] * B_tilde
            Bu = jnp.einsum('blh,ph->blp', input_sequence.astype(jnp.complex64), B_bar)
            xs = jax.vmap(lambda bu: _scan_ssm(Lambda_bar, bu))(Bu)
            state = xs[:, -1, :]
            ys = 2.0 * jnp.einsum('blp,hp->blh', xs, C_tilde).real
            out = ys + D * input_sequence
            return (out, state)
        key = jax.random.key(seed)
        ks = jax.random.split(key, 6)
        input_sequence = jax.random.normal(ks[0], (B_, L_, H_), jnp.float32)
        Lambda_re = -0.5 * jnp.ones((P_,), jnp.float32)
        Lambda_im = jnp.pi * jnp.arange(P_, dtype=jnp.float32)
        B = jax.random.normal(ks[1], (P_, H_, 2), jnp.float32) / np.sqrt(2.0 * H_)
        C = jax.random.normal(ks[2], (H_, P_, 2), jnp.float32) / np.sqrt(float(P_))
        D = jax.random.normal(ks[3], (H_,), jnp.float32)
        log_step = jax.random.uniform(ks[4], (P_,), jnp.float32, float(np.log(DT_MIN)), float(np.log(DT_MAX)))
        return dict(input_sequence=input_sequence, Lambda_re=Lambda_re, Lambda_im=Lambda_im, B=B, C=C, D=D, log_step=log_step)
    _L3_attn_all = _L3_attn_setup()
    _L3_attn_in = {k: v for k, v in _L3_attn_all.items() if k in ('Lambda_re', 'Lambda_im', 'B', 'C', 'D', 'log_step')}
    del _L3_attn_all

    def _L3_ffn_setup():
        import jax, jax.numpy as jnp
        import numpy as np
        B, S, D = (4, 512, 128)
        I = 96
        E = 16
        K = 2

        def _inv_softplus(v):
            return float(np.log(np.expm1(v)))

        def swiglu5(h, alpha, gate_scale, up_shift, gate_clamp_raw, up_clamp_raw):
            gate_clamp = jax.nn.softplus(gate_clamp_raw)
            up_clamp = jax.nn.softplus(up_clamp_raw)
            g = jnp.clip(h[..., ::2], -gate_clamp, gate_clamp)
            u = jnp.clip(h[..., 1::2], -up_clamp, up_clamp)
            return g * jax.nn.sigmoid(g * alpha) * gate_scale * (u + up_shift)
        key = jax.random.key(seed)
        ks = jax.random.split(key, 10)
        std = 0.02
        raw = _inv_softplus(7.0)
        act = jnp.array([1.702, 1.0, 1.0, raw, raw], dtype=jnp.float32)
        return {'x': jax.random.normal(ks[0], (B, S, D), dtype=jnp.float32), 'gate_w': jax.random.normal(ks[1], (D, E), dtype=jnp.float32) * 0.01, 'gate_b': jnp.zeros((E,), dtype=jnp.float32), 'shared_w1': jax.random.normal(ks[2], (D, 2 * I), dtype=jnp.float32) * std, 'shared_b1': jnp.zeros((2 * I,), dtype=jnp.float32), 'shared_w2': jax.random.normal(ks[3], (I, D), dtype=jnp.float32) * std, 'shared_b2': jnp.zeros((D,), dtype=jnp.float32), 'shared_act': act, 'expert_w1': jax.random.normal(ks[4], (E, D, 2 * I), dtype=jnp.float32) * std, 'expert_b1': jnp.zeros((E, 2 * I), dtype=jnp.float32), 'expert_w2': jax.random.normal(ks[5], (E, I, D), dtype=jnp.float32) * std, 'expert_b2': jnp.zeros((E, D), dtype=jnp.float32), 'expert_act': jnp.tile(act[None, :], (E, 1))}
    _L3_ffn_all = _L3_ffn_setup()
    _L3_ffn_in = {k: v for k, v in _L3_ffn_all.items() if k in ('gate_w', 'gate_b', 'shared_w1', 'shared_b1', 'shared_w2', 'shared_b2', 'shared_act', 'expert_w1', 'expert_b1', 'expert_w2', 'expert_b2', 'expert_act')}
    del _L3_ffn_all
    return {'x': x, 'L0_tok_feature_table': _L0_tok_in['feature_table'], 'L0_tok_special_embed': _L0_tok_in['special_embed'], 'L0_tok_W1': _L0_tok_in['W1'], 'L0_tok_b1': _L0_tok_in['b1'], 'L0_tok_W2': _L0_tok_in['W2'], 'L0_tok_b2': _L0_tok_in['b2'], 'L0_attn_Wq': _L0_attn_in['Wq'], 'L0_attn_bq': _L0_attn_in['bq'], 'L0_attn_Wk': _L0_attn_in['Wk'], 'L0_attn_bk': _L0_attn_in['bk'], 'L0_attn_Wv': _L0_attn_in['Wv'], 'L0_attn_bv': _L0_attn_in['bv'], 'L0_ffn_fc1_w': _L0_ffn_in['fc1_w'], 'L0_ffn_fc1_b': _L0_ffn_in['fc1_b'], 'L0_ffn_fc2_w': _L0_ffn_in['fc2_w'], 'L0_ffn_fc2_b': _L0_ffn_in['fc2_b'], 'L1_attn_w_attn': _L1_attn_in['w_attn'], 'L1_attn_w_proj': _L1_attn_in['w_proj'], 'L1_ffn_ln_g': _L1_ffn_in['ln_g'], 'L1_ffn_ln_b': _L1_ffn_in['ln_b'], 'L1_ffn_w_r': _L1_ffn_in['w_r'], 'L1_ffn_b_r': _L1_ffn_in['b_r'], 'L1_ffn_W1': _L1_ffn_in['W1'], 'L1_ffn_b1': _L1_ffn_in['b1'], 'L1_ffn_W2': _L1_ffn_in['W2'], 'L1_ffn_b2': _L1_ffn_in['b2'], 'L2_attn_w_qkv': _L2_attn_in['w_qkv'], 'L2_attn_w_proj': _L2_attn_in['w_proj'], 'L2_attn_b_proj': _L2_attn_in['b_proj'], 'L2_ffn_pos_w': _L2_ffn_in['pos_w'], 'L2_ffn_pos_b': _L2_ffn_in['pos_b'], 'L2_ffn_qkv_w': _L2_ffn_in['qkv_w'], 'L2_ffn_qkv_b': _L2_ffn_in['qkv_b'], 'L2_ffn_wo_w': _L2_ffn_in['wo_w'], 'L2_ffn_wo_b': _L2_ffn_in['wo_b'], 'L3_attn_Lambda_re': _L3_attn_in['Lambda_re'], 'L3_attn_Lambda_im': _L3_attn_in['Lambda_im'], 'L3_attn_B': _L3_attn_in['B'], 'L3_attn_C': _L3_attn_in['C'], 'L3_attn_D': _L3_attn_in['D'], 'L3_attn_log_step': _L3_attn_in['log_step'], 'L3_ffn_gate_w': _L3_ffn_in['gate_w'], 'L3_ffn_gate_b': _L3_ffn_in['gate_b'], 'L3_ffn_shared_w1': _L3_ffn_in['shared_w1'], 'L3_ffn_shared_b1': _L3_ffn_in['shared_b1'], 'L3_ffn_shared_w2': _L3_ffn_in['shared_w2'], 'L3_ffn_shared_b2': _L3_ffn_in['shared_b2'], 'L3_ffn_shared_act': _L3_ffn_in['shared_act'], 'L3_ffn_expert_w1': _L3_ffn_in['expert_w1'], 'L3_ffn_expert_b1': _L3_ffn_in['expert_b1'], 'L3_ffn_expert_w2': _L3_ffn_in['expert_w2'], 'L3_ffn_expert_b2': _L3_ffn_in['expert_b2'], 'L3_ffn_expert_act': _L3_ffn_in['expert_act']}

def reference(x, L0_tok_feature_table, L0_tok_special_embed, L0_tok_W1, L0_tok_b1, L0_tok_W2, L0_tok_b2, L0_attn_Wq, L0_attn_bq, L0_attn_Wk, L0_attn_bk, L0_attn_Wv, L0_attn_bv, L0_ffn_fc1_w, L0_ffn_fc1_b, L0_ffn_fc2_w, L0_ffn_fc2_b, L1_attn_w_attn, L1_attn_w_proj, L1_ffn_ln_g, L1_ffn_ln_b, L1_ffn_w_r, L1_ffn_b_r, L1_ffn_W1, L1_ffn_b1, L1_ffn_W2, L1_ffn_b2, L2_attn_w_qkv, L2_attn_w_proj, L2_attn_b_proj, L2_ffn_pos_w, L2_ffn_pos_b, L2_ffn_qkv_w, L2_ffn_qkv_b, L2_ffn_wo_w, L2_ffn_wo_b, L3_attn_Lambda_re, L3_attn_Lambda_im, L3_attn_B, L3_attn_C, L3_attn_D, L3_attn_log_step, L3_ffn_gate_w, L3_ffn_gate_b, L3_ffn_shared_w1, L3_ffn_shared_b1, L3_ffn_shared_w2, L3_ffn_shared_b2, L3_ffn_shared_act, L3_ffn_expert_w1, L3_ffn_expert_b1, L3_ffn_expert_w2, L3_ffn_expert_b2, L3_ffn_expert_act):
    import jax
    import jax.numpy as jnp

    def _L0_tok_ref(feature_table, special_embed, W1, b1, W2, b2, token_ids):
        import jax, jax.numpy as jnp
        import numpy as np
        import math
        D_MODEL = 128
        HIDDEN = 64
        FEATURE_DIM = 37
        MAX_TOKEN_ID = 120
        SPECIAL_IDS = np.array([0, 107, 108, 109], dtype=np.int64)

        def gelu_approx(x):
            c = math.sqrt(2.0 / math.pi)
            return 0.5 * x * (1.0 + jnp.tanh(c * (x + 0.044715 * x * x * x)))
        special_ids = jnp.asarray(SPECIAL_IDS)
        matches = token_ids[..., None] == special_ids
        is_special = jnp.any(matches, axis=-1)
        special_idx = jnp.argmax(matches, axis=-1)
        special_embeds = special_embed[special_idx]
        feats = feature_table[token_ids]
        h = jnp.maximum(feats @ W1 + b1, 0.0)
        prod = h @ W2 + b2
        prod = gelu_approx(prod) * math.sqrt(D_MODEL)
        return jnp.where(is_special[..., None], special_embeds, prod)

    def _L0_attn_ref(x, Wq, bq, Wk, bk, Wv, bv):
        import jax, jax.numpy as jnp
        import numpy as np
        B, N, D = (4, 512, 128)
        q = jnp.einsum('bnd,ed->bne', x, Wq) + bq
        k = jnp.einsum('bnd,ed->bne', x, Wk) + bk
        v = jnp.einsum('bnd,ed->bne', x, Wv) + bv
        scale = 1.0 / jnp.sqrt(jnp.asarray(q.shape[-1], q.dtype))
        scores = jnp.einsum('bqd,bkd->bqk', q, k) * scale
        weights = jax.nn.softmax(scores, axis=-1)
        return jnp.einsum('bqk,bkd->bqd', weights, v)

    def _L0_ffn_ref(x, fc1_w, fc1_b, fc2_w, fc2_b):
        import jax, jax.numpy as jnp
        import numpy as np

        def _haar_dwt2(x):
            a = x[:, ::2, ::2]
            b = x[:, ::2, 1::2]
            c = x[:, 1::2, ::2]
            d = x[:, 1::2, 1::2]
            ll = (a + b + c + d) * 0.5
            lh = (a + b - c - d) * 0.5
            hl = (a - b + c - d) * 0.5
            hh = (a - b - c + d) * 0.5
            return (ll, lh, hl, hh)

        def _haar_idwt2(ll, lh, hl, hh):
            a = (ll + lh + hl + hh) * 0.5
            b = (ll + lh - hl - hh) * 0.5
            c = (ll - lh + hl - hh) * 0.5
            d = (ll - lh - hl + hh) * 0.5
            B, H2, W2 = ll.shape
            out = jnp.zeros((B, 2 * H2, 2 * W2), ll.dtype)
            out = out.at[:, ::2, ::2].set(a)
            out = out.at[:, ::2, 1::2].set(b)
            out = out.at[:, 1::2, ::2].set(c)
            out = out.at[:, 1::2, 1::2].set(d)
            return out

        def _interp_linear_last(x, m):
            n = x.shape[-1]
            pos = jnp.linspace(0.0, 1.0, m, dtype=x.dtype) * (n - 1)
            i0 = jnp.clip(jnp.floor(pos).astype(jnp.int32), 0, n - 2)
            w = pos - i0.astype(x.dtype)
            return x[..., i0] * (1.0 - w) + x[..., i0 + 1] * w
        b, f, c = x.shape
        ll, lh, hl, hh = _haar_dwt2(x)
        ll_up = _interp_linear_last(ll, c)
        h = jax.nn.gelu(jnp.einsum('bfc,hc->bfh', ll_up, fc1_w) + fc1_b, approximate=False)
        ll_new = jnp.einsum('bfh,oh->bfo', h, fc2_w) + fc2_b
        return _haar_idwt2(ll_new, lh, hl, hh)

    def _L1_attn_ref(x, w_attn, w_proj):
        import jax, jax.numpy as jnp
        import numpy as np
        import math
        H, D, DEG = (8, 64, 2)
        GATE_BIAS = 6.906768

        def _rope(x, sin, cos):
            x1, x2 = (x[..., ::2], x[..., 1::2])
            s = sin[None, :, None, :]
            c = cos[None, :, None, :]
            even = x1 * c - x2 * s
            odd = x2 * c + x1 * s
            return jnp.stack([even, odd], axis=-1).reshape(x.shape)

        def _forward(x, w_attn, w_proj):
            B, T, C = x.shape
            h, d, deg = (H, D, DEG)
            hd = h * d
            scale = 1.0 / math.sqrt(d)
            qkvg = x @ w_attn
            q = qkvg[..., :hd].reshape(B, T, h, d)
            k = qkvg[..., hd:2 * hd].reshape(B, T, h, d)
            v = qkvg[..., 2 * hd:3 * hd].reshape(B, T, h, d)
            log_g = jax.nn.log_sigmoid(GATE_BIAS + qkvg[..., 3 * hd:].astype(jnp.float32))
            pos = jnp.arange(T, dtype=jnp.float32)
            div = 2.0 * math.pi / float(T) ** (jnp.arange(0, d, 2, dtype=jnp.float32) / d)
            ang = pos[:, None] * div[None, :]
            sin, cos = (jnp.sin(ang), jnp.cos(ang))
            q = _rope(q, sin, cos)
            k = _rope(k, sin, cos)
            L = jnp.cumsum(log_g, axis=1).transpose(0, 2, 1)
            qk = jnp.einsum('bthd,bshd->bhts', q, k) * scale
            log_gate = L[:, :, :, None] - L[:, :, None, :]
            causal = jnp.tril(jnp.ones((T, T), dtype=bool))
            scores = jnp.where(causal, qk ** deg * jnp.exp(log_gate), 0.0)
            denom = jnp.maximum(scores.sum(-1, keepdims=True), 1e-06)
            y = jnp.einsum('bhts,bshd->bthd', scores / denom, v)
            return y.reshape(B, T, hd) @ w_proj
        return _forward(x, w_attn, w_proj)

    def _L1_ffn_ref(x, ln_g, ln_b, w_r, b_r, W1, b1, W2, b2):
        import jax, jax.numpy as jnp
        import numpy as np
        D = 128
        E = 8
        K = 2
        EXP = 4
        LN_EPS = 1e-05
        B, T, d = x.shape
        mu = jnp.mean(x, axis=-1, keepdims=True)
        var = jnp.mean(jnp.square(x - mu), axis=-1, keepdims=True)
        h = (x - mu) * jax.lax.rsqrt(var + LN_EPS) * ln_g + ln_b
        logits = jnp.einsum('btd,ed->bte', h, w_r) + b_r
        topk_vals, topk_idx = jax.lax.top_k(logits, K)
        gates = jax.nn.softmax(topk_vals, axis=-1)
        hf = h.reshape(B * T, d)
        hid = jax.nn.gelu(jnp.einsum('nd,edf->nef', hf, W1) + b1, approximate=False)
        expert_stack = jnp.einsum('nef,efd->ned', hid, W2) + b2
        idx_flat = topk_idx.reshape(B * T, K)
        gates_flat = gates.reshape(B * T, K)
        gathered = jnp.take_along_axis(expert_stack, idx_flat[:, :, None], axis=1)
        mixed = jnp.sum(gathered * gates_flat[:, :, None], axis=1).reshape(B, T, d)
        return x + mixed

    def _L2_attn_ref(x, w_qkv, w_proj, b_proj):
        import jax, jax.numpy as jnp
        import numpy as np
        H = 8
        W = 64
        SHIFT = True
        DIM = 128
        SCALE = (DIM // H) ** (-0.5)
        B, N, C = x.shape
        if SHIFT:
            x = jnp.roll(x, -W // 2, axis=1)
        pad = (W - N % W) % W
        if pad:
            x = jnp.pad(x, ((0, 0), (0, pad), (0, 0)))
        nw = x.shape[1] // W
        xw = x.reshape(B * nw, W, C)
        qkv = xw @ w_qkv.T
        qkv = qkv.reshape(B * nw, W, 3, H, C // H)
        q, k, v = (qkv[:, :, 0], qkv[:, :, 1], qkv[:, :, 2])
        attn = jnp.einsum('bwhd,bwgd->bwhg', q, k) * SCALE
        attn = jax.nn.softmax(attn, axis=-1)
        out = jnp.einsum('bwhg,bwgd->bwhd', attn, v)
        out = out.transpose(0, 2, 1, 3).reshape(B * nw, W, C)
        out = out @ w_proj.T + b_proj
        out = out.reshape(B, nw * W, C)[:, :N]
        if SHIFT:
            out = jnp.roll(out, W // 2, axis=1)
        return out

    def _L2_ffn_ref(x, pos_w, pos_b, qkv_w, qkv_b, wo_w, wo_b):
        import jax, jax.numpy as jnp
        import numpy as np
        from jax import lax
        N, M, DIM, HEADS, TOPK = (4, 512, 128, 8, 16)

        def _split_heads(t, h):
            n, m, c = t.shape
            return t.reshape(n, m, h, c // h).transpose(0, 2, 1, 3).reshape(n * h, m, c // h)
        n, m, c = x.shape
        h = HEADS
        scale = c ** (-0.5)
        pos = lax.conv_general_dilated(x.transpose(0, 2, 1), pos_w, window_strides=(1,), padding=[(1, 1)], feature_group_count=c, dimension_numbers=('NCH', 'OIH', 'NCH'))
        x = x + (pos + pos_b[None, :, None]).transpose(0, 2, 1)
        qkv = x @ qkv_w.T + qkv_b
        q, k, v = jnp.split(qkv, [c, 2 * c], axis=-1)
        q = _split_heads(q, h)
        k = _split_heads(k, h)
        v = _split_heads(v, h)
        qd = lax.stop_gradient(q)
        kd = lax.stop_gradient(k)
        logits = jnp.einsum('bmd,bpd->bmp', qd * scale, kd)
        _, idx = lax.top_k(logits, TOPK)
        gather = jax.vmap(lambda t, i: t[i])
        k_sel = gather(k, idx)
        v_sel = gather(v, idx)
        attn = jax.nn.softmax(jnp.einsum('bmd,bmkd->bmk', q * scale, k_sel), axis=-1)
        out = jnp.einsum('bmk,bmkd->bmd', attn, v_sel)
        d = c // h
        out = out.reshape(n, h, m, d).transpose(0, 2, 1, 3).reshape(n, m, c)
        return out @ wo_w.T + wo_b

    def _L3_attn_ref(input_sequence, Lambda_re, Lambda_im, B, C, D, log_step):
        import jax, jax.numpy as jnp
        import numpy as np
        B_, L_, H_, P_ = (8, 1024, 128, 64)
        DT_MIN, DT_MAX = (0.001, 0.1)

        def _scan_ssm(Lambda_bar, Bu):
            A = jnp.broadcast_to(Lambda_bar, Bu.shape)

            def binop(e_i, e_j):
                a_i, b_i = e_i
                a_j, b_j = e_j
                return (a_j * a_i, a_j * b_i + b_j)
            _, xs = jax.lax.associative_scan(binop, (A, Bu))
            return xs

        def _reference_tuple_inner(input_sequence, Lambda_re, Lambda_im, B, C, D, log_step):
            Lambda = (Lambda_re + 1j * Lambda_im).astype(jnp.complex64)
            B_tilde = (B[..., 0] + 1j * B[..., 1]).astype(jnp.complex64)
            C_tilde = (C[..., 0] + 1j * C[..., 1]).astype(jnp.complex64)
            step = jnp.exp(log_step)
            Lambda_bar = jnp.exp(Lambda * step)
            B_bar = (1.0 / Lambda * (Lambda_bar - 1.0))[:, None] * B_tilde
            Bu = jnp.einsum('blh,ph->blp', input_sequence.astype(jnp.complex64), B_bar)
            xs = jax.vmap(lambda bu: _scan_ssm(Lambda_bar, bu))(Bu)
            state = xs[:, -1, :]
            ys = 2.0 * jnp.einsum('blp,hp->blh', xs, C_tilde).real
            out = ys + D * input_sequence
            return (out, state)
        return _reference_tuple_inner(input_sequence, Lambda_re, Lambda_im, B, C, D, log_step)[0]

    def _L3_ffn_ref(x, gate_w, gate_b, shared_w1, shared_b1, shared_w2, shared_b2, shared_act, expert_w1, expert_b1, expert_w2, expert_b2, expert_act):
        import jax, jax.numpy as jnp
        import numpy as np
        B, S, D = (4, 512, 128)
        I = 96
        E = 16
        K = 2

        def _inv_softplus(v):
            return float(np.log(np.expm1(v)))

        def swiglu5(h, alpha, gate_scale, up_shift, gate_clamp_raw, up_clamp_raw):
            gate_clamp = jax.nn.softplus(gate_clamp_raw)
            up_clamp = jax.nn.softplus(up_clamp_raw)
            g = jnp.clip(h[..., ::2], -gate_clamp, gate_clamp)
            u = jnp.clip(h[..., 1::2], -up_clamp, up_clamp)
            return g * jax.nn.sigmoid(g * alpha) * gate_scale * (u + up_shift)
        shape = x.shape
        xf = x.reshape(-1, shape[-1])
        h = xf @ shared_w1 + shared_b1
        t = swiglu5(h, shared_act[0], shared_act[1], shared_act[2], shared_act[3], shared_act[4])
        z = t @ shared_w2 + shared_b2
        gate_logits = xf @ gate_w + gate_b
        gate_probs = jax.nn.softmax(gate_logits, -1)
        w, idx = jax.lax.top_k(gate_probs, K)
        w = w / jnp.sum(w, axis=-1, keepdims=True)
        cw = jnp.sum(jax.nn.one_hot(idx, E, dtype=xf.dtype) * w[..., None], axis=1)
        he = jnp.einsum('nd,edh->enh', xf, expert_w1) + expert_b1[:, None, :]
        a = expert_act
        te = swiglu5(he, a[:, 0, None, None], a[:, 1, None, None], a[:, 2, None, None], a[:, 3, None, None], a[:, 4, None, None])
        oe = jnp.einsum('enh,ehd->end', te, expert_w2) + expert_b2[:, None, :]
        y = jnp.einsum('ne,end->nd', cw, oe)
        return (y + z).reshape(shape)
    h = _L0_tok_ref(L0_tok_feature_table, L0_tok_special_embed, L0_tok_W1, L0_tok_b1, L0_tok_W2, L0_tok_b2, x)
    h = h + _L0_attn_ref(_layernorm(h, axis=-1), L0_attn_Wq, L0_attn_bq, L0_attn_Wk, L0_attn_bk, L0_attn_Wv, L0_attn_bv)
    h = h + _L0_ffn_ref(_layernorm(h, axis=-1), L0_ffn_fc1_w, L0_ffn_fc1_b, L0_ffn_fc2_w, L0_ffn_fc2_b)
    h = h + _L1_attn_ref(_layernorm(h, axis=-1), L1_attn_w_attn, L1_attn_w_proj)
    h = h + _L1_ffn_ref(_layernorm(h, axis=-1), L1_ffn_ln_g, L1_ffn_ln_b, L1_ffn_w_r, L1_ffn_b_r, L1_ffn_W1, L1_ffn_b1, L1_ffn_W2, L1_ffn_b2)
    h = h + _L2_attn_ref(_layernorm(h, axis=-1), L2_attn_w_qkv, L2_attn_w_proj, L2_attn_b_proj)
    h = h + _L2_ffn_ref(_layernorm(h, axis=-1), L2_ffn_pos_w, L2_ffn_pos_b, L2_ffn_qkv_w, L2_ffn_qkv_b, L2_ffn_wo_w, L2_ffn_wo_b)
    h = h + _L3_attn_ref(_layernorm(h, axis=-1), L3_attn_Lambda_re, L3_attn_Lambda_im, L3_attn_B, L3_attn_C, L3_attn_D, L3_attn_log_step)
    h = h + _L3_ffn_ref(_layernorm(h, axis=-1), L3_ffn_gate_w, L3_ffn_gate_b, L3_ffn_shared_w1, L3_ffn_shared_b1, L3_ffn_shared_w2, L3_ffn_shared_b2, L3_ffn_shared_act, L3_ffn_expert_w1, L3_ffn_expert_b1, L3_ffn_expert_w2, L3_ffn_expert_b2, L3_ffn_expert_act)
    return h

_drawn_inputs = setup_inputs


def setup_inputs(seed=0):
    import zlib

    import numpy as np

    out = dict(_drawn_inputs(seed))
    spreads = {'L0_ffn_fc1_b': (0.0, 0.8),
     'L0_ffn_fc2_b': (0.0, 0.8),
     'L1_ffn_ln_g': (1.0, 0.6),
     'L1_ffn_ln_b': (0.0, 0.367),
     'L1_ffn_b_r': (0.0, 0.8),
     'L1_ffn_b1': (0.0, 0.8),
     'L1_ffn_b2': (0.0, 0.626),
     'L3_attn_Lambda_re': (-0.5, 0.6),
     'L3_ffn_gate_b': (0.0, 0.648),
     'L3_ffn_shared_b1': (0.0, 0.8),
     'L3_ffn_shared_b2': (0.0, 0.55),
     'L3_ffn_expert_b1': (0.0, 0.8),
     'L3_ffn_expert_b2': (0.0, 0.738)}
    factors = {'L0_tok_b1': 5.024,
     'L0_tok_b2': 3.629,
     'L0_attn_Wq': 6.701,
     'L0_attn_bq': 8.0,
     'L0_attn_Wk': 6.675,
     'L0_attn_bk': 8.0,
     'L0_attn_bv': 4.595,
     'L0_ffn_fc1_w': 8.0,
     'L0_ffn_fc2_w': 8.0,
     'L1_attn_w_attn': 5.315,
     'L1_attn_w_proj': 5.255,
     'L2_attn_w_qkv': 8.0,
     'L2_attn_w_proj': 8.0,
     'L2_attn_b_proj': 8.0,
     'L2_ffn_pos_w': 8.0,
     'L2_ffn_pos_b': 8.0,
     'L2_ffn_qkv_w': 8.0,
     'L2_ffn_qkv_b': 8.0,
     'L2_ffn_wo_w': 8.0,
     'L2_ffn_wo_b': 8.0,
     'L3_ffn_gate_w': 6.825,
     'L3_ffn_shared_w1': 8.0,
     'L3_ffn_shared_w2': 8.0,
     'L3_ffn_expert_w1': 8.0,
     'L3_ffn_expert_w2': 8.0}
    for name, (base, spread) in spreads.items():
        noise = np.random.default_rng([zlib.crc32(name.encode()), seed]).standard_normal(out[name].shape)
        drawn = base * np.exp(spread * noise) if base else spread * noise
        out[name] = jnp.asarray(drawn.astype(out[name].dtype))
    for name, factor in factors.items():
        out[name] = (out[name] * factor).astype(out[name].dtype)
    return out
```

```python
from contextlib import ExitStack

import numpy as np

import concourse.bass as bass
from concourse import mybir

F32 = mybir.dt.float32
I32 = mybir.dt.int32
ACT = mybir.ActivationFunctionType
ALU = mybir.AluOpType
AX = mybir.AxisListType

P = 128
D = 128
B = 2
S = 1024
N = B * S
TILES = N // P
CH = S // P
VOC = 121
EPS = 1e-5
BANK = 512
BIG = 1.0e30
FROM = 1


def signals(nc, m, prefix):
    def sem(name):
        m.signals.append(nc.alloc_semaphore(prefix + name))
        return m.signals[-1]

    return sem


def recycle(nc, m, w):
    nc.clear_and_free_semaphores(m.signals)
    m.signals = []
    nc.all_engine_barrier()


class Core:
    pass


def row(ap1d):
    return ap1d.rearrange("(a d) -> a d", a=1)


def col(ap1d):
    return ap1d.rearrange("(d a) -> d a", a=1)


RET_H, RET_D = 8, 64
CONST_COLS = {"ident": 128, "interp": 128, "pairmean": 128, "one": 128, "sel8": 8 * 128, "ropecos": S, "ropesin": S,
              "expand": 256, "pid": 1, "lower8": 64, "lower16": 256}


def constants():
    out = {}
    out["ident"] = np.eye(P, dtype=np.float32)
    half, pos = D // 2, np.linspace(0.0, 1.0, D, dtype=np.float32) * np.float32(D // 2 - 1)
    i0 = np.clip(np.floor(pos).astype(np.int32), 0, half - 2)
    w = pos - i0.astype(np.float32)
    up = np.zeros((D, half), np.float32)
    up[np.arange(D), i0] += 1.0 - w
    up[np.arange(D), i0 + 1] += w
    out["interp"] = np.repeat(up, 2, axis=1) * np.float32(0.5)
    pair = np.arange(D) // 2
    out["pairmean"] = np.where(pair[:, None] == pair[None, :], np.float32(-0.25), np.float32(0)).astype(np.float32)
    out["one"] = np.ones((P, P), np.float32)
    sel = np.zeros((P, 8, P), np.float32)
    for h in range(8):
        sel[h, h, :] = 1.0
    out["sel8"] = sel.reshape(P, -1)
    div = np.float32(2.0 * np.pi) / np.power(np.float32(S), np.arange(0, RET_D, 2, dtype=np.float32) / np.float32(RET_D))
    ang = np.arange(S, dtype=np.float32)[:, None] * div[None, :].astype(np.float32)
    freq = (np.arange(P) % RET_D) // 2
    out["ropecos"] = np.cos(ang).T[freq].astype(np.float32)
    out["ropesin"] = np.sin(ang).T[freq].astype(np.float32)
    tok = np.arange(2 * P).reshape(1, 2, P)
    out["expand"] = (np.arange(P).reshape(P, 1, 1) == tok // 2).astype(np.float32).reshape(P, 256)
    out["pid"] = np.arange(P, dtype=np.float32)[:, None]
    for e in (8, 16):
        low = (np.arange(e)[:, None] > np.arange(e)[None, :]).astype(np.float32)
        out[f"lower{e}"] = np.broadcast_to(low.reshape(1, -1), (P, e * e))
    return np.ascontiguousarray(np.concatenate([out[k] for k in CONST_COLS], axis=1), dtype=np.float32)


def layernorm(nc, m, name, src, dst, dstT, gain=None, shift=None):
    with ExitStack() as ctx:
        stats = ctx.enter_context(nc.sbuf_tensor(f"{name}_stats", [P, TILES, 6], F32))
        small = ctx.enter_context(nc.sbuf_tensor(f"{name}_small", [P, 8, TILES], F32))
        ps = ctx.enter_context(nc.psum_tensor(f"{name}_ps", [P, 4, BANK], F32))
        sem = signals(nc, m, f"{name}_")
        chain, var_ready, pool_step, normed, turned = (sem(x) for x in ("chain", "var_ready", "pool_step", "normed", "turned"))
        mean, rstd = small[:, 0, :], small[:, 1, :]
        diff, sumsq, var = small[:, 2, :], small[:, 3, :], small[:, 4, :]
        block = ctx.enter_context(nc.Block())

        @block.vector
        def _(dve):
            for t in range(TILES):
                ins = dve.bn_stats(stats[:, t, :], src[:, t, :])
            ins.then_inc(chain, 1)
            dve.wait_ge(chain, 1)
            dve.tensor_tensor(diff, stats[:, :, 1], stats[:, :, 4], ALU.subtract)
            dve.tensor_tensor(sumsq, stats[:, :, 2], stats[:, :, 5], ALU.add)
            dve.tensor_tensor(mean, stats[:, :, 1], stats[:, :, 4], ALU.add).then_inc(chain, 1)
            dve.wait_ge(chain, 2)
            dve.tensor_scalar(mean, mean, 0.5, None, ALU.mult)
            dve.scalar_tensor_tensor(diff, diff, 0.25, diff, ALU.mult, ALU.mult).then_inc(chain, 1)
            dve.wait_ge(chain, 3)
            dve.scalar_tensor_tensor(var, sumsq, 1.0 / D, diff, ALU.mult, ALU.add).then_inc(var_ready, 1)
            dve.wait_ge(pool_step, 2)
            for t in range(TILES):
                dve.tensor_scalar(dst[:, t, :], src[:, t, :], mean[:, t:t + 1], rstd[:, t:t + 1],
                                  ALU.subtract, ALU.mult).then_inc(normed, 1)

        @block.gpsimd
        def _(pool):
            pool.wait_ge(var_ready, 1)
            pool.tensor_scalar(var, var, EPS, None, ALU.add).then_inc(pool_step, 1)
            pool.wait_ge(pool_step, 1)
            pool.tensor_tensor(rstd, var, m.neghalf[:, :], ALU.pow).then_inc(pool_step, 1)

        if dstT is None:
            return

        @block.tensor
        def _(pe):
            for t in range(TILES):
                pe.wait_ge(normed, t + 1)
                ins = pe.transpose(ps[:, t // 4, (t % 4) * P:(t % 4 + 1) * P], dst[:, t, :], m.ident)
                if t % 4 == 3:
                    ins.then_inc(turned, 1)

        @block.scalar
        def _(act):
            for g in range(TILES // 4):
                act.wait_ge(turned, g + 1)
                out = dstT[:, g * BANK:(g + 1) * BANK]
                if gain is None:
                    act.activation(out, ps[:, g, :], ACT.Copy)
                else:
                    act.activation(out, ps[:, g, :], ACT.Identity, bias=shift, scale=gain)


def load_stage(nc, m, w):
    with ExitStack() as ctx:
        def raw(name, shape, dt=F32):
            return ctx.enter_context(nc.sbuf_tensor(f"raw_{name}", shape, dt))

        sem = signals(nc, m, "")

        raw_qkv0 = raw("qkv0", [P, 3, D])
        raw_fc1 = raw("fc1", [P, 4, D])
        raw_fc2 = raw("fc2", [64, 512])
        raw_qkv2 = raw("qkv2", [P, 3, D])
        raw_proj2 = raw("proj2", [P, D])
        raw_qkvw = raw("qkvw", [P, 3, D])
        raw_wo = raw("wo", [P, D])
        raw_wr = raw("wr", [8, D])
        ps = ctx.enter_context(nc.psum_tensor("turn_ps", [P, 8, BANK], F32))
        w_first, w_turn = sem("w_first"), sem("w_turn")
        turned, copied = sem("w_turned"), sem("w_copied")
        sp_loads = [
            (m.consts[:, :], w["consts"]),
            (m.ids[:, :], w["x"].rearrange("(o b) n -> o (b n)", o=1).broadcast_to([P, N])),
            (raw_qkv0[:, 0, :], w["L0_attn_Wq"]), (raw_qkv0[:, 1, :], w["L0_attn_Wk"]), (raw_qkv0[:, 2, :], w["L0_attn_Wv"]),
            (m.feat[:, :], w["L0_tok_feature_table"]), (m.tok_w1[:, :], w["L0_tok_W1"]), (m.tok_w2[:, :], w["L0_tok_W2"]),
            (m.tok_b1[:, :], col(w["L0_tok_b1"])), (m.tok_b2[:, :], row(w["L0_tok_b2"])),
            (m.bq[:, :], col(w["L0_attn_bq"])), (m.bk[:, :], col(w["L0_attn_bk"])), (m.bv[:, :], row(w["L0_attn_bv"])),
            (raw_fc1[:, :, :], w["L0_ffn_fc1_w"].rearrange("(c p) d -> p c d", p=P)),
            (raw_fc2[:, :], w["L0_ffn_fc2_w"]),
            (m.fc1_b[:, :], w["L0_ffn_fc1_b"].rearrange("(c p) -> p c", p=P)),
            (m.fc2_b[:, :], row(w["L0_ffn_fc2_b"])),
        ]
        act_loads = [
            (raw_qkv2[:, :, :], w["L2_attn_w_qkv"].rearrange("(c p) d -> p c d", p=P)),
            (raw_proj2[:, :], w["L2_attn_w_proj"]),
            (raw_qkvw[:, :, :], w["L2_ffn_qkv_w"].rearrange("(c p) d -> p c d", p=P)),
            (raw_wo[:, :], w["L2_ffn_wo_w"]),
            (raw_wr[:, :], w["L1_ffn_w_r"]),
        ]
        m.n_first = 16 * len(sp_loads)
        jobs = [(raw_qkv0[:, c, :], m.wqkv0[:, c, :]) for c in range(3)]
        jobs += [(raw_fc1[:, c, :], m.fc1T[:, c, :]) for c in range(4)]
        jobs += [(raw_fc2[:, c * P:(c + 1) * P], m.fc2T[:, c, :]) for c in range(4)]
        n_early = len(jobs)
        jobs += [(raw_qkv2[:, c, :], m.wqkv2[:, c, :]) for c in range(3)]
        jobs += [(raw_proj2[:, :], m.wproj2[:, :])]
        jobs += [(raw_qkvw[:, c, :], m.wqkv3[:, c, :]) for c in range(3)]
        jobs += [(raw_wo[:, :], m.wo[:, :])]
        jobs += [(raw_wr[:, :], m.wrT[:, :])]
        block = ctx.enter_context(nc.Block())

        @block.sync
        def _(sp):
            for dst, src in sp_loads:
                sp.dma_start(dst, src, allow_slow_non_contiguous=True).then_inc(w_first, 16)
            for dst, src, s in m.later_loads:
                sp.dma_start(dst, src, allow_slow_non_contiguous=True).then_inc(s, 16)

        @block.scalar
        def _(act):
            for dst, src in act_loads:
                act.dma_start(dst, src, allow_slow_non_contiguous=True).then_inc(w_turn, 16)
            for i, (_, dst) in enumerate(jobs):
                act.wait_ge(turned, i + 1)
                r, c = dst.shape
                act.activation(dst, ps[0:r, i % 8, 0:c], ACT.Copy).then_inc(copied, 1)

        @block.tensor
        def _(pe):
            pe.wait_ge(w_first, 16 * len(sp_loads))
            for i, (src, dst) in enumerate(jobs):
                if i == n_early:
                    pe.wait_ge(w_turn, 16 * len(act_loads))
                if i >= 8:
                    pe.wait_ge(copied, i - 7)
                r, c = dst.shape
                pe.transpose(ps[0:r, i % 8, 0:c], src, m.ident[0:c, 0:c]).then_inc(turned, 1)


def stage_l0_tables(nc, m, w):
    with ExitStack() as ctx:
        def sb(name, shape, dt=F32):
            return ctx.enter_context(nc.sbuf_tensor(f"l0_{name}", shape, dt))

        sem = signals(nc, m, "l0_")

        featT, hid = sb("featT", [37, VOC]), sb("hid", [64, VOC])
        gelu, emb, emb_n = sb("gelu", [VOC, D]), sb("emb", [VOC, D]), sb("emb_n", [VOC, D])
        emb_nT = sb("emb_nT", [P, VOC])
        qT, kT, v = sb("qT", [P, VOC]), sb("kT", [P, VOC]), sb("v", [VOC, D + 1])
        vw = sb("vw", [VOC, B, D + 1])
        count, absent, diag = sb("count", [VOC, B]), sb("absent", [VOC, B]), sb("diag", [VOC, B, VOC])
        mx, nmx = sb("mx", [VOC, B]), sb("nmx", [VOC, B])
        prob, probT = sb("prob", [VOC, B, VOC]), sb("probT", [VOC, B, VOC])
        rden = sb("rden", [VOC, B])
        h1 = sb("h1", [VOC, B, D])
        stats, small = sb("stats", [VOC, 3, 6]), sb("small", [VOC, 3, 8])
        ps_a = ctx.enter_context(nc.psum_tensor("l0_ps_a", [P, BANK], F32))
        ps_e = ctx.enter_context(nc.psum_tensor("l0_ps_e", [P, BANK], F32))
        ps_q = ctx.enter_context(nc.psum_tensor("l0_ps_q", [P, BANK], F32))
        ps_k = ctx.enter_context(nc.psum_tensor("l0_ps_k", [P, BANK], F32))
        ps_v = ctx.enter_context(nc.psum_tensor("l0_ps_v", [P, BANK], F32))
        ps_s = ctx.enter_context(nc.psum_tensor("l0_ps_s", [P, BANK], F32))
        ps_f = ctx.enter_context(nc.psum_tensor("l0_ps_f", [P, BANK], F32))
        pe_step, act_step, dve_step, pool_step, special = (sem(x) for x in ("pe", "act", "dve", "pool", "special"))
        v_ones = sem("v_ones")
        SC = float(D) ** -0.5
        block = ctx.enter_context(nc.Block())

        @block.tensor
        def _(pe):
            pe.transpose(ps_a[0:37, 0:VOC], m.feat[:, :], m.ident[0:VOC, 0:VOC]).then_inc(pe_step, 1)
            pe.matmul(ps_f[:, :], m.interp, m.fc1T[:, :, :].rearrange("p c d -> p (c d)"), start=True, stop=True).then_inc(pe_step, 1)
            pe.wait_ge(act_step, 1)
            pe.matmul(ps_e[0:64, 0:VOC], m.tok_w1[:, :], featT[:, :], start=True, stop=True).then_inc(pe_step, 1)
            pe.wait_ge(act_step, 3)
            pe.matmul(ps_a[0:VOC, 0:D], hid[:, :], m.tok_w2[:, :], start=True, stop=False)
            pe.matmul(ps_a[0:VOC, 0:D], m.one[0:1, 0:VOC], m.tok_b2[:, :], start=False, stop=True).then_inc(pe_step, 1)
            pe.wait_ge(dve_step, 9)
            pe.transpose(ps_e[:, 0:VOC], emb_n[:, :], m.ident[0:VOC, 0:VOC]).then_inc(pe_step, 1)
            pe.wait_ge(act_step, 5)
            pe.matmul(ps_q[:, 0:VOC], m.wqkv0[:, 0, :], emb_nT[:, :], start=True, stop=True).then_inc(pe_step, 1)
            pe.matmul(ps_k[:, 0:VOC], m.wqkv0[:, 1, :], emb_nT[:, :], start=True, stop=True).then_inc(pe_step, 1)
            pe.matmul(ps_v[0:VOC, 0:D], emb_nT[:, :], m.wqkv0[:, 2, :], start=True, stop=False)
            pe.matmul(ps_v[0:VOC, 0:D], m.one[0:1, 0:VOC], m.bv[:, :], start=False, stop=True).then_inc(pe_step, 1)
            pe.wait_ge(act_step, 7)
            pe.wait_ge(dve_step, 12)
            for b in range(B):
                pe.matmul(ps_s[0:VOC, b * VOC:(b + 1) * VOC], qT[:, :], kT[:, :], start=True, stop=False)
                pe.matmul(ps_s[0:VOC, b * VOC:(b + 1) * VOC], m.one[0:VOC, 0:VOC], diag[:, b, :],
                          start=False, stop=True).then_inc(pe_step, 1)
            for b in range(B):
                pe.wait_ge(act_step, 8 + b)
                pe.transpose(ps_f[0:VOC, b * VOC:(b + 1) * VOC], prob[:, b, :], m.ident[0:VOC, 0:VOC]).then_inc(pe_step, 1)
            pe.wait_ge(act_step, 10)
            pe.wait_ge(dve_step, 16)
            for b in range(B):
                pe.matmul(ps_a[0:VOC, b * 256:b * 256 + D + 1], probT[:, b, :], vw[:, b, :], start=True, stop=True).then_inc(pe_step, 1)

        @block.scalar
        def _(act):
            act.wait_ge(pe_step, 1)
            act.activation(featT[:, :], ps_a[0:37, 0:VOC], ACT.Copy).then_inc(act_step, 1)
            act.wait_ge(pe_step, 2)
            act.activation(m.w1f[:, :], ps_f[:, :], ACT.Copy).then_inc(act_step, 1)
            act.wait_ge(pe_step, 3)
            act.activation(hid[:, :], ps_e[0:64, 0:VOC], ACT.Relu, bias=m.tok_b1[:, 0:1]).then_inc(act_step, 1)
            act.wait_ge(pe_step, 4)
            act.activation(gelu[:, :], ps_a[0:VOC, 0:D], ACT.Gelu_apprx_tanh).then_inc(act_step, 1)
            act.wait_ge(pe_step, 5)
            act.activation(emb_nT[:, :], ps_e[:, 0:VOC], ACT.Copy).then_inc(act_step, 1)
            act.wait_ge(pe_step, 6)
            act.activation(qT[:, :], ps_q[:, 0:VOC], ACT.Identity, bias=m.bq[:, 0:1]).then_inc(act_step, 1)
            act.wait_ge(pe_step, 7)
            act.activation(kT[:, :], ps_k[:, 0:VOC], ACT.Identity, bias=m.bk[:, 0:1]).then_inc(act_step, 1)
            act.wait_ge(dve_step, 14)
            for b in range(B):
                act.activation(prob[:, b, :], ps_s[0:VOC, b * VOC:(b + 1) * VOC], ACT.Exp, bias=nmx[:, b:b + 1],
                               scale=SC).then_inc(act_step, 1)
            act.wait_ge(pe_step, 12)
            act.activation(probT[:, :, :].rearrange("p b v -> p (b v)"), ps_f[0:VOC, 0:B * VOC], ACT.Copy).then_inc(act_step, 1)

        @block.sync
        def _(sp):
            sp.wait_ge(dve_step, 1)
            sp.dma_start(emb[0:1, :], w["L0_tok_special_embed"][0:1, :]).then_inc(special, 16)
            sp.dma_start(emb[107:110, :], w["L0_tok_special_embed"][1:4, :]).then_inc(special, 16)

        @block.gpsimd
        def _(pool):
            pool.tensor_scalar(m.onehot[:, :], m.ids[0:VOC, :], m.pid[0:VOC, :], None, ALU.is_equal).then_inc(pool_step, 1)
            pool.wait_ge(pool_step, 1)
            pairs = m.onehot[:, :].rearrange("p (n two) -> p n two", two=2)
            pool.tensor_tensor(m.pairhot[:, :], pairs[:, :, 0], pairs[:, :, 1], ALU.add).then_inc(pool_step, 1)
            pool.wait_ge(dve_step, 6)
            pool.tensor_scalar(small[:, 0, 4:5], small[:, 0, 4:5], EPS, None, ALU.add).then_inc(pool_step, 1)
            pool.wait_ge(pool_step, 3)
            pool.tensor_tensor(small[:, 0, 1:2], small[:, 0, 4:5], m.neghalf[0:VOC, 0:1], ALU.pow).then_inc(pool_step, 1)
            for b in range(B):
                pool.wait_ge(dve_step, 23 + 11 * b)
                pool.tensor_scalar(small[:, 1 + b, 4:5], small[:, 1 + b, 4:5], EPS, None, ALU.add).then_inc(pool_step, 1)
                pool.wait_ge(pool_step, 5 + 2 * b)
                pool.tensor_tensor(small[:, 1 + b, 1:2], small[:, 1 + b, 4:5], m.neghalf[0:VOC, 0:1], ALU.pow).then_inc(pool_step, 1)

        @block.vector
        def _(dve):
            steps = [0]

            def link(ins):
                steps[0] += 1
                ins.then_inc(dve_step, 1)
                dve.wait_ge(dve_step, steps[0])

            def moments(src, k):
                s = small[:, k, :]
                link(dve.bn_stats(stats[:, k, :], src))
                link(dve.tensor_tensor(s[:, 2:3], stats[:, k, 1:2], stats[:, k, 4:5], ALU.subtract))
                link(dve.tensor_tensor(s[:, 3:4], stats[:, k, 2:3], stats[:, k, 5:6], ALU.add))
                link(dve.scalar_tensor_tensor(s[:, 2:3], s[:, 2:3], 0.25, s[:, 2:3], ALU.mult, ALU.mult))
                link(dve.scalar_tensor_tensor(s[:, 4:5], s[:, 3:4], 1.0 / D, s[:, 2:3], ALU.mult, ALU.add))
                link(dve.tensor_tensor(s[:, 0:1], stats[:, k, 1:2], stats[:, k, 4:5], ALU.add))
                link(dve.tensor_scalar(s[:, 0:1], s[:, 0:1], 0.5, None, ALU.mult))

            dve.wait_ge(act_step, 4)
            link(dve.tensor_scalar(emb[:, :], gelu[:, :], float(D) ** 0.5, None, ALU.mult))
            dve.wait_ge(special, 32)
            moments(emb[:, :], 0)
            dve.wait_ge(pool_step, 4)
            link(dve.tensor_scalar(emb_n[:, :], emb[:, :], small[:, 0, 0:1], small[:, 0, 1:2], ALU.subtract, ALU.mult))
            dve.wait_ge(pool_step, 2)
            link(dve.tensor_reduce(count[:, :], m.onehot[:, :].rearrange("p (b n) -> p b n", b=B), AX.X, ALU.add))
            link(dve.tensor_scalar(absent[:, :], count[:, :], 0.0, -BIG, ALU.is_equal, ALU.mult))
            for b in range(B):
                ins = dve.tensor_scalar(diag[:, b, :], m.ident[0:VOC, 0:VOC], absent[:, b:b + 1], None, ALU.mult)
            link(ins)
            dve.wait_ge(pe_step, 10)
            link(dve.tensor_reduce(mx[:, :], ps_s[0:VOC, 0:B * VOC].rearrange("p (b v) -> p b v", b=B), AX.X, ALU.max))
            link(dve.tensor_scalar(nmx[:, :], mx[:, :], -SC, None, ALU.mult))
            dve.memset(v[:, D:D + 1], 1.0).then_inc(v_ones, 1)
            link(dve.tensor_copy(v[:, 0:D], ps_v[0:VOC, 0:D]))
            dve.wait_ge(v_ones, 1)
            for b in range(B):
                ins = dve.tensor_scalar(vw[:, b, :], v[:, :], count[:, b:b + 1], None, ALU.mult)
            link(ins)
            for b in range(B):
                att = ps_a[0:VOC, b * 256:b * 256 + D + 1]
                dve.wait_ge(pe_step, 14)
                link(dve.reciprocal(rden[:, b:b + 1], att[:, D:D + 1]))
                link(dve.scalar_tensor_tensor(h1[:, b, :], att[:, 0:D], rden[:, b:b + 1], emb[:, :], ALU.mult, ALU.add))
                moments(h1[:, b, :], 1 + b)
                dve.wait_ge(pool_step, 6 + 2 * b)
                link(dve.tensor_scalar(m.table_x[:, b, :], h1[:, b, :], small[:, 1 + b, 0:1], small[:, 1 + b, 1:2],
                                       ALU.subtract, ALU.mult))
                link(dve.tensor_tensor(m.table_tx[:, b, :], h1[:, b, :], m.table_x[:, b, :], ALU.add))


def stage_l0_ffn(nc, m, w):
    NP = N // 2
    with ExitStack() as ctx:
        def sb(name, shape, dt=F32):
            return ctx.enter_context(nc.sbuf_tensor(f"l0f_{name}", shape, dt))

        sem = signals(nc, m, "l0f_")

        sT, hid = sb("sT", [P, NP]), sb("hid", [P, 4, NP])
        change = sb("change", [P, NP // P, D])
        fc2_bd = sb("fc2_bd", [1, D])
        fc2_wd = sb("fc2_wd", [P, 4, D])
        ps_s = ctx.enter_context(nc.psum_tensor("l0f_ps_s", [P, 2, BANK], F32))
        ps_h = ctx.enter_context(nc.psum_tensor("l0f_ps_h", [P, 2, BANK], F32))
        ps_c = ctx.enter_context(nc.psum_tensor("l0f_ps_c", [P, 2, BANK], F32))
        ps_o = ctx.enter_context(nc.psum_tensor("l0f_ps_o", [P, 2, BANK], F32))
        pairs_summed, pairs_copied = sem("pairs_summed"), sem("pairs_copied")
        hid_ready, hid_done, out_ready, out_done, dup = (sem(x) for x in ("hid_ready", "hid_done", "out_ready", "out_done", "dup"))
        change_ready, change_done = sem("change_ready"), sem("change_done")
        block = ctx.enter_context(nc.Block())

        @block.tensor
        def _(pe):
            for b in range(B):
                pe.matmul(ps_s[:, b, :], m.table_x[:, b, :], m.pairhot[:, b * BANK:(b + 1) * BANK], start=True,
                          stop=True).then_inc(pairs_summed, 1)
            for i in range(8):
                b, c = i // 4, i % 4
                pe.wait_ge(pairs_copied, b + 1)
                if i >= 2:
                    pe.wait_ge(hid_done, i - 1)
                pe.matmul(ps_h[:, i % 2, :], m.w1f[:, c * P:(c + 1) * P], sT[:, b * BANK:(b + 1) * BANK], start=True,
                          stop=True).then_inc(hid_ready, 1)
            pe.wait_ge(dup, 2)
            pe.wait_ge(hid_done, 8)
            for j in range(NP // P):
                if j >= 2:
                    pe.wait_ge(change_done, j - 1)
                out = ps_c[:, j % 2, 0:D]
                pe.matmul(out, sT[:, j * P:(j + 1) * P], m.pairmean, start=True, stop=False)
                pe.matmul(out, m.one[0:1, :], fc2_bd[:, :], start=False, stop=False)
                for c in range(4):
                    ins = pe.matmul(out, hid[:, c, j * P:(j + 1) * P], fc2_wd[:, c, :], start=False, stop=(c == 3))
                ins.then_inc(change_ready, 1)
            for t in range(TILES):
                b, g, j = t // CH, t // 4, t // 2
                pe.wait_ge(change_done, j + 1)
                if t % 4 == 0 and g >= 2:
                    pe.wait_ge(out_done, g - 1)
                out = ps_o[:, g % 2, (t % 4) * P:(t % 4 + 1) * P]
                pe.matmul(out, m.onehot[:, t * P:(t + 1) * P], m.table_tx[:, b, :], start=True, stop=False)
                ins = pe.matmul(out, m.expand[:, (t % 2) * P:(t % 2 + 1) * P], change[:, j, :], start=False, stop=True)
                if t % 4 == 3:
                    ins.then_inc(out_ready, 1)

        @block.scalar
        def _(act):
            for b in range(B):
                act.wait_ge(pairs_summed, b + 1)
                act.activation(sT[:, b * BANK:(b + 1) * BANK], ps_s[:, b, :], ACT.Copy).then_inc(pairs_copied, 1)
            for i in range(8):
                b, c = i // 4, i % 4
                act.wait_ge(hid_ready, i + 1)
                act.activation(hid[:, c, b * BANK:(b + 1) * BANK], ps_h[:, i % 2, :], ACT.Gelu,
                               bias=m.fc1_b[:, c:c + 1]).then_inc(hid_done, 1)

        @block.vector
        def _(dve):
            wd = fc2_wd[:, :, :].rearrange("p c (d two) -> p (c d) two", two=2)
            dve.tensor_scalar(wd, m.fc2T[:, :, :].rearrange("p c d -> p (c d)").unsqueeze(2).broadcast_to([P, 256, 2]),
                              0.5, None, ALU.mult).then_inc(dup, 1)
            dve.tensor_scalar(fc2_bd[:, :].rearrange("p (d two) -> p d two", two=2),
                              m.fc2_b[:, :].unsqueeze(2).broadcast_to([1, 64, 2]), 0.5, None, ALU.mult).then_inc(dup, 1)
            for j in range(NP // P):
                dve.wait_ge(change_ready, j + 1)
                dve.tensor_copy(change[:, j, :], ps_c[:, j % 2, 0:D]).then_inc(change_done, 1)
            for g in range(TILES // 4):
                dve.wait_ge(out_ready, g + 1)
                dve.tensor_copy(m.h[:, 4 * g:4 * g + 4, :], ps_o[:, g % 2, :].rearrange("p (t d) -> p t d", t=4)).then_inc(out_done, 1)


GATE_BIAS = 6.906768
HD = RET_H * RET_D
WIDE_PER_HEAD = 9


def stage_l1_attn(nc, m, w):
    layernorm(nc, m, "ln_l1a", m.h, m.xn, m.xnT)
    with ExitStack() as ctx:
        def sb(name, shape, dt=F32):
            return ctx.enter_context(nc.sbuf_tensor(f"l1_{name}", shape, dt))

        r = Core()
        r.LT = sb("LT", [RET_H, N])
        r.Lcol = sb("Lcol", [P, TILES, RET_H])
        r.Lfirst = sb("Lfirst", [P, TILES, RET_H])
        r.fade = sb("fade", [P, TILES, RET_H])
        r.keyfade = sb("keyfade", [P, B, CH, CH, RET_H])
        r.v = sb("v", [P, TILES, RET_H, RET_D + 1])
        r.wswap = sb("wswap", [P, 2 * HD])
        l1_gates(nc, m, r)
        l1_heads(nc, m, r)


def l1_gates(nc, m, r):
    with ExitStack() as ctx:
        def sb(name, shape, dt=F32):
            return ctx.enter_context(nc.sbuf_tensor(f"l1g_{name}", shape, dt))

        sem = signals(nc, m, "l1g_")

        x, u, w1, lw = sb("x", [RET_H, N]), sb("u", [RET_H, N]), sb("w1", [RET_H, N]), sb("lw", [RET_H, N])
        gap = sb("gap", [P, TILES, RET_H])
        ps_g = ctx.enter_context(nc.psum_tensor("l1g_ps_g", [P, 4, BANK], F32))
        ps_v = ctx.enter_context(nc.psum_tensor("l1g_ps_v", [P, 2, BANK], F32))
        ps_l = ctx.enter_context(nc.psum_tensor("l1g_ps_l", [P, 2, BANK], F32))
        gates_ready, dve_step, act_step, pe_step = sem("gates_ready"), sem("dve_step"), sem("act_step"), sem("pe_step")
        v_ready, v_done, v_ones = sem("v_ready"), sem("v_done"), sem("v_ones")
        swapped = sem("swapped")
        block = ctx.enter_context(nc.Block())

        @block.tensor
        def _(pe):
            pe.wait_ge(m.s_wattn, 16)
            for g in range(4):
                ins = pe.matmul(ps_g[0:RET_H, g, :], m.w_attn[:, 3 * HD:3 * HD + RET_H], m.xnT[:, g * BANK:(g + 1) * BANK],
                                start=True, stop=True)
            ins.then_inc(gates_ready, 1)
            for t in range(TILES):
                if t >= 2:
                    pe.wait_ge(v_done, t - 1)
                pe.matmul(ps_v[:, t % 2, :], m.xnT[:, t * P:(t + 1) * P], m.w_attn[:, 2 * HD:3 * HD], start=True,
                          stop=True).then_inc(v_ready, 1)
            pe.wait_ge(dve_step, 9)
            for t in range(TILES):
                ins = pe.transpose(ps_l[:, 0, t * RET_H:(t + 1) * RET_H], r.LT[:, t * P:(t + 1) * P], m.ident[0:RET_H, 0:RET_H])
            ins.then_inc(pe_step, 1)
            pe.wait_ge(dve_step, 10)
            pe.matmul(ps_l[:, 1, 0:TILES * RET_H], m.one[0:1, :], r.Lcol[0:1, :, :].rearrange("p t h -> p (t h)"),
                      start=True, stop=True).then_inc(pe_step, 1)

        @block.gpsimd
        def _(pool):
            pool.memset(r.v[:, :, :, RET_D:RET_D + 1], 1.0).then_inc(v_ones, 1)
            pool.wait_ge(m.s_wattn, 16)
            pairs = m.w_attn[:, 0:2 * HD].rearrange("p (c two) -> p c two", two=2)
            swap = r.wswap[:, :].rearrange("p (c two) -> p c two", two=2)
            pool.tensor_scalar(swap[:, :, 0], pairs[:, :, 1], -1.0, None, ALU.mult).then_inc(swapped, 1)
            pool.tensor_copy(swap[:, :, 1], pairs[:, :, 0]).then_inc(swapped, 1)

        @block.scalar
        def _(act):
            act.wait_ge(dve_step, 2)
            act.activation(u[:, :], w1[:, :], ACT.Exp, scale=-1.0).then_inc(act_step, 1)
            act.wait_ge(dve_step, 3)
            act.activation(lw[:, :], w1[:, :], ACT.Ln).then_inc(act_step, 1)
            for t in range(TILES):
                act.wait_ge(v_ready, t + 1)
                act.activation(r.v[:, t, :, 0:RET_D], ps_v[:, t % 2, :].rearrange("p (h d) -> p h d", h=RET_H), ACT.Copy)\
                   .then_inc(v_done, 1)
            act.wait_ge(dve_step, 12)
            act.activation(r.fade[:, :, :], gap[:, :, :], ACT.Exp).then_inc(act_step, 1)
            act.wait_ge(dve_step, 14)
            kf = r.keyfade[:, :, :, :, :].rearrange("p b j i h -> p (b j i h)")
            act.activation(kf, kf, ACT.Exp, scale=0.5).then_inc(act_step, 1)

        @block.vector
        def _(dve):
            steps = [0]

            def link(ins):
                steps[0] += 1
                ins.then_inc(dve_step, 1)
                dve.wait_ge(dve_step, steps[0])

            dve.wait_ge(gates_ready, 1)
            link(dve.tensor_scalar(x[:, :], ps_g[0:RET_H, :, :].rearrange("p g n -> p (g n)"), GATE_BIAS, None, ALU.add))
            link(dve.scalar_tensor_tensor(w1[:, :], x[:, :], -1.0, x[:, :], ALU.mult, ALU.max))
            dve.wait_ge(act_step, 1)
            link(dve.tensor_scalar(w1[:, :], u[:, :], 1.0, None, ALU.add))
            dve.wait_ge(act_step, 2)
            link(dve.tensor_scalar(w1[:, :], w1[:, :], -1.0, 1e-30, ALU.add, ALU.max))
            link(dve.reciprocal(w1[:, :], w1[:, :]))
            link(dve.tensor_tensor(lw[:, :], lw[:, :], u[:, :], ALU.mult))
            link(dve.tensor_tensor(lw[:, :], lw[:, :], w1[:, :], ALU.mult))
            link(dve.scalar_tensor_tensor(x[:, :], x[:, :], 0.0, lw[:, :], ALU.min, ALU.subtract))
            for b in range(B):
                ins = dve.tensor_tensor_scan(r.LT[:, b * S:(b + 1) * S], x[:, b * S:(b + 1) * S], x[:, b * S:(b + 1) * S],
                                             0.0, ALU.add, ALU.bypass)
            link(ins)
            dve.wait_ge(pe_step, 1)
            link(dve.tensor_copy(r.Lcol[:, :, :].rearrange("p t h -> p (t h)"), ps_l[:, 0, 0:TILES * RET_H]))
            dve.wait_ge(pe_step, 2)
            link(dve.tensor_copy(r.Lfirst[:, :, :].rearrange("p t h -> p (t h)"), ps_l[:, 1, 0:TILES * RET_H]))
            link(dve.tensor_tensor(gap[:, :, :], r.Lcol[:, :, :], r.Lfirst[:, :, :], ALU.subtract))
            for b in range(B):
                tiles = slice(b * CH, (b + 1) * CH)
                for j in range(CH):
                    ins = dve.tensor_tensor(r.keyfade[:, b, j, :, :], r.Lfirst[:, tiles, :],
                                            r.Lcol[:, b * CH + j, :].unsqueeze(1).broadcast_to([P, CH, RET_H]), ALU.subtract)
            link(ins)
            kf = r.keyfade[:, :, :, :, :].rearrange("p b j i h -> p (b j i h)")
            link(dve.tensor_scalar(kf, kf, 0.0, None, ALU.min))
            dve.wait_ge(act_step, 4)
            link(dve.tensor_scalar(kf, kf, float(RET_D) ** -0.5, None, ALU.mult))


def l1_heads(nc, m, r):
    WIDE = WIDE_PER_HEAD * RET_H + CH // 2
    YJOBS = 4 * RET_H + CH // 2
    ROPES = 16
    OFF = [sum(CH - 1 - k for k in range(j)) * P for j in range(CH)]
    with ExitStack() as ctx:
        def sb(name, shape, dt=F32):
            return ctx.enter_context(nc.sbuf_tensor(f"l1h_{name}", shape, dt))

        sem = signals(nc, m, "l1h_")

        qk = sb("qk", [P, 2, 2, S])
        rc, rs = sb("rc", [P, 2, BANK]), sb("rs", [P, 2, BANK])
        sq = sb("sq", [P, 2, 28 * P])
        sqd = sb("sqd", [P, 2, S])
        decay = sb("decay", [P, 2, S])
        ty = sb("ty", [P, 2, RET_D + 1])
        yraw = sb("yraw", [P, CH, RET_H, RET_D + 1])
        rden = sb("rden", [P, CH, RET_H])
        yn = sq[:, :, :].rearrange("p a n -> p (a n)")[:, 0:CH * HD].rearrange("p (i n) -> p i n", i=CH)
        yT = sb("yT", [P, 2, 2, HD])
        ab = ctx.enter_context(nc.psum_tensor("l1h_ab", [P, 2, BANK], F32))
        wide = ctx.enter_context(nc.psum_tensor("l1h_wide", [P, 2, 2 * BANK], F32))
        yps = ctx.enter_context(nc.psum_tensor("l1h_y", [P, 2, BANK], F32))
        a_filled, b_filled, a_used, b_used, rope_ready = (sem(x) for x in ("a_filled", "b_filled", "a_used", "b_used", "rope_ready"))
        wide_filled, wide_free = sem("wide_filled"), [sem("wide_free0"), sem("wide_free1")]
        scaled, off_squared = sem("scaled"), sem("off_squared")
        gap_ready, exp_ready, decay_ready, diag_squared, diag_ready = (sem(x) for x in ("gap_ready", "exp_ready", "decay_ready", "diag_squared", "diag_ready"))
        y_filled, y_used, ty_ready = sem("y_filled"), sem("y_used"), sem("ty_ready")
        norm_step, yT_ready, yT_used = sem("norm_step"), sem("yT_ready"), sem("yT_used")
        block = ctx.enter_context(nc.Block())

        def order():
            yield "rope", 0
            for h in range(RET_H):
                yield "scores", h
                if h % 2 == 1 and h < RET_H - 1:
                    yield "rope", h // 2 + 1
                if h >= 1:
                    yield "values", h - 1
            yield "values", RET_H - 1

        @block.tensor
        def _(pe):
            pe.wait_ge(m.s_wproj1, 16)
            for signal in (y_filled, wide_filled):
                pe.sem_inc(signal, FROM)
            with pe.Fori(0, B) as b:
                def rope(hp):
                    for n in range(4):
                        job, kind, half = 4 * hp + n, n // 2, n % 2
                        cols = slice(kind * HD + hp * P, kind * HD + (hp + 1) * P)
                        x = m.xnT[:, bass.ds(b * S + half * BANK, BANK)]
                        pe.wait_ge(a_used, FROM + b * ROPES + job)
                        pe.matmul(ab[:, 0, :], m.w_attn[:, cols], x, start=True, stop=True).then_inc(a_filled, 1)
                        pe.wait_ge(b_used, FROM + b * ROPES + job)
                        pe.matmul(ab[:, 1, :], r.wswap[:, cols], x, start=True, stop=True).then_inc(b_filled, 1)

                def scores(h):
                    job = WIDE_PER_HEAD * h
                    slot, top = job % 2, 64 * (h % 2)
                    pe.wait_ge(wide_free[slot], FROM + b * (WIDE // 2) + job // 2)
                    pe.nop(nofuse=True)
                    for half in range(2):
                        ins = pe.matmul(wide[:, slot, half * BANK:(half + 1) * BANK], m.sel8[0:8, h * P:(h + 1) * P],
                                        r.LT[:, bass.ds(b * S + half * BANK, BANK)], start=True, stop=True)
                    ins.then_inc(wide_filled, 1)
                    if h % 2 == 0:
                        pe.wait_ge(rope_ready, FROM + b * ROPES + 4 * (h // 2 + 1))
                    q, k = qk[top:top + 64, (h // 2) % 2, 0, :], qk[top:top + 64, (h // 2) % 2, 1, :]
                    job += 1
                    slot = job % 2
                    pe.wait_ge(wide_free[slot], FROM + b * (WIDE // 2) + job // 2)
                    for i in range(CH):
                        t = slice(i * P, (i + 1) * P)
                        ins = pe.matmul(wide[:, slot, t], k[:, t], q[:, t], start=True, stop=True)
                    ins.then_inc(wide_filled, 1)
                    for j in range(CH - 1):
                        job += 1
                        slot = job % 2
                        pe.wait_ge(wide_free[slot], FROM + b * (WIDE // 2) + job // 2)
                        width = (CH - 1 - j) * P
                        for c in range(0, width, BANK):
                            n = min(BANK, width - c)
                            t0 = (j + 1) * P + c
                            ins = pe.matmul(wide[:, slot, c:c + n], k[:, j * P:(j + 1) * P], q[:, t0:t0 + n], start=True, stop=True)
                        ins.then_inc(wide_filled, 1)

                def values(h):
                    pe.wait_ge(diag_ready, FROM + b * RET_H + h + 1)
                    pe.wait_ge(off_squared, b * 7 * RET_H + 7 * (h + 1))
                    for g in range(4):
                        y = yps[:, (4 * h + g) % 2, :]
                        pe.wait_ge(y_used, FROM + b * YJOBS + max(4 * h + g - 1, 0))
                        for e in range(2):
                            i = 2 * g + e
                            for j in range(i):
                                block_at = OFF[j] + (i - j - 1) * P
                                pe.matmul(y[:, e * 130:e * 130 + 65], sq[:, h % 2, block_at:block_at + P],
                                          r.v[:, bass.ds(b * CH + j, 1), h, :].rearrange("p a d -> p (a d)"), start=(j == 0), stop=(j == i - 1))
                            ins = pe.matmul(y[:, e * 130 + 65:e * 130 + 130], sqd[:, h % 2, i * P:(i + 1) * P],
                                            r.v[:, bass.ds(b * CH + i, 1), h, :].rearrange("p a d -> p (a d)"), start=True, stop=True)
                        ins.then_inc(y_filled, 1)

                for what, k in order():
                    {"rope": rope, "scores": scores, "values": values}[what](k)
                for g in range(CH // 2):
                    job = WIDE_PER_HEAD * RET_H + g
                    slot = job % 2
                    pe.wait_ge(norm_step, b * 3 + 3)
                    pe.wait_ge(wide_free[slot], FROM + b * (WIDE // 2) + job // 2)
                    for e in range(2):
                        for c in range(4):
                            ins = pe.transpose(wide[:, slot, e * BANK + c * P:e * BANK + (c + 1) * P],
                                               yn[:, 2 * g + e, c * P:(c + 1) * P], m.ident)
                    ins.then_inc(wide_filled, 1)
                    pe.wait_ge(yT_ready, b * 4 + g + 1)
                    yjob = 4 * RET_H + g
                    pe.wait_ge(y_used, FROM + b * YJOBS + yjob - 1)
                    for e in range(2):
                        for c in range(4):
                            ins = pe.matmul(yps[:, yjob % 2, e * P:(e + 1) * P], yT[:, g % 2, e, c * P:(c + 1) * P],
                                            m.w_proj1[:, c, :], start=(c == 0), stop=(c == 3))
                    ins.then_inc(y_filled, 1)

        @block.vector
        def _(dve):
            for signal in (a_used, b_used, *wide_free, y_used, diag_ready):
                dve.sem_inc(signal, FROM)
            with dve.Fori(0, B) as b:
                def rope(hp):
                    for n in range(4):
                        job, half = 4 * hp + n, n % 2
                        t = slice(half * BANK, (half + 1) * BANK)
                        dve.wait_ge(rope_ready, FROM + b * ROPES + max(job - 1, 0))
                        dve.wait_ge(a_filled, b * ROPES + job + 1)
                        dve.tensor_tensor(rc[:, job % 2, :], ab[:, 0, :], m.ropecos[:, t], ALU.mult).then_inc(a_used, 1)
                        dve.wait_ge(b_filled, b * ROPES + job + 1)
                        dve.tensor_tensor(rs[:, job % 2, :], ab[:, 1, :], m.ropesin[:, t], ALU.mult).then_inc(b_used, 1)

                def scores(h):
                    job = WIDE_PER_HEAD * h
                    dve.wait_ge(wide_filled, FROM + b * WIDE + job + 1)
                    dve.wait_ge(diag_ready, FROM + b * RET_H + max(h - 1, 0))
                    dve.tensor_tensor(decay[:, h % 2, :].rearrange("p (i t) -> p i t", i=CH),
                                      wide[:, job % 2, :].rearrange("p (i t) -> p i t", i=CH),
                                      r.Lcol[:, bass.ds(b * CH, CH), h].unsqueeze(2).broadcast_to([P, CH, P]),
                                      ALU.subtract).then_inc(gap_ready, 1)
                    dve.wait_ge(gap_ready, b * RET_H + h + 1)
                    dve.sem_inc(wide_free[job % 2], 1)
                    dve.wait_ge(y_filled, FROM + b * YJOBS + 4 * max(h - 1, 0))
                    for j in range(CH - 1):
                        job = WIDE_PER_HEAD * h + 2 + j
                        width = (CH - 1 - j) * P
                        dve.wait_ge(wide_filled, FROM + b * WIDE + job + 1)
                        dve.tensor_tensor(sq[:, h % 2, OFF[j]:OFF[j] + width].rearrange("p (i t) -> p i t", t=P),
                                          wide[:, job % 2, 0:width].rearrange("p (i t) -> p i t", t=P),
                                          r.keyfade[:, bass.ds(b, 1), j, j + 1:CH, h].rearrange("p a i -> p (a i)").unsqueeze(2)
                                          .broadcast_to([P, CH - 1 - j, P]), ALU.mult).then_inc(scaled, 1)
                        dve.wait_ge(scaled, b * 7 * RET_H + 7 * h + j + 1)
                        dve.sem_inc(wide_free[job % 2], 1)
                    dve.wait_ge(diag_squared, b * RET_H + h + 1)
                    dve.wait_ge(decay_ready, b * RET_H + h + 1)
                    dve.tensor_tensor(sqd[:, h % 2, :], sqd[:, h % 2, :], decay[:, h % 2, :], ALU.mult).then_inc(diag_ready, 1)

                def values(h):
                    for g in range(4):
                        y = yps[:, (4 * h + g) % 2, 0:260].rearrange("p (e k d) -> p e k d", e=2, k=2)
                        dve.wait_ge(y_filled, FROM + b * YJOBS + 4 * h + g + 1)
                        fade = r.fade[:, bass.ds(b * CH + 2 * g, 2), h]
                        out = yraw[:, 2 * g:2 * g + 2, h, :]
                        if g == 0:
                            dve.tensor_tensor(ty[:, 1:2, :], y[:, 1:2, 0, :], fade[:, 1:2].unsqueeze(2).broadcast_to([P, 1, RET_D + 1]),
                                              ALU.mult).then_inc(ty_ready, 1)
                            dve.wait_ge(ty_ready, b * 4 * RET_H + 4 * h + g + 1)
                            dve.tensor_copy(out[:, 0:1, :], y[:, 0:1, 1, :])
                            dve.tensor_tensor(out[:, 1:2, :], ty[:, 1:2, :], y[:, 1:2, 1, :], ALU.add).then_inc(y_used, 1)
                        else:
                            dve.tensor_tensor(ty[:, :, :], y[:, :, 0, :], fade.unsqueeze(2).broadcast_to([P, 2, RET_D + 1]),
                                              ALU.mult).then_inc(ty_ready, 1)
                            dve.wait_ge(ty_ready, b * 4 * RET_H + 4 * h + g + 1)
                            dve.tensor_tensor(out, ty[:, :, :], y[:, :, 1, :], ALU.add).then_inc(y_used, 1)
                        dve.wait_ge(y_used, FROM + b * YJOBS + 4 * h + g + 1)

                for what, k in order():
                    {"rope": rope, "scores": scores, "values": values}[what](k)
                dve.tensor_scalar(rden[:, :, :], yraw[:, :, :, RET_D], 1e-6, None, ALU.max).then_inc(norm_step, 1)
                dve.wait_ge(norm_step, b * 3 + 1)
                dve.reciprocal(rden[:, :, :], rden[:, :, :]).then_inc(norm_step, 1)
                dve.wait_ge(norm_step, b * 3 + 2)
                for i in range(CH):
                    ins = dve.tensor_tensor(yn[:, i, :].rearrange("p (h d) -> p h d", h=RET_H), yraw[:, i, :, 0:RET_D],
                                            rden[:, i, :].unsqueeze(2).broadcast_to([P, RET_H, RET_D]), ALU.mult)
                ins.then_inc(norm_step, 1)
                for g in range(CH // 2):
                    yjob = 4 * RET_H + g
                    dve.wait_ge(y_filled, FROM + b * YJOBS + yjob + 1)
                    hh = m.h[:, bass.ds(b * CH + 2 * g, 2), :]
                    dve.tensor_tensor(hh, hh, yps[:, yjob % 2, 0:2 * P].rearrange("p (e d) -> p e d", e=2), ALU.add).then_inc(y_used, 1)

        @block.scalar
        def _(act):
            with act.Fori(0, B) as b:
                def scores(h):
                    act.wait_ge(gap_ready, b * RET_H + h + 1)
                    act.activation(decay[:, h % 2, :], decay[:, h % 2, :], ACT.Exp).then_inc(exp_ready, 1)
                    job = WIDE_PER_HEAD * h + 1
                    act.wait_ge(wide_filled, FROM + b * WIDE + job + 1)
                    act.wait_ge(y_filled, FROM + b * YJOBS + 4 * max(h - 1, 0))
                    act.activation(sqd[:, h % 2, :], wide[:, job % 2, :], ACT.Square, scale=float(RET_D) ** -0.5).then_inc(diag_squared, 1)
                    act.wait_ge(diag_squared, b * RET_H + h + 1)
                    act.sem_inc(wide_free[job % 2], 1)
                    for j in range(CH - 1):
                        act.wait_ge(scaled, b * 7 * RET_H + 7 * h + j + 1)
                        s = sq[:, h % 2, OFF[j]:OFF[j] + (CH - 1 - j) * P]
                        act.activation(s, s, ACT.Square).then_inc(off_squared, 1)

                for what, k in order():
                    if what == "scores":
                        scores(k)
                for g in range(CH // 2):
                    job = WIDE_PER_HEAD * RET_H + g
                    act.wait_ge(wide_filled, FROM + b * WIDE + job + 1)
                    act.wait_ge(y_filled, FROM + b * YJOBS + 4 * RET_H + max(g - 1, 0))
                    act.activation(yT[:, g % 2, :, :].rearrange("p e n -> p (e n)"), wide[:, job % 2, :], ACT.Copy).then_inc(yT_ready, 1)
                    act.wait_ge(yT_ready, b * 4 + g + 1)
                    act.sem_inc(wide_free[job % 2], 1)

        @block.gpsimd
        def _(pool):
            pool.sem_inc(rope_ready, FROM)
            with pool.Fori(0, B) as b:
                def rope(hp):
                    pool.wait_ge(wide_filled, FROM + b * WIDE + WIDE_PER_HEAD * max(2 * hp - 2, 0))
                    for n in range(4):
                        job, kind, half = 4 * hp + n, n // 2, n % 2
                        pool.wait_ge(b_used, FROM + b * ROPES + job + 1)
                        pool.wait_ge(a_used, FROM + b * ROPES + job + 1)
                        pool.tensor_tensor(qk[:, hp % 2, kind, half * BANK:(half + 1) * BANK], rc[:, job % 2, :], rs[:, job % 2, :],
                                           ALU.add).then_inc(rope_ready, 1)

                def scores(h):
                    pool.wait_ge(exp_ready, b * RET_H + h + 1)
                    pool.nop(nofuse=True)
                    g = decay[:, h % 2, :].rearrange("p (i t) -> p i t", i=CH)
                    pool.affine_select(out=g, in_=g, compare_op=ALU.is_ge, fill=0.0, base=0, pattern=[[0, CH], [1, P]],
                                       channel_multiplier=-1).then_inc(decay_ready, 1)

                for what, k in order():
                    if what != "values":
                        {"rope": rope, "scores": scores}[what](k)


def router(nc, m, r, name, E, wrT, lower, extra):
    G = E + extra
    with ExitStack() as ctx:
        def sb(x, shape, dt=F32):
            return ctx.enter_context(nc.sbuf_tensor(f"{name}_{x}", shape, dt))

        sem = signals(nc, m, f"{name}_")

        lg, gt, ge = sb("lg", [P, TILES, E]), sb("gt", [P, TILES, E, E]), sb("ge", [P, TILES, E, E])
        rank, mx = sb("rank", [P, TILES, E]), sb("mx", [P, TILES])
        gT, b2 = sb("gT", [G, N]), sb("b2", [G, D])
        ps_l = ctx.enter_context(nc.psum_tensor(f"{name}_ps_l", [P, BANK], F32))
        ps_g = ctx.enter_context(nc.psum_tensor(f"{name}_ps_g", [P, 4, BANK], F32))
        ps_b = ctx.enter_context(nc.psum_tensor(f"{name}_ps_b", [P, 2, BANK], F32))
        logits, exps, dve_step, turned, copied, biased, bias_used, b2_in = (
            sem(k) for k in ("logits", "exps", "dve_step", "turned", "copied", "biased", "bias_used", "b2_in"))
        block = ctx.enter_context(nc.Block())

        @block.sync
        def _(sp):
            sp.dma_start(b2[0:E, :], r.b2_dram).then_inc(b2_in, 16)
            if extra:
                sp.dma_start(b2[E:G, :], r.b2_shared).then_inc(b2_in, 16)

        @block.tensor
        def _(pe):
            pe.wait_ge(r.s_router, r.n_router)
            for t in range(TILES):
                out = ps_l[:, t * E:(t + 1) * E]
                pe.matmul(out, r.hT[:, t * P:(t + 1) * P], wrT, start=True, stop=False)
                ins = pe.matmul(out, m.one[0:1, :], r.b_r[:, :], start=False, stop=True)
            ins.then_inc(logits, 1)
            pe.wait_ge(dve_step, 12)
            for t in range(TILES):
                ins = pe.transpose(ps_g[0:G, t // 4, (t % 4) * P:(t % 4 + 1) * P], r.gates[:, t, :], m.ident)
                if t % 4 == 3:
                    ins.then_inc(turned, 1)
            pe.wait_ge(b2_in, 16 + 16 * extra)
            for t in range(TILES):
                g = t // 4
                pe.wait_ge(copied, g + 1)
                if g >= 2 and t % 4 == 0:
                    pe.wait_ge(bias_used, g - 1)
                ins = pe.matmul(ps_b[:, g % 2, (t % 4) * P:(t % 4 + 1) * P], gT[:, t * P:(t + 1) * P], b2[:, :], start=True, stop=True)
                if t % 4 == 3:
                    ins.then_inc(biased, 1)

        @block.scalar
        def _(act):
            act.wait_ge(dve_step, 4)
            act.activation(r.gates[:, :, 0:E], lg[:, :, :], ACT.Exp).then_inc(exps, 1)
            for g in range(4):
                act.wait_ge(turned, g + 1)
                act.activation(gT[:, g * BANK:(g + 1) * BANK], ps_g[0:G, g, :], ACT.Copy).then_inc(copied, 1)

        @block.vector
        def _(dve):
            steps = [0]

            def link(ins):
                steps[0] += 1
                ins.then_inc(dve_step, 1)
                dve.wait_ge(dve_step, steps[0])

            def others(x):
                return x.unsqueeze(2).broadcast_to([P, TILES, E, E])

            def own(x):
                return x.unsqueeze(3).broadcast_to([P, TILES, E, E])

            dve.wait_ge(logits, 1)
            link(dve.tensor_copy(lg[:, :, :].rearrange("p t e -> p (t e)"), ps_l[:, 0:TILES * E]))
            link(dve.tensor_tensor(gt[:, :, :, :], others(lg[:, :, :]), own(lg[:, :, :]), ALU.is_gt))
            link(dve.tensor_tensor(ge[:, :, :, :], others(lg[:, :, :]), own(lg[:, :, :]), ALU.is_ge))
            dve.tensor_reduce(mx[:, :], lg[:, :, :], AX.X, ALU.max).then_inc(exps, 1)
            dve.wait_ge(exps, 1)
            link(dve.tensor_tensor(lg[:, :, :], lg[:, :, :], mx[:, :].unsqueeze(2).broadcast_to([P, TILES, E]), ALU.subtract))
            low = lower.bitcast(I32).unsqueeze(1).broadcast_to([P, TILES, E * E])
            link(dve.copy_predicated(gt[:, :, :, :].rearrange("p t i j -> p t (i j)"), low, ge[:, :, :, :].rearrange("p t i j -> p t (i j)")))
            link(dve.tensor_reduce(rank[:, :, :], gt[:, :, :, :], AX.X, ALU.add))
            link(dve.tensor_scalar(rank[:, :, :], rank[:, :, :], 1.5, None, ALU.is_lt))
            dve.wait_ge(exps, 2)
            link(dve.tensor_tensor(r.gates[:, :, 0:E], r.gates[:, :, 0:E], rank[:, :, :], ALU.mult))
            link(dve.tensor_reduce(mx[:, :], r.gates[:, :, 0:E], AX.X, ALU.add))
            link(dve.reciprocal(mx[:, :], mx[:, :]))
            link(dve.tensor_tensor(r.gates[:, :, 0:E], r.gates[:, :, 0:E], mx[:, :].unsqueeze(2).broadcast_to([P, TILES, E]), ALU.mult))
            if extra:
                link(dve.memset(r.gates[:, :, E:G], 1.0))
            else:
                link(dve.tensor_tensor(m.h[:, :, :], m.h[:, :, :], m.xn[:, :, :], ALU.add))
            for g in range(4):
                dve.wait_ge(biased, g + 1)
                hh = m.h[:, 4 * g:4 * g + 4, :]
                dve.tensor_tensor(hh, hh, ps_b[:, g % 2, :].rearrange("p (t d) -> p t d", t=4), ALU.add).then_inc(bias_used, 1)


def l1_experts(nc, m, r):
    E, UNITS = 8, 8
    with ExitStack() as ctx:
        def sb(name, shape, dt=F32):
            return ctx.enter_context(nc.sbuf_tensor(f"l1e_{name}", shape, dt))

        sem = signals(nc, m, "l1e_")

        w1, w2, b1 = sb("w1", [P, 2, 512]), sb("w2", [P, 2, 4, D]), sb("b1", [P, 2, 4])
        hid = sb("hid", [P, 2, 4, BANK])
        prime = sb("prime", [P, 1])
        ps_u = ctx.enter_context(nc.psum_tensor("l1e_ps_u", [P, 4, BANK], F32))
        ps_d = ctx.enter_context(nc.psum_tensor("l1e_ps_d", [P, 2, BANK], F32))
        slot_in = [sem("slot0_in"), sem("slot1_in")]
        up_ready, hid_ready, down_ready, down_used = sem("up_ready"), sem("hid_ready"), sem("down_ready"), sem("down_used")
        block = ctx.enter_context(nc.Block())

        @block.sync
        def _(sp):
            with sp.Fori(0, E // 2) as it:
                for k in range(2):
                    e = it * 2 + k
                    sp.wait_ge(down_ready, FROM + it * UNITS)
                    sp.dma_start(w1[:, k, :], r.W1_dram[bass.ds(e, 1), :, :].rearrange("e p f -> p (e f)")).then_inc(slot_in[k], 16)
                    sp.dma_start(w2[:, k, :, :], r.W2_dram[bass.ds(e, 1), :, :].rearrange("e (c p) d -> p (e c) d", p=P)).then_inc(slot_in[k], 16)
                    sp.dma_start(b1[:, k, :], r.b1_dram[bass.ds(e, 1), :].rearrange("e (c p) -> p (e c)", p=P),
                                 allow_slow_non_contiguous=True).then_inc(slot_in[k], 16)

        @block.tensor
        def _(pe):
            pe.sem_inc(down_ready, FROM)
            with pe.Fori(0, E // 2) as it:
                def up(u):
                    k, g = u // 4, u % 4
                    if g == 0:
                        pe.wait_ge(slot_in[k], it * 48 + 48)
                    for c in range(4):
                        pe.wait_ge(hid_ready, FROM + it * 32 + max(4 * u + c - 3, 0))
                        pe.matmul(ps_u[:, c, :], w1[:, k, c * P:(c + 1) * P], r.hT[:, g * BANK:(g + 1) * BANK], start=True,
                                  stop=True).then_inc(up_ready, 1)

                def down(u):
                    k, g = u // 4, u % 4
                    pe.wait_ge(hid_ready, FROM + it * 32 + 4 * u + 4)
                    pe.wait_ge(down_used, FROM + it * UNITS + max(u - 1, 0))
                    for t in range(4):
                        for c in range(4):
                            ins = pe.matmul(ps_d[:, u % 2, t * P:(t + 1) * P], hid[:, u % 2, c, t * P:(t + 1) * P], w2[:, k, c, :],
                                            start=(c == 0), stop=(c == 3))
                    ins.then_inc(down_ready, 1)

                for u in range(UNITS):
                    up(u)
                    if u >= 1:
                        down(u - 1)
                down(UNITS - 1)

        @block.scalar
        def _(act):
            act.sem_inc(hid_ready, FROM)
            act.activation(prime[:, :], m.pid, ACT.Gelu)
            with act.Fori(0, E // 2) as it:
                for u in range(UNITS):
                    act.wait_ge(down_ready, FROM + it * UNITS + max(u - 1, 0))
                    for c in range(4):
                        act.wait_ge(up_ready, it * 32 + 4 * u + c + 1)
                        act.activation(hid[:, u % 2, c, :], ps_u[:, c, :], ACT.Gelu, bias=b1[:, u // 4, c:c + 1]).then_inc(hid_ready, 1)

        @block.vector
        def _(dve):
            dve.sem_inc(down_used, FROM)
            with dve.Fori(0, E // 2) as it:
                for u in range(UNITS):
                    k, g = u // 4, u % 4
                    dve.wait_ge(down_ready, FROM + it * UNITS + u + 1)
                    for t in range(4):
                        hh = m.h[:, 4 * g + t, :]
                        ins = dve.scalar_tensor_tensor(hh, ps_d[:, u % 2, t * P:(t + 1) * P],
                                                       r.gates[:, 4 * g + t, bass.ds(it * 2 + k, 1)], hh, ALU.mult, ALU.add)
                    ins.then_inc(down_used, 1)
                    dve.wait_ge(down_used, FROM + it * UNITS + u + 1)


def stage_l1_ffn(nc, m, w):
    with ExitStack() as ctx:
        def sb(name, shape, dt=F32):
            return ctx.enter_context(nc.sbuf_tensor(f"l1f_{name}", shape, dt))

        r = Core()
        r.hn, r.hT = sb("hn", [P, TILES, D]), sb("hT", [P, N])
        r.gates = sb("gates", [P, TILES, 8])
        r.b_r, r.ln_g, r.ln_b = sb("b_r", [1, 8]), sb("ln_g", [P, 1]), sb("ln_b", [P, 1])
        r.b2_dram, r.b1_dram, r.W1_dram, r.W2_dram = w["L1_ffn_b2"], w["L1_ffn_b1"], w["L1_ffn_W1"], w["L1_ffn_W2"]
        r.s_router, r.n_router = signals(nc, m, "l1f_")("router"), 48
        with nc.Block() as block:
            @block.sync
            def _(sp):
                sp.dma_start(r.b_r[:, :], row(w["L1_ffn_b_r"])).then_inc(r.s_router, 16)
                sp.dma_start(r.ln_g[:, :], col(w["L1_ffn_ln_g"]), allow_slow_non_contiguous=True).then_inc(r.s_router, 16)
                sp.dma_start(r.ln_b[:, :], col(w["L1_ffn_ln_b"]), allow_slow_non_contiguous=True).then_inc(r.s_router, 16)
                sp.wait_ge(r.s_router, 48)
        layernorm(nc, m, "ln_l1f", m.h, m.xn, None)
        layernorm(nc, m, "ln_l1g", m.xn, r.hn, r.hT, gain=r.ln_g[:, 0:1], shift=r.ln_b[:, 0:1])
        router(nc, m, r, "l1r", 8, m.wrT[:, :], m.lower8, 0)
        l1_experts(nc, m, r)


def move_heads():
    out = np.zeros((4, 2, 16, 2, 8, 8, 16), np.float32)
    for a in range(2):
        for l in range(8):
            for d in range(16):
                out[:, a, d, a, l, l, d] = 1.0
    return out.reshape(P, 2, 8, P)


def stage_l2_attn(nc, m, w):
    H, HW, ROLL, WIN = 8, 16, 32, 64
    with ExitStack() as ctx:
        def sb(name, shape, dt=F32):
            return ctx.enter_context(nc.sbuf_tensor(f"l2_{name}", shape, dt))

        sem = signals(nc, m, "l2_")

        move = sb("move", [P, 2, 8, P])
        b_proj = sb("b_proj", [1, D])
        const_in = sem("const_in")
        with nc.Block() as block:
            @block.sync
            def _(sp):
                sp.dma_start(move[:, :, :, :], w["move"]).then_inc(const_in, 16)
                sp.dma_start(b_proj[:, :], row(w["L2_attn_b_proj"])).then_inc(const_in, 16)
        layernorm(nc, m, "ln_l2a", m.h, m.xn, m.xnT)
        qkv = sb("qkv", [P, 4, 3 * D])
        qk = sb("qk", [P, 2, H, H, HW])
        s, e = sb("s", [P, 4, H, H]), sb("e", [P, 4, H, H])
        mx = sb("mx", [P, 4, H])
        av = sb("av", [P, 2, H, HW, H])
        o = sb("o", [P, 4, D])
        oT = sb("oT", [P, S])
        yT = sb("yT", [P, S + ROLL])
        prime = sb("prime", [P, 1])
        ps_q = ctx.enter_context(nc.psum_tensor("l2_ps_q", [P, 4, BANK], F32))
        ps_t = ctx.enter_context(nc.psum_tensor("l2_ps_t", [P, BANK], F32))
        ps_g = ps_q[:, :, 0:2 * P].rearrange("p q (a n) -> p q a n", a=2)
        ps_o = ctx.enter_context(nc.psum_tensor("l2_ps_o", [P, BANK], F32))
        qkv_ready, qkv_in, qk_ready = (sem(x) for x in ("qkv_ready", "qkv_in", "qk_ready"))
        dve_step, exps, o_ready, o_turned, oT_in, moved, yT_in, out_ready, out_used = (
            sem(x) for x in ("dve_step", "exps", "o_ready", "o_turned", "oT_in", "moved", "yT_in", "out_ready", "out_used"))
        block = ctx.enter_context(nc.Block())
        STEPS = 4 + 2 + 3 + 8

        @block.tensor
        def _(pe):
            pe.wait_ge(const_in, 32)
            for signal in (moved, out_ready, o_turned):
                pe.sem_inc(signal, FROM)
            for b in range(B):
                for g in range(2 * b, 2 * b + 2):
                    if g >= 1:
                        pe.wait_ge(qkv_in, g)
                        pe.wait_ge(yT_in, b)
                    for t in range(4):
                        n = 4 * g + t
                        ins = pe.matmul(ps_q[:, t, 0:3 * D], m.xnT[:, n * P:(n + 1) * P], m.wqkv2[:, :, :].rearrange("p c d -> p (c d)"),
                                        start=True, stop=True)
                    ins.then_inc(qkv_ready, 1)
                    pe.wait_ge(o_ready, FROM + g + 1)
                    if g >= 1:
                        pe.wait_ge(oT_in, g)
                    for t in range(4):
                        ins = pe.transpose(ps_t[:, t * P:(t + 1) * P], o[:, t, :], m.ident)
                    ins.then_inc(o_turned, 1)
                pe.wait_ge(oT_in, 2 * b + 2)
                pe.wait_ge(qkv_in, 2 * b + 2)
                for h in range(H):
                    q = 32 * (h // 2)
                    for l in range(8):
                        ins = pe.matmul(ps_g[:, h // 2, h % 2, :], move[q:q + 32, h % 2, l, :], oT[q:q + 32, l:S:8], start=(l == 0), stop=(l == 7))
                ins.then_inc(moved, 1)
                pe.wait_ge(yT_in, b + 1)
                for g in range(2 * b, 2 * b + 2):
                    if g >= 1:
                        pe.wait_ge(out_used, g)
                    for t in range(4):
                        n = (4 * g + t) % CH
                        pe.matmul(ps_o[:, t * P:(t + 1) * P], yT[:, n * P:(n + 1) * P], m.wproj2[:, :], start=True, stop=False)
                        ins = pe.matmul(ps_o[:, t * P:(t + 1) * P], m.one[0:1, :], b_proj[:, :], start=False, stop=True)
                    ins.then_inc(out_ready, 1)

        @block.scalar
        def _(act):
            act.activation(prime[:, :], m.pid, ACT.Exp, scale=-1.0)
            with act.Fori(0, B) as b:
                for half in range(2):
                    g = b * 2 + half
                    act.wait_ge(qkv_ready, g + 1)
                    act.wait_ge(o_ready, FROM + g)
                    act.activation(qkv[:, :, :], ps_q[:, :, 0:3 * D], ACT.Copy).then_inc(qkv_in, 1)
                    act.wait_ge(dve_step, FROM + g * STEPS + 6)
                    act.activation(e[:, :, :, :], s[:, :, :, :], ACT.Exp, scale=float(HW) ** -0.5).then_inc(exps, 1)
                    act.wait_ge(o_turned, FROM + g + 1)
                    act.wait_ge(moved, FROM + b)
                    if half == 0:
                        act.activation(oT[:, S - ROLL:S], ps_t[:, 0:ROLL], ACT.Copy)
                        act.activation(oT[:, 0:BANK - ROLL], ps_t[:, ROLL:BANK], ACT.Copy).then_inc(oT_in, 1)
                    else:
                        act.activation(oT[:, BANK - ROLL:S - ROLL], ps_t[:, :], ACT.Copy).then_inc(oT_in, 1)
                act.wait_ge(moved, FROM + b + 1)
                act.wait_ge(out_ready, FROM + b * 2)
                of = ps_g.rearrange("p q a (k r) -> p q a k r", r=8)
                to = yT[:, ROLL:ROLL + S].rearrange("p (k h r) -> p k h r", h=H, r=8)
                for h in range(H):
                    act.activation(to[:, 0:15, h, :], of[:, h // 2, h % 2, 0:15, :], ACT.Copy)
                for half in range(2):
                    place = (to[:, 15, 0:4, :] if half == 0 else yT[:, 0:ROLL].rearrange("p (h r) -> p h r", r=8))
                    ins = act.activation(place.rearrange("p (q a) r -> p q a r", a=2), of[:, 2 * half:2 * half + 2, :, 15, :], ACT.Copy)
                ins.then_inc(yT_in, 1)

        @block.gpsimd
        def _(pool):
            with pool.Fori(0, 2 * B) as g:
                pool.wait_ge(qkv_in, g + 1)
                for t in range(4):
                    pool.wait_ge(dve_step, FROM + g * STEPS + max(t - 1, 0))
                    q = qkv[:, t, 0:D].rearrange("p (h d) -> p h d", h=H).unsqueeze(2).broadcast_to([P, H, H, HW])
                    k = qkv[:, t, D:2 * D].rearrange("p (h d) -> p h d", h=H).unsqueeze(1).broadcast_to([P, H, H, HW])
                    pool.tensor_tensor(qk[:, t % 2, :, :, :], q, k, ALU.mult).then_inc(qk_ready, 1)

        @block.vector
        def _(dve):
            for signal in (o_ready, dve_step):
                dve.sem_inc(signal, FROM)
            with dve.Fori(0, B) as b:
                for half in range(2):
                    g = b * 2 + half
                    steps = [0]

                    def link(ins):
                        steps[0] += 1
                        ins.then_inc(dve_step, 1)
                        dve.wait_ge(dve_step, FROM + g * STEPS + steps[0])

                    for t in range(4):
                        dve.wait_ge(qk_ready, g * 4 + t + 1)
                        link(dve.tensor_reduce(s[:, t, :, :].rearrange("p h g -> p (h g)"), qk[:, t % 2, :, :, :].rearrange("p h g d -> p (h g) d"), AX.X, ALU.add))
                    s2, e2 = (x.rearrange("p t h g -> p (t h) g") for x in (s[:, :, :, :], e[:, :, :, :]))
                    mx1 = mx[:, :, :].rearrange("p t h -> p (t h)")
                    wide_mx = mx1.unsqueeze(2).broadcast_to([P, 4 * H, H])
                    link(dve.tensor_reduce(mx1, s2, AX.X, ALU.max))
                    link(dve.tensor_tensor(s2, s2, wide_mx, ALU.subtract))
                    dve.wait_ge(exps, g + 1)
                    link(dve.tensor_reduce(mx1, e2, AX.X, ALU.add))
                    link(dve.reciprocal(mx1, mx1))
                    link(dve.tensor_tensor(e2, e2, wide_mx, ALU.mult))
                    dve.wait_ge(o_turned, FROM + g)
                    for t in range(4):
                        a = e[:, t, :, :].unsqueeze(2).broadcast_to([P, H, HW, H])
                        v = qkv[:, t, 2 * D:3 * D].rearrange("p (g d) -> p d g", g=H).unsqueeze(1).broadcast_to([P, H, HW, H])
                        link(dve.tensor_tensor(av[:, t % 2, :, :, :], a, v, ALU.mult))
                        link(dve.tensor_reduce(o[:, t, :], av[:, t % 2, :, :, :].rearrange("p h d g -> p (h d) g"), AX.X, ALU.add))
                    dve.sem_inc(o_ready, 1)
                for half in range(2):
                    g = b * 2 + half
                    dve.wait_ge(out_ready, FROM + g + 1)
                    hh = m.h[:, bass.ds(g * 4, 4), :]
                    dve.tensor_tensor(hh, hh, ps_o[:, :].rearrange("p (t d) -> p t d", t=4), ALU.add).then_inc(out_used, 1)


TOPK = 16
TH, TW = 8, 16


def stage_l2_ffn(nc, m, w):
    layernorm(nc, m, "ln_l2f", m.h, m.xn, m.xnT)
    with ExitStack() as ctx:
        def sb(name, shape, dt=F32):
            return ctx.enter_context(nc.sbuf_tensor(f"t_{name}", shape, dt))

        r = Core()
        r.xc = sb("xc", [P, N])
        r.v = sb("v", [P, TILES, TH, TW + 1])
        r.wpad = sb("wpad", [P, 2, 2, P])
        r.bpad = sb("bpad", [P, 2, 2])
        r.wo_b = sb("wo_b", [1, D])
        topk_prepare(nc, m, r, w)
        topk_attend(nc, m, r)


def topk_prepare(nc, m, r, w):
    with ExitStack() as ctx:
        def sb(name, shape, dt=F32):
            return ctx.enter_context(nc.sbuf_tensor(f"tp_{name}", shape, dt))

        sem = signals(nc, m, "tp_")

        posw, posb, qkvb = sb("posw", [P, 3]), sb("posb", [P, 1]), sb("qkvb", [1, 3 * D])
        brow = sb("brow", [1, 2, 2, P])
        ps_v = ctx.enter_context(nc.psum_tensor("tp_ps_v", [P, 2, BANK], F32))
        ps_b = ctx.enter_context(nc.psum_tensor("tp_ps_b", [P, BANK], F32))
        loaded, dve_step, pool_step, v_ready, v_done, b_ready = (
            sem(x) for x in ("loaded", "dve_step", "pool_step", "v_ready", "v_done", "b_ready"))
        block = ctx.enter_context(nc.Block())

        @block.sync
        def _(sp):
            sp.dma_start(posw[:, :], w["L2_ffn_pos_w"].rearrange("d a k -> d (a k)")).then_inc(loaded, 16)
            sp.dma_start(posb[:, :], col(w["L2_ffn_pos_b"]), allow_slow_non_contiguous=True).then_inc(loaded, 16)
            sp.dma_start(qkvb[:, :], row(w["L2_ffn_qkv_b"])).then_inc(loaded, 16)
            sp.dma_start(r.wo_b[:, :], row(w["L2_ffn_wo_b"])).then_inc(loaded, 16)
            sp.wait_ge(loaded, 64)

        @block.gpsimd
        def _(pool):
            pool.memset(r.v[:, :, :, TW:TW + 1], 1.0)
            pool.memset(r.wpad[:, :, :, :], 0.0).then_inc(pool_step, 1)
            pool.memset(brow[:, :, :, :], 0.0).then_inc(pool_step, 1)
            pool.wait_ge(loaded, 64)
            pool.wait_ge(pool_step, 2)
            for kind in range(2):
                pool.tensor_copy(r.wpad[:, kind, :, :].rearrange("p g (h x) -> p (g h) x", x=32)[:, :, 0:TW],
                                 m.wqkv3[:, kind, :].rearrange("p (gh d) -> p gh d", d=TW)).then_inc(pool_step, 1)
                pool.tensor_copy(brow[:, kind, :, :].rearrange("p g (h x) -> p (g h) x", x=32)[:, :, 0:TW],
                                 qkvb[:, kind * D:(kind + 1) * D].rearrange("p (gh d) -> p gh d", d=TW)).then_inc(pool_step, 1)

        @block.tensor
        def _(pe):
            pe.wait_ge(pool_step, 6)
            for n in range(4):
                ins = pe.matmul(ps_b[:, n:n + 1], brow[0:1, n // 2, n % 2, :], m.one[0:1, 0:1], start=True, stop=True)
            ins.then_inc(b_ready, 1)
            pe.wait_ge(dve_step, 6)
            for t in range(TILES):
                if t >= 2:
                    pe.wait_ge(v_done, t - 1)
                pe.matmul(ps_v[:, t % 2, 0:D], r.xc[:, t * P:(t + 1) * P], m.wqkv3[:, 2, :], start=True, stop=False)
                pe.matmul(ps_v[:, t % 2, 0:D], m.one[0:1, :], qkvb[:, 2 * D:3 * D], start=False, stop=True).then_inc(v_ready, 1)

        @block.scalar
        def _(act):
            for t in range(TILES):
                act.wait_ge(v_ready, t + 1)
                act.activation(r.v[:, t, :, 0:TW], ps_v[:, t % 2, 0:D].rearrange("p (h d) -> p h d", h=TH), ACT.Copy).then_inc(v_done, 1)

        @block.vector
        def _(dve):
            steps = [0]

            def link(ins):
                steps[0] += 1
                ins.then_inc(dve_step, 1)
                dve.wait_ge(dve_step, steps[0])

            dve.wait_ge(loaded, 64)
            mid = posw[:, 1:2]
            link(dve.tensor_scalar(mid, mid, 1.0, None, ALU.add))
            link(dve.tensor_scalar(r.xc[:, :], m.xnT[:, :], mid, posb[:, 0:1], ALU.mult, ALU.add))
            for b in range(B):
                a, z = b * S, (b + 1) * S
                link(dve.scalar_tensor_tensor(r.xc[:, a + 1:z], m.xnT[:, a:z - 1], posw[:, 0:1], r.xc[:, a + 1:z], ALU.mult, ALU.add))
                link(dve.scalar_tensor_tensor(r.xc[:, a:z - 1], m.xnT[:, a + 1:z], posw[:, 2:3], r.xc[:, a:z - 1], ALU.mult, ALU.add))
            dve.wait_ge(b_ready, 1)
            dve.tensor_copy(r.bpad[:, :, :].rearrange("p a b -> p (a b)"), ps_b[:, 0:4])


def topk_attend(nc, m, r):
    SC = float(D) ** -0.5
    PAIR, FIRST, AHEAD = 2 * TH, 5, 3
    KEPT = 4
    nc.disable_value_cache = True
    with ExitStack() as ctx:
        def sb(name, shape, dt=F32):
            return ctx.enter_context(nc.sbuf_tensor(f"ta_{name}", shape, dt))

        sem = signals(nc, m, "ta_")
        qT, kT = sb("qT", [P, 2, S]), sb("kT", [P, 2, S])
        vseq = sb("vseq", [P, CH, TH, 2 * TW])
        qs = sb("qs", [P, 2, 2, P])
        top, ntop = sb("top", [P, 2, 2, 8]), sb("ntop", [P, 4])
        left = sb("left", [P, 4, S])
        ex = sb("ex", [P, 4, S])
        exT = sb("exT", [P, 2, CH, P])
        acc = sb("acc", [P, 2, P])
        rden, o, oT = sb("rden", [P, TH]), sb("o", [P, D]), sb("oT", [P, D])
        prime = sb("prime", [P, 1])
        ps_s = ctx.enter_context(nc.psum_tensor("ta_ps_s", [P, 2, S], F32))
        ps_t = ctx.enter_context(nc.psum_tensor("ta_ps_t", [P, S], F32))
        ps_o = ctx.enter_context(nc.psum_tensor("ta_ps_o", [P, BANK], F32))
        ps_p = ctx.enter_context(nc.psum_tensor("ta_ps_p", [P, BANK], F32))
        proj_ready, proj_done, q_in, v_in = sem("proj_ready"), sem("proj_done"), sem("q_in"), sem("v_in")
        s_ready, s_free, first_out, dve_step, left_ready, left_exp, kept, turned, exT_in = (
            sem(x) for x in ("s_ready", "s_free", "first_out", "dve_step", "left_ready", "left_exp", "kept", "turned", "exT_in"))
        acc_out, acc_turned = sem("acc_out"), sem("acc_turned")
        values_done, rden_ready, o_ready, o_turned, oT_in, out_ready, out_used = (
            sem(x) for x in ("values_done", "rden_ready", "o_ready", "o_turned", "oT_in", "out_ready", "out_used"))
        block = ctx.enter_context(nc.Block())
        PAIRS = CH // 2

        def sequence(eng, b, step):
            def place(tp):
                return eng.snap(b * (PAIRS * PAIR) + tp * PAIR), eng.snap(b * CH + tp * 2), tp * (2 * P)

            item0, tile0, query0 = place(0)
            for i in range(FIRST):
                step(item0, tile0, query0, i, False)
            with eng.Fori(0, PAIRS - 1) as tp:
                item0, tile0, query0 = place(tp)
                for i in range(FIRST, PAIR + FIRST):
                    step(item0, tile0, query0, i, False)
            item0, tile0, query0 = place(PAIRS - 1)
            for i in range(FIRST, PAIR + FIRST):
                step(item0, tile0, query0, i, True)

        @block.tensor
        def _(pe):
            with pe.Fori(0, B) as b:
                def logits(item0, tile0, i):
                    h, odd, n = i % TH, (i // TH) % 2, item0 + i
                    grp, a = h // 4, 32 * (h % 4)
                    if h == 0:
                        pe.wait_ge(q_in, tile0 + (i // TH + 1))
                    pe.wait_ge(s_free, n + 1)
                    for half in range(2):
                        ins = pe.matmul(ps_s[:, i % 2, half * BANK:(half + 1) * BANK], qs[a:a + TW, odd, grp, :],
                                        kT[a:a + TW, grp, half * BANK:(half + 1) * BANK], start=True, stop=True)
                    ins.then_inc(s_ready, 1)

                def step(item0, tile0, query0, i, last):
                    h, n = i % TH, item0 + i
                    if i >= TH and h == 1:
                        tile = tile0 + (i // TH - 1)
                        pe.wait_ge(acc_out, tile + 2)
                        pe.wait_ge(out_used, tile + 1)
                        for grp in range(2):
                            ins = pe.transpose(ps_p[:, grp * P:(grp + 1) * P], acc[:, grp, :], m.ident)
                        ins.then_inc(acc_turned, 1)
                    if i >= TH and h == 2:
                        tile = tile0 + (i // TH - 1)
                        pe.wait_ge(o_ready, tile + 1)
                        pe.transpose(ps_p[:, 0:P], o[:, :], m.ident).then_inc(o_turned, 1)
                    if i >= TH and h == 3:
                        tile = tile0 + (i // TH - 1)
                        pe.wait_ge(oT_in, tile + 1)
                        pe.matmul(ps_p[:, 0:P], oT[:, :], m.wo[:, :], start=True, stop=False)
                        pe.matmul(ps_p[:, 0:P], m.one[0:1, :], r.wo_b[:, :], start=False, stop=True).then_inc(out_ready, 1)
                    if i < PAIR or not last:
                        pe.wait_ge(kept, n + (KEPT + 1))
                        for j in range(CH):
                            ins = pe.transpose(ps_t[:, j * P:(j + 1) * P], ex[:, i % 4, j * P:(j + 1) * P], m.ident)
                        ins.then_inc(turned, 1)
                    if i + AHEAD < PAIR or not last:
                        logits(item0, tile0, i + AHEAD)
                    if i < PAIR or not last:
                        pe.wait_ge(exT_in, n + 1)
                        if h == 0:
                            pe.wait_ge(acc_out, tile0 + (i // TH + 1))
                        a, grp = 32 * (h % 4), h // 4
                        for j in range(CH):
                            ins = pe.matmul(ps_o[a:a + 2 * TW, grp * P:(grp + 1) * P], vseq[:, j, h, :], exT[:, i % 2, j, :],
                                            start=(j == 0), stop=(j == CH - 1))
                        if h == TH - 1:
                            ins.then_inc(values_done, 1)

                pe.wait_ge(out_used, b * CH + 1)
                for n in range(8):
                    kind, grp, half = n // 4, (n // 2) % 2, n % 2
                    pe.wait_ge(proj_done, b * 8 + (n + 1))
                    pe.matmul(ps_p[:, :], r.wpad[:, kind, grp, :], r.xc[:, bass.ds(b * S + half * BANK, BANK)],
                              start=True, stop=True).then_inc(proj_ready, 1)
                pe.wait_ge(proj_done, b * 8 + 9)
                pe.wait_ge(v_in, b + 2)
                for i in range(AHEAD):
                    logits(pe.snap(b * (PAIRS * PAIR)), pe.snap(b * CH), i)
                sequence(pe, b, step)

        @block.scalar
        def _(act):
            def query(tile_rel, query0):
                k = tile_rel % 2
                act.activation(qs[:, k, :, :], qT[:, :, bass.ds(query0 + tile_rel * P, P)], ACT.Copy).then_inc(q_in, 1)

            def all_exp(item0, i):
                act.wait_ge(first_out, item0 + (i + 1))
                act.nop(nofuse=True)
                act.activation(ex[:, i % 4, :], ps_s[:, i % 2, :], ACT.Exp, bias=ntop[:, i % 4:i % 4 + 1], scale=SC).then_inc(s_free, 1)

            def turn(item0, i):
                act.wait_ge(turned, item0 + (i + 1))
                act.activation(exT[:, i % 2, :, :].rearrange("p j q -> p (j q)"), ps_t[:, :], ACT.Copy).then_inc(exT_in, 1)

            def step(item0, tile0, query0, i, last):
                h, n = i % TH, item0 + i
                if i < PAIR or not last:
                    act.wait_ge(left_ready, n + 1)
                    act.activation(left[:, i % 4, :], left[:, i % 4, :], ACT.Exp, bias=ntop[:, i % 4:i % 4 + 1], scale=SC).then_inc(left_exp, 1)
                if i >= TH and h == 1:
                    act.wait_ge(values_done, tile0 + i // TH)
                    act.activation(acc[:, :, :].rearrange("p g q -> p (g q)"), ps_o[:, 0:2 * P], ACT.Copy).then_inc(acc_out, 1)
                if i >= TH and h == 3:
                    act.wait_ge(o_turned, tile0 + i // TH)
                    act.activation(oT[:, :], ps_p[:, 0:P], ACT.Copy).then_inc(oT_in, 1)
                if 1 <= i <= PAIR or (i > PAIR and not last):
                    turn(item0, i - 1)
                if i + 1 < PAIR or not last:
                    all_exp(item0, i + 1)
                if h == 3 and (i < TH or not last):
                    query(i // TH + 1, query0)

            act.activation(prime[:, :], m.pid, ACT.Exp, scale=-1.0)
            act.sem_inc(proj_done, 1)
            act.sem_inc(s_free, 2)
            act.sem_inc(acc_out, 1)
            with act.Fori(0, B) as b:
                for n in range(8):
                    kind, grp, half = n // 4, (n // 2) % 2, n % 2
                    act.wait_ge(proj_ready, b * 8 + n + 1)
                    act.nop(nofuse=True)
                    to = (qT, kT)[kind]
                    act.activation(to[:, grp, half * BANK:(half + 1) * BANK], ps_p[:, :], ACT.Identity,
                                   bias=r.bpad[:, kind, grp:grp + 1]).then_inc(proj_done, 1)
                act.wait_ge(v_in, b + 1)
                act.nop(nofuse=True)
                act.activation(vseq[:, :, :, 0:TW + 1], r.v[:, bass.ds(b * CH, CH), :, :],
                               ACT.Copy).then_inc(v_in, 1)
                act.wait_ge(proj_done, b * 8 + 9)
                query(0, 0)
                all_exp(act.snap(b * (PAIRS * PAIR)), 0)
                sequence(act, b, step)

        @block.gpsimd
        def _(pool):
            def step(item0, tile0, query0, i, last):
                if i < PAIR or not last:
                    pool.wait_ge(left_exp, item0 + (i + 1))
                    pool.tensor_tensor(ex[:, i % 4, :], ex[:, i % 4, :], left[:, i % 4, :], ALU.subtract).then_inc(kept, 1)

            pool.memset(vseq[:, :, :, :], 0.0).then_inc(v_in, 1)
            pool.sem_inc(kept, KEPT)
            with pool.Fori(0, B) as b:
                sequence(pool, b, step)

        @block.vector
        def _(dve):
            def step(item0, tile0, query0, i, last):
                h, n, k = i % TH, item0 + i, i % 2
                logits, rest = ps_s[:, k, :], left[:, i % 4, :]
                if i < PAIR or not last:
                    dve.wait_ge(s_ready, n + 1)
                    dve.nop(nofuse=True)
                    dve.max(top[:, k, 0, :], logits).then_inc(dve_step, 1)
                    dve.wait_ge(dve_step, n * 3 + 1)
                    dve.tensor_scalar(ntop[:, i % 4:i % 4 + 1], top[:, k, 0, 0:1], -SC, None, ALU.mult)
                    dve.wait_ge(kept, n + 1)
                    dve.nop(nofuse=True)
                    dve.match_replace(rest, top[:, k, 0, :], logits, -BIG).then_inc(first_out, 1)
                    dve.wait_ge(first_out, n + 1)
                    dve.nop(nofuse=True)
                    dve.max(top[:, k, 1, :], rest).then_inc(dve_step, 1)
                    dve.wait_ge(dve_step, n * 3 + 2)
                    dve.nop(nofuse=True)
                    dve.match_replace(rest, top[:, k, 1, :], rest, -BIG).then_inc(left_ready, 1)
                    dve.sem_inc(dve_step, 1)
                if i >= TH and h == 2:
                    tile = tile0 + (i // TH - 1)
                    out = ps_p[:, 0:2 * P].rearrange("p (h d) -> p h d", h=TH)
                    dve.wait_ge(acc_turned, tile + 1)
                    dve.reciprocal(rden[:, :], out[:, :, TW]).then_inc(rden_ready, 1)
                    dve.wait_ge(rden_ready, tile + 1)
                    dve.tensor_tensor(o[:, :].rearrange("p (h d) -> p h d", h=TH), out[:, :, 0:TW],
                                      rden[:, :].unsqueeze(2).broadcast_to([P, TH, TW]), ALU.mult).then_inc(o_ready, 1)
                if i >= TH and h == 4:
                    tile = tile0 + (i // TH - 1)
                    dve.wait_ge(out_ready, tile + 1)
                    hh = m.h[:, bass.ds(tile, 1), :]
                    dve.tensor_tensor(hh, hh, ps_p[:, 0:P].unsqueeze(1), ALU.add).then_inc(out_used, 1)

            dve.sem_inc(out_used, 1)
            with dve.Fori(0, B) as b:
                sequence(dve, b, step)


def stage_l3_attn(nc, m, w):
    ST = 64
    with ExitStack() as ctx:
        def sb(name, shape, dt=F32):
            return ctx.enter_context(nc.sbuf_tensor(f"l3_{name}", shape, dt))

        r = Core()
        r.B, r.C, r.D = sb("B", [ST, D, 2]), sb("C", [P, ST, 2]), sb("D", [P, 1])
        r.par = sb("par", [P, 3])
        r.w1, r.w2, r.v1, r.v2, r.dd = (sb(x, [P, P]) for x in ("w1", "w2", "v1", "v2", "dd"))
        r.cos, r.sin, r.fade = sb("cos", [P, S]), sb("sin", [P, S]), sb("fade", [P, 1])
        r.par_in = signals(nc, m, "l3_")("par_in")
        with nc.Block() as block:
            @block.sync
            def _(sp):
                for half in range(2):
                    for i, name in enumerate(("Lambda_re", "Lambda_im", "log_step")):
                        sp.dma_start(r.par[half * ST:(half + 1) * ST, i:i + 1], col(w["L3_attn_" + name]),
                                     allow_slow_non_contiguous=True).then_inc(r.par_in, 16)
                sp.dma_start(r.B[:, :, :], w["L3_attn_B"]).then_inc(r.par_in, 16)
                sp.dma_start(r.C[:, :, :], w["L3_attn_C"]).then_inc(r.par_in, 16)
                sp.dma_start(r.D[:, :], col(w["L3_attn_D"]), allow_slow_non_contiguous=True).then_inc(r.par_in, 16)
        r.n_par = 9 * 16
        layernorm(nc, m, "ln_l3a", m.h, m.xn, m.xnT)
        ssm_prepare(nc, m, r, ST)
        ssm_run(nc, m, r)


def ssm_prepare(nc, m, r, ST):
    with ExitStack() as ctx:
        def sb(name, shape, dt=F32):
            return ctx.enter_context(nc.sbuf_tensor(f"l3p_{name}", shape, dt))

        small = sb("small", [P, 32])
        names = ("step angle turns r half sh sr c s a b den t1 t2 gr gi magr pc ps").split()
        v = {name: small[:, i:i + 1] for i, name in enumerate(names)}
        power = sb("power", [P, 2, 12])
        tmp = sb("tmp", [P, 2, S // 2])
        bbar = sb("bbar", [ST, 2, D])
        tb = sb("tb", [ST, 2, D])
        x1, x2 = sb("x1", [P, 2, ST]), sb("x2", [P, 2, ST])
        ps_b = ctx.enter_context(nc.psum_tensor("l3p_ps_b", [P, BANK], F32))
        ps_c = ctx.enter_context(nc.psum_tensor("l3p_ps_c", [P, BANK], F32))
        sem = signals(nc, m, "l3p_")
        dve_step, act_step, outs, turned, x_ready = (sem(k) for k in ("dve_step", "act_step", "outs", "turned", "x_ready"))
        TWO_PI = 2.0 * np.pi
        TWO_PI_HI = 6.28125
        ROUND = 12582912.0
        PI_BELOW = 3.1415925
        block = ctx.enter_context(nc.Block())

        @block.scalar
        def _(act):
            act.wait_ge(r.par_in, r.n_par)
            act.activation(v["step"], r.par[:, 2:3], ACT.Exp).then_inc(act_step, 1)
            act.wait_ge(act_step, 1)
            act.activation(r.fade[:, :], r.par[:, 0:1], ACT.Exp, scale=v["step"]).then_inc(act_step, 1)
            act.wait_ge(dve_step, 7)
            act.activation(v["sr"], v["r"], ACT.Sin).then_inc(act_step, 1)
            act.activation(v["sh"], v["half"], ACT.Sin).then_inc(act_step, 1)
            act.wait_ge(turned, 1)
            act.activation(r.w1[:, :], ps_b[:, 0:P], ACT.Copy)
            act.activation(r.w2[:, 0:ST], ps_b[:, ST:2 * ST], ACT.Copy)
            act.activation(r.w2[:, ST:P], ps_b[:, 0:ST], ACT.Copy, scale=-1.0)
            act.activation(r.v1[:, :], ps_c[:, 0:P], ACT.Copy)
            act.activation(r.v2[:, :], ps_c[:, P:2 * P], ACT.Copy)

        @block.gpsimd
        def _(pool):
            pool.wait_ge(r.par_in, r.n_par)
            pool.tensor_scalar(x1[:, 0, :], r.C[:, :, 0], 2.0, None, ALU.mult)
            pool.tensor_scalar(x1[:, 1, :], r.C[:, :, 1], -2.0, None, ALU.mult)
            pool.tensor_scalar(x2[:, 0, :], r.C[:, :, 1], -2.0, None, ALU.mult)
            pool.tensor_scalar(x2[:, 1, :], r.C[:, :, 0], -2.0, None, ALU.mult)
            pool.tensor_scalar(r.dd[:, :], m.ident, r.D[:, 0:1], None, ALU.mult).then_inc(x_ready, 1)

        @block.tensor
        def _(pe):
            pe.wait_ge(x_ready, 1)
            pe.transpose(ps_c[:, 0:P], x1[:, :, :].rearrange("p a s -> p (a s)"), m.ident)
            pe.transpose(ps_c[:, P:2 * P], x2[:, :, :].rearrange("p a s -> p (a s)"), m.ident)
            pe.wait_ge(outs, 1)
            pe.transpose(ps_b[:, 0:ST], bbar[:, 0, :], m.ident[0:ST, 0:ST])
            pe.transpose(ps_b[:, ST:P], bbar[:, 1, :], m.ident[0:ST, 0:ST]).then_inc(turned, 1)

        @block.vector
        def _(dve):
            steps = [0]

            def link(ins):
                steps[0] += 1
                ins.then_inc(dve_step, 1)
                dve.wait_ge(dve_step, steps[0])

            re, im = r.par[:, 0:1], r.par[:, 1:2]
            dve.wait_ge(act_step, 1)
            link(dve.tensor_tensor(v["angle"], im, v["step"], ALU.mult))
            link(dve.tensor_scalar(v["turns"], v["angle"], 1.0 / TWO_PI, ROUND, ALU.mult, ALU.add))
            link(dve.tensor_scalar(v["turns"], v["turns"], ROUND, None, ALU.subtract))
            link(dve.scalar_tensor_tensor(v["r"], v["turns"], -TWO_PI_HI, v["angle"], ALU.mult, ALU.add))
            link(dve.scalar_tensor_tensor(v["r"], v["turns"], -(TWO_PI - TWO_PI_HI), v["r"], ALU.mult, ALU.add))
            link(dve.tensor_scalar(v["r"], v["r"], PI_BELOW, -PI_BELOW, ALU.min, ALU.max))
            link(dve.tensor_scalar(v["half"], v["r"], 0.5, None, ALU.mult))
            link(dve.tensor_tensor(v["t1"], re, re, ALU.mult))
            link(dve.scalar_tensor_tensor(v["den"], im, im, v["t1"], ALU.mult, ALU.add))
            link(dve.reciprocal(v["den"], v["den"]))
            dve.wait_ge(act_step, 4)
            link(dve.tensor_copy(power[:, 1, 0:1], v["sr"]))
            link(dve.tensor_tensor(v["t1"], v["sh"], v["sh"], ALU.mult))
            link(dve.tensor_scalar(power[:, 0, 0:1], v["t1"], -2.0, 1.0, ALU.mult, ALU.add))
            link(dve.tensor_scalar(v["a"], power[:, 0, 0:1], r.fade[:, 0:1], 1.0, ALU.mult, ALU.subtract))
            link(dve.tensor_tensor(v["b"], power[:, 1, 0:1], r.fade[:, 0:1], ALU.mult))
            link(dve.tensor_tensor(v["t1"], v["a"], re, ALU.mult))
            link(dve.scalar_tensor_tensor(v["gr"], v["b"], im, v["t1"], ALU.mult, ALU.add))
            link(dve.tensor_tensor(v["gr"], v["gr"], v["den"], ALU.mult))
            link(dve.tensor_tensor(v["t2"], v["a"], im, ALU.mult))
            link(dve.scalar_tensor_tensor(v["gi"], v["b"], re, v["t2"], ALU.mult, ALU.subtract))
            link(dve.tensor_tensor(v["gi"], v["gi"], v["den"], ALU.mult))
            gr, gi = small[0:ST, names.index("gr"):names.index("gr") + 1], small[0:ST, names.index("gi"):names.index("gi") + 1]
            link(dve.tensor_scalar(tb[:, 0, :], r.B[:, :, 1], gi, None, ALU.mult))
            link(dve.tensor_scalar(tb[:, 1, :], r.B[:, :, 0], gi, None, ALU.mult))
            link(dve.scalar_tensor_tensor(bbar[:, 0, :], r.B[:, :, 0], gr, tb[:, 0, :], ALU.mult, ALU.subtract))
            link(dve.scalar_tensor_tensor(bbar[:, 1, :], r.B[:, :, 1], gr, tb[:, 1, :], ALU.mult, ALU.add))
            dve.memset(r.cos[:, 0:1], 1.0).then_inc(outs, 1)
            link(dve.memset(r.sin[:, 0:1], 0.0))
            for i in range(10):
                n = 1 << i
                pc, ps = power[:, 0, i:i + 1], power[:, 1, i:i + 1]
                c0, s0, c1, s1 = r.cos[:, 0:n], r.sin[:, 0:n], r.cos[:, n:2 * n], r.sin[:, n:2 * n]
                dve.tensor_scalar(tmp[:, 0, 0:n], s0, ps, None, ALU.mult)
                dve.tensor_scalar(tmp[:, 1, 0:n], c0, ps, None, ALU.mult)
                link(dve.tensor_tensor(v["t1"], ps, ps, ALU.mult))
                dve.scalar_tensor_tensor(c1, c0, pc, tmp[:, 0, 0:n], ALU.mult, ALU.subtract)
                dve.scalar_tensor_tensor(s1, s0, pc, tmp[:, 1, 0:n], ALU.mult, ALU.add)
                dve.scalar_tensor_tensor(power[:, 0, i + 1:i + 2], pc, pc, v["t1"], ALU.mult, ALU.subtract)
                link(dve.scalar_tensor_tensor(power[:, 1, i + 1:i + 2], pc, 2.0, ps, ALU.mult, ALU.mult))


def ssm_run(nc, m, r):
    JOBS = N // BANK
    with ExitStack() as ctx:
        def sb(name, shape, dt=F32):
            return ctx.enter_context(nc.sbuf_tensor(f"l3r_{name}", shape, dt))

        sem = signals(nc, m, "l3r_")

        z1, z2, z = sb("z1", [P, 2, BANK]), sb("z2", [P, 2, BANK]), sb("z", [P, 2, BANK])
        y, u, v = sb("y", [P, JOBS, BANK]), sb("u", [P, 2, BANK]), sb("v", [P, 2, BANK])
        ps_1 = ctx.enter_context(nc.psum_tensor("l3r_ps_1", [P, 2, BANK], F32))
        ps_2 = ctx.enter_context(nc.psum_tensor("l3r_ps_2", [P, 2, BANK], F32))
        ps_o = ctx.enter_context(nc.psum_tensor("l3r_ps_o", [P, 2, BANK], F32))
        bu_ready, bu_used, z_ready, y_ready, u_ready, v_ready, out_ready, out_used = (
            sem(k) for k in ("bu_ready", "bu_used", "z_ready", "y_ready", "u_ready", "v_ready", "out_ready", "out_used"))
        block = ctx.enter_context(nc.Block())

        @block.tensor
        def _(pe):
            def drive(j):
                if j >= 2:
                    pe.wait_ge(bu_used, j - 1)
                pe.matmul(ps_1[:, j % 2, :], r.w1[:, :], m.xnT[:, j * BANK:(j + 1) * BANK], start=True, stop=True)
                pe.matmul(ps_2[:, j % 2, :], r.w2[:, :], m.xnT[:, j * BANK:(j + 1) * BANK], start=True, stop=True).then_inc(bu_ready, 1)

            drive(0)
            for j in range(JOBS):
                if j + 1 < JOBS:
                    drive(j + 1)
                pe.wait_ge(u_ready, j + 1)
                pe.wait_ge(v_ready, j + 1)
                if j >= 2:
                    pe.wait_ge(out_used, j - 1)
                for t in range(4):
                    c = slice(t * P, (t + 1) * P)
                    pe.matmul(ps_o[:, j % 2, c], u[:, j % 2, c], r.v1[:, :], start=True, stop=False)
                    pe.matmul(ps_o[:, j % 2, c], v[:, j % 2, c], r.v2[:, :], start=False, stop=False)
                    ins = pe.matmul(ps_o[:, j % 2, c], m.xnT[:, j * BANK + t * P:j * BANK + (t + 1) * P], r.dd[:, :], start=False, stop=True)
                ins.then_inc(out_ready, 1)

        @block.vector
        def _(dve):
            def add(j):
                dve.wait_ge(out_ready, j + 1)
                hh = m.h[:, 4 * j:4 * j + 4, :]
                dve.tensor_tensor(hh, hh, ps_o[:, j % 2, :].rearrange("p (t d) -> p t d", t=4), ALU.add).then_inc(out_used, 1)

            for j in range(JOBS):
                k, c = j % 2, slice((j % 2) * BANK, (j % 2 + 1) * BANK)
                dve.wait_ge(bu_ready, j + 1)
                dve.tensor_tensor(z1[:, k, :], ps_1[:, k, :], r.cos[:, c], ALU.mult)
                dve.tensor_tensor(z2[:, k, :], ps_2[:, k, :], r.sin[:, c], ALU.mult).then_inc(bu_used, 1)
                dve.wait_ge(bu_used, j + 1)
                dve.tensor_tensor(z[:, k, :], z1[:, k, :], z2[:, k, :], ALU.add).then_inc(z_ready, 1)
                dve.wait_ge(z_ready, j + 1)
                start = 0.0 if k == 0 else y[:, j - 1, BANK - 1:BANK]
                dve.tensor_tensor_scan(y[:, j, :], r.fade[:, 0:1].broadcast_to([P, BANK]), z[:, k, :], start, ALU.mult, ALU.add)\
                   .then_inc(y_ready, 1)
                dve.wait_ge(y_ready, j + 1)
                if j >= 2:
                    dve.wait_ge(out_ready, j - 1)
                dve.tensor_tensor(u[:, k, :], y[:, j, :], r.cos[:, c], ALU.mult).then_inc(u_ready, 1)
                if j >= 1:
                    add(j - 1)
            add(JOBS - 1)

        @block.gpsimd
        def _(pool):
            for j in range(JOBS):
                k, c = j % 2, slice((j % 2) * BANK, (j % 2 + 1) * BANK)
                pool.wait_ge(y_ready, j + 1)
                if j >= 2:
                    pool.wait_ge(out_ready, j - 1)
                pool.tensor_tensor(v[:, k, :], y[:, j, :], r.sin[:, c], ALU.mult).then_inc(v_ready, 1)


L3_E, L3_I = 16, 96


def stage_l3_ffn(nc, m, w):
    G = L3_E + 1
    with ExitStack() as ctx:
        def sb(name, shape, dt=F32):
            return ctx.enter_context(nc.sbuf_tensor(f"l3f_{name}", shape, dt))

        r = Core()
        r.hT, r.gates = m.xnT, sb("gates", [P, TILES, G])
        r.gate_w, r.b_r = sb("gate_w", [P, L3_E]), sb("b_r", [1, L3_E])
        r.raw_act, r.raw_b1 = sb("raw_act", [P, G, 5]), sb("raw_b1", [G, 2 * L3_I])
        r.g_low, r.g_high, r.g_bias, r.u_bias, r.ag_bias = (sb(x, [L3_I, G]) for x in ("g_low", "g_high", "g_bias", "u_bias", "ag_bias"))
        r.clamp, r.u_limit = sb("clamp", [P, G, 2]), sb("u_limit", [P, G, 2])
        r.b2_dram, r.b2_shared = w["L3_ffn_expert_b2"], row(w["L3_ffn_shared_b2"])
        sem = signals(nc, m, "l3f_")
        r.s_router, r.n_router = sem("router"), 32
        r.s_par, r.n_par = sem("par"), 64
        with nc.Block() as block:
            @block.sync
            def _(sp):
                sp.dma_start(r.gate_w[:, :], w["L3_ffn_gate_w"]).then_inc(r.s_router, 16)
                sp.dma_start(r.b_r[:, :], row(w["L3_ffn_gate_b"])).then_inc(r.s_router, 16)
                sp.dma_start(r.raw_act[:, 0:L3_E, :], w["L3_ffn_expert_act"].rearrange("(o e) a -> o e a", o=1)
                             .broadcast_to([P, L3_E, 5])).then_inc(r.s_par, 16)
                sp.dma_start(r.raw_act[:, L3_E, :], row(w["L3_ffn_shared_act"]).broadcast_to([P, 5])).then_inc(r.s_par, 16)
                sp.dma_start(r.raw_b1[0:L3_E, :], w["L3_ffn_expert_b1"]).then_inc(r.s_par, 16)
                sp.dma_start(r.raw_b1[L3_E:G, :], row(w["L3_ffn_shared_b1"])).then_inc(r.s_par, 16)
        layernorm(nc, m, "ln_l3f", m.h, m.xn, m.xnT)
        router(nc, m, r, "l3r", L3_E, r.gate_w[:, :], m.lower16, 1)
        l3_expert_scalars(nc, m, r)
        l3_experts(nc, m, r, w)


def l3_expert_scalars(nc, m, r):
    G = L3_E + 1
    with ExitStack() as ctx:
        size, ex = (ctx.enter_context(nc.sbuf_tensor(f"l3s_{x}", [P, G, 2], F32)) for x in ("size", "ex"))
        ps = ctx.enter_context(nc.psum_tensor("l3s_ps", [P, BANK], F32))
        sem = signals(nc, m, "l3s_")
        turned, dve_step, act_step = (sem(x) for x in ("turned", "dve_step", "act_step"))
        block = ctx.enter_context(nc.Block())

        @block.tensor
        def _(pe):
            pe.wait_ge(r.s_par, r.n_par)
            pairs = r.raw_b1[:, :].rearrange("e (i two) -> e i two", two=2)
            for k in range(2):
                ins = pe.transpose(ps[0:L3_I, k * G:(k + 1) * G], pairs[:, :, k], m.ident[0:G, 0:G])
            ins.then_inc(turned, 1)

        @block.scalar
        def _(act):
            act.wait_ge(dve_step, 1)
            act.activation(ex[:, :, :], size[:, :, :], ACT.Exp, scale=-1.0).then_inc(act_step, 1)
            act.wait_ge(dve_step, 2)
            act.activation(ex[:, :, :], ex[:, :, :], ACT.Ln).then_inc(act_step, 1)

        @block.vector
        def _(dve):
            steps = [0]

            def link(ins):
                steps[0] += 1
                ins.then_inc(dve_step, 1)
                dve.wait_ge(dve_step, steps[0])

            raw = r.raw_act[:, :, 3:5]
            dve.wait_ge(r.s_par, r.n_par)
            link(dve.scalar_tensor_tensor(size[:, :, :], raw, -1.0, raw, ALU.mult, ALU.max))
            dve.wait_ge(act_step, 1)
            link(dve.tensor_scalar(ex[:, :, :], ex[:, :, :], 1.0, None, ALU.add))
            dve.wait_ge(act_step, 2)
            link(dve.scalar_tensor_tensor(r.clamp[:, :, :], raw, 0.0, ex[:, :, :], ALU.max, ALU.add))
            dve.wait_ge(turned, 1)
            link(dve.tensor_copy(r.g_bias[:, :], ps[0:L3_I, 0:G]))
            link(dve.tensor_copy(r.u_bias[:, :], ps[0:L3_I, G:2 * G]))
            dve.tensor_tensor(r.g_high[:, :], r.clamp[0:L3_I, :, 0], r.g_bias[:, :], ALU.subtract)
            dve.scalar_tensor_tensor(r.g_low[:, :], r.clamp[0:L3_I, :, 0], -1.0, r.g_bias[:, :], ALU.mult, ALU.subtract)
            dve.tensor_tensor(r.ag_bias[:, :], r.g_bias[:, :], r.raw_act[0:L3_I, :, 0], ALU.mult)
            dve.tensor_copy(r.u_limit[:, :, 0], r.clamp[:, :, 1])
            dve.tensor_scalar(r.u_limit[:, :, 1], r.clamp[:, :, 1], -1.0, None, ALU.mult)
            dve.tensor_tensor(r.gates[:, :, :], r.gates[:, :, :], r.raw_act[:, :, 1].unsqueeze(1).broadcast_to([P, TILES, G]), ALU.mult)


def l3_experts(nc, m, r, w):
    G, GROUPS = L3_E + 1, 4
    UNITS = 2 * GROUPS
    LOOPS = L3_E // 2
    with ExitStack() as ctx:
        def sb(name, shape, dt=F32):
            return ctx.enter_context(nc.sbuf_tensor(f"l3e_{name}", shape, dt))

        sem = signals(nc, m, "l3e_")

        w1, w2 = sb("w1", [P, 2, 2 * L3_I]), sb("w2", [L3_I, 2, D])
        gate, sig, up_, te = (sb(x, [L3_I, GROUPS, BANK]) for x in ("gate", "sig", "up", "te"))
        limit = sb("limit", [P, 2, 2])
        prime = sb("prime", [P, 1])
        ps_g = ctx.enter_context(nc.psum_tensor("l3e_ps_g", [P, 2, BANK], F32))
        ps_u = ctx.enter_context(nc.psum_tensor("l3e_ps_u", [P, 2, BANK], F32))
        ps_d = ctx.enter_context(nc.psum_tensor("l3e_ps_d", [P, 2, BANK], F32))
        w1_in, w2_in = [sem("w1_in0"), sem("w1_in1")], [sem("w2_in0"), sem("w2_in1")]
        limit_in = sem("limit_in")
        g_ready, u_ready, g_clipped, u_out, u_clipped, sig_ready, t1_ready, te_ready, down_ready, down_free = (
            sem(k) for k in ("g_ready", "u_ready", "g_clipped", "u_out", "u_clipped", "sig_ready", "t1_ready", "te_ready",
                             "down_ready", "down_free"))
        block = ctx.enter_context(nc.Block())

        @block.sync
        def _(sp):
            def load(k, w1_src, w2_src, units):
                sp.wait_ge(u_ready, FROM + units)
                sp.dma_start(w1[:, k, :], w1_src).then_inc(w1_in[k], 16)
                sp.wait_ge(down_ready, FROM + units)
                sp.dma_start(w2[:, k, :], w2_src).then_inc(w2_in[k], 16)

            def expert(e):
                return (w["L3_ffn_expert_w1"][bass.ds(e, 1), :, :].rearrange("e p f -> p (e f)"),
                        w["L3_ffn_expert_w2"][bass.ds(e, 1), :, :].rearrange("e p f -> p (e f)"))

            load(0, *expert(0), 0)
            with sp.Fori(0, LOOPS - 1) as it:
                load(1, *expert(it * 2 + 1), it * UNITS)
                load(0, *expert(it * 2 + 2), it * UNITS + GROUPS)
            load(1, *expert(L3_E - 1), (LOOPS - 1) * UNITS)
            load(0, w["L3_ffn_shared_w1"], w["L3_ffn_shared_w2"], (LOOPS - 1) * UNITS + GROUPS)

        @block.tensor
        def _(pe):
            def up(it, u):
                k, g, n = (u // GROUPS) % 2, u % GROUPS, it * UNITS + u
                if g == 0:
                    pe.wait_ge(w1_in[k], (it + u // UNITS) * 16 + 16)
                if not (isinstance(n, int) and n < 2):
                    pe.wait_ge(g_clipped, n - 1)
                pe.matmul(ps_g[0:L3_I, u % 2, :], w1[:, k, 0::2], r.hT[:, g * BANK:(g + 1) * BANK], start=True, stop=True).then_inc(g_ready, 1)
                if not (isinstance(n, int) and n < 2):
                    pe.wait_ge(u_out, n - 1)
                pe.matmul(ps_u[0:L3_I, u % 2, :], w1[:, k, 1::2], r.hT[:, g * BANK:(g + 1) * BANK], start=True, stop=True).then_inc(u_ready, 1)

            def down(it, u):
                k, g, n = (u // GROUPS) % 2, u % GROUPS, it * UNITS + u
                if g == 0:
                    pe.wait_ge(w2_in[k], it * 16 + 16)
                pe.wait_ge(te_ready, n + 1)
                pe.wait_ge(down_free, n + 1)
                for t in range(4):
                    ins = pe.matmul(ps_d[:, u % 2, t * P:(t + 1) * P], te[:, g, t * P:(t + 1) * P], w2[:, k, :], start=True, stop=True)
                ins.then_inc(down_ready, 1)

            for signal in (u_ready, down_ready):
                pe.sem_inc(signal, FROM)
            for u in range(3):
                up(0, u)
            with pe.Fori(0, LOOPS) as it:
                for u in range(UNITS):
                    up(it, u + 3)
                    down(it, u)
            up(LOOPS, 3)
            for u in range(GROUPS):
                down(LOOPS, u)

        @block.scalar
        def _(act):
            def unit(it, u):
                g, n, e = u % GROUPS, it * UNITS + u, it * 2 + u // GROUPS
                act.wait_ge(u_ready, FROM + n + 1)
                act.nop(nofuse=True)
                if g == 0:
                    act.activation(limit[:, (u // GROUPS) % 2, :], r.u_limit[:, bass.ds(e, 1), :].rearrange("p a k -> p (a k)"),
                                   ACT.Copy).then_inc(limit_in, 1)
                act.activation(up_[:, g, :], ps_u[0:L3_I, u % 2, :], ACT.Identity, bias=r.u_bias[:, bass.ds(e, 1)]).then_inc(u_out, 1)
                act.wait_ge(g_clipped, n + 1)
                act.nop(nofuse=True)
                act.activation(sig[:, g, :], gate[:, g, :], ACT.Sigmoid, bias=r.ag_bias[:, bass.ds(e, 1)],
                               scale=r.raw_act[0:L3_I, bass.ds(e, 1), 0]).then_inc(sig_ready, 1)

            act.activation(prime[:, :], m.pid, ACT.Sigmoid)
            with act.Fori(0, LOOPS) as it:
                for u in range(UNITS):
                    unit(it, u)
            for u in range(GROUPS):
                unit(LOOPS, u)

        @block.gpsimd
        def _(pool):
            def unit(it, u):
                g, n, e = u % GROUPS, it * UNITS + u, it * 2 + u // GROUPS
                k = (u // GROUPS) % 2
                pool.wait_ge(limit_in, e + 1)
                pool.wait_ge(u_out, n + 1)
                pool.nop(nofuse=True)
                pool.tensor_scalar(up_[:, g, :], up_[:, g, :], limit[0:L3_I, k, 0:1], limit[0:L3_I, k, 1:2],
                                   ALU.min, ALU.max).then_inc(u_clipped, 1)

            with pool.Fori(0, LOOPS) as it:
                for u in range(UNITS):
                    unit(it, u)
            for u in range(GROUPS):
                unit(LOOPS, u)

        @block.vector
        def _(dve):
            def clip(it, u):
                g, n, e = u % GROUPS, it * UNITS + u, it * 2 + u // GROUPS
                dve.wait_ge(g_ready, n + 1)
                dve.tensor_scalar(gate[:, g, :], ps_g[0:L3_I, u % 2, :], r.g_high[:, bass.ds(e, 1)], r.g_low[:, bass.ds(e, 1)],
                                  ALU.min, ALU.max).then_inc(g_clipped, 1)

            def hidden(it, u):
                g, n, e = u % GROUPS, it * UNITS + u, it * 2 + u // GROUPS
                dve.wait_ge(sig_ready, n + 1)
                dve.scalar_tensor_tensor(sig[:, g, :], gate[:, g, :], r.g_bias[:, bass.ds(e, 1)], sig[:, g, :], ALU.add, ALU.mult)\
                   .then_inc(t1_ready, 1)
                dve.wait_ge(u_clipped, n + 1)
                dve.wait_ge(t1_ready, n + 1)
                dve.scalar_tensor_tensor(te[:, g, :], up_[:, g, :], r.raw_act[0:L3_I, bass.ds(e, 1), 2], sig[:, g, :],
                                         ALU.add, ALU.mult).then_inc(te_ready, 1)

            def add(it, u):
                g, n, e = u % GROUPS, it * UNITS + u, it * 2 + u // GROUPS
                dve.wait_ge(down_free, n + 1)
                dve.wait_ge(down_ready, FROM + n + 1)
                for t in range(4):
                    hh = m.h[:, 4 * g + t, :]
                    ins = dve.scalar_tensor_tensor(hh, ps_d[:, u % 2, t * P:(t + 1) * P], r.gates[:, 4 * g + t, bass.ds(e, 1)], hh,
                                                   ALU.mult, ALU.add)
                ins.then_inc(down_free, 1)

            dve.sem_inc(down_free, 2)
            clip(0, 0)
            clip(0, 1)
            hidden(0, 0)
            clip(0, 2)
            hidden(0, 1)
            with dve.Fori(0, LOOPS) as it:
                for u in range(UNITS):
                    clip(it, u + 3)
                    hidden(it, u + 2)
                    add(it, u)
            clip(LOOPS, 3)
            for u in range(GROUPS):
                if u + 2 < GROUPS:
                    hidden(LOOPS, u + 2)
                add(LOOPS, u)


def tower_memory(nc, m, ctx):
    def sb(name, shape, dt=F32):
        return ctx.enter_context(nc.sbuf_tensor(name, shape, dt))

    m.consts = sb("consts", [P, sum(CONST_COLS.values())])
    at, part = 0, {}
    for name, width in CONST_COLS.items():
        part[name] = m.consts[:, at:at + width]
        at += width
    m.ident, m.interp, m.pairmean, m.one, m.sel8 = (part[x] for x in ("ident", "interp", "pairmean", "one", "sel8"))
    m.ropecos, m.ropesin, m.expand, m.pid = (part[x] for x in ("ropecos", "ropesin", "expand", "pid"))
    m.lower8, m.lower16 = part["lower8"], part["lower16"]
    m.h, m.xn, m.xnT = sb("h", [P, TILES, D]), sb("xn", [P, TILES, D]), sb("xnT", [P, N])
    m.neghalf = sb("neghalf", [P, TILES])
    m.wqkv0, m.fc1T, m.fc2T = sb("wqkv0", [P, 3, D]), sb("fc1T", [P, 4, D]), sb("fc2T", [P, 4, 64])
    m.w1f, m.fc1_b, m.fc2_b = sb("w1f", [P, 512]), sb("fc1_b", [P, 4]), sb("fc2_b", [1, 64])
    m.wqkv2, m.wproj2, m.wqkv3, m.wo = sb("wqkv2", [P, 3, D]), sb("wproj2", [P, D]), sb("wqkv3", [P, 3, D]), sb("wo", [P, D])
    m.wrT = sb("wrT", [P, 8])
    m.w_attn, m.w_proj1 = sb("w_attn", [P, 3 * HD + RET_H]), sb("w_proj1", [P, 4, D])
    m.s_wattn = ctx.enter_context(nc.semaphore("s_wattn"))
    m.s_wproj1 = ctx.enter_context(nc.semaphore("s_wproj1"))


def l0_memory(nc, m, ctx):
    def sb(name, shape, dt=F32):
        return ctx.enter_context(nc.sbuf_tensor(name, shape, dt))

    m.ids, m.onehot, m.pairhot = sb("ids", [P, N], I32), sb("onehot", [VOC, N]), sb("pairhot", [VOC, N // 2])
    m.feat, m.tok_w1, m.tok_w2 = sb("feat", [VOC, 37]), sb("tok_w1", [37, 64]), sb("tok_w2", [64, D])
    m.tok_b1, m.tok_b2 = sb("tok_b1", [64, 1]), sb("tok_b2", [1, D])
    m.bq, m.bk, m.bv = sb("bq", [P, 1]), sb("bk", [P, 1]), sb("bv", [1, D])
    m.table_x, m.table_tx = sb("table_x", [VOC, B, D]), sb("table_tx", [VOC, B, D])


def stage_l0(nc, m, w):
    stage_l0_tables(nc, m, w)
    stage_l0_ffn(nc, m, w)


def tower(nc, w, out, l0=stage_l0, stages=(stage_l1_attn, stage_l1_ffn, recycle, stage_l2_attn, stage_l2_ffn, recycle,
                                           stage_l3_attn, stage_l3_ffn)):
    with ExitStack() as ctx:
        m = Core()
        m.signals = []
        tower_memory(nc, m, ctx)
        m.later_loads = [
            (m.w_attn[:, :], w["L1_attn_w_attn"], m.s_wattn),
            (m.w_proj1[:, :, :], w["L1_attn_w_proj"].rearrange("(c p) d -> p c d", p=P), m.s_wproj1),
        ]
        with ExitStack() as l0_ctx:
            l0_memory(nc, m, l0_ctx)
            with nc.Block() as block:
                @block.gpsimd
                def _(pool):
                    pool.memset(m.neghalf[:, :], -0.5)
            load_stage(nc, m, w)
            l0(nc, m, w)
        for stage in stages:
            stage(nc, m, w)
        with nc.semaphore("stored") as stored, nc.Block() as block:
            @block.sync
            def _(sp):
                sp.dma_start(out.rearrange("b (t p) d -> p (b t) d", p=P), m.h[:, :, :]).then_inc(stored, 16)
                sp.wait_ge(stored, 16)


def kernel(**inputs):
    import concourse.bacc as _bacc
    from concourse.bass_utils import run_bass_kernel_spmd as _run

    nc = _bacc.Bacc("TRN2", target_bir_lowering=False, num_devices=1)
    arrays, w = {}, {}
    for name, value in list(inputs.items()) + [("consts", constants()), ("move", move_heads())]:
        a = np.ascontiguousarray(value)
        arrays[f"in_{name}_dram"] = a
        w[name] = nc.dram_tensor(f"in_{name}_dram", a.shape, mybir.dt.from_np(a.dtype), kind="ExternalInput").ap()
    out = nc.dram_tensor("out_0_dram", (B, S, D), F32, kind="ExternalOutput").ap()
    tower(nc, w, out)
    r = _run(nc, [arrays], core_ids=[0])
    return r.results[0]["out_0_dram"]
```

```python
from contextlib import ExitStack

import numpy as np

import concourse.bass as bass
from concourse import mybir

F32 = mybir.dt.float32
I32 = mybir.dt.int32
ACT = mybir.ActivationFunctionType
ALU = mybir.AluOpType
AX = mybir.AxisListType

P = 128
D = 128
B = 2
S = 1024
N = B * S
TILES = N // P
CH = S // P
VOC = 121
EPS = 1e-5
BANK = 512
BIG = 1.0e30
FROM = 1


def signals(nc, m, prefix):
    def sem(name):
        m.signals.append(nc.alloc_semaphore(prefix + name))
        return m.signals[-1]

    return sem


def recycle(nc, m, w):
    nc.clear_and_free_semaphores(m.signals)
    m.signals = []
    nc.all_engine_barrier()


class Core:
    pass


def row(ap1d):
    return ap1d.rearrange("(a d) -> a d", a=1)


def col(ap1d):
    return ap1d.rearrange("(d a) -> d a", a=1)


RET_H, RET_D = 8, 64
CONST_COLS = {"ident": 128, "interp": 128, "pairmean": 128, "one": 128, "sel8": 8 * 128, "ropecos": S, "ropesin": S,
              "expand": 256, "pid": 1, "quarter": 4, "lower8": 64, "lower16": 256}


def constants():
    out = {}
    out["ident"] = np.eye(P, dtype=np.float32)
    half, pos = D // 2, np.linspace(0.0, 1.0, D, dtype=np.float32) * np.float32(D // 2 - 1)
    i0 = np.clip(np.floor(pos).astype(np.int32), 0, half - 2)
    w = pos - i0.astype(np.float32)
    up = np.zeros((D, half), np.float32)
    up[np.arange(D), i0] += 1.0 - w
    up[np.arange(D), i0 + 1] += w
    out["interp"] = np.repeat(up, 2, axis=1) * np.float32(0.5)
    pair = np.arange(D) // 2
    out["pairmean"] = np.where(pair[:, None] == pair[None, :], np.float32(-0.25), np.float32(0)).astype(np.float32)
    out["one"] = np.ones((P, P), np.float32)
    sel = np.zeros((P, 8, P), np.float32)
    for h in range(8):
        sel[h, h, :] = 1.0
    out["sel8"] = sel.reshape(P, -1)
    div = np.float32(2.0 * np.pi) / np.power(np.float32(S), np.arange(0, RET_D, 2, dtype=np.float32) / np.float32(RET_D))
    ang = np.arange(S, dtype=np.float32)[:, None] * div[None, :].astype(np.float32)
    freq = (np.arange(P) % RET_D) // 2
    out["ropecos"] = np.cos(ang).T[freq].astype(np.float32)
    out["ropesin"] = np.sin(ang).T[freq].astype(np.float32)
    tok = np.arange(2 * P).reshape(1, 2, P)
    out["expand"] = (np.arange(P).reshape(P, 1, 1) == tok // 2).astype(np.float32).reshape(P, 256)
    out["pid"] = np.arange(P, dtype=np.float32)[:, None]
    out["quarter"] = (np.arange(P)[:, None] // 32 == np.arange(4)[None, :]).astype(np.float32)
    for e in (8, 16):
        low = (np.arange(e)[:, None] > np.arange(e)[None, :]).astype(np.float32)
        out[f"lower{e}"] = np.broadcast_to(low.reshape(1, -1), (P, e * e))
    return np.ascontiguousarray(np.concatenate([out[k] for k in CONST_COLS], axis=1), dtype=np.float32)


def layernorm(nc, m, name, src, dst, dstT, gain=None, shift=None):
    with ExitStack() as ctx:
        stats = ctx.enter_context(nc.sbuf_tensor(f"{name}_stats", [P, TILES, 6], F32))
        small = ctx.enter_context(nc.sbuf_tensor(f"{name}_small", [P, 8, TILES], F32))
        ps = ctx.enter_context(nc.psum_tensor(f"{name}_ps", [P, 4, BANK], F32))
        sem = signals(nc, m, f"{name}_")
        chain, var_ready, pool_step, normed, turned = (sem(x) for x in ("chain", "var_ready", "pool_step", "normed", "turned"))
        mean, rstd = small[:, 0, :], small[:, 1, :]
        diff, sumsq, var = small[:, 2, :], small[:, 3, :], small[:, 4, :]
        block = ctx.enter_context(nc.Block())

        @block.vector
        def _(dve):
            for t in range(TILES):
                ins = dve.bn_stats(stats[:, t, :], src[:, t, :])
            ins.then_inc(chain, 1)
            dve.wait_ge(chain, 1)
            dve.tensor_tensor(diff, stats[:, :, 1], stats[:, :, 4], ALU.subtract)
            dve.tensor_tensor(sumsq, stats[:, :, 2], stats[:, :, 5], ALU.add)
            dve.tensor_tensor(mean, stats[:, :, 1], stats[:, :, 4], ALU.add).then_inc(chain, 1)
            dve.wait_ge(chain, 2)
            dve.tensor_scalar(mean, mean, 0.5, None, ALU.mult)
            dve.scalar_tensor_tensor(diff, diff, 0.25, diff, ALU.mult, ALU.mult).then_inc(chain, 1)
            dve.wait_ge(chain, 3)
            dve.scalar_tensor_tensor(var, sumsq, 1.0 / D, diff, ALU.mult, ALU.add).then_inc(var_ready, 1)
            dve.wait_ge(pool_step, 2)
            for t in range(TILES):
                dve.tensor_scalar(dst[:, t, :], src[:, t, :], mean[:, t:t + 1], rstd[:, t:t + 1],
                                  ALU.subtract, ALU.mult).then_inc(normed, 1)

        @block.gpsimd
        def _(pool):
            pool.wait_ge(var_ready, 1)
            pool.tensor_scalar(var, var, EPS, None, ALU.add).then_inc(pool_step, 1)
            pool.wait_ge(pool_step, 1)
            pool.tensor_tensor(rstd, var, m.neghalf[:, :], ALU.pow).then_inc(pool_step, 1)

        if dstT is None:
            return

        @block.tensor
        def _(pe):
            for t in range(TILES):
                pe.wait_ge(normed, t + 1)
                ins = pe.transpose(ps[:, t // 4, (t % 4) * P:(t % 4 + 1) * P], dst[:, t, :], m.ident)
                if t % 4 == 3:
                    ins.then_inc(turned, 1)

        @block.scalar
        def _(act):
            for g in range(TILES // 4):
                act.wait_ge(turned, g + 1)
                out = dstT[:, g * BANK:(g + 1) * BANK]
                if gain is None:
                    act.activation(out, ps[:, g, :], ACT.Copy)
                else:
                    act.activation(out, ps[:, g, :], ACT.Identity, bias=shift, scale=gain)


def load_stage(nc, m, w):
    with ExitStack() as ctx:
        def raw(name, shape, dt=F32):
            return ctx.enter_context(nc.sbuf_tensor(f"raw_{name}", shape, dt))

        sem = signals(nc, m, "")

        raw_qkv0 = raw("qkv0", [P, 3, D])
        raw_fc1 = raw("fc1", [P, 4, D])
        raw_fc2 = raw("fc2", [64, 512])
        raw_qkv2 = raw("qkv2", [P, 3, D])
        raw_proj2 = raw("proj2", [P, D])
        raw_qkvw = raw("qkvw", [P, 3, D])
        raw_wo = raw("wo", [P, D])
        raw_wr = raw("wr", [8, D])
        ps = ctx.enter_context(nc.psum_tensor("turn_ps", [P, 8, BANK], F32))
        w_first, w_turn = sem("w_first"), sem("w_turn")
        turned, copied = sem("w_turned"), sem("w_copied")
        sp_loads = [
            (m.consts[:, :], w["consts"]),
            (m.ids[:, :], w["x"].rearrange("(o b) n -> o (b n)", o=1).broadcast_to([P, N])),
            (raw_qkv0[:, 0, :], w["L0_attn_Wq"]), (raw_qkv0[:, 1, :], w["L0_attn_Wk"]), (raw_qkv0[:, 2, :], w["L0_attn_Wv"]),
            (m.feat[:, :], w["L0_tok_feature_table"]), (m.tok_w1[:, :], w["L0_tok_W1"]), (m.tok_w2[:, :], w["L0_tok_W2"]),
            (m.tok_b1[:, :], col(w["L0_tok_b1"])), (m.tok_b2[:, :], row(w["L0_tok_b2"])),
            (m.bq[:, :], col(w["L0_attn_bq"])), (m.bk[:, :], col(w["L0_attn_bk"])), (m.bv[:, :], row(w["L0_attn_bv"])),
            (raw_fc1[:, :, :], w["L0_ffn_fc1_w"].rearrange("(c p) d -> p c d", p=P)),
            (raw_fc2[:, :], w["L0_ffn_fc2_w"]),
            (m.fc1_b[:, :], w["L0_ffn_fc1_b"].rearrange("(c p) -> p c", p=P)),
            (m.fc2_b[:, :], row(w["L0_ffn_fc2_b"])),
        ]
        act_loads = [
            (raw_qkv2[:, :, :], w["L2_attn_w_qkv"].rearrange("(c p) d -> p c d", p=P)),
            (raw_proj2[:, :], w["L2_attn_w_proj"]),
            (raw_qkvw[:, :, :], w["L2_ffn_qkv_w"].rearrange("(c p) d -> p c d", p=P)),
            (raw_wo[:, :], w["L2_ffn_wo_w"]),
            (raw_wr[:, :], w["L1_ffn_w_r"]),
        ]
        m.n_first = 16 * len(sp_loads)
        jobs = [(raw_qkv0[:, c, :], m.wqkv0[:, c, :]) for c in range(3)]
        jobs += [(raw_fc1[:, c, :], m.fc1T[:, c, :]) for c in range(4)]
        jobs += [(raw_fc2[:, c * P:(c + 1) * P], m.fc2T[:, c, :]) for c in range(4)]
        n_early = len(jobs)
        jobs += [(raw_qkv2[:, c, :], m.wqkv2[:, c, :]) for c in range(3)]
        jobs += [(raw_proj2[:, :], m.wproj2[:, :])]
        jobs += [(raw_qkvw[:, c, :], m.wqkv3[:, c, :]) for c in range(3)]
        jobs += [(raw_wo[:, :], m.wo[:, :])]
        jobs += [(raw_wr[:, :], m.wrT[:, :])]
        block = ctx.enter_context(nc.Block())

        @block.sync
        def _(sp):
            for dst, src in sp_loads:
                sp.dma_start(dst, src, allow_slow_non_contiguous=True).then_inc(w_first, 16)
            for dst, src, s in m.later_loads:
                sp.dma_start(dst, src, allow_slow_non_contiguous=True).then_inc(s, 16)

        @block.scalar
        def _(act):
            for dst, src in act_loads:
                act.dma_start(dst, src, allow_slow_non_contiguous=True).then_inc(w_turn, 16)
            for i, (_, dst) in enumerate(jobs):
                act.wait_ge(turned, i + 1)
                r, c = dst.shape
                act.activation(dst, ps[0:r, i % 8, 0:c], ACT.Copy).then_inc(copied, 1)

        @block.tensor
        def _(pe):
            pe.wait_ge(w_first, 16 * len(sp_loads))
            for i, (src, dst) in enumerate(jobs):
                if i == n_early:
                    pe.wait_ge(w_turn, 16 * len(act_loads))
                if i >= 8:
                    pe.wait_ge(copied, i - 7)
                r, c = dst.shape
                pe.transpose(ps[0:r, i % 8, 0:c], src, m.ident[0:c, 0:c]).then_inc(turned, 1)


def stage_l0_tables(nc, m, w):
    with ExitStack() as ctx:
        def sb(name, shape, dt=F32):
            return ctx.enter_context(nc.sbuf_tensor(f"l0_{name}", shape, dt))

        sem = signals(nc, m, "l0_")

        featT, hid = sb("featT", [37, VOC]), sb("hid", [64, VOC])
        gelu, emb, emb_n = sb("gelu", [VOC, D]), sb("emb", [VOC, D]), sb("emb_n", [VOC, D])
        emb_nT = sb("emb_nT", [P, VOC])
        qT, kT, v = sb("qT", [P, VOC]), sb("kT", [P, VOC]), sb("v", [VOC, D + 1])
        vw = sb("vw", [VOC, B, D + 1])
        count, absent, diag = sb("count", [VOC, B]), sb("absent", [VOC, B]), sb("diag", [VOC, B, VOC])
        mx, nmx = sb("mx", [VOC, B]), sb("nmx", [VOC, B])
        prob, probT = sb("prob", [VOC, B, VOC]), sb("probT", [VOC, B, VOC])
        rden = sb("rden", [VOC, B])
        h1 = sb("h1", [VOC, B, D])
        stats, small = sb("stats", [VOC, 3, 6]), sb("small", [VOC, 3, 8])
        ps_a = ctx.enter_context(nc.psum_tensor("l0_ps_a", [P, BANK], F32))
        ps_e = ctx.enter_context(nc.psum_tensor("l0_ps_e", [P, BANK], F32))
        ps_q = ctx.enter_context(nc.psum_tensor("l0_ps_q", [P, BANK], F32))
        ps_k = ctx.enter_context(nc.psum_tensor("l0_ps_k", [P, BANK], F32))
        ps_v = ctx.enter_context(nc.psum_tensor("l0_ps_v", [P, BANK], F32))
        ps_s = ctx.enter_context(nc.psum_tensor("l0_ps_s", [P, BANK], F32))
        ps_f = ctx.enter_context(nc.psum_tensor("l0_ps_f", [P, BANK], F32))
        pe_step, act_step, dve_step, pool_step, special = (sem(x) for x in ("pe", "act", "dve", "pool", "special"))
        v_ones = sem("v_ones")
        SC = float(D) ** -0.5
        block = ctx.enter_context(nc.Block())

        @block.tensor
        def _(pe):
            pe.transpose(ps_a[0:37, 0:VOC], m.feat[:, :], m.ident[0:VOC, 0:VOC]).then_inc(pe_step, 1)
            pe.matmul(ps_f[:, :], m.interp, m.fc1T[:, :, :].rearrange("p c d -> p (c d)"), start=True, stop=True).then_inc(pe_step, 1)
            pe.wait_ge(act_step, 1)
            pe.matmul(ps_e[0:64, 0:VOC], m.tok_w1[:, :], featT[:, :], start=True, stop=True).then_inc(pe_step, 1)
            pe.wait_ge(act_step, 3)
            pe.matmul(ps_a[0:VOC, 0:D], hid[:, :], m.tok_w2[:, :], start=True, stop=False)
            pe.matmul(ps_a[0:VOC, 0:D], m.one[0:1, 0:VOC], m.tok_b2[:, :], start=False, stop=True).then_inc(pe_step, 1)
            pe.wait_ge(dve_step, 9)
            pe.transpose(ps_e[:, 0:VOC], emb_n[:, :], m.ident[0:VOC, 0:VOC]).then_inc(pe_step, 1)
            pe.wait_ge(act_step, 5)
            pe.matmul(ps_q[:, 0:VOC], m.wqkv0[:, 0, :], emb_nT[:, :], start=True, stop=True).then_inc(pe_step, 1)
            pe.matmul(ps_k[:, 0:VOC], m.wqkv0[:, 1, :], emb_nT[:, :], start=True, stop=True).then_inc(pe_step, 1)
            pe.matmul(ps_v[0:VOC, 0:D], emb_nT[:, :], m.wqkv0[:, 2, :], start=True, stop=False)
            pe.matmul(ps_v[0:VOC, 0:D], m.one[0:1, 0:VOC], m.bv[:, :], start=False, stop=True).then_inc(pe_step, 1)
            pe.wait_ge(act_step, 7)
            pe.wait_ge(dve_step, 12)
            for b in range(B):
                pe.matmul(ps_s[0:VOC, b * VOC:(b + 1) * VOC], qT[:, :], kT[:, :], start=True, stop=False)
                pe.matmul(ps_s[0:VOC, b * VOC:(b + 1) * VOC], m.one[0:VOC, 0:VOC], diag[:, b, :],
                          start=False, stop=True).then_inc(pe_step, 1)
            for b in range(B):
                pe.wait_ge(act_step, 8 + b)
                pe.transpose(ps_f[0:VOC, b * VOC:(b + 1) * VOC], prob[:, b, :], m.ident[0:VOC, 0:VOC]).then_inc(pe_step, 1)
            pe.wait_ge(act_step, 10)
            pe.wait_ge(dve_step, 16)
            for b in range(B):
                pe.matmul(ps_a[0:VOC, b * 256:b * 256 + D + 1], probT[:, b, :], vw[:, b, :], start=True, stop=True).then_inc(pe_step, 1)

        @block.scalar
        def _(act):
            act.wait_ge(pe_step, 1)
            act.activation(featT[:, :], ps_a[0:37, 0:VOC], ACT.Copy).then_inc(act_step, 1)
            act.wait_ge(pe_step, 2)
            act.activation(m.w1f[:, :], ps_f[:, :], ACT.Copy).then_inc(act_step, 1)
            act.wait_ge(pe_step, 3)
            act.activation(hid[:, :], ps_e[0:64, 0:VOC], ACT.Relu, bias=m.tok_b1[:, 0:1]).then_inc(act_step, 1)
            act.wait_ge(pe_step, 4)
            act.activation(gelu[:, :], ps_a[0:VOC, 0:D], ACT.Gelu_apprx_tanh).then_inc(act_step, 1)
            act.wait_ge(pe_step, 5)
            act.activation(emb_nT[:, :], ps_e[:, 0:VOC], ACT.Copy).then_inc(act_step, 1)
            act.wait_ge(pe_step, 6)
            act.activation(qT[:, :], ps_q[:, 0:VOC], ACT.Identity, bias=m.bq[:, 0:1]).then_inc(act_step, 1)
            act.wait_ge(pe_step, 7)
            act.activation(kT[:, :], ps_k[:, 0:VOC], ACT.Identity, bias=m.bk[:, 0:1]).then_inc(act_step, 1)
            act.wait_ge(dve_step, 14)
            for b in range(B):
                act.activation(prob[:, b, :], ps_s[0:VOC, b * VOC:(b + 1) * VOC], ACT.Exp, bias=nmx[:, b:b + 1],
                               scale=SC).then_inc(act_step, 1)
            act.wait_ge(pe_step, 12)
            act.activation(probT[:, :, :].rearrange("p b v -> p (b v)"), ps_f[0:VOC, 0:B * VOC], ACT.Copy).then_inc(act_step, 1)

        @block.sync
        def _(sp):
            sp.wait_ge(dve_step, 1)
            sp.dma_start(emb[0:1, :], w["L0_tok_special_embed"][0:1, :]).then_inc(special, 16)
            sp.dma_start(emb[107:110, :], w["L0_tok_special_embed"][1:4, :]).then_inc(special, 16)

        @block.gpsimd
        def _(pool):
            pool.tensor_scalar(m.onehot[:, :], m.ids[0:VOC, :], m.pid[0:VOC, :], None, ALU.is_equal).then_inc(pool_step, 1)
            pool.wait_ge(pool_step, 1)
            pairs = m.onehot[:, :].rearrange("p (n two) -> p n two", two=2)
            pool.tensor_tensor(m.pairhot[:, :], pairs[:, :, 0], pairs[:, :, 1], ALU.add).then_inc(pool_step, 1)
            pool.wait_ge(dve_step, 6)
            pool.tensor_scalar(small[:, 0, 4:5], small[:, 0, 4:5], EPS, None, ALU.add).then_inc(pool_step, 1)
            pool.wait_ge(pool_step, 3)
            pool.tensor_tensor(small[:, 0, 1:2], small[:, 0, 4:5], m.neghalf[0:VOC, 0:1], ALU.pow).then_inc(pool_step, 1)
            for b in range(B):
                pool.wait_ge(dve_step, 23 + 11 * b)
                pool.tensor_scalar(small[:, 1 + b, 4:5], small[:, 1 + b, 4:5], EPS, None, ALU.add).then_inc(pool_step, 1)
                pool.wait_ge(pool_step, 5 + 2 * b)
                pool.tensor_tensor(small[:, 1 + b, 1:2], small[:, 1 + b, 4:5], m.neghalf[0:VOC, 0:1], ALU.pow).then_inc(pool_step, 1)

        @block.vector
        def _(dve):
            steps = [0]

            def link(ins):
                steps[0] += 1
                ins.then_inc(dve_step, 1)
                dve.wait_ge(dve_step, steps[0])

            def moments(src, k):
                s = small[:, k, :]
                link(dve.bn_stats(stats[:, k, :], src))
                link(dve.tensor_tensor(s[:, 2:3], stats[:, k, 1:2], stats[:, k, 4:5], ALU.subtract))
                link(dve.tensor_tensor(s[:, 3:4], stats[:, k, 2:3], stats[:, k, 5:6], ALU.add))
                link(dve.scalar_tensor_tensor(s[:, 2:3], s[:, 2:3], 0.25, s[:, 2:3], ALU.mult, ALU.mult))
                link(dve.scalar_tensor_tensor(s[:, 4:5], s[:, 3:4], 1.0 / D, s[:, 2:3], ALU.mult, ALU.add))
                link(dve.tensor_tensor(s[:, 0:1], stats[:, k, 1:2], stats[:, k, 4:5], ALU.add))
                link(dve.tensor_scalar(s[:, 0:1], s[:, 0:1], 0.5, None, ALU.mult))

            dve.wait_ge(act_step, 4)
            link(dve.tensor_scalar(emb[:, :], gelu[:, :], float(D) ** 0.5, None, ALU.mult))
            dve.wait_ge(special, 32)
            moments(emb[:, :], 0)
            dve.wait_ge(pool_step, 4)
            link(dve.tensor_scalar(emb_n[:, :], emb[:, :], small[:, 0, 0:1], small[:, 0, 1:2], ALU.subtract, ALU.mult))
            dve.wait_ge(pool_step, 2)
            link(dve.tensor_reduce(count[:, :], m.onehot[:, :].rearrange("p (b n) -> p b n", b=B), AX.X, ALU.add))
            link(dve.tensor_scalar(absent[:, :], count[:, :], 0.0, -BIG, ALU.is_equal, ALU.mult))
            for b in range(B):
                ins = dve.tensor_scalar(diag[:, b, :], m.ident[0:VOC, 0:VOC], absent[:, b:b + 1], None, ALU.mult)
            link(ins)
            dve.wait_ge(pe_step, 10)
            link(dve.tensor_reduce(mx[:, :], ps_s[0:VOC, 0:B * VOC].rearrange("p (b v) -> p b v", b=B), AX.X, ALU.max))
            link(dve.tensor_scalar(nmx[:, :], mx[:, :], -SC, None, ALU.mult))
            dve.memset(v[:, D:D + 1], 1.0).then_inc(v_ones, 1)
            link(dve.tensor_copy(v[:, 0:D], ps_v[0:VOC, 0:D]))
            dve.wait_ge(v_ones, 1)
            for b in range(B):
                ins = dve.tensor_scalar(vw[:, b, :], v[:, :], count[:, b:b + 1], None, ALU.mult)
            link(ins)
            for b in range(B):
                att = ps_a[0:VOC, b * 256:b * 256 + D + 1]
                dve.wait_ge(pe_step, 14)
                link(dve.reciprocal(rden[:, b:b + 1], att[:, D:D + 1]))
                link(dve.scalar_tensor_tensor(h1[:, b, :], att[:, 0:D], rden[:, b:b + 1], emb[:, :], ALU.mult, ALU.add))
                moments(h1[:, b, :], 1 + b)
                dve.wait_ge(pool_step, 6 + 2 * b)
                link(dve.tensor_scalar(m.table_x[:, b, :], h1[:, b, :], small[:, 1 + b, 0:1], small[:, 1 + b, 1:2],
                                       ALU.subtract, ALU.mult))
                link(dve.tensor_tensor(m.table_tx[:, b, :], h1[:, b, :], m.table_x[:, b, :], ALU.add))


def stage_l0_ffn(nc, m, w):
    NP = N // 2
    with ExitStack() as ctx:
        def sb(name, shape, dt=F32):
            return ctx.enter_context(nc.sbuf_tensor(f"l0f_{name}", shape, dt))

        sem = signals(nc, m, "l0f_")

        sT, hid = sb("sT", [P, NP]), sb("hid", [P, 4, NP])
        change = sb("change", [P, NP // P, D])
        fc2_bd = sb("fc2_bd", [1, D])
        fc2_wd = sb("fc2_wd", [P, 4, D])
        ps_s = ctx.enter_context(nc.psum_tensor("l0f_ps_s", [P, 2, BANK], F32))
        ps_h = ctx.enter_context(nc.psum_tensor("l0f_ps_h", [P, 2, BANK], F32))
        ps_c = ctx.enter_context(nc.psum_tensor("l0f_ps_c", [P, 2, BANK], F32))
        ps_o = ctx.enter_context(nc.psum_tensor("l0f_ps_o", [P, 2, BANK], F32))
        pairs_summed, pairs_copied = sem("pairs_summed"), sem("pairs_copied")
        hid_ready, hid_done, out_ready, out_done, dup = (sem(x) for x in ("hid_ready", "hid_done", "out_ready", "out_done", "dup"))
        change_ready, change_done = sem("change_ready"), sem("change_done")
        block = ctx.enter_context(nc.Block())

        @block.tensor
        def _(pe):
            for b in range(B):
                pe.matmul(ps_s[:, b, :], m.table_x[:, b, :], m.pairhot[:, b * BANK:(b + 1) * BANK], start=True,
                          stop=True).then_inc(pairs_summed, 1)
            for i in range(8):
                b, c = i // 4, i % 4
                pe.wait_ge(pairs_copied, b + 1)
                if i >= 2:
                    pe.wait_ge(hid_done, i - 1)
                pe.matmul(ps_h[:, i % 2, :], m.w1f[:, c * P:(c + 1) * P], sT[:, b * BANK:(b + 1) * BANK], start=True,
                          stop=True).then_inc(hid_ready, 1)
            pe.wait_ge(dup, 2)
            pe.wait_ge(hid_done, 8)
            for j in range(NP // P):
                if j >= 2:
                    pe.wait_ge(change_done, j - 1)
                out = ps_c[:, j % 2, 0:D]
                pe.matmul(out, sT[:, j * P:(j + 1) * P], m.pairmean, start=True, stop=False)
                pe.matmul(out, m.one[0:1, :], fc2_bd[:, :], start=False, stop=False)
                for c in range(4):
                    ins = pe.matmul(out, hid[:, c, j * P:(j + 1) * P], fc2_wd[:, c, :], start=False, stop=(c == 3))
                ins.then_inc(change_ready, 1)
            for t in range(TILES):
                b, g, j = t // CH, t // 4, t // 2
                pe.wait_ge(change_done, j + 1)
                if t % 4 == 0 and g >= 2:
                    pe.wait_ge(out_done, g - 1)
                out = ps_o[:, g % 2, (t % 4) * P:(t % 4 + 1) * P]
                pe.matmul(out, m.onehot[:, t * P:(t + 1) * P], m.table_tx[:, b, :], start=True, stop=False)
                ins = pe.matmul(out, m.expand[:, (t % 2) * P:(t % 2 + 1) * P], change[:, j, :], start=False, stop=True)
                if t % 4 == 3:
                    ins.then_inc(out_ready, 1)

        @block.scalar
        def _(act):
            for b in range(B):
                act.wait_ge(pairs_summed, b + 1)
                act.activation(sT[:, b * BANK:(b + 1) * BANK], ps_s[:, b, :], ACT.Copy).then_inc(pairs_copied, 1)
            for i in range(8):
                b, c = i // 4, i % 4
                act.wait_ge(hid_ready, i + 1)
                act.activation(hid[:, c, b * BANK:(b + 1) * BANK], ps_h[:, i % 2, :], ACT.Gelu,
                               bias=m.fc1_b[:, c:c + 1]).then_inc(hid_done, 1)

        @block.vector
        def _(dve):
            wd = fc2_wd[:, :, :].rearrange("p c (d two) -> p (c d) two", two=2)
            dve.tensor_scalar(wd, m.fc2T[:, :, :].rearrange("p c d -> p (c d)").unsqueeze(2).broadcast_to([P, 256, 2]),
                              0.5, None, ALU.mult).then_inc(dup, 1)
            dve.tensor_scalar(fc2_bd[:, :].rearrange("p (d two) -> p d two", two=2),
                              m.fc2_b[:, :].unsqueeze(2).broadcast_to([1, 64, 2]), 0.5, None, ALU.mult).then_inc(dup, 1)
            for j in range(NP // P):
                dve.wait_ge(change_ready, j + 1)
                dve.tensor_copy(change[:, j, :], ps_c[:, j % 2, 0:D]).then_inc(change_done, 1)
            for g in range(TILES // 4):
                dve.wait_ge(out_ready, g + 1)
                dve.tensor_copy(m.h[:, 4 * g:4 * g + 4, :], ps_o[:, g % 2, :].rearrange("p (t d) -> p t d", t=4)).then_inc(out_done, 1)


GATE_BIAS = 6.906768
HD = RET_H * RET_D
WIDE_PER_HEAD = 9


def stage_l1_attn(nc, m, w):
    layernorm(nc, m, "ln_l1a", m.h, m.xn, m.xnT)
    with ExitStack() as ctx:
        def sb(name, shape, dt=F32):
            return ctx.enter_context(nc.sbuf_tensor(f"l1_{name}", shape, dt))

        r = Core()
        r.LT = sb("LT", [P, N])
        r.Lcol = sb("Lcol", [P, TILES, RET_H])
        r.Lfirst = sb("Lfirst", [P, TILES, RET_H])
        r.fade = sb("fade", [P, TILES, RET_H])
        r.keyfade = sb("keyfade", [P, B, CH, CH, RET_H])
        r.v = sb("v", [P, TILES, RET_H, RET_D + 1])
        r.wswap = sb("wswap", [P, 2 * HD])
        l1_gates(nc, m, r)
        l1_heads(nc, m, r)


def l1_gates(nc, m, r):
    with ExitStack() as ctx:
        def sb(name, shape, dt=F32):
            return ctx.enter_context(nc.sbuf_tensor(f"l1g_{name}", shape, dt))

        sem = signals(nc, m, "l1g_")

        x, u, w1, lw = (sb(k, [P, TILES * RET_H]) for k in ("x", "u", "w1", "lw"))
        gap = sb("gap", [P, TILES, RET_H])
        ps_g = ctx.enter_context(nc.psum_tensor("l1g_ps_g", [P, 4, BANK], F32))
        ps_v = ctx.enter_context(nc.psum_tensor("l1g_ps_v", [P, 2, BANK], F32))
        ps_l = ctx.enter_context(nc.psum_tensor("l1g_ps_l", [P, 2, BANK], F32))
        gates_ready, dve_step, act_step, pe_step = sem("gates_ready"), sem("dve_step"), sem("act_step"), sem("pe_step")
        v_ready, v_done, v_ones = sem("v_ready"), sem("v_done"), sem("v_ones")
        swapped = sem("swapped")
        block = ctx.enter_context(nc.Block())

        @block.tensor
        def _(pe):
            pe.wait_ge(m.s_wattn, 16)
            for t in range(TILES):
                ins = pe.matmul(ps_l[:, 1, t * RET_H:(t + 1) * RET_H], m.xnT[:, t * P:(t + 1) * P],
                                m.w_attn[:, 3 * HD:3 * HD + RET_H], start=True, stop=True)
            ins.then_inc(gates_ready, 1)
            for t in range(TILES):
                if t >= 2:
                    pe.wait_ge(v_done, t - 1)
                pe.matmul(ps_v[:, t % 2, :], m.xnT[:, t * P:(t + 1) * P], m.w_attn[:, 2 * HD:3 * HD], start=True,
                          stop=True).then_inc(v_ready, 1)
            pe.wait_ge(dve_step, 8)
            for t in range(TILES):
                ins = pe.transpose(ps_g[0:RET_H, t // 4, (t % 4) * P:(t % 4 + 1) * P], x[:, t * RET_H:(t + 1) * RET_H], m.ident)
            ins.then_inc(gates_ready, 1)
            pe.wait_ge(dve_step, 9)
            for t in range(TILES):
                ins = pe.transpose(ps_l[:, 0, t * RET_H:(t + 1) * RET_H], r.LT[0:RET_H, t * P:(t + 1) * P], m.ident[0:RET_H, 0:RET_H])
            ins.then_inc(pe_step, 1)
            pe.wait_ge(dve_step, 10)
            pe.matmul(ps_l[:, 1, 0:TILES * RET_H], m.one[0:1, :], r.Lcol[0:1, :, :].rearrange("p t h -> p (t h)"),
                      start=True, stop=True).then_inc(pe_step, 1)

        @block.gpsimd
        def _(pool):
            pool.memset(r.v[:, :, :, RET_D:RET_D + 1], 1.0)
            pool.memset(r.LT[:, :], 0.0).then_inc(v_ones, 1)
            pool.wait_ge(m.s_wattn, 16)
            pairs = m.w_attn[:, 0:2 * HD].rearrange("p (c two) -> p c two", two=2)
            swap = r.wswap[:, :].rearrange("p (c two) -> p c two", two=2)
            pool.tensor_scalar(swap[:, :, 0], pairs[:, :, 1], -1.0, None, ALU.mult).then_inc(swapped, 1)
            pool.tensor_copy(swap[:, :, 1], pairs[:, :, 0]).then_inc(swapped, 1)

        @block.scalar
        def _(act):
            act.wait_ge(dve_step, 2)
            act.activation(u[:, :], w1[:, :], ACT.Exp, scale=-1.0).then_inc(act_step, 1)
            act.wait_ge(dve_step, 3)
            act.activation(lw[:, :], w1[:, :], ACT.Ln).then_inc(act_step, 1)
            for t in range(TILES):
                act.wait_ge(v_ready, t + 1)
                act.activation(r.v[:, t, :, 0:RET_D], ps_v[:, t % 2, :].rearrange("p (h d) -> p h d", h=RET_H), ACT.Copy)\
                   .then_inc(v_done, 1)
            act.wait_ge(dve_step, 12)
            act.activation(r.fade[:, :, :], gap[:, :, :], ACT.Exp).then_inc(act_step, 1)
            act.wait_ge(dve_step, 14)
            kf = r.keyfade[:, :, :, :, :].rearrange("p b j i h -> p (b j i h)")
            act.activation(kf, kf, ACT.Exp, scale=0.5).then_inc(act_step, 1)

        @block.vector
        def _(dve):
            steps = [0]

            def link(ins):
                steps[0] += 1
                ins.then_inc(dve_step, 1)
                dve.wait_ge(dve_step, steps[0])

            dve.wait_ge(gates_ready, 1)
            link(dve.tensor_scalar(x[:, :], ps_l[:, 1, 0:TILES * RET_H], GATE_BIAS, None, ALU.add))
            link(dve.scalar_tensor_tensor(w1[:, :], x[:, :], -1.0, x[:, :], ALU.mult, ALU.max))
            dve.wait_ge(act_step, 1)
            link(dve.tensor_scalar(w1[:, :], u[:, :], 1.0, None, ALU.add))
            dve.wait_ge(act_step, 2)
            link(dve.tensor_scalar(w1[:, :], w1[:, :], -1.0, 1e-30, ALU.add, ALU.max))
            link(dve.reciprocal(w1[:, :], w1[:, :]))
            link(dve.tensor_tensor(lw[:, :], lw[:, :], u[:, :], ALU.mult))
            link(dve.tensor_tensor(lw[:, :], lw[:, :], w1[:, :], ALU.mult))
            link(dve.scalar_tensor_tensor(x[:, :], x[:, :], 0.0, lw[:, :], ALU.min, ALU.subtract))
            dve.wait_ge(v_ones, 1)
            dve.wait_ge(gates_ready, 2)
            for b in range(B):
                lg = ps_g[0:RET_H, 2 * b:2 * b + 2, :].rearrange("p g n -> p (g n)")
                to = r.LT[0:RET_H, b * S:(b + 1) * S]
                ins = dve.tensor_tensor_scan(to, lg, to, 0.0, ALU.add, ALU.add)
            link(ins)
            dve.wait_ge(pe_step, 1)
            link(dve.tensor_copy(r.Lcol[:, :, :].rearrange("p t h -> p (t h)"), ps_l[:, 0, 0:TILES * RET_H]))
            dve.wait_ge(pe_step, 2)
            link(dve.tensor_copy(r.Lfirst[:, :, :].rearrange("p t h -> p (t h)"), ps_l[:, 1, 0:TILES * RET_H]))
            link(dve.tensor_tensor(gap[:, :, :], r.Lcol[:, :, :], r.Lfirst[:, :, :], ALU.subtract))
            for b in range(B):
                tiles = slice(b * CH, (b + 1) * CH)
                for j in range(CH):
                    ins = dve.tensor_tensor(r.keyfade[:, b, j, :, :], r.Lfirst[:, tiles, :],
                                            r.Lcol[:, b * CH + j, :].unsqueeze(1).broadcast_to([P, CH, RET_H]), ALU.subtract)
            link(ins)
            kf = r.keyfade[:, :, :, :, :].rearrange("p b j i h -> p (b j i h)")
            link(dve.tensor_scalar(kf, kf, 0.0, None, ALU.min))
            dve.wait_ge(act_step, 4)
            link(dve.tensor_scalar(kf, kf, float(RET_D) ** -0.5, None, ALU.mult))


def l1_heads(nc, m, r):
    WIDE = WIDE_PER_HEAD * RET_H + CH // 2
    YJOBS = 4 * RET_H + CH // 2
    ROPES = 16
    OFF = [sum(CH - 1 - k for k in range(j)) * P for j in range(CH)]
    with ExitStack() as ctx:
        def sb(name, shape, dt=F32):
            return ctx.enter_context(nc.sbuf_tensor(f"l1h_{name}", shape, dt))

        sem = signals(nc, m, "l1h_")

        qr = sb("qr", [P, 2, S])
        kz = sb("kz", [P, 2, 2, S])
        rc, rs = sb("rc", [P, 2, BANK]), sb("rs", [P, 2, BANK])
        sq = sb("sq", [P, 2, 28 * P])
        sqd = sb("sqd", [P, 2, S])
        decay = sb("decay", [P, 2, S])
        ty = sb("ty", [P, 2, RET_D + 1])
        yraw = sb("yraw", [P, CH, RET_H, RET_D + 1])
        rden = sb("rden", [P, CH, RET_H])
        yn = sq[:, :, :].rearrange("p a n -> p (a n)")[:, 0:CH * HD].rearrange("p (i n) -> p i n", i=CH)
        yT = decay[:, :, :].rearrange("p a (e n) -> p a e n", e=2)
        ab = ctx.enter_context(nc.psum_tensor("l1h_ab", [P, 2, BANK], F32))
        wide = ctx.enter_context(nc.psum_tensor("l1h_wide", [P, 2, 2 * BANK], F32))
        yps = ctx.enter_context(nc.psum_tensor("l1h_y", [P, 2, BANK], F32))
        a_filled, b_filled, a_used, b_used, q_ready, k_ready = (
            sem(x) for x in ("a_filled", "b_filled", "a_used", "b_used", "q_ready", "k_ready"))
        wide_filled, wide_free = sem("wide_filled"), [sem("wide_free0"), sem("wide_free1")]
        scaled, off_squared = sem("scaled"), sem("off_squared")
        gap_ready, exp_ready, decay_ready, diag_squared, diag_ready = (sem(x) for x in ("gap_ready", "exp_ready", "decay_ready", "diag_squared", "diag_ready"))
        y_filled, y_used, ty_ready = sem("y_filled"), sem("y_used"), sem("ty_ready")
        norm_step, yT_ready, yT_used, kz_clear = sem("norm_step"), sem("yT_ready"), sem("yT_used"), sem("kz_clear")
        block = ctx.enter_context(nc.Block())

        def order():
            for n in range(4):
                yield "rope", 0, n
            for h in range(RET_H + 1):
                parts = [("gap", h, 0), ("diag", h, 0), ("values", h - 1, 0), ("rope", h // 2 + 1, 2 * (h % 2)), ("off", h, 0),
                         ("values", h - 1, 1), ("off", h, 1), ("rope", h // 2 + 1, 2 * (h % 2) + 1), ("off", h, 2),
                         ("values", h - 1, 2), ("off", h, 3), ("off", h, 4), ("values", h - 1, 3), ("off", h, 5), ("off", h, 6),
                         ("mask", h, 0)]
                for kind, k, part in parts:
                    if kind == "values" and k >= 0 or kind == "rope" and k < RET_H // 2 and h < RET_H or \
                            kind in ("gap", "diag", "off", "mask") and k < RET_H:
                        yield kind, k, part

        @block.tensor
        def _(pe):
            pe.wait_ge(m.s_wproj1, 16)
            pe.wait_ge(kz_clear, 1)
            for signal in (y_filled, wide_filled):
                pe.sem_inc(signal, FROM)
            with pe.Fori(0, B) as b:
                def rope(hp, n):
                    job, kind, half = 4 * hp + n, n // 2, n % 2
                    cols = slice(kind * HD + hp * P, kind * HD + (hp + 1) * P)
                    x = m.xnT[:, bass.ds(b * S + half * BANK, BANK)]
                    pe.wait_ge(a_used, FROM + b * ROPES + job)
                    pe.matmul(ab[:, 0, :], m.w_attn[:, cols], x, start=True, stop=True).then_inc(a_filled, 1)
                    pe.wait_ge(b_used, FROM + b * ROPES + job)
                    pe.matmul(ab[:, 1, :], r.wswap[:, cols], x, start=True, stop=True).then_inc(b_filled, 1)

                def gap(h, _):
                    job = WIDE_PER_HEAD * h
                    slot = job % 2
                    pe.wait_ge(wide_free[slot], FROM + b * (WIDE // 2) + job // 2)
                    pe.nop(nofuse=True)
                    for half in range(2):
                        ins = pe.matmul(wide[:, slot, half * BANK:(half + 1) * BANK], m.sel8[:, h * P:(h + 1) * P],
                                        r.LT[:, bass.ds(b * S + half * BANK, BANK)], start=True, stop=True)
                    ins.then_inc(wide_filled, 1)

                def rotated(h):
                    return qr[:, (h // 2) % 2, :], kz[:, (h // 2) % 2, h % 2, :]

                def diag(h, _):
                    if h % 2 == 0:
                        pe.wait_ge(q_ready, FROM + b * (ROPES // 2) + 2 * (h // 2 + 1))
                        pe.wait_ge(k_ready, FROM + b * (ROPES // 2) + 2 * (h // 2 + 1))
                    q, k = rotated(h)
                    job = WIDE_PER_HEAD * h + 1
                    slot = job % 2
                    pe.wait_ge(wide_free[slot], FROM + b * (WIDE // 2) + job // 2)
                    for i in range(CH):
                        t = slice(i * P, (i + 1) * P)
                        ins = pe.matmul(wide[:, slot, t], k[:, t], q[:, t], start=True, stop=True)
                    ins.then_inc(wide_filled, 1)

                def off(h, j):
                    q, k = rotated(h)
                    job = WIDE_PER_HEAD * h + 2 + j
                    slot = job % 2
                    pe.wait_ge(wide_free[slot], FROM + b * (WIDE // 2) + job // 2)
                    width = (CH - 1 - j) * P
                    for c in range(0, width, BANK):
                        n = min(BANK, width - c)
                        t0 = (j + 1) * P + c
                        ins = pe.matmul(wide[:, slot, c:c + n], k[:, j * P:(j + 1) * P], q[:, t0:t0 + n], start=True, stop=True)
                    ins.then_inc(wide_filled, 1)

                def values(h, g):
                    if g == 0:
                        pe.wait_ge(diag_ready, FROM + b * RET_H + h + 1)
                        pe.wait_ge(off_squared, b * 7 * RET_H + 7 * (h + 1))
                    y = yps[:, (4 * h + g) % 2, :]
                    pe.wait_ge(y_used, FROM + b * YJOBS + max(4 * h + g - 1, 0))
                    for e in range(2):
                        i = 2 * g + e
                        for j in range(i):
                            block_at = OFF[j] + (i - j - 1) * P
                            pe.matmul(y[:, e * 130:e * 130 + 65], sq[:, h % 2, block_at:block_at + P],
                                      r.v[:, bass.ds(b * CH + j, 1), h, :].rearrange("p a d -> p (a d)"), start=(j == 0), stop=(j == i - 1))
                        ins = pe.matmul(y[:, e * 130 + 65:e * 130 + 130], sqd[:, h % 2, i * P:(i + 1) * P],
                                        r.v[:, bass.ds(b * CH + i, 1), h, :].rearrange("p a d -> p (a d)"), start=True, stop=True)
                    ins.then_inc(y_filled, 1)

                work = {"rope": rope, "gap": gap, "diag": diag, "off": off, "values": values}
                for kind, k, part in order():
                    if kind in work:
                        work[kind](k, part)
                for g in range(CH // 2):
                    job = WIDE_PER_HEAD * RET_H + g
                    slot = job % 2
                    pe.wait_ge(norm_step, b * 3 + 3)
                    pe.wait_ge(wide_free[slot], FROM + b * (WIDE // 2) + job // 2)
                    for e in range(2):
                        for c in range(4):
                            ins = pe.transpose(wide[:, slot, e * BANK + c * P:e * BANK + (c + 1) * P],
                                               yn[:, 2 * g + e, c * P:(c + 1) * P], m.ident)
                    ins.then_inc(wide_filled, 1)
                    pe.wait_ge(yT_ready, b * 4 + g + 1)
                    yjob = 4 * RET_H + g
                    pe.wait_ge(y_used, FROM + b * YJOBS + yjob - 1)
                    for e in range(2):
                        for c in range(4):
                            ins = pe.matmul(yps[:, yjob % 2, e * P:(e + 1) * P], yT[:, g % 2, e, c * P:(c + 1) * P],
                                            m.w_proj1[:, c, :], start=(c == 0), stop=(c == 3))
                    ins.then_inc(y_filled, 1)

        @block.vector
        def _(dve):
            for signal in (a_used, b_used, k_ready, *wide_free, y_used, diag_ready):
                dve.sem_inc(signal, FROM)
            with dve.Fori(0, B) as b:
                def rope(hp, n):
                    job, half = 4 * hp + n, n % 2
                    t = slice(half * BANK, (half + 1) * BANK)
                    if n < 2:
                        dve.wait_ge(k_ready, FROM + b * (ROPES // 2) + max(2 * hp - 1 + n, 0))
                    else:
                        dve.wait_ge(q_ready, FROM + b * (ROPES // 2) + 2 * hp + n - 1)
                    dve.wait_ge(a_filled, b * ROPES + job + 1)
                    dve.tensor_tensor(rc[:, job % 2, :], ab[:, 0, :], m.ropecos[:, t], ALU.mult).then_inc(a_used, 1)
                    dve.wait_ge(b_filled, b * ROPES + job + 1)
                    dve.tensor_tensor(rs[:, job % 2, :], ab[:, 1, :], m.ropesin[:, t], ALU.mult).then_inc(b_used, 1)
                    if n >= 2:
                        dve.wait_ge(b_used, FROM + b * ROPES + job + 1)
                        dve.wait_ge(wide_filled, FROM + b * WIDE + WIDE_PER_HEAD * max(2 * hp - 2, 0))
                        for k in range(2):
                            c = slice(64 * k, 64 * k + 64)
                            ins = dve.tensor_tensor(kz[c, hp % 2, k, t], rc[c, job % 2, :], rs[c, job % 2, :], ALU.add)
                        ins.then_inc(k_ready, 1)

                def gap(h, _):
                    job = WIDE_PER_HEAD * h
                    dve.wait_ge(wide_filled, FROM + b * WIDE + job + 1)
                    dve.wait_ge(diag_ready, FROM + b * RET_H + max(h - 1, 0))
                    dve.tensor_tensor(decay[:, h % 2, :].rearrange("p (i t) -> p i t", i=CH),
                                      wide[:, job % 2, :].rearrange("p (i t) -> p i t", i=CH),
                                      r.Lcol[:, bass.ds(b * CH, CH), h].unsqueeze(2).broadcast_to([P, CH, P]),
                                      ALU.subtract).then_inc(gap_ready, 1)
                    dve.wait_ge(gap_ready, b * RET_H + h + 1)
                    dve.sem_inc(wide_free[job % 2], 1)

                def off(h, j):
                    if j == 0:
                        dve.wait_ge(y_filled, FROM + b * YJOBS + 4 * max(h - 1, 0))
                    job = WIDE_PER_HEAD * h + 2 + j
                    width = (CH - 1 - j) * P
                    dve.wait_ge(wide_filled, FROM + b * WIDE + job + 1)
                    dve.tensor_tensor(sq[:, h % 2, OFF[j]:OFF[j] + width].rearrange("p (i t) -> p i t", t=P),
                                      wide[:, job % 2, 0:width].rearrange("p (i t) -> p i t", t=P),
                                      r.keyfade[:, bass.ds(b, 1), j, j + 1:CH, h].rearrange("p a i -> p (a i)").unsqueeze(2)
                                      .broadcast_to([P, CH - 1 - j, P]), ALU.mult).then_inc(scaled, 1)
                    dve.wait_ge(scaled, b * 7 * RET_H + 7 * h + j + 1)
                    dve.sem_inc(wide_free[job % 2], 1)

                def mask(h, _):
                    dve.wait_ge(diag_squared, b * RET_H + h + 1)
                    dve.wait_ge(decay_ready, b * RET_H + h + 1)
                    dve.tensor_tensor(sqd[:, h % 2, :], sqd[:, h % 2, :], decay[:, h % 2, :], ALU.mult).then_inc(diag_ready, 1)

                def values(h, g):
                    y = yps[:, (4 * h + g) % 2, 0:260].rearrange("p (e k d) -> p e k d", e=2, k=2)
                    dve.wait_ge(y_filled, FROM + b * YJOBS + 4 * h + g + 1)
                    fade = r.fade[:, bass.ds(b * CH + 2 * g, 2), h]
                    out = yraw[:, 2 * g:2 * g + 2, h, :]
                    if g == 0:
                        dve.tensor_tensor(ty[:, 1:2, :], y[:, 1:2, 0, :], fade[:, 1:2].unsqueeze(2).broadcast_to([P, 1, RET_D + 1]),
                                          ALU.mult).then_inc(ty_ready, 1)
                        dve.wait_ge(ty_ready, b * 4 * RET_H + 4 * h + g + 1)
                        dve.tensor_copy(out[:, 0:1, :], y[:, 0:1, 1, :])
                        dve.tensor_tensor(out[:, 1:2, :], ty[:, 1:2, :], y[:, 1:2, 1, :], ALU.add).then_inc(y_used, 1)
                    else:
                        dve.tensor_tensor(ty[:, :, :], y[:, :, 0, :], fade.unsqueeze(2).broadcast_to([P, 2, RET_D + 1]),
                                          ALU.mult).then_inc(ty_ready, 1)
                        dve.wait_ge(ty_ready, b * 4 * RET_H + 4 * h + g + 1)
                        dve.tensor_tensor(out, ty[:, :, :], y[:, :, 1, :], ALU.add).then_inc(y_used, 1)
                    dve.wait_ge(y_used, FROM + b * YJOBS + 4 * h + g + 1)

                work = {"rope": rope, "gap": gap, "off": off, "mask": mask, "values": values}
                for kind, k, part in order():
                    if kind in work:
                        work[kind](k, part)
                dve.tensor_scalar(rden[:, :, :], yraw[:, :, :, RET_D], 1e-6, None, ALU.max).then_inc(norm_step, 1)
                dve.wait_ge(norm_step, b * 3 + 1)
                dve.reciprocal(rden[:, :, :], rden[:, :, :]).then_inc(norm_step, 1)
                dve.wait_ge(norm_step, b * 3 + 2)
                for i in range(CH):
                    ins = dve.tensor_tensor(yn[:, i, :].rearrange("p (h d) -> p h d", h=RET_H), yraw[:, i, :, 0:RET_D],
                                            rden[:, i, :].unsqueeze(2).broadcast_to([P, RET_H, RET_D]), ALU.mult)
                ins.then_inc(norm_step, 1)
                for g in range(CH // 2):
                    yjob = 4 * RET_H + g
                    dve.wait_ge(y_filled, FROM + b * YJOBS + yjob + 1)
                    hh = m.h[:, bass.ds(b * CH + 2 * g, 2), :]
                    dve.tensor_tensor(hh, hh, yps[:, yjob % 2, 0:2 * P].rearrange("p (e d) -> p e d", e=2), ALU.add).then_inc(y_used, 1)

        @block.scalar
        def _(act):
            with act.Fori(0, B) as b:
                def gap(h, _):
                    act.wait_ge(gap_ready, b * RET_H + h + 1)
                    act.activation(decay[:, h % 2, :], decay[:, h % 2, :], ACT.Exp).then_inc(exp_ready, 1)

                def diag(h, _):
                    job = WIDE_PER_HEAD * h + 1
                    act.wait_ge(wide_filled, FROM + b * WIDE + job + 1)
                    act.wait_ge(y_filled, FROM + b * YJOBS + 4 * max(h - 1, 0))
                    act.activation(sqd[:, h % 2, :], wide[:, job % 2, :], ACT.Square, scale=float(RET_D) ** -0.5).then_inc(diag_squared, 1)
                    act.wait_ge(diag_squared, b * RET_H + h + 1)
                    act.sem_inc(wide_free[job % 2], 1)

                def off(h, j):
                    act.wait_ge(scaled, b * 7 * RET_H + 7 * h + j + 1)
                    s = sq[:, h % 2, OFF[j]:OFF[j] + (CH - 1 - j) * P]
                    act.activation(s, s, ACT.Square).then_inc(off_squared, 1)

                work = {"gap": gap, "diag": diag, "off": off}
                for kind, k, part in order():
                    if kind in work:
                        work[kind](k, part)
                for g in range(CH // 2):
                    job = WIDE_PER_HEAD * RET_H + g
                    act.wait_ge(wide_filled, FROM + b * WIDE + job + 1)
                    act.wait_ge(y_filled, FROM + b * YJOBS + 4 * RET_H + max(g - 1, 0))
                    act.activation(yT[:, g % 2, :, :].rearrange("p e n -> p (e n)"), wide[:, job % 2, :], ACT.Copy).then_inc(yT_ready, 1)
                    act.wait_ge(yT_ready, b * 4 + g + 1)
                    act.sem_inc(wide_free[job % 2], 1)

        @block.gpsimd
        def _(pool):
            for k in range(2):
                ins = pool.memset(kz[64 * (1 - k):64 * (2 - k), :, k, :], 0.0)
            ins.then_inc(kz_clear, 1)
            pool.sem_inc(q_ready, FROM)
            with pool.Fori(0, B) as b:
                def rope(hp, half):
                    if half > 1:
                        return
                    pool.wait_ge(wide_filled, FROM + b * WIDE + WIDE_PER_HEAD * max(2 * hp - 2, 0))
                    job = 4 * hp + half
                    pool.wait_ge(b_used, FROM + b * ROPES + job + 1)
                    pool.wait_ge(a_used, FROM + b * ROPES + job + 1)
                    pool.tensor_tensor(qr[:, hp % 2, half * BANK:(half + 1) * BANK], rc[:, job % 2, :], rs[:, job % 2, :],
                                       ALU.add).then_inc(q_ready, 1)

                def gap(h, _):
                    pool.wait_ge(exp_ready, b * RET_H + h + 1)
                    pool.nop(nofuse=True)
                    g = decay[:, h % 2, :].rearrange("p (i t) -> p i t", i=CH)
                    pool.affine_select(out=g, in_=g, compare_op=ALU.is_ge, fill=0.0, base=0, pattern=[[0, CH], [1, P]],
                                       channel_multiplier=-1).then_inc(decay_ready, 1)

                work = {"rope": rope, "gap": gap}
                for kind, k, part in order():
                    if kind in work:
                        work[kind](k, part)


def router(nc, m, r, name, E, wrT, lower, extra):
    G = E + extra
    with ExitStack() as ctx:
        def sb(x, shape, dt=F32):
            return ctx.enter_context(nc.sbuf_tensor(f"{name}_{x}", shape, dt))

        sem = signals(nc, m, f"{name}_")

        lg, gt, ge = sb("lg", [P, TILES, E]), sb("gt", [P, TILES, E, E]), sb("ge", [P, TILES, E, E])
        rank, mx = sb("rank", [P, TILES, E]), sb("mx", [P, TILES])
        gT, b2 = sb("gT", [G, N]), sb("b2", [G, D])
        ps_l = ctx.enter_context(nc.psum_tensor(f"{name}_ps_l", [P, BANK], F32))
        ps_g = ctx.enter_context(nc.psum_tensor(f"{name}_ps_g", [P, 4, BANK], F32))
        ps_b = ctx.enter_context(nc.psum_tensor(f"{name}_ps_b", [P, 2, BANK], F32))
        logits, exps, dve_step, turned, copied, biased, bias_used, b2_in = (
            sem(k) for k in ("logits", "exps", "dve_step", "turned", "copied", "biased", "bias_used", "b2_in"))
        block = ctx.enter_context(nc.Block())

        @block.sync
        def _(sp):
            sp.dma_start(b2[0:E, :], r.b2_dram).then_inc(b2_in, 16)
            if extra:
                sp.dma_start(b2[E:G, :], r.b2_shared).then_inc(b2_in, 16)

        @block.tensor
        def _(pe):
            pe.wait_ge(r.s_router, r.n_router)
            for t in range(TILES):
                out = ps_l[:, t * E:(t + 1) * E]
                pe.matmul(out, r.hT[:, t * P:(t + 1) * P], wrT, start=True, stop=False)
                ins = pe.matmul(out, m.one[0:1, :], r.b_r[:, :], start=False, stop=True)
            ins.then_inc(logits, 1)
            pe.wait_ge(dve_step, 12)
            for t in range(TILES):
                ins = pe.transpose(ps_g[0:G, t // 4, (t % 4) * P:(t % 4 + 1) * P], r.gates[:, t, :], m.ident)
                if t % 4 == 3:
                    ins.then_inc(turned, 1)
            pe.wait_ge(b2_in, 16 + 16 * extra)
            for t in range(TILES):
                g = t // 4
                pe.wait_ge(copied, g + 1)
                if g >= 2 and t % 4 == 0:
                    pe.wait_ge(bias_used, g - 1)
                ins = pe.matmul(ps_b[:, g % 2, (t % 4) * P:(t % 4 + 1) * P], gT[:, t * P:(t + 1) * P], b2[:, :], start=True, stop=True)
                if t % 4 == 3:
                    ins.then_inc(biased, 1)

        @block.scalar
        def _(act):
            act.wait_ge(dve_step, 4)
            act.activation(r.gates[:, :, 0:E], lg[:, :, :], ACT.Exp).then_inc(exps, 1)
            for g in range(4):
                act.wait_ge(turned, g + 1)
                act.activation(gT[:, g * BANK:(g + 1) * BANK], ps_g[0:G, g, :], ACT.Copy).then_inc(copied, 1)

        @block.vector
        def _(dve):
            steps = [0]

            def link(ins):
                steps[0] += 1
                ins.then_inc(dve_step, 1)
                dve.wait_ge(dve_step, steps[0])

            def others(x):
                return x.unsqueeze(2).broadcast_to([P, TILES, E, E])

            def own(x):
                return x.unsqueeze(3).broadcast_to([P, TILES, E, E])

            dve.wait_ge(logits, 1)
            link(dve.tensor_copy(lg[:, :, :].rearrange("p t e -> p (t e)"), ps_l[:, 0:TILES * E]))
            link(dve.tensor_tensor(gt[:, :, :, :], others(lg[:, :, :]), own(lg[:, :, :]), ALU.is_gt))
            link(dve.tensor_tensor(ge[:, :, :, :], others(lg[:, :, :]), own(lg[:, :, :]), ALU.is_ge))
            dve.tensor_reduce(mx[:, :], lg[:, :, :], AX.X, ALU.max).then_inc(exps, 1)
            dve.wait_ge(exps, 1)
            link(dve.tensor_tensor(lg[:, :, :], lg[:, :, :], mx[:, :].unsqueeze(2).broadcast_to([P, TILES, E]), ALU.subtract))
            low = lower.bitcast(I32).unsqueeze(1).broadcast_to([P, TILES, E * E])
            link(dve.copy_predicated(gt[:, :, :, :].rearrange("p t i j -> p t (i j)"), low, ge[:, :, :, :].rearrange("p t i j -> p t (i j)")))
            link(dve.tensor_reduce(rank[:, :, :], gt[:, :, :, :], AX.X, ALU.add))
            link(dve.tensor_scalar(rank[:, :, :], rank[:, :, :], 1.5, None, ALU.is_lt))
            dve.wait_ge(exps, 2)
            link(dve.tensor_tensor(r.gates[:, :, 0:E], r.gates[:, :, 0:E], rank[:, :, :], ALU.mult))
            link(dve.tensor_reduce(mx[:, :], r.gates[:, :, 0:E], AX.X, ALU.add))
            link(dve.reciprocal(mx[:, :], mx[:, :]))
            link(dve.tensor_tensor(r.gates[:, :, 0:E], r.gates[:, :, 0:E], mx[:, :].unsqueeze(2).broadcast_to([P, TILES, E]), ALU.mult))
            if extra:
                link(dve.memset(r.gates[:, :, E:G], 1.0))
            else:
                link(dve.tensor_tensor(m.h[:, :, :], m.h[:, :, :], m.xn[:, :, :], ALU.add))
            for g in range(4):
                dve.wait_ge(biased, g + 1)
                hh = m.h[:, 4 * g:4 * g + 4, :]
                dve.tensor_tensor(hh, hh, ps_b[:, g % 2, :].rearrange("p (t d) -> p t d", t=4), ALU.add).then_inc(bias_used, 1)


def l1_experts(nc, m, r):
    E, UNITS = 8, 8
    with ExitStack() as ctx:
        def sb(name, shape, dt=F32):
            return ctx.enter_context(nc.sbuf_tensor(f"l1e_{name}", shape, dt))

        sem = signals(nc, m, "l1e_")

        w1, w2, b1 = sb("w1", [P, 2, 512]), sb("w2", [P, 2, 4, D]), sb("b1", [P, 2, 4])
        hid = sb("hid", [P, 2, 4, BANK])
        prime = sb("prime", [P, 1])
        ps_u = ctx.enter_context(nc.psum_tensor("l1e_ps_u", [P, 4, BANK], F32))
        ps_d = ctx.enter_context(nc.psum_tensor("l1e_ps_d", [P, 2, BANK], F32))
        slot_in = [sem("slot0_in"), sem("slot1_in")]
        up_ready, hid_ready, down_ready, down_used = sem("up_ready"), sem("hid_ready"), sem("down_ready"), sem("down_used")
        block = ctx.enter_context(nc.Block())

        @block.sync
        def _(sp):
            with sp.Fori(0, E // 2) as it:
                for k in range(2):
                    e = it * 2 + k
                    sp.wait_ge(down_ready, FROM + it * UNITS)
                    sp.dma_start(w1[:, k, :], r.W1_dram[bass.ds(e, 1), :, :].rearrange("e p f -> p (e f)")).then_inc(slot_in[k], 16)
                    sp.dma_start(w2[:, k, :, :], r.W2_dram[bass.ds(e, 1), :, :].rearrange("e (c p) d -> p (e c) d", p=P)).then_inc(slot_in[k], 16)
                    sp.dma_start(b1[:, k, :], r.b1_dram[bass.ds(e, 1), :].rearrange("e (c p) -> p (e c)", p=P),
                                 allow_slow_non_contiguous=True).then_inc(slot_in[k], 16)

        @block.tensor
        def _(pe):
            pe.sem_inc(down_ready, FROM)
            with pe.Fori(0, E // 2) as it:
                def up(u):
                    k, g = u // 4, u % 4
                    if g == 0:
                        pe.wait_ge(slot_in[k], it * 48 + 48)
                    for c in range(4):
                        pe.wait_ge(hid_ready, FROM + it * 32 + max(4 * u + c - 3, 0))
                        pe.matmul(ps_u[:, c, :], w1[:, k, c * P:(c + 1) * P], r.hT[:, g * BANK:(g + 1) * BANK], start=True,
                                  stop=True).then_inc(up_ready, 1)

                def down(u):
                    k, g = u // 4, u % 4
                    pe.wait_ge(hid_ready, FROM + it * 32 + 4 * u + 4)
                    pe.wait_ge(down_used, FROM + it * UNITS + max(u - 1, 0))
                    for t in range(4):
                        for c in range(4):
                            ins = pe.matmul(ps_d[:, u % 2, t * P:(t + 1) * P], hid[:, u % 2, c, t * P:(t + 1) * P], w2[:, k, c, :],
                                            start=(c == 0), stop=(c == 3))
                    ins.then_inc(down_ready, 1)

                for u in range(UNITS):
                    up(u)
                    if u >= 1:
                        down(u - 1)
                down(UNITS - 1)

        @block.scalar
        def _(act):
            act.sem_inc(hid_ready, FROM)
            act.activation(prime[:, :], m.pid, ACT.Gelu)
            with act.Fori(0, E // 2) as it:
                for u in range(UNITS):
                    act.wait_ge(down_ready, FROM + it * UNITS + max(u - 1, 0))
                    for c in range(4):
                        act.wait_ge(up_ready, it * 32 + 4 * u + c + 1)
                        act.activation(hid[:, u % 2, c, :], ps_u[:, c, :], ACT.Gelu, bias=b1[:, u // 4, c:c + 1]).then_inc(hid_ready, 1)

        @block.vector
        def _(dve):
            dve.sem_inc(down_used, FROM)
            with dve.Fori(0, E // 2) as it:
                for u in range(UNITS):
                    k, g = u // 4, u % 4
                    dve.wait_ge(down_ready, FROM + it * UNITS + u + 1)
                    for t in range(4):
                        hh = m.h[:, 4 * g + t, :]
                        ins = dve.scalar_tensor_tensor(hh, ps_d[:, u % 2, t * P:(t + 1) * P],
                                                       r.gates[:, 4 * g + t, bass.ds(it * 2 + k, 1)], hh, ALU.mult, ALU.add)
                    ins.then_inc(down_used, 1)
                    dve.wait_ge(down_used, FROM + it * UNITS + u + 1)


def stage_l1_ffn(nc, m, w):
    with ExitStack() as ctx:
        def sb(name, shape, dt=F32):
            return ctx.enter_context(nc.sbuf_tensor(f"l1f_{name}", shape, dt))

        r = Core()
        r.hn, r.hT = sb("hn", [P, TILES, D]), sb("hT", [P, N])
        r.gates = sb("gates", [P, TILES, 8])
        r.b_r, r.ln_g, r.ln_b = sb("b_r", [1, 8]), sb("ln_g", [P, 1]), sb("ln_b", [P, 1])
        r.b2_dram, r.b1_dram, r.W1_dram, r.W2_dram = w["L1_ffn_b2"], w["L1_ffn_b1"], w["L1_ffn_W1"], w["L1_ffn_W2"]
        r.s_router, r.n_router = signals(nc, m, "l1f_")("router"), 48
        with nc.Block() as block:
            @block.sync
            def _(sp):
                sp.dma_start(r.b_r[:, :], row(w["L1_ffn_b_r"])).then_inc(r.s_router, 16)
                sp.dma_start(r.ln_g[:, :], col(w["L1_ffn_ln_g"]), allow_slow_non_contiguous=True).then_inc(r.s_router, 16)
                sp.dma_start(r.ln_b[:, :], col(w["L1_ffn_ln_b"]), allow_slow_non_contiguous=True).then_inc(r.s_router, 16)
                sp.wait_ge(r.s_router, 48)
        layernorm(nc, m, "ln_l1f", m.h, m.xn, None)
        layernorm(nc, m, "ln_l1g", m.xn, r.hn, r.hT, gain=r.ln_g[:, 0:1], shift=r.ln_b[:, 0:1])
        router(nc, m, r, "l1r", 8, m.wrT[:, :], m.lower8, 0)
        l1_experts(nc, m, r)


def move_heads():
    out = np.zeros((4, 2, 16, 2, 8, 8, 16), np.float32)
    for a in range(2):
        for l in range(8):
            for d in range(16):
                out[:, a, d, a, l, l, d] = 1.0
    return out.reshape(P, 2, 8, P)


def stage_l2_attn(nc, m, w):
    H, HW, ROLL, WIN = 8, 16, 32, 64
    with ExitStack() as ctx:
        def sb(name, shape, dt=F32):
            return ctx.enter_context(nc.sbuf_tensor(f"l2_{name}", shape, dt))

        sem = signals(nc, m, "l2_")

        move = sb("move", [P, 2, 8, P])
        b_proj = sb("b_proj", [1, D])
        const_in = sem("const_in")
        with nc.Block() as block:
            @block.sync
            def _(sp):
                sp.dma_start(move[:, :, :, :], w["move"]).then_inc(const_in, 16)
                sp.dma_start(b_proj[:, :], row(w["L2_attn_b_proj"])).then_inc(const_in, 16)
        layernorm(nc, m, "ln_l2a", m.h, m.xn, m.xnT)
        qkv = sb("qkv", [P, 4, 3 * D])
        qk = sb("qk", [P, 2, H, H, HW])
        s, e = sb("s", [P, 4, H, H]), sb("e", [P, 4, H, H])
        mx = sb("mx", [P, 4, H])
        av = sb("av", [P, 2, H, HW, H])
        o = sb("o", [P, 4, D])
        oT = sb("oT", [P, S])
        yT = sb("yT", [P, S + ROLL])
        prime = sb("prime", [P, 1])
        ps_q = ctx.enter_context(nc.psum_tensor("l2_ps_q", [P, 4, BANK], F32))
        ps_t = ctx.enter_context(nc.psum_tensor("l2_ps_t", [P, BANK], F32))
        ps_g = ps_q[:, :, 0:2 * P].rearrange("p q (a n) -> p q a n", a=2)
        ps_o = ctx.enter_context(nc.psum_tensor("l2_ps_o", [P, BANK], F32))
        qkv_ready, qkv_in, qk_ready = (sem(x) for x in ("qkv_ready", "qkv_in", "qk_ready"))
        dve_step, exps, o_ready, o_turned, oT_in, moved, yT_in, out_ready, out_used = (
            sem(x) for x in ("dve_step", "exps", "o_ready", "o_turned", "oT_in", "moved", "yT_in", "out_ready", "out_used"))
        block = ctx.enter_context(nc.Block())
        STEPS = 4 + 2 + 3 + 8

        @block.tensor
        def _(pe):
            pe.wait_ge(const_in, 32)
            for signal in (moved, out_ready, o_turned):
                pe.sem_inc(signal, FROM)
            for b in range(B):
                for g in range(2 * b, 2 * b + 2):
                    if g >= 1:
                        pe.wait_ge(qkv_in, g)
                        pe.wait_ge(yT_in, b)
                    for t in range(4):
                        n = 4 * g + t
                        ins = pe.matmul(ps_q[:, t, 0:3 * D], m.xnT[:, n * P:(n + 1) * P], m.wqkv2[:, :, :].rearrange("p c d -> p (c d)"),
                                        start=True, stop=True)
                    ins.then_inc(qkv_ready, 1)
                    pe.wait_ge(o_ready, FROM + g + 1)
                    if g >= 1:
                        pe.wait_ge(oT_in, g)
                    for t in range(4):
                        ins = pe.transpose(ps_t[:, t * P:(t + 1) * P], o[:, t, :], m.ident)
                    ins.then_inc(o_turned, 1)
                pe.wait_ge(oT_in, 2 * b + 2)
                pe.wait_ge(qkv_in, 2 * b + 2)
                for h in range(H):
                    q = 32 * (h // 2)
                    for l in range(8):
                        ins = pe.matmul(ps_g[:, h // 2, h % 2, :], move[q:q + 32, h % 2, l, :], oT[q:q + 32, l:S:8], start=(l == 0), stop=(l == 7))
                ins.then_inc(moved, 1)
                pe.wait_ge(yT_in, b + 1)
                for g in range(2 * b, 2 * b + 2):
                    if g >= 1:
                        pe.wait_ge(out_used, g)
                    for t in range(4):
                        n = (4 * g + t) % CH
                        pe.matmul(ps_o[:, t * P:(t + 1) * P], yT[:, n * P:(n + 1) * P], m.wproj2[:, :], start=True, stop=False)
                        ins = pe.matmul(ps_o[:, t * P:(t + 1) * P], m.one[0:1, :], b_proj[:, :], start=False, stop=True)
                    ins.then_inc(out_ready, 1)

        @block.scalar
        def _(act):
            act.activation(prime[:, :], m.pid, ACT.Exp, scale=-1.0)
            with act.Fori(0, B) as b:
                for half in range(2):
                    g = b * 2 + half
                    act.wait_ge(qkv_ready, g + 1)
                    act.wait_ge(o_ready, FROM + g)
                    act.activation(qkv[:, :, :], ps_q[:, :, 0:3 * D], ACT.Copy).then_inc(qkv_in, 1)
                    act.wait_ge(dve_step, FROM + g * STEPS + 6)
                    act.activation(e[:, :, :, :], s[:, :, :, :], ACT.Exp, scale=float(HW) ** -0.5).then_inc(exps, 1)
                    act.wait_ge(o_turned, FROM + g + 1)
                    act.wait_ge(moved, FROM + b)
                    if half == 0:
                        act.activation(oT[:, S - ROLL:S], ps_t[:, 0:ROLL], ACT.Copy)
                        act.activation(oT[:, 0:BANK - ROLL], ps_t[:, ROLL:BANK], ACT.Copy).then_inc(oT_in, 1)
                    else:
                        act.activation(oT[:, BANK - ROLL:S - ROLL], ps_t[:, :], ACT.Copy).then_inc(oT_in, 1)
                act.wait_ge(moved, FROM + b + 1)
                act.wait_ge(out_ready, FROM + b * 2)
                of = ps_g.rearrange("p q a (k r) -> p q a k r", r=8)
                to = yT[:, ROLL:ROLL + S].rearrange("p (k h r) -> p k h r", h=H, r=8)
                for h in range(H):
                    act.activation(to[:, 0:15, h, :], of[:, h // 2, h % 2, 0:15, :], ACT.Copy)
                for half in range(2):
                    place = (to[:, 15, 0:4, :] if half == 0 else yT[:, 0:ROLL].rearrange("p (h r) -> p h r", r=8))
                    ins = act.activation(place.rearrange("p (q a) r -> p q a r", a=2), of[:, 2 * half:2 * half + 2, :, 15, :], ACT.Copy)
                ins.then_inc(yT_in, 1)

        @block.gpsimd
        def _(pool):
            with pool.Fori(0, 2 * B) as g:
                pool.wait_ge(qkv_in, g + 1)
                for t in range(4):
                    pool.wait_ge(dve_step, FROM + g * STEPS + max(t - 1, 0))
                    q = qkv[:, t, 0:D].rearrange("p (h d) -> p h d", h=H).unsqueeze(2).broadcast_to([P, H, H, HW])
                    k = qkv[:, t, D:2 * D].rearrange("p (h d) -> p h d", h=H).unsqueeze(1).broadcast_to([P, H, H, HW])
                    pool.tensor_tensor(qk[:, t % 2, :, :, :], q, k, ALU.mult).then_inc(qk_ready, 1)

        @block.vector
        def _(dve):
            for signal in (o_ready, dve_step):
                dve.sem_inc(signal, FROM)
            with dve.Fori(0, B) as b:
                for half in range(2):
                    g = b * 2 + half
                    steps = [0]

                    def link(ins):
                        steps[0] += 1
                        ins.then_inc(dve_step, 1)
                        dve.wait_ge(dve_step, FROM + g * STEPS + steps[0])

                    for t in range(4):
                        dve.wait_ge(qk_ready, g * 4 + t + 1)
                        link(dve.tensor_reduce(s[:, t, :, :].rearrange("p h g -> p (h g)"), qk[:, t % 2, :, :, :].rearrange("p h g d -> p (h g) d"), AX.X, ALU.add))
                    s2, e2 = (x.rearrange("p t h g -> p (t h) g") for x in (s[:, :, :, :], e[:, :, :, :]))
                    mx1 = mx[:, :, :].rearrange("p t h -> p (t h)")
                    wide_mx = mx1.unsqueeze(2).broadcast_to([P, 4 * H, H])
                    link(dve.tensor_reduce(mx1, s2, AX.X, ALU.max))
                    link(dve.tensor_tensor(s2, s2, wide_mx, ALU.subtract))
                    dve.wait_ge(exps, g + 1)
                    link(dve.tensor_reduce(mx1, e2, AX.X, ALU.add))
                    link(dve.reciprocal(mx1, mx1))
                    link(dve.tensor_tensor(e2, e2, wide_mx, ALU.mult))
                    dve.wait_ge(o_turned, FROM + g)
                    for t in range(4):
                        a = e[:, t, :, :].unsqueeze(2).broadcast_to([P, H, HW, H])
                        v = qkv[:, t, 2 * D:3 * D].rearrange("p (g d) -> p d g", g=H).unsqueeze(1).broadcast_to([P, H, HW, H])
                        link(dve.tensor_tensor(av[:, t % 2, :, :, :], a, v, ALU.mult))
                        link(dve.tensor_reduce(o[:, t, :], av[:, t % 2, :, :, :].rearrange("p h d g -> p (h d) g"), AX.X, ALU.add))
                    dve.sem_inc(o_ready, 1)
                for half in range(2):
                    g = b * 2 + half
                    dve.wait_ge(out_ready, FROM + g + 1)
                    hh = m.h[:, bass.ds(g * 4, 4), :]
                    dve.tensor_tensor(hh, hh, ps_o[:, :].rearrange("p (t d) -> p t d", t=4), ALU.add).then_inc(out_used, 1)


TOPK = 16
TH, TW = 8, 16


def stage_l2_ffn(nc, m, w):
    layernorm(nc, m, "ln_l2f", m.h, m.xn, m.xnT)
    with ExitStack() as ctx:
        def sb(name, shape, dt=F32):
            return ctx.enter_context(nc.sbuf_tensor(f"t_{name}", shape, dt))

        r = Core()
        r.xc = sb("xc", [P, N])
        r.v = sb("v", [P, TILES, TH, TW + 1])
        r.wpad = sb("wpad", [P, 2, 2, P])
        r.bpad = sb("bpad", [P, 2, 2])
        r.wo_b = sb("wo_b", [1, D])
        topk_prepare(nc, m, r, w)
        topk_attend(nc, m, r)


def topk_prepare(nc, m, r, w):
    with ExitStack() as ctx:
        def sb(name, shape, dt=F32):
            return ctx.enter_context(nc.sbuf_tensor(f"tp_{name}", shape, dt))

        sem = signals(nc, m, "tp_")

        posw, posb, qkvb = sb("posw", [P, 3]), sb("posb", [P, 1]), sb("qkvb", [1, 3 * D])
        brow = sb("brow", [1, 2, 2, P])
        ps_v = ctx.enter_context(nc.psum_tensor("tp_ps_v", [P, 2, BANK], F32))
        ps_b = ctx.enter_context(nc.psum_tensor("tp_ps_b", [P, BANK], F32))
        loaded, dve_step, pool_step, v_ready, v_done, b_ready = (
            sem(x) for x in ("loaded", "dve_step", "pool_step", "v_ready", "v_done", "b_ready"))
        block = ctx.enter_context(nc.Block())

        @block.sync
        def _(sp):
            sp.dma_start(posw[:, :], w["L2_ffn_pos_w"].rearrange("d a k -> d (a k)")).then_inc(loaded, 16)
            sp.dma_start(posb[:, :], col(w["L2_ffn_pos_b"]), allow_slow_non_contiguous=True).then_inc(loaded, 16)
            sp.dma_start(qkvb[:, :], row(w["L2_ffn_qkv_b"])).then_inc(loaded, 16)
            sp.dma_start(r.wo_b[:, :], row(w["L2_ffn_wo_b"])).then_inc(loaded, 16)
            sp.wait_ge(loaded, 64)

        @block.gpsimd
        def _(pool):
            pool.memset(r.v[:, :, :, TW:TW + 1], 1.0)
            pool.memset(r.wpad[:, :, :, :], 0.0).then_inc(pool_step, 1)
            pool.memset(brow[:, :, :, :], 0.0).then_inc(pool_step, 1)
            pool.wait_ge(loaded, 64)
            pool.wait_ge(pool_step, 2)
            for kind in range(2):
                pool.tensor_copy(r.wpad[:, kind, :, :].rearrange("p g (h x) -> p (g h) x", x=32)[:, :, 0:TW],
                                 m.wqkv3[:, kind, :].rearrange("p (gh d) -> p gh d", d=TW)).then_inc(pool_step, 1)
                pool.tensor_copy(brow[:, kind, :, :].rearrange("p g (h x) -> p (g h) x", x=32)[:, :, 0:TW],
                                 qkvb[:, kind * D:(kind + 1) * D].rearrange("p (gh d) -> p gh d", d=TW)).then_inc(pool_step, 1)

        @block.tensor
        def _(pe):
            pe.wait_ge(pool_step, 6)
            for n in range(4):
                ins = pe.matmul(ps_b[:, n:n + 1], brow[0:1, n // 2, n % 2, :], m.one[0:1, 0:1], start=True, stop=True)
            ins.then_inc(b_ready, 1)
            pe.wait_ge(dve_step, 6)
            for t in range(TILES):
                if t >= 2:
                    pe.wait_ge(v_done, t - 1)
                pe.matmul(ps_v[:, t % 2, 0:D], r.xc[:, t * P:(t + 1) * P], m.wqkv3[:, 2, :], start=True, stop=False)
                pe.matmul(ps_v[:, t % 2, 0:D], m.one[0:1, :], qkvb[:, 2 * D:3 * D], start=False, stop=True).then_inc(v_ready, 1)

        @block.scalar
        def _(act):
            for t in range(TILES):
                act.wait_ge(v_ready, t + 1)
                act.activation(r.v[:, t, :, 0:TW], ps_v[:, t % 2, 0:D].rearrange("p (h d) -> p h d", h=TH), ACT.Copy).then_inc(v_done, 1)

        @block.vector
        def _(dve):
            steps = [0]

            def link(ins):
                steps[0] += 1
                ins.then_inc(dve_step, 1)
                dve.wait_ge(dve_step, steps[0])

            dve.wait_ge(loaded, 64)
            mid = posw[:, 1:2]
            link(dve.tensor_scalar(mid, mid, 1.0, None, ALU.add))
            link(dve.tensor_scalar(r.xc[:, :], m.xnT[:, :], mid, posb[:, 0:1], ALU.mult, ALU.add))
            for b in range(B):
                a, z = b * S, (b + 1) * S
                link(dve.scalar_tensor_tensor(r.xc[:, a + 1:z], m.xnT[:, a:z - 1], posw[:, 0:1], r.xc[:, a + 1:z], ALU.mult, ALU.add))
                link(dve.scalar_tensor_tensor(r.xc[:, a:z - 1], m.xnT[:, a + 1:z], posw[:, 2:3], r.xc[:, a:z - 1], ALU.mult, ALU.add))
            dve.wait_ge(b_ready, 1)
            dve.tensor_copy(r.bpad[:, :, :].rearrange("p a b -> p (a b)"), ps_b[:, 0:4])


def topk_attend(nc, m, r):
    SC = float(D) ** -0.5
    PAIR, FIRST, AHEAD = 2 * TH, 8, 3
    KEPT = 4
    nc.disable_value_cache = True
    with ExitStack() as ctx:
        def sb(name, shape, dt=F32):
            return ctx.enter_context(nc.sbuf_tensor(f"ta_{name}", shape, dt))

        sem = signals(nc, m, "ta_")
        qT, kT = sb("qT", [P, 2, N]), sb("kT", [P, 2, N])
        vseq = sb("vseq", [P, CH, TH, 2 * TW])
        qz = sb("qz", [P, 2, TH, P])
        top, ntop = sb("top", [P, 2, 2, 8]), sb("ntop", [P, 4])
        left = sb("left", [P, 4, S])
        ex = sb("ex", [P, 4, S])
        exT = sb("exT", [P, 2, CH, P])
        acc = sb("acc", [P, 2, P])
        rden, o, oT = sb("rden", [P, TH]), sb("o", [P, D]), sb("oT", [P, D])
        prime = sb("prime", [P, 1])
        ps_s = ctx.enter_context(nc.psum_tensor("ta_ps_s", [P, 2, S], F32))
        ps_t = ctx.enter_context(nc.psum_tensor("ta_ps_t", [P, S], F32))
        ps_o = ctx.enter_context(nc.psum_tensor("ta_ps_o", [P, BANK], F32))
        ps_p = ctx.enter_context(nc.psum_tensor("ta_ps_p", [P, BANK], F32))
        proj_ready, proj_done, q_in, v_in = sem("proj_ready"), sem("proj_done"), sem("q_in"), sem("v_in")
        max_done = [sem("first_max"), sem("second_max")]
        s_ready, s_free, first_out, left_ready, left_exp, kept, turned, exT_in = (
            sem(x) for x in ("s_ready", "s_free", "first_out", "left_ready", "left_exp", "kept", "turned", "exT_in"))
        acc_out, acc_turned = sem("acc_out"), sem("acc_turned")
        values_done, rden_ready, o_ready, o_turned, oT_in, out_ready, out_used = (
            sem(x) for x in ("values_done", "rden_ready", "o_ready", "o_turned", "oT_in", "out_ready", "out_used"))
        block = ctx.enter_context(nc.Block())
        PAIRS = TILES // 2

        def place(eng, pair):
            at = Core()
            at.pair, at.item0, at.tile0 = pair, pair * PAIR, pair * 2
            at.key0 = [(pair + k) // (PAIRS // B) * S for k in range(2)]
            if not isinstance(pair, int):
                at.item0, at.tile0 = eng.snap(at.item0), eng.snap(at.tile0)
                if eng is nc.tensor:
                    at.key0 = [eng.snap(x) for x in at.key0]
            return at

        def steps(eng, step):
            for i in range(FIRST):
                step(place(eng, 0), i, False)
            with eng.Fori(0, PAIRS - 1) as pair:
                at = place(eng, pair)
                for i in range(FIRST, PAIR + FIRST):
                    step(at, i, False)
            for i in range(FIRST, PAIR + FIRST):
                step(place(eng, PAIRS - 1), i, True)

        @block.tensor
        def _(pe):
            def logits(at, i):
                h, odd, n = i % TH, (i // TH) % 2, at.item0 + i
                grp = h // 4
                if h == 0:
                    pe.wait_ge(q_in, at.tile0 + (i // TH + 1))
                pe.wait_ge(s_free, n + 1)
                for half in range(2):
                    ins = pe.matmul(ps_s[:, i % 2, half * BANK:(half + 1) * BANK], qz[:, odd, h, :],
                                    kT[:, grp, bass.ds(at.key0[i // PAIR] + half * BANK, BANK)], start=True, stop=True)
                ins.then_inc(s_ready, 1)

            def step(at, i, last):
                h, n = i % TH, at.item0 + i
                if i + AHEAD < PAIR or not last:
                    logits(at, i + AHEAD)
                if i >= TH and h == 1:
                    tile = at.tile0 + (i // TH - 1)
                    pe.wait_ge(acc_out, tile + 2)
                    pe.wait_ge(out_used, tile + 1)
                    for grp in range(2):
                        ins = pe.transpose(ps_p[:, grp * P:(grp + 1) * P], acc[:, grp, :], m.ident)
                    ins.then_inc(acc_turned, 1)
                if i >= TH and h == 4:
                    tile = at.tile0 + (i // TH - 1)
                    pe.wait_ge(o_ready, tile + 1)
                    pe.transpose(ps_p[:, 0:P], o[:, :], m.ident).then_inc(o_turned, 1)
                if i >= TH and h == 5:
                    tile = at.tile0 + (i // TH - 1)
                    pe.wait_ge(oT_in, tile + 1)
                    pe.matmul(ps_p[:, 0:P], oT[:, :], m.wo[:, :], start=True, stop=False)
                    pe.matmul(ps_p[:, 0:P], m.one[0:1, :], r.wo_b[:, :], start=False, stop=True).then_inc(out_ready, 1)
                if i < PAIR or not last:
                    pe.wait_ge(kept, n + (KEPT + 1))
                    for j in range(CH):
                        ins = pe.transpose(ps_t[:, j * P:(j + 1) * P], ex[:, i % 4, j * P:(j + 1) * P], m.ident)
                    ins.then_inc(turned, 1)
                if i < PAIR or not last:
                    pe.wait_ge(exT_in, n + 1)
                    if i % PAIR == 0:
                        pe.wait_ge(v_in, at.pair + (i // PAIR + 2))
                    if h == 0:
                        pe.wait_ge(acc_out, at.tile0 + (i // TH + 1))
                    a, grp = 32 * (h % 4), h // 4
                    for j in range(CH):
                        ins = pe.matmul(ps_o[a:a + 2 * TW, grp * P:(grp + 1) * P], vseq[:, j, h, :], exT[:, i % 2, j, :],
                                        start=(j == 0), stop=(j == CH - 1))
                    if h == TH - 1:
                        ins.then_inc(values_done, 1)

            for n in range(4 * B * 2):
                kind, grp, g = n // 8, (n // 4) % 2, n % 4
                if n >= 4:
                    pe.wait_ge(proj_done, n - 3)
                pe.matmul(ps_s[:, (n // 2) % 2, (n % 2) * BANK:(n % 2 + 1) * BANK], r.wpad[:, kind, grp, :],
                          r.xc[:, g * BANK:(g + 1) * BANK], start=True, stop=True).then_inc(proj_ready, 1)
            pe.wait_ge(proj_done, 16)
            for i in range(AHEAD):
                logits(place(pe, 0), i)
            steps(pe, step)

        @block.scalar
        def _(act):
            def fetch_values(tile):
                act.activation(vseq[:, :, :, 0:TW + 1], r.v[:, bass.ds(tile, CH), :, :], ACT.Copy).then_inc(v_in, 1)

            def all_exp(at, i):
                act.wait_ge(first_out, at.item0 + (i + 1))
                act.nop(nofuse=True)
                act.activation(ex[:, i % 4, :], ps_s[:, i % 2, :], ACT.Exp, bias=ntop[:, i % 4:i % 4 + 1], scale=SC).then_inc(s_free, 1)

            def turn(at, i):
                act.wait_ge(turned, at.item0 + (i + 1))
                act.activation(exT[:, i % 2, :, :].rearrange("p j q -> p (j q)"), ps_t[:, :], ACT.Copy).then_inc(exT_in, 1)

            def step(at, i, last):
                h, n = i % TH, at.item0 + i
                if i + 1 < PAIR or not last:
                    all_exp(at, i + 1)
                if i < PAIR or not last:
                    act.wait_ge(left_ready, n + 1)
                    act.activation(left[:, i % 4, :], left[:, i % 4, :], ACT.Exp, bias=ntop[:, i % 4:i % 4 + 1], scale=SC).then_inc(left_exp, 1)
                if i >= TH and h == 1:
                    act.wait_ge(values_done, at.tile0 + i // TH)
                    act.activation(acc[:, :, :].rearrange("p g q -> p (g q)"), ps_o[:, 0:2 * P], ACT.Copy).then_inc(acc_out, 1)
                if i >= TH and h == 5:
                    act.wait_ge(o_turned, at.tile0 + i // TH)
                    act.activation(oT[:, :], ps_p[:, 0:P], ACT.Copy).then_inc(oT_in, 1)
                if 1 <= i <= PAIR or (i > PAIR and not last):
                    turn(at, i - 1)
                if i == PAIR and not last:
                    act.wait_ge(values_done, at.tile0 + 2)
                    act.nop(nofuse=True)
                    fetch_values((at.pair + 1) // (PAIRS // B) * CH)

            act.activation(prime[:, :], m.pid, ACT.Exp, scale=-1.0)
            act.sem_inc(s_free, 2)
            act.sem_inc(acc_out, 1)
            for n in range(4 * B * 2):
                kind, grp, g = n // 8, (n // 4) % 2, n % 4
                act.wait_ge(proj_ready, n + 1)
                act.activation((qT, kT)[kind][:, grp, g * BANK:(g + 1) * BANK], ps_s[:, (n // 2) % 2, (n % 2) * BANK:(n % 2 + 1) * BANK],
                               ACT.Identity, bias=r.bpad[:, kind, grp:grp + 1]).then_inc(proj_done, 1)
            act.wait_ge(v_in, 1)
            fetch_values(0)
            all_exp(place(act, 0), 0)
            steps(act, step)

        @block.gpsimd
        def _(pool):
            def query(at, tile_rel):
                for grp in range(2):
                    ins = pool.tensor_tensor(qz[:, tile_rel % 2, 4 * grp:4 * grp + 4, :],
                                             qT[:, grp, bass.ds(at.pair * (2 * P) + tile_rel * P, P)].unsqueeze(1).broadcast_to([P, 4, P]),
                                             m.quarter.unsqueeze(2).broadcast_to([P, 4, P]), ALU.mult)
                ins.then_inc(q_in, 1)

            def step(at, i, last):
                if i < PAIR or not last:
                    pool.wait_ge(left_exp, at.item0 + (i + 1))
                    pool.tensor_tensor(ex[:, i % 4, :], ex[:, i % 4, :], left[:, i % 4, :], ALU.subtract).then_inc(kept, 1)
                if i % TH == 2 and (i < TH or not last):
                    query(at, i // TH + 1)

            pool.memset(vseq[:, :, :, :], 0.0).then_inc(v_in, 1)
            pool.sem_inc(kept, KEPT)
            pool.wait_ge(proj_done, 16)
            query(place(pool, 0), 0)
            steps(pool, step)

        @block.vector
        def _(dve):
            def first_max(at, i):
                dve.wait_ge(s_ready, at.item0 + (i + 1))
                dve.nop(nofuse=True)
                dve.max(top[:, i % 2, 0, :], ps_s[:, i % 2, :]).then_inc(max_done[0], 1)

            def first_replace(at, i):
                dve.wait_ge(max_done[0], at.item0 + (i + 1))
                dve.tensor_scalar(ntop[:, i % 4:i % 4 + 1], top[:, i % 2, 0, 0:1], -SC, None, ALU.mult)
                dve.wait_ge(kept, at.item0 + (i + 1))
                dve.nop(nofuse=True)
                dve.match_replace(left[:, i % 4, :], top[:, i % 2, 0, :], ps_s[:, i % 2, :], -BIG).then_inc(first_out, 1)

            def second_max(at, i):
                dve.wait_ge(first_out, at.item0 + (i + 1))
                dve.nop(nofuse=True)
                dve.max(top[:, i % 2, 1, :], left[:, i % 4, :]).then_inc(max_done[1], 1)

            def second_replace(at, i):
                dve.wait_ge(max_done[1], at.item0 + (i + 1))
                dve.nop(nofuse=True)
                dve.match_replace(left[:, i % 4, :], top[:, i % 2, 1, :], left[:, i % 4, :], -BIG).then_inc(left_ready, 1)

            def step(at, i, last):
                h = i % TH
                more, here = i + 1 < PAIR or not last, i < PAIR or not last
                if more:
                    first_max(at, i + 1)
                if here:
                    second_max(at, i)
                if more:
                    first_replace(at, i + 1)
                if here:
                    second_replace(at, i)
                if i >= TH and h == 3:
                    tile = at.tile0 + (i // TH - 1)
                    out = ps_p[:, 0:2 * P].rearrange("p (h d) -> p h d", h=TH)
                    dve.wait_ge(acc_turned, tile + 1)
                    dve.reciprocal(rden[:, :], out[:, :, TW]).then_inc(rden_ready, 1)
                    dve.wait_ge(rden_ready, tile + 1)
                    dve.tensor_tensor(o[:, :].rearrange("p (h d) -> p h d", h=TH), out[:, :, 0:TW],
                                      rden[:, :].unsqueeze(2).broadcast_to([P, TH, TW]), ALU.mult).then_inc(o_ready, 1)
                if i >= TH and h == 7:
                    tile = at.tile0 + (i // TH - 1)
                    dve.wait_ge(out_ready, tile + 1)
                    hh = m.h[:, bass.ds(tile, 1), :]
                    dve.tensor_tensor(hh, hh, ps_p[:, 0:P].unsqueeze(1), ALU.add).then_inc(out_used, 1)

            dve.sem_inc(out_used, 1)
            first_max(place(dve, 0), 0)
            first_replace(place(dve, 0), 0)
            steps(dve, step)


def stage_l3_attn(nc, m, w):
    ST = 64
    with ExitStack() as ctx:
        def sb(name, shape, dt=F32):
            return ctx.enter_context(nc.sbuf_tensor(f"l3_{name}", shape, dt))

        r = Core()
        r.B, r.C, r.D = sb("B", [ST, D, 2]), sb("C", [P, ST, 2]), sb("D", [P, 1])
        r.par = sb("par", [P, 3])
        r.w1, r.w2, r.v1, r.v2, r.dd = (sb(x, [P, P]) for x in ("w1", "w2", "v1", "v2", "dd"))
        r.cos, r.sin, r.fade = sb("cos", [P, S]), sb("sin", [P, S]), sb("fade", [P, 1])
        r.par_in = signals(nc, m, "l3_")("par_in")
        with nc.Block() as block:
            @block.sync
            def _(sp):
                for half in range(2):
                    for i, name in enumerate(("Lambda_re", "Lambda_im", "log_step")):
                        sp.dma_start(r.par[half * ST:(half + 1) * ST, i:i + 1], col(w["L3_attn_" + name]),
                                     allow_slow_non_contiguous=True).then_inc(r.par_in, 16)
                sp.dma_start(r.B[:, :, :], w["L3_attn_B"]).then_inc(r.par_in, 16)
                sp.dma_start(r.C[:, :, :], w["L3_attn_C"]).then_inc(r.par_in, 16)
                sp.dma_start(r.D[:, :], col(w["L3_attn_D"]), allow_slow_non_contiguous=True).then_inc(r.par_in, 16)
        r.n_par = 9 * 16
        layernorm(nc, m, "ln_l3a", m.h, m.xn, m.xnT)
        ssm_prepare(nc, m, r, ST)
        ssm_run(nc, m, r)


def ssm_prepare(nc, m, r, ST):
    with ExitStack() as ctx:
        def sb(name, shape, dt=F32):
            return ctx.enter_context(nc.sbuf_tensor(f"l3p_{name}", shape, dt))

        small = sb("small", [P, 32])
        names = ("step angle turns r half sh sr c s a b den t1 t2 gr gi magr pc ps").split()
        v = {name: small[:, i:i + 1] for i, name in enumerate(names)}
        power = sb("power", [P, 2, 12])
        tmp = sb("tmp", [P, 2, S // 2])
        bbar = sb("bbar", [ST, 2, D])
        tb = sb("tb", [ST, 2, D])
        x1, x2 = sb("x1", [P, 2, ST]), sb("x2", [P, 2, ST])
        ps_b = ctx.enter_context(nc.psum_tensor("l3p_ps_b", [P, BANK], F32))
        ps_c = ctx.enter_context(nc.psum_tensor("l3p_ps_c", [P, BANK], F32))
        sem = signals(nc, m, "l3p_")
        dve_step, act_step, outs, turned, x_ready = (sem(k) for k in ("dve_step", "act_step", "outs", "turned", "x_ready"))
        TWO_PI = 2.0 * np.pi
        TWO_PI_HI = 6.28125
        ROUND = 12582912.0
        PI_BELOW = 3.1415925
        block = ctx.enter_context(nc.Block())

        @block.scalar
        def _(act):
            act.wait_ge(r.par_in, r.n_par)
            act.activation(v["step"], r.par[:, 2:3], ACT.Exp).then_inc(act_step, 1)
            act.wait_ge(act_step, 1)
            act.activation(r.fade[:, :], r.par[:, 0:1], ACT.Exp, scale=v["step"]).then_inc(act_step, 1)
            act.wait_ge(dve_step, 7)
            act.activation(v["sr"], v["r"], ACT.Sin).then_inc(act_step, 1)
            act.activation(v["sh"], v["half"], ACT.Sin).then_inc(act_step, 1)
            act.wait_ge(turned, 1)
            act.activation(r.w1[:, :], ps_b[:, 0:P], ACT.Copy)
            act.activation(r.w2[:, 0:ST], ps_b[:, ST:2 * ST], ACT.Copy)
            act.activation(r.w2[:, ST:P], ps_b[:, 0:ST], ACT.Copy, scale=-1.0)
            act.activation(r.v1[:, :], ps_c[:, 0:P], ACT.Copy)
            act.activation(r.v2[:, :], ps_c[:, P:2 * P], ACT.Copy)

        @block.gpsimd
        def _(pool):
            pool.wait_ge(r.par_in, r.n_par)
            pool.tensor_scalar(x1[:, 0, :], r.C[:, :, 0], 2.0, None, ALU.mult)
            pool.tensor_scalar(x1[:, 1, :], r.C[:, :, 1], -2.0, None, ALU.mult)
            pool.tensor_scalar(x2[:, 0, :], r.C[:, :, 1], -2.0, None, ALU.mult)
            pool.tensor_scalar(x2[:, 1, :], r.C[:, :, 0], -2.0, None, ALU.mult)
            pool.tensor_scalar(r.dd[:, :], m.ident, r.D[:, 0:1], None, ALU.mult).then_inc(x_ready, 1)

        @block.tensor
        def _(pe):
            pe.wait_ge(x_ready, 1)
            pe.transpose(ps_c[:, 0:P], x1[:, :, :].rearrange("p a s -> p (a s)"), m.ident)
            pe.transpose(ps_c[:, P:2 * P], x2[:, :, :].rearrange("p a s -> p (a s)"), m.ident)
            pe.wait_ge(outs, 1)
            pe.transpose(ps_b[:, 0:ST], bbar[:, 0, :], m.ident[0:ST, 0:ST])
            pe.transpose(ps_b[:, ST:P], bbar[:, 1, :], m.ident[0:ST, 0:ST]).then_inc(turned, 1)

        @block.vector
        def _(dve):
            steps = [0]

            def link(ins):
                steps[0] += 1
                ins.then_inc(dve_step, 1)
                dve.wait_ge(dve_step, steps[0])

            re, im = r.par[:, 0:1], r.par[:, 1:2]
            dve.wait_ge(act_step, 1)
            link(dve.tensor_tensor(v["angle"], im, v["step"], ALU.mult))
            link(dve.tensor_scalar(v["turns"], v["angle"], 1.0 / TWO_PI, ROUND, ALU.mult, ALU.add))
            link(dve.tensor_scalar(v["turns"], v["turns"], ROUND, None, ALU.subtract))
            link(dve.scalar_tensor_tensor(v["r"], v["turns"], -TWO_PI_HI, v["angle"], ALU.mult, ALU.add))
            link(dve.scalar_tensor_tensor(v["r"], v["turns"], -(TWO_PI - TWO_PI_HI), v["r"], ALU.mult, ALU.add))
            link(dve.tensor_scalar(v["r"], v["r"], PI_BELOW, -PI_BELOW, ALU.min, ALU.max))
            link(dve.tensor_scalar(v["half"], v["r"], 0.5, None, ALU.mult))
            link(dve.tensor_tensor(v["t1"], re, re, ALU.mult))
            link(dve.scalar_tensor_tensor(v["den"], im, im, v["t1"], ALU.mult, ALU.add))
            link(dve.reciprocal(v["den"], v["den"]))
            dve.wait_ge(act_step, 4)
            link(dve.tensor_copy(power[:, 1, 0:1], v["sr"]))
            link(dve.tensor_tensor(v["t1"], v["sh"], v["sh"], ALU.mult))
            link(dve.tensor_scalar(power[:, 0, 0:1], v["t1"], -2.0, 1.0, ALU.mult, ALU.add))
            link(dve.tensor_scalar(v["a"], power[:, 0, 0:1], r.fade[:, 0:1], 1.0, ALU.mult, ALU.subtract))
            link(dve.tensor_tensor(v["b"], power[:, 1, 0:1], r.fade[:, 0:1], ALU.mult))
            link(dve.tensor_tensor(v["t1"], v["a"], re, ALU.mult))
            link(dve.scalar_tensor_tensor(v["gr"], v["b"], im, v["t1"], ALU.mult, ALU.add))
            link(dve.tensor_tensor(v["gr"], v["gr"], v["den"], ALU.mult))
            link(dve.tensor_tensor(v["t2"], v["a"], im, ALU.mult))
            link(dve.scalar_tensor_tensor(v["gi"], v["b"], re, v["t2"], ALU.mult, ALU.subtract))
            link(dve.tensor_tensor(v["gi"], v["gi"], v["den"], ALU.mult))
            gr, gi = small[0:ST, names.index("gr"):names.index("gr") + 1], small[0:ST, names.index("gi"):names.index("gi") + 1]
            link(dve.tensor_scalar(tb[:, 0, :], r.B[:, :, 1], gi, None, ALU.mult))
            link(dve.tensor_scalar(tb[:, 1, :], r.B[:, :, 0], gi, None, ALU.mult))
            link(dve.scalar_tensor_tensor(bbar[:, 0, :], r.B[:, :, 0], gr, tb[:, 0, :], ALU.mult, ALU.subtract))
            link(dve.scalar_tensor_tensor(bbar[:, 1, :], r.B[:, :, 1], gr, tb[:, 1, :], ALU.mult, ALU.add))
            dve.memset(r.cos[:, 0:1], 1.0).then_inc(outs, 1)
            link(dve.memset(r.sin[:, 0:1], 0.0))
            for i in range(10):
                n = 1 << i
                pc, ps = power[:, 0, i:i + 1], power[:, 1, i:i + 1]
                c0, s0, c1, s1 = r.cos[:, 0:n], r.sin[:, 0:n], r.cos[:, n:2 * n], r.sin[:, n:2 * n]
                dve.tensor_scalar(tmp[:, 0, 0:n], s0, ps, None, ALU.mult)
                dve.tensor_scalar(tmp[:, 1, 0:n], c0, ps, None, ALU.mult)
                link(dve.tensor_tensor(v["t1"], ps, ps, ALU.mult))
                dve.scalar_tensor_tensor(c1, c0, pc, tmp[:, 0, 0:n], ALU.mult, ALU.subtract)
                dve.scalar_tensor_tensor(s1, s0, pc, tmp[:, 1, 0:n], ALU.mult, ALU.add)
                dve.scalar_tensor_tensor(power[:, 0, i + 1:i + 2], pc, pc, v["t1"], ALU.mult, ALU.subtract)
                link(dve.scalar_tensor_tensor(power[:, 1, i + 1:i + 2], pc, 2.0, ps, ALU.mult, ALU.mult))


def ssm_run(nc, m, r):
    JOBS = N // BANK
    with ExitStack() as ctx:
        def sb(name, shape, dt=F32):
            return ctx.enter_context(nc.sbuf_tensor(f"l3r_{name}", shape, dt))

        sem = signals(nc, m, "l3r_")

        z1, z2, z = sb("z1", [P, 2, BANK]), sb("z2", [P, 2, BANK]), sb("z", [P, 2, BANK])
        y, u, v = sb("y", [P, JOBS, BANK]), sb("u", [P, 2, BANK]), sb("v", [P, 2, BANK])
        ps_1 = ctx.enter_context(nc.psum_tensor("l3r_ps_1", [P, 2, BANK], F32))
        ps_2 = ctx.enter_context(nc.psum_tensor("l3r_ps_2", [P, 2, BANK], F32))
        ps_o = ctx.enter_context(nc.psum_tensor("l3r_ps_o", [P, 2, BANK], F32))
        bu_ready, bu_used, z_ready, y_ready, u_ready, v_ready, out_ready, out_used = (
            sem(k) for k in ("bu_ready", "bu_used", "z_ready", "y_ready", "u_ready", "v_ready", "out_ready", "out_used"))
        block = ctx.enter_context(nc.Block())

        @block.tensor
        def _(pe):
            def drive(j):
                if j >= 2:
                    pe.wait_ge(bu_used, j - 1)
                pe.matmul(ps_1[:, j % 2, :], r.w1[:, :], m.xnT[:, j * BANK:(j + 1) * BANK], start=True, stop=True)
                pe.matmul(ps_2[:, j % 2, :], r.w2[:, :], m.xnT[:, j * BANK:(j + 1) * BANK], start=True, stop=True).then_inc(bu_ready, 1)

            drive(0)
            for j in range(JOBS):
                if j + 1 < JOBS:
                    drive(j + 1)
                pe.wait_ge(u_ready, j + 1)
                pe.wait_ge(v_ready, j + 1)
                if j >= 2:
                    pe.wait_ge(out_used, j - 1)
                for t in range(4):
                    c = slice(t * P, (t + 1) * P)
                    pe.matmul(ps_o[:, j % 2, c], u[:, j % 2, c], r.v1[:, :], start=True, stop=False)
                    pe.matmul(ps_o[:, j % 2, c], v[:, j % 2, c], r.v2[:, :], start=False, stop=False)
                    ins = pe.matmul(ps_o[:, j % 2, c], m.xnT[:, j * BANK + t * P:j * BANK + (t + 1) * P], r.dd[:, :], start=False, stop=True)
                ins.then_inc(out_ready, 1)

        @block.vector
        def _(dve):
            def add(j):
                dve.wait_ge(out_ready, j + 1)
                hh = m.h[:, 4 * j:4 * j + 4, :]
                dve.tensor_tensor(hh, hh, ps_o[:, j % 2, :].rearrange("p (t d) -> p t d", t=4), ALU.add).then_inc(out_used, 1)

            for j in range(JOBS):
                k, c = j % 2, slice((j % 2) * BANK, (j % 2 + 1) * BANK)
                dve.wait_ge(bu_ready, j + 1)
                dve.tensor_tensor(z1[:, k, :], ps_1[:, k, :], r.cos[:, c], ALU.mult)
                dve.tensor_tensor(z2[:, k, :], ps_2[:, k, :], r.sin[:, c], ALU.mult).then_inc(bu_used, 1)
                dve.wait_ge(bu_used, j + 1)
                dve.tensor_tensor(z[:, k, :], z1[:, k, :], z2[:, k, :], ALU.add).then_inc(z_ready, 1)
                dve.wait_ge(z_ready, j + 1)
                start = 0.0 if k == 0 else y[:, j - 1, BANK - 1:BANK]
                dve.tensor_tensor_scan(y[:, j, :], r.fade[:, 0:1].broadcast_to([P, BANK]), z[:, k, :], start, ALU.mult, ALU.add)\
                   .then_inc(y_ready, 1)
                dve.wait_ge(y_ready, j + 1)
                if j >= 2:
                    dve.wait_ge(out_ready, j - 1)
                dve.tensor_tensor(u[:, k, :], y[:, j, :], r.cos[:, c], ALU.mult).then_inc(u_ready, 1)
                if j >= 1:
                    add(j - 1)
            add(JOBS - 1)

        @block.gpsimd
        def _(pool):
            for j in range(JOBS):
                k, c = j % 2, slice((j % 2) * BANK, (j % 2 + 1) * BANK)
                pool.wait_ge(y_ready, j + 1)
                if j >= 2:
                    pool.wait_ge(out_ready, j - 1)
                pool.tensor_tensor(v[:, k, :], y[:, j, :], r.sin[:, c], ALU.mult).then_inc(v_ready, 1)


L3_E, L3_I = 16, 96


def stage_l3_ffn(nc, m, w):
    G = L3_E + 1
    with ExitStack() as ctx:
        def sb(name, shape, dt=F32):
            return ctx.enter_context(nc.sbuf_tensor(f"l3f_{name}", shape, dt))

        r = Core()
        r.hT, r.gates = m.xnT, sb("gates", [P, TILES, G])
        r.gate_w, r.b_r = sb("gate_w", [P, L3_E]), sb("b_r", [1, L3_E])
        r.raw_act, r.raw_b1 = sb("raw_act", [P, G, 5]), sb("raw_b1", [G, 2 * L3_I])
        r.g_low, r.g_high, r.g_bias, r.u_bias, r.ag_bias = (sb(x, [L3_I, G]) for x in ("g_low", "g_high", "g_bias", "u_bias", "ag_bias"))
        r.clamp, r.u_limit = sb("clamp", [P, G, 2]), sb("u_limit", [P, G, 2])
        r.b2_dram, r.b2_shared = w["L3_ffn_expert_b2"], row(w["L3_ffn_shared_b2"])
        sem = signals(nc, m, "l3f_")
        r.s_router, r.n_router = sem("router"), 32
        r.s_par, r.n_par = sem("par"), 64
        with nc.Block() as block:
            @block.sync
            def _(sp):
                sp.dma_start(r.gate_w[:, :], w["L3_ffn_gate_w"]).then_inc(r.s_router, 16)
                sp.dma_start(r.b_r[:, :], row(w["L3_ffn_gate_b"])).then_inc(r.s_router, 16)
                sp.dma_start(r.raw_act[:, 0:L3_E, :], w["L3_ffn_expert_act"].rearrange("(o e) a -> o e a", o=1)
                             .broadcast_to([P, L3_E, 5])).then_inc(r.s_par, 16)
                sp.dma_start(r.raw_act[:, L3_E, :], row(w["L3_ffn_shared_act"]).broadcast_to([P, 5])).then_inc(r.s_par, 16)
                sp.dma_start(r.raw_b1[0:L3_E, :], w["L3_ffn_expert_b1"]).then_inc(r.s_par, 16)
                sp.dma_start(r.raw_b1[L3_E:G, :], row(w["L3_ffn_shared_b1"])).then_inc(r.s_par, 16)
        layernorm(nc, m, "ln_l3f", m.h, m.xn, m.xnT)
        router(nc, m, r, "l3r", L3_E, r.gate_w[:, :], m.lower16, 1)
        l3_expert_scalars(nc, m, r)
        l3_experts(nc, m, r, w)


def l3_expert_scalars(nc, m, r):
    G = L3_E + 1
    with ExitStack() as ctx:
        size, ex = (ctx.enter_context(nc.sbuf_tensor(f"l3s_{x}", [P, G, 2], F32)) for x in ("size", "ex"))
        ps = ctx.enter_context(nc.psum_tensor("l3s_ps", [P, BANK], F32))
        sem = signals(nc, m, "l3s_")
        turned, dve_step, act_step = (sem(x) for x in ("turned", "dve_step", "act_step"))
        block = ctx.enter_context(nc.Block())

        @block.tensor
        def _(pe):
            pe.wait_ge(r.s_par, r.n_par)
            pairs = r.raw_b1[:, :].rearrange("e (i two) -> e i two", two=2)
            for k in range(2):
                ins = pe.transpose(ps[0:L3_I, k * G:(k + 1) * G], pairs[:, :, k], m.ident[0:G, 0:G])
            ins.then_inc(turned, 1)

        @block.scalar
        def _(act):
            act.wait_ge(dve_step, 1)
            act.activation(ex[:, :, :], size[:, :, :], ACT.Exp, scale=-1.0).then_inc(act_step, 1)
            act.wait_ge(dve_step, 2)
            act.activation(ex[:, :, :], ex[:, :, :], ACT.Ln).then_inc(act_step, 1)

        @block.vector
        def _(dve):
            steps = [0]

            def link(ins):
                steps[0] += 1
                ins.then_inc(dve_step, 1)
                dve.wait_ge(dve_step, steps[0])

            raw = r.raw_act[:, :, 3:5]
            dve.wait_ge(r.s_par, r.n_par)
            link(dve.scalar_tensor_tensor(size[:, :, :], raw, -1.0, raw, ALU.mult, ALU.max))
            dve.wait_ge(act_step, 1)
            link(dve.tensor_scalar(ex[:, :, :], ex[:, :, :], 1.0, None, ALU.add))
            dve.wait_ge(act_step, 2)
            link(dve.scalar_tensor_tensor(r.clamp[:, :, :], raw, 0.0, ex[:, :, :], ALU.max, ALU.add))
            dve.wait_ge(turned, 1)
            link(dve.tensor_copy(r.g_bias[:, :], ps[0:L3_I, 0:G]))
            link(dve.tensor_copy(r.u_bias[:, :], ps[0:L3_I, G:2 * G]))
            dve.tensor_tensor(r.g_high[:, :], r.clamp[0:L3_I, :, 0], r.g_bias[:, :], ALU.subtract)
            dve.scalar_tensor_tensor(r.g_low[:, :], r.clamp[0:L3_I, :, 0], -1.0, r.g_bias[:, :], ALU.mult, ALU.subtract)
            dve.tensor_tensor(r.ag_bias[:, :], r.g_bias[:, :], r.raw_act[0:L3_I, :, 0], ALU.mult)
            dve.tensor_copy(r.u_limit[:, :, 0], r.clamp[:, :, 1])
            dve.tensor_scalar(r.u_limit[:, :, 1], r.clamp[:, :, 1], -1.0, None, ALU.mult)
            dve.tensor_tensor(r.gates[:, :, :], r.gates[:, :, :], r.raw_act[:, :, 1].unsqueeze(1).broadcast_to([P, TILES, G]), ALU.mult)


def l3_experts(nc, m, r, w):
    G, GROUPS = L3_E + 1, 4
    UNITS = 2 * GROUPS
    LOOPS = L3_E // 2
    with ExitStack() as ctx:
        def sb(name, shape, dt=F32):
            return ctx.enter_context(nc.sbuf_tensor(f"l3e_{name}", shape, dt))

        sem = signals(nc, m, "l3e_")

        w1, w2 = sb("w1", [P, 2, 2 * L3_I]), sb("w2", [L3_I, 2, D])
        gate, sig, up_, te = (sb(x, [L3_I, GROUPS, BANK]) for x in ("gate", "sig", "up", "te"))
        limit = sb("limit", [P, 2, 2])
        prime = sb("prime", [P, 1])
        ps_g = ctx.enter_context(nc.psum_tensor("l3e_ps_g", [P, 2, BANK], F32))
        ps_u = ctx.enter_context(nc.psum_tensor("l3e_ps_u", [P, 2, BANK], F32))
        ps_d = ctx.enter_context(nc.psum_tensor("l3e_ps_d", [P, 2, BANK], F32))
        w1_in, w2_in = [sem("w1_in0"), sem("w1_in1")], [sem("w2_in0"), sem("w2_in1")]
        limit_in = sem("limit_in")
        g_ready, u_ready, g_clipped, u_out, u_clipped, sig_ready, t1_ready, te_ready, down_ready, down_free = (
            sem(k) for k in ("g_ready", "u_ready", "g_clipped", "u_out", "u_clipped", "sig_ready", "t1_ready", "te_ready",
                             "down_ready", "down_free"))
        block = ctx.enter_context(nc.Block())

        @block.sync
        def _(sp):
            def load(k, w1_src, w2_src, units):
                sp.wait_ge(u_ready, FROM + units)
                sp.dma_start(w1[:, k, :], w1_src).then_inc(w1_in[k], 16)
                sp.wait_ge(down_ready, FROM + units)
                sp.dma_start(w2[:, k, :], w2_src).then_inc(w2_in[k], 16)

            def expert(e):
                return (w["L3_ffn_expert_w1"][bass.ds(e, 1), :, :].rearrange("e p f -> p (e f)"),
                        w["L3_ffn_expert_w2"][bass.ds(e, 1), :, :].rearrange("e p f -> p (e f)"))

            load(0, *expert(0), 0)
            with sp.Fori(0, LOOPS - 1) as it:
                load(1, *expert(it * 2 + 1), it * UNITS)
                load(0, *expert(it * 2 + 2), it * UNITS + GROUPS)
            load(1, *expert(L3_E - 1), (LOOPS - 1) * UNITS)
            load(0, w["L3_ffn_shared_w1"], w["L3_ffn_shared_w2"], (LOOPS - 1) * UNITS + GROUPS)

        @block.tensor
        def _(pe):
            def up(it, u):
                k, g, n = (u // GROUPS) % 2, u % GROUPS, it * UNITS + u
                if g == 0:
                    pe.wait_ge(w1_in[k], (it + u // UNITS) * 16 + 16)
                if not (isinstance(n, int) and n < 2):
                    pe.wait_ge(g_clipped, n - 1)
                pe.matmul(ps_g[0:L3_I, u % 2, :], w1[:, k, 0::2], r.hT[:, g * BANK:(g + 1) * BANK], start=True, stop=True).then_inc(g_ready, 1)
                if not (isinstance(n, int) and n < 2):
                    pe.wait_ge(u_out, n - 1)
                pe.matmul(ps_u[0:L3_I, u % 2, :], w1[:, k, 1::2], r.hT[:, g * BANK:(g + 1) * BANK], start=True, stop=True).then_inc(u_ready, 1)

            def down(it, u):
                k, g, n = (u // GROUPS) % 2, u % GROUPS, it * UNITS + u
                if g == 0:
                    pe.wait_ge(w2_in[k], it * 16 + 16)
                pe.wait_ge(te_ready, n + 1)
                pe.wait_ge(down_free, n + 1)
                for t in range(4):
                    ins = pe.matmul(ps_d[:, u % 2, t * P:(t + 1) * P], te[:, g, t * P:(t + 1) * P], w2[:, k, :], start=True, stop=True)
                ins.then_inc(down_ready, 1)

            for signal in (u_ready, down_ready):
                pe.sem_inc(signal, FROM)
            for u in range(3):
                up(0, u)
            with pe.Fori(0, LOOPS) as it:
                for u in range(UNITS):
                    up(it, u + 3)
                    down(it, u)
            up(LOOPS, 3)
            for u in range(GROUPS):
                down(LOOPS, u)

        @block.scalar
        def _(act):
            def unit(it, u):
                g, n, e = u % GROUPS, it * UNITS + u, it * 2 + u // GROUPS
                act.wait_ge(u_ready, FROM + n + 1)
                act.nop(nofuse=True)
                if g == 0:
                    act.activation(limit[:, (u // GROUPS) % 2, :], r.u_limit[:, bass.ds(e, 1), :].rearrange("p a k -> p (a k)"),
                                   ACT.Copy).then_inc(limit_in, 1)
                act.activation(up_[:, g, :], ps_u[0:L3_I, u % 2, :], ACT.Identity, bias=r.u_bias[:, bass.ds(e, 1)]).then_inc(u_out, 1)
                act.wait_ge(g_clipped, n + 1)
                act.nop(nofuse=True)
                act.activation(sig[:, g, :], gate[:, g, :], ACT.Sigmoid, bias=r.ag_bias[:, bass.ds(e, 1)],
                               scale=r.raw_act[0:L3_I, bass.ds(e, 1), 0]).then_inc(sig_ready, 1)

            act.activation(prime[:, :], m.pid, ACT.Sigmoid)
            with act.Fori(0, LOOPS) as it:
                for u in range(UNITS):
                    unit(it, u)
            for u in range(GROUPS):
                unit(LOOPS, u)

        @block.gpsimd
        def _(pool):
            def unit(it, u):
                g, n, e = u % GROUPS, it * UNITS + u, it * 2 + u // GROUPS
                k = (u // GROUPS) % 2
                pool.wait_ge(limit_in, e + 1)
                pool.wait_ge(u_out, n + 1)
                pool.nop(nofuse=True)
                pool.tensor_scalar(up_[:, g, :], up_[:, g, :], limit[0:L3_I, k, 0:1], limit[0:L3_I, k, 1:2],
                                   ALU.min, ALU.max).then_inc(u_clipped, 1)

            with pool.Fori(0, LOOPS) as it:
                for u in range(UNITS):
                    unit(it, u)
            for u in range(GROUPS):
                unit(LOOPS, u)

        @block.vector
        def _(dve):
            def clip(it, u):
                g, n, e = u % GROUPS, it * UNITS + u, it * 2 + u // GROUPS
                dve.wait_ge(g_ready, n + 1)
                dve.tensor_scalar(gate[:, g, :], ps_g[0:L3_I, u % 2, :], r.g_high[:, bass.ds(e, 1)], r.g_low[:, bass.ds(e, 1)],
                                  ALU.min, ALU.max).then_inc(g_clipped, 1)

            def hidden(it, u):
                g, n, e = u % GROUPS, it * UNITS + u, it * 2 + u // GROUPS
                dve.wait_ge(sig_ready, n + 1)
                dve.scalar_tensor_tensor(sig[:, g, :], gate[:, g, :], r.g_bias[:, bass.ds(e, 1)], sig[:, g, :], ALU.add, ALU.mult)\
                   .then_inc(t1_ready, 1)
                dve.wait_ge(u_clipped, n + 1)
                dve.wait_ge(t1_ready, n + 1)
                dve.scalar_tensor_tensor(te[:, g, :], up_[:, g, :], r.raw_act[0:L3_I, bass.ds(e, 1), 2], sig[:, g, :],
                                         ALU.add, ALU.mult).then_inc(te_ready, 1)

            def add(it, u):
                g, n, e = u % GROUPS, it * UNITS + u, it * 2 + u // GROUPS
                dve.wait_ge(down_free, n + 1)
                dve.wait_ge(down_ready, FROM + n + 1)
                for t in range(4):
                    hh = m.h[:, 4 * g + t, :]
                    ins = dve.scalar_tensor_tensor(hh, ps_d[:, u % 2, t * P:(t + 1) * P], r.gates[:, 4 * g + t, bass.ds(e, 1)], hh,
                                                   ALU.mult, ALU.add)
                ins.then_inc(down_free, 1)

            dve.sem_inc(down_free, 2)
            clip(0, 0)
            clip(0, 1)
            hidden(0, 0)
            clip(0, 2)
            hidden(0, 1)
            with dve.Fori(0, LOOPS) as it:
                for u in range(UNITS):
                    clip(it, u + 3)
                    hidden(it, u + 2)
                    add(it, u)
            clip(LOOPS, 3)
            for u in range(GROUPS):
                if u + 2 < GROUPS:
                    hidden(LOOPS, u + 2)
                add(LOOPS, u)


def tower_memory(nc, m, ctx):
    def sb(name, shape, dt=F32):
        return ctx.enter_context(nc.sbuf_tensor(name, shape, dt))

    m.consts = sb("consts", [P, sum(CONST_COLS.values())])
    at, part = 0, {}
    for name, width in CONST_COLS.items():
        part[name] = m.consts[:, at:at + width]
        at += width
    m.ident, m.interp, m.pairmean, m.one, m.sel8 = (part[x] for x in ("ident", "interp", "pairmean", "one", "sel8"))
    m.ropecos, m.ropesin, m.expand, m.pid = (part[x] for x in ("ropecos", "ropesin", "expand", "pid"))
    m.quarter, m.lower8, m.lower16 = part["quarter"], part["lower8"], part["lower16"]
    m.h, m.xn, m.xnT = sb("h", [P, TILES, D]), sb("xn", [P, TILES, D]), sb("xnT", [P, N])
    m.neghalf = sb("neghalf", [P, TILES])
    m.wqkv0, m.fc1T, m.fc2T = sb("wqkv0", [P, 3, D]), sb("fc1T", [P, 4, D]), sb("fc2T", [P, 4, 64])
    m.w1f, m.fc1_b, m.fc2_b = sb("w1f", [P, 512]), sb("fc1_b", [P, 4]), sb("fc2_b", [1, 64])
    m.wqkv2, m.wproj2, m.wqkv3, m.wo = sb("wqkv2", [P, 3, D]), sb("wproj2", [P, D]), sb("wqkv3", [P, 3, D]), sb("wo", [P, D])
    m.wrT = sb("wrT", [P, 8])
    m.w_attn, m.w_proj1 = sb("w_attn", [P, 3 * HD + RET_H]), sb("w_proj1", [P, 4, D])
    m.s_wattn = ctx.enter_context(nc.semaphore("s_wattn"))
    m.s_wproj1 = ctx.enter_context(nc.semaphore("s_wproj1"))


def l0_memory(nc, m, ctx):
    def sb(name, shape, dt=F32):
        return ctx.enter_context(nc.sbuf_tensor(name, shape, dt))

    m.ids, m.onehot, m.pairhot = sb("ids", [P, N], I32), sb("onehot", [VOC, N]), sb("pairhot", [VOC, N // 2])
    m.feat, m.tok_w1, m.tok_w2 = sb("feat", [VOC, 37]), sb("tok_w1", [37, 64]), sb("tok_w2", [64, D])
    m.tok_b1, m.tok_b2 = sb("tok_b1", [64, 1]), sb("tok_b2", [1, D])
    m.bq, m.bk, m.bv = sb("bq", [P, 1]), sb("bk", [P, 1]), sb("bv", [1, D])
    m.table_x, m.table_tx = sb("table_x", [VOC, B, D]), sb("table_tx", [VOC, B, D])


def stage_l0(nc, m, w):
    stage_l0_tables(nc, m, w)
    stage_l0_ffn(nc, m, w)


def tower(nc, w, out, l0=stage_l0, stages=(stage_l1_attn, stage_l1_ffn, recycle, stage_l2_attn, stage_l2_ffn, recycle,
                                           stage_l3_attn, stage_l3_ffn)):
    with ExitStack() as ctx:
        m = Core()
        m.signals = []
        tower_memory(nc, m, ctx)
        m.later_loads = [
            (m.w_attn[:, :], w["L1_attn_w_attn"], m.s_wattn),
            (m.w_proj1[:, :, :], w["L1_attn_w_proj"].rearrange("(c p) d -> p c d", p=P), m.s_wproj1),
        ]
        with ExitStack() as l0_ctx:
            l0_memory(nc, m, l0_ctx)
            with nc.Block() as block:
                @block.gpsimd
                def _(pool):
                    pool.memset(m.neghalf[:, :], -0.5)
            load_stage(nc, m, w)
            l0(nc, m, w)
        for stage in stages:
            stage(nc, m, w)
        with nc.semaphore("stored") as stored, nc.Block() as block:
            @block.sync
            def _(sp):
                sp.dma_start(out.rearrange("b (t p) d -> p (b t) d", p=P), m.h[:, :, :]).then_inc(stored, 16)
                sp.wait_ge(stored, 16)


def kernel(**inputs):
    import concourse.bacc as _bacc
    from concourse.bass_utils import run_bass_kernel_spmd as _run

    nc = _bacc.Bacc("TRN2", target_bir_lowering=False, num_devices=1)
    arrays, w = {}, {}
    for name, value in list(inputs.items()) + [("consts", constants()), ("move", move_heads())]:
        a = np.ascontiguousarray(value)
        arrays[f"in_{name}_dram"] = a
        w[name] = nc.dram_tensor(f"in_{name}_dram", a.shape, mybir.dt.from_np(a.dtype), kind="ExternalInput").ap()
    out = nc.dram_tensor("out_0_dram", (B, S, D), F32, kind="ExternalOutput").ap()
    tower(nc, w, out)
    r = _run(nc, [arrays], core_ids=[0])
    return r.results[0]["out_0_dram"]
```

```python
from contextlib import ExitStack

import numpy as np

import concourse.bass as bass
from concourse import mybir

F32 = mybir.dt.float32
I32 = mybir.dt.int32
ACT = mybir.ActivationFunctionType
ALU = mybir.AluOpType
AX = mybir.AxisListType

P = 128
D = 128
B = 2
S = 1024
N = B * S
TILES = N // P
CH = S // P
BF16 = mybir.dt.bfloat16
VOC = 121
EPS = 1e-5
BANK = 512
BIG = 1.0e30
FROM = 1


def signals(nc, m, prefix):
    def sem(name):
        m.signals.append(nc.alloc_semaphore(prefix + name))
        return m.signals[-1]

    return sem


def recycle(nc, m, w):
    nc.clear_and_free_semaphores(m.signals)
    m.signals = []
    nc.all_engine_barrier()


class Core:
    pass


def row(ap1d):
    return ap1d.rearrange("(a d) -> a d", a=1)


def col(ap1d):
    return ap1d.rearrange("(d a) -> d a", a=1)


RET_H, RET_D = 8, 64
CONST_COLS = {"ident": 128, "interp": 128, "pairmean": 128, "one": 128, "pid": 1, "quarter": 4, "order": 16,
              "expand": 256, "ropecos": S, "ropesin": S}
FIRST_CONSTS = sum(CONST_COLS.values()) - 2 * S


def constants():
    out = {}
    out["ident"] = np.eye(P, dtype=np.float32)
    half, pos = D // 2, np.linspace(0.0, 1.0, D, dtype=np.float32) * np.float32(D // 2 - 1)
    i0 = np.clip(np.floor(pos).astype(np.int32), 0, half - 2)
    w = pos - i0.astype(np.float32)
    up = np.zeros((D, half), np.float32)
    up[np.arange(D), i0] += 1.0 - w
    up[np.arange(D), i0 + 1] += w
    out["interp"] = np.repeat(up, 2, axis=1) * np.float32(0.5)
    pair = np.arange(D) // 2
    out["pairmean"] = np.where(pair[:, None] == pair[None, :], np.float32(-0.25), np.float32(0)).astype(np.float32)
    out["one"] = np.ones((P, P), np.float32)
    div = np.float32(2.0 * np.pi) / np.power(np.float32(S), np.arange(0, RET_D, 2, dtype=np.float32) / np.float32(RET_D))
    ang = np.arange(S, dtype=np.float32)[:, None] * div[None, :].astype(np.float32)
    freq = (np.arange(P) % RET_D) // 2
    out["ropecos"] = np.cos(ang).T[freq].astype(np.float32)
    out["ropesin"] = np.sin(ang).T[freq].astype(np.float32)
    tok = np.arange(2 * P).reshape(1, 2, P)
    out["expand"] = (np.arange(P).reshape(P, 1, 1) == tok // 2).astype(np.float32).reshape(P, 256)
    out["pid"] = np.arange(P, dtype=np.float32)[:, None]
    out["quarter"] = (np.arange(P)[:, None] // 32 == np.arange(4)[None, :]).astype(np.float32)
    out["order"] = np.broadcast_to(np.arange(16, 0, -1, dtype=np.float32), (P, 16))
    return np.ascontiguousarray(np.concatenate([out[k] for k in CONST_COLS], axis=1), dtype=np.float32)


def layernorm(nc, m, name, src, dst, dstT, gain=None, shift=None):
    with ExitStack() as ctx:
        stats = ctx.enter_context(nc.sbuf_tensor(f"{name}_stats", [P, TILES, 6], F32))
        small = ctx.enter_context(nc.sbuf_tensor(f"{name}_small", [P, 8, TILES], F32))
        ps = ctx.enter_context(nc.psum_tensor(f"{name}_ps", [P, 4, BANK], F32))
        sem = signals(nc, m, f"{name}_")
        chain, var_ready, rstd_ready, normed, turned = (sem(x) for x in ("chain", "var_ready", "rstd_ready", "normed", "turned"))
        mean, rstd = small[:, 0, :], small[:, 1, :]
        HALF = TILES // 2
        halves = [slice(k * HALF, (k + 1) * HALF) for k in range(2)]
        block = ctx.enter_context(nc.Block())

        @block.vector
        def _(dve):
            for k, of in enumerate(halves):
                for t in range(k * HALF, (k + 1) * HALF):
                    ins = dve.bn_stats(stats[:, t, :], src[:, t, :])
                ins.then_inc(chain, 1)
                dve.wait_ge(chain, 3 * k + 1)
                diff, sumsq, var = small[:, 2, of], small[:, 3, of], small[:, 4, of]
                dve.tensor_tensor(diff, stats[:, of, 1], stats[:, of, 4], ALU.subtract)
                dve.tensor_tensor(sumsq, stats[:, of, 2], stats[:, of, 5], ALU.add)
                dve.tensor_tensor(mean[:, of], stats[:, of, 1], stats[:, of, 4], ALU.add).then_inc(chain, 1)
                dve.wait_ge(chain, 3 * k + 2)
                dve.tensor_scalar(mean[:, of], mean[:, of], 0.5, None, ALU.mult)
                dve.tensor_scalar(sumsq, sumsq, 1.0 / D, EPS, ALU.mult, ALU.add)
                dve.scalar_tensor_tensor(diff, diff, 0.25, diff, ALU.mult, ALU.mult).then_inc(chain, 1)
                dve.wait_ge(chain, 3 * k + 3)
                dve.tensor_tensor(var, sumsq, diff, ALU.add).then_inc(var_ready, 1)
            for t in range(TILES):
                if t % HALF == 0:
                    dve.wait_ge(rstd_ready, t // HALF + 1)
                dve.tensor_scalar(dst[:, t, :], src[:, t, :], mean[:, t:t + 1], rstd[:, t:t + 1],
                                  ALU.subtract, ALU.mult).then_inc(normed, 1)

        @block.gpsimd
        def _(pool):
            for k, of in enumerate(halves):
                pool.wait_ge(var_ready, k + 1)
                pool.tensor_tensor(rstd[:, of], small[:, 4, of], m.neghalf[:, of], ALU.pow).then_inc(rstd_ready, 1)

        if dstT is None:
            return

        @block.tensor
        def _(pe):
            for t in range(TILES):
                pe.wait_ge(normed, t + 1)
                ins = pe.transpose(ps[:, t // 4, (t % 4) * P:(t % 4 + 1) * P], dst[:, t, :], m.ident)
                if t % 4 == 3:
                    ins.then_inc(turned, 1)

        @block.scalar
        def _(act):
            for g in range(TILES // 4):
                act.wait_ge(turned, g + 1)
                out = dstT[:, g * BANK:(g + 1) * BANK]
                if gain is None:
                    act.activation(out, ps[:, g, :], ACT.Copy)
                else:
                    act.activation(out, ps[:, g, :], ACT.Identity, bias=shift, scale=gain)


def load_stage(nc, m, w):
    with ExitStack() as ctx:
        def raw(name, shape, dt=F32):
            return ctx.enter_context(nc.sbuf_tensor(f"raw_{name}", shape, dt))

        sem = signals(nc, m, "")

        raw_qkv0 = raw("qkv0", [P, 3, D])
        raw_fc1 = raw("fc1", [P, 4, D])
        raw_fc2 = raw("fc2", [64, 512])
        raw_qkv2 = raw("qkv2", [P, 3, D])
        raw_proj2 = raw("proj2", [P, D])
        raw_qkvw = raw("qkvw", [P, 3, D])
        raw_wo = raw("wo", [P, D])
        raw_wr = raw("wr", [8, D])
        w_first, w_turn = sem("w_first"), sem("w_turn")
        turned, copied = sem("w_turned"), sem("w_copied")
        sp_loads = [
            (m.consts[:, 0:FIRST_CONSTS], w["consts"][:, 0:FIRST_CONSTS]),
            (m.ids[:, :], w["x"].rearrange("(o b) n -> o (b n)", o=1).broadcast_to([P, N])),
            (raw_qkv0[:, 0, :], w["L0_attn_Wq"]), (raw_qkv0[:, 1, :], w["L0_attn_Wk"]), (raw_qkv0[:, 2, :], w["L0_attn_Wv"]),
            (m.feat[:, :], w["L0_tok_feature_table"]), (m.tok_w1[:, :], w["L0_tok_W1"]), (m.tok_w2[:, :], w["L0_tok_W2"]),
            (m.tok_b1[:, :], col(w["L0_tok_b1"])), (m.tok_b2[:, :], row(w["L0_tok_b2"])),
            (m.bq[:, :], col(w["L0_attn_bq"])), (m.bk[:, :], col(w["L0_attn_bk"])), (m.bv[:, :], row(w["L0_attn_bv"])),
            (raw_fc1[:, :, :], w["L0_ffn_fc1_w"].rearrange("(c p) d -> p c d", p=P)),
            (raw_fc2[:, :], w["L0_ffn_fc2_w"]),
            (m.fc1_b[:, :], w["L0_ffn_fc1_b"].rearrange("(c p) -> p c", p=P)),
            (m.fc2_b[:, :], row(w["L0_ffn_fc2_b"])),
        ]
        act_loads = [
            (raw_qkv2[:, :, :], w["L2_attn_w_qkv"].rearrange("(c p) d -> p c d", p=P)),
            (raw_proj2[:, :], w["L2_attn_w_proj"]),
            (raw_qkvw[:, :, :], w["L2_ffn_qkv_w"].rearrange("(c p) d -> p c d", p=P)),
            (raw_wo[:, :], w["L2_ffn_wo_w"]),
            (raw_wr[:, :], w["L1_ffn_w_r"]),
        ]
        jobs = [(raw_qkv0[:, c, :], m.wqkv0[:, c, :]) for c in range(3)]
        jobs += [(raw_fc1[:, c, :], m.fc1T[:, c, :]) for c in range(4)]
        jobs += [(raw_fc2[:, c * P:(c + 1) * P], m.fc2T[:, c, :]) for c in range(4)]
        n_early = len(jobs)
        jobs += [(raw_qkv2[:, c, :], m.wqkv2[:, c, :]) for c in range(3)]
        jobs += [(raw_proj2[:, :], m.wproj2[:, :])]
        jobs += [(raw_qkvw[:, c, :], m.wqkv3[:, c, :]) for c in range(3)]
        jobs += [(raw_wo[:, :], m.wo[:, :])]
        jobs += [(raw_wr[:, :], m.wrT[:, :])]
        ssm_prepare(nc, m, m.ssm, w, sp_loads, act_loads, w_first, w_turn)
        ps = ctx.enter_context(nc.psum_tensor("turn_ps", [P, 8, BANK], F32))
        block = ctx.enter_context(nc.Block())

        @block.scalar
        def _(act):
            for i, (_, dst) in enumerate(jobs):
                act.wait_ge(turned, i + 1)
                r, c = dst.shape
                act.activation(dst, ps[0:r, i % 8, 0:c], ACT.Copy).then_inc(copied, 1)

        @block.tensor
        def _(pe):
            pe.wait_ge(w_first, 16 * len(sp_loads))
            for i, (src, dst) in enumerate(jobs):
                if i == n_early:
                    pe.wait_ge(w_turn, 16 * len(act_loads))
                if i >= 8:
                    pe.wait_ge(copied, i - 7)
                r, c = dst.shape
                pe.transpose(ps[0:r, i % 8, 0:c], src, m.ident[0:c, 0:c]).then_inc(turned, 1)


def stage_l0_tables(nc, m, w):
    with ExitStack() as ctx:
        def sb(name, shape, dt=F32):
            return ctx.enter_context(nc.sbuf_tensor(f"l0_{name}", shape, dt))

        sem = signals(nc, m, "l0_")

        featT, hid = sb("featT", [37, VOC]), sb("hid", [64, VOC])
        gelu, emb, emb_n = sb("gelu", [VOC, D]), sb("emb", [VOC, D]), sb("emb_n", [VOC, D])
        emb_nT = sb("emb_nT", [P, VOC])
        qT, kT, v = sb("qT", [P, VOC]), sb("kT", [P, VOC]), sb("v", [VOC, D + 1])
        vw = sb("vw", [VOC, B, D + 1])
        count, absent, diag = sb("count", [VOC, B]), sb("absent", [VOC, B]), sb("diag", [VOC, B, VOC])
        mx, nmx = sb("mx", [VOC, B]), sb("nmx", [VOC, B])
        prob, probT = sb("prob", [VOC, B, VOC]), sb("probT", [VOC, B, VOC])
        rden = sb("rden", [VOC, B])
        h1 = sb("h1", [VOC, B, D])
        stats, small = sb("stats", [VOC, 3, 6]), sb("small", [VOC, 3, 8])
        ps_a = ctx.enter_context(nc.psum_tensor("l0_ps_a", [P, BANK], F32))
        ps_e = ctx.enter_context(nc.psum_tensor("l0_ps_e", [P, BANK], F32))
        ps_q = ctx.enter_context(nc.psum_tensor("l0_ps_q", [P, BANK], F32))
        ps_k = ctx.enter_context(nc.psum_tensor("l0_ps_k", [P, BANK], F32))
        ps_v = ctx.enter_context(nc.psum_tensor("l0_ps_v", [P, BANK], F32))
        ps_s = ctx.enter_context(nc.psum_tensor("l0_ps_s", [P, BANK], F32))
        ps_f = ctx.enter_context(nc.psum_tensor("l0_ps_f", [P, BANK], F32))
        pe_step, act_step, dve_step, pool_step, special = (sem(x) for x in ("pe", "act", "dve", "pool", "special"))
        v_ones = sem("v_ones")
        SC = float(D) ** -0.5
        block = ctx.enter_context(nc.Block())

        @block.tensor
        def _(pe):
            pe.transpose(ps_a[0:37, 0:VOC], m.feat[:, :], m.ident[0:VOC, 0:VOC]).then_inc(pe_step, 1)
            pe.matmul(ps_f[:, :], m.interp, m.fc1T[:, :, :].rearrange("p c d -> p (c d)"), start=True, stop=True).then_inc(pe_step, 1)
            pe.wait_ge(act_step, 1)
            pe.matmul(ps_e[0:64, 0:VOC], m.tok_w1[:, :], featT[:, :], start=True, stop=True).then_inc(pe_step, 1)
            pe.wait_ge(act_step, 3)
            pe.matmul(ps_a[0:VOC, 0:D], hid[:, :], m.tok_w2[:, :], start=True, stop=False)
            pe.matmul(ps_a[0:VOC, 0:D], m.one[0:1, 0:VOC], m.tok_b2[:, :], start=False, stop=True).then_inc(pe_step, 1)
            pe.wait_ge(dve_step, 9)
            pe.transpose(ps_e[:, 0:VOC], emb_n[:, :], m.ident[0:VOC, 0:VOC]).then_inc(pe_step, 1)
            pe.wait_ge(act_step, 5)
            pe.matmul(ps_q[:, 0:VOC], m.wqkv0[:, 0, :], emb_nT[:, :], start=True, stop=True).then_inc(pe_step, 1)
            pe.matmul(ps_k[:, 0:VOC], m.wqkv0[:, 1, :], emb_nT[:, :], start=True, stop=True).then_inc(pe_step, 1)
            pe.matmul(ps_v[0:VOC, 0:D], emb_nT[:, :], m.wqkv0[:, 2, :], start=True, stop=False)
            pe.matmul(ps_v[0:VOC, 0:D], m.one[0:1, 0:VOC], m.bv[:, :], start=False, stop=True).then_inc(pe_step, 1)
            pe.wait_ge(act_step, 7)
            pe.wait_ge(dve_step, 12)
            for b in range(B):
                pe.matmul(ps_s[0:VOC, b * VOC:(b + 1) * VOC], qT[:, :], kT[:, :], start=True, stop=False)
                pe.matmul(ps_s[0:VOC, b * VOC:(b + 1) * VOC], m.one[0:VOC, 0:VOC], diag[:, b, :],
                          start=False, stop=True).then_inc(pe_step, 1)
            for b in range(B):
                pe.wait_ge(act_step, 8 + b)
                pe.transpose(ps_f[0:VOC, b * VOC:(b + 1) * VOC], prob[:, b, :], m.ident[0:VOC, 0:VOC]).then_inc(pe_step, 1)
            pe.wait_ge(act_step, 10)
            pe.wait_ge(dve_step, 16)
            for b in range(B):
                pe.matmul(ps_a[0:VOC, b * 256:b * 256 + D + 1], probT[:, b, :], vw[:, b, :], start=True, stop=True).then_inc(pe_step, 1)

        @block.scalar
        def _(act):
            act.wait_ge(pe_step, 1)
            act.activation(featT[:, :], ps_a[0:37, 0:VOC], ACT.Copy).then_inc(act_step, 1)
            act.wait_ge(pe_step, 2)
            act.activation(m.w1f[:, :], ps_f[:, :], ACT.Copy).then_inc(act_step, 1)
            act.wait_ge(pe_step, 3)
            act.activation(hid[:, :], ps_e[0:64, 0:VOC], ACT.Relu, bias=m.tok_b1[:, 0:1]).then_inc(act_step, 1)
            act.wait_ge(pe_step, 4)
            act.activation(gelu[:, :], ps_a[0:VOC, 0:D], ACT.Gelu_apprx_tanh).then_inc(act_step, 1)
            act.wait_ge(pe_step, 5)
            act.activation(emb_nT[:, :], ps_e[:, 0:VOC], ACT.Copy).then_inc(act_step, 1)
            act.wait_ge(pe_step, 6)
            act.activation(qT[:, :], ps_q[:, 0:VOC], ACT.Identity, bias=m.bq[:, 0:1]).then_inc(act_step, 1)
            act.wait_ge(pe_step, 7)
            act.activation(kT[:, :], ps_k[:, 0:VOC], ACT.Identity, bias=m.bk[:, 0:1]).then_inc(act_step, 1)
            act.wait_ge(dve_step, 14)
            for b in range(B):
                act.activation(prob[:, b, :], ps_s[0:VOC, b * VOC:(b + 1) * VOC], ACT.Exp, bias=nmx[:, b:b + 1],
                               scale=SC).then_inc(act_step, 1)
            act.wait_ge(pe_step, 12)
            act.activation(probT[:, :, :].rearrange("p b v -> p (b v)"), ps_f[0:VOC, 0:B * VOC], ACT.Copy).then_inc(act_step, 1)

        @block.sync
        def _(sp):
            sp.wait_ge(dve_step, 1)
            sp.dma_start(emb[0:1, :], w["L0_tok_special_embed"][0:1, :]).then_inc(special, 16)
            sp.dma_start(emb[107:110, :], w["L0_tok_special_embed"][1:4, :]).then_inc(special, 16)

        @block.gpsimd
        def _(pool):
            pool.tensor_scalar(m.onehot[:, :], m.ids[0:VOC, :], m.pid[0:VOC, :], None, ALU.is_equal).then_inc(pool_step, 1)
            pool.wait_ge(pool_step, 1)
            pairs = m.onehot[:, :].rearrange("p (n two) -> p n two", two=2)
            pool.tensor_tensor(m.pairhot[:, :], pairs[:, :, 0], pairs[:, :, 1], ALU.add).then_inc(pool_step, 1)
            pool.wait_ge(dve_step, 6)
            pool.tensor_scalar(small[:, 0, 4:5], small[:, 0, 4:5], EPS, None, ALU.add).then_inc(pool_step, 1)
            pool.wait_ge(pool_step, 3)
            pool.tensor_tensor(small[:, 0, 1:2], small[:, 0, 4:5], m.neghalf[0:VOC, 0:1], ALU.pow).then_inc(pool_step, 1)
            for b in range(B):
                pool.wait_ge(dve_step, 23 + 11 * b)
                pool.tensor_scalar(small[:, 1 + b, 4:5], small[:, 1 + b, 4:5], EPS, None, ALU.add).then_inc(pool_step, 1)
                pool.wait_ge(pool_step, 5 + 2 * b)
                pool.tensor_tensor(small[:, 1 + b, 1:2], small[:, 1 + b, 4:5], m.neghalf[0:VOC, 0:1], ALU.pow).then_inc(pool_step, 1)

        @block.vector
        def _(dve):
            steps = [0]

            def link(ins):
                steps[0] += 1
                ins.then_inc(dve_step, 1)
                dve.wait_ge(dve_step, steps[0])

            def moments(src, k):
                s = small[:, k, :]
                link(dve.bn_stats(stats[:, k, :], src))
                link(dve.tensor_tensor(s[:, 2:3], stats[:, k, 1:2], stats[:, k, 4:5], ALU.subtract))
                link(dve.tensor_tensor(s[:, 3:4], stats[:, k, 2:3], stats[:, k, 5:6], ALU.add))
                link(dve.scalar_tensor_tensor(s[:, 2:3], s[:, 2:3], 0.25, s[:, 2:3], ALU.mult, ALU.mult))
                link(dve.scalar_tensor_tensor(s[:, 4:5], s[:, 3:4], 1.0 / D, s[:, 2:3], ALU.mult, ALU.add))
                link(dve.tensor_tensor(s[:, 0:1], stats[:, k, 1:2], stats[:, k, 4:5], ALU.add))
                link(dve.tensor_scalar(s[:, 0:1], s[:, 0:1], 0.5, None, ALU.mult))

            dve.wait_ge(act_step, 4)
            link(dve.tensor_scalar(emb[:, :], gelu[:, :], float(D) ** 0.5, None, ALU.mult))
            dve.wait_ge(special, 32)
            moments(emb[:, :], 0)
            dve.wait_ge(pool_step, 4)
            link(dve.tensor_scalar(emb_n[:, :], emb[:, :], small[:, 0, 0:1], small[:, 0, 1:2], ALU.subtract, ALU.mult))
            dve.wait_ge(pool_step, 2)
            link(dve.tensor_reduce(count[:, :], m.onehot[:, :].rearrange("p (b n) -> p b n", b=B), AX.X, ALU.add))
            link(dve.tensor_scalar(absent[:, :], count[:, :], 0.0, -BIG, ALU.is_equal, ALU.mult))
            for b in range(B):
                ins = dve.tensor_scalar(diag[:, b, :], m.ident[0:VOC, 0:VOC], absent[:, b:b + 1], None, ALU.mult)
            link(ins)
            dve.wait_ge(pe_step, 10)
            link(dve.tensor_reduce(mx[:, :], ps_s[0:VOC, 0:B * VOC].rearrange("p (b v) -> p b v", b=B), AX.X, ALU.max))
            link(dve.tensor_scalar(nmx[:, :], mx[:, :], -SC, None, ALU.mult))
            dve.memset(v[:, D:D + 1], 1.0).then_inc(v_ones, 1)
            link(dve.tensor_copy(v[:, 0:D], ps_v[0:VOC, 0:D]))
            dve.wait_ge(v_ones, 1)
            for b in range(B):
                ins = dve.tensor_scalar(vw[:, b, :], v[:, :], count[:, b:b + 1], None, ALU.mult)
            link(ins)
            for b in range(B):
                att = ps_a[0:VOC, b * 256:b * 256 + D + 1]
                dve.wait_ge(pe_step, 14)
                link(dve.reciprocal(rden[:, b:b + 1], att[:, D:D + 1]))
                link(dve.scalar_tensor_tensor(h1[:, b, :], att[:, 0:D], rden[:, b:b + 1], emb[:, :], ALU.mult, ALU.add))
                moments(h1[:, b, :], 1 + b)
                dve.wait_ge(pool_step, 6 + 2 * b)
                link(dve.tensor_scalar(m.table_x[:, b, :], h1[:, b, :], small[:, 1 + b, 0:1], small[:, 1 + b, 1:2],
                                       ALU.subtract, ALU.mult))
                link(dve.tensor_tensor(m.table_tx[:, b, :], h1[:, b, :], m.table_x[:, b, :], ALU.add))


def stage_l0_ffn(nc, m, w):
    NP = N // 2
    with ExitStack() as ctx:
        def sb(name, shape, dt=F32):
            return ctx.enter_context(nc.sbuf_tensor(f"l0f_{name}", shape, dt))

        sem = signals(nc, m, "l0f_")

        sT, hid = sb("sT", [P, NP]), sb("hid", [P, 4, NP])
        change = sb("change", [P, NP // P, D])
        fc2_bd = sb("fc2_bd", [1, D])
        fc2_wd = sb("fc2_wd", [P, 4, D])
        ps_s = ctx.enter_context(nc.psum_tensor("l0f_ps_s", [P, 2, BANK], F32))
        ps_h = ctx.enter_context(nc.psum_tensor("l0f_ps_h", [P, 2, BANK], F32))
        ps_c = ctx.enter_context(nc.psum_tensor("l0f_ps_c", [P, 2, BANK], F32))
        ps_o = ctx.enter_context(nc.psum_tensor("l0f_ps_o", [P, 2, BANK], F32))
        pairs_summed, pairs_copied = sem("pairs_summed"), sem("pairs_copied")
        hid_ready, hid_done, out_ready, out_done, dup = (sem(x) for x in ("hid_ready", "hid_done", "out_ready", "out_done", "dup"))
        change_ready, change_done = sem("change_ready"), sem("change_done")
        block = ctx.enter_context(nc.Block())

        @block.tensor
        def _(pe):
            for b in range(B):
                pe.matmul(ps_s[:, b, :], m.table_x[:, b, :], m.pairhot[:, b * BANK:(b + 1) * BANK], start=True,
                          stop=True).then_inc(pairs_summed, 1)
            for i in range(8):
                b, c = i // 4, i % 4
                pe.wait_ge(pairs_copied, b + 1)
                if i >= 2:
                    pe.wait_ge(hid_done, i - 1)
                pe.matmul(ps_h[:, i % 2, :], m.w1f[:, c * P:(c + 1) * P], sT[:, b * BANK:(b + 1) * BANK], start=True,
                          stop=True).then_inc(hid_ready, 1)
            pe.wait_ge(dup, 2)
            pe.wait_ge(hid_done, 8)
            for j in range(NP // P):
                if j >= 2:
                    pe.wait_ge(change_done, j - 1)
                out = ps_c[:, j % 2, 0:D]
                pe.matmul(out, sT[:, j * P:(j + 1) * P], m.pairmean, start=True, stop=False)
                pe.matmul(out, m.one[0:1, :], fc2_bd[:, :], start=False, stop=False)
                for c in range(4):
                    ins = pe.matmul(out, hid[:, c, j * P:(j + 1) * P], fc2_wd[:, c, :], start=False, stop=(c == 3))
                ins.then_inc(change_ready, 1)
            for t in range(TILES):
                b, g, j = t // CH, t // 4, t // 2
                pe.wait_ge(change_done, j + 1)
                if t % 4 == 0 and g >= 2:
                    pe.wait_ge(out_done, g - 1)
                out = ps_o[:, g % 2, (t % 4) * P:(t % 4 + 1) * P]
                pe.matmul(out, m.onehot[:, t * P:(t + 1) * P], m.table_tx[:, b, :], start=True, stop=False)
                ins = pe.matmul(out, m.expand[:, (t % 2) * P:(t % 2 + 1) * P], change[:, j, :], start=False, stop=True)
                if t % 4 == 3:
                    ins.then_inc(out_ready, 1)

        @block.scalar
        def _(act):
            for b in range(B):
                act.wait_ge(pairs_summed, b + 1)
                act.activation(sT[:, b * BANK:(b + 1) * BANK], ps_s[:, b, :], ACT.Copy).then_inc(pairs_copied, 1)
            for i in range(8):
                b, c = i // 4, i % 4
                act.wait_ge(hid_ready, i + 1)
                act.activation(hid[:, c, b * BANK:(b + 1) * BANK], ps_h[:, i % 2, :], ACT.Gelu,
                               bias=m.fc1_b[:, c:c + 1]).then_inc(hid_done, 1)

        @block.vector
        def _(dve):
            wd = fc2_wd[:, :, :].rearrange("p c (d two) -> p (c d) two", two=2)
            dve.tensor_scalar(wd, m.fc2T[:, :, :].rearrange("p c d -> p (c d)").unsqueeze(2).broadcast_to([P, 256, 2]),
                              0.5, None, ALU.mult).then_inc(dup, 1)
            dve.tensor_scalar(fc2_bd[:, :].rearrange("p (d two) -> p d two", two=2),
                              m.fc2_b[:, :].unsqueeze(2).broadcast_to([1, 64, 2]), 0.5, None, ALU.mult).then_inc(dup, 1)
            for j in range(NP // P):
                dve.wait_ge(change_ready, j + 1)
                dve.tensor_copy(change[:, j, :], ps_c[:, j % 2, 0:D]).then_inc(change_done, 1)
            for g in range(TILES // 4):
                dve.wait_ge(out_ready, g + 1)
                dve.tensor_copy(m.h[:, 4 * g:4 * g + 4, :], ps_o[:, g % 2, :].rearrange("p (t d) -> p t d", t=4)).then_inc(out_done, 1)


GATE_BIAS = 6.906768
HD = RET_H * RET_D
WIDE_PER_HEAD = 9


def stage_l1_attn(nc, m, w):
    layernorm(nc, m, "ln_l1a", m.h, m.xn, m.xnT)
    with ExitStack() as ctx:
        def sb(name, shape, dt=F32):
            return ctx.enter_context(nc.sbuf_tensor(f"l1_{name}", shape, dt))

        r = Core()
        r.Lsplit = sb("Lsplit", [P, N], BF16)
        r.Lcol = sb("Lcol", [P, TILES, RET_H])
        r.Lfirst = sb("Lfirst", [P, TILES, RET_H])
        r.fade = sb("fade", [P, TILES, RET_H])
        r.keyfade = sb("keyfade", [P, B, CH, CH, RET_H])
        r.v = sb("v", [P, TILES, RET_H, RET_D + 1])
        r.pick = sb("pick", [P, RET_H, P], BF16)
        r.wswap = sb("wswap", [P, 2 * HD])
        l1_gates(nc, m, r)
        l1_heads(nc, m, r)


SPLIT = 3 * 32


def l1_gates(nc, m, r):
    with ExitStack() as ctx:
        def sb(name, shape, dt=F32):
            return ctx.enter_context(nc.sbuf_tensor(f"l1g_{name}", shape, dt))

        sem = signals(nc, m, "l1g_")

        x, u, w1, lw = (sb(k, [P, TILES * RET_H]) for k in ("x", "u", "w1", "lw"))
        spread = sb("spread", [P, TILES, SPLIT])
        LT, rest = sb("LT", [SPLIT, N]), sb("rest", [SPLIT, N])
        rows = sb("rows", [P, RET_H])
        gap = sb("gap", [P, TILES, RET_H])
        ps_g = ctx.enter_context(nc.psum_tensor("l1g_ps_g", [P, 4, BANK], F32))
        ps_v = ctx.enter_context(nc.psum_tensor("l1g_ps_v", [P, 2, BANK], F32))
        ps_l = ctx.enter_context(nc.psum_tensor("l1g_ps_l", [P, 2, BANK], F32))
        gates_ready, dve_step, act_step, pe_step = sem("gates_ready"), sem("dve_step"), sem("act_step"), sem("pe_step")
        v_ready, v_done, v_ones = sem("v_ready"), sem("v_done"), sem("v_ones")
        swapped, split_step = sem("swapped"), sem("split_step")
        block = ctx.enter_context(nc.Block())

        @block.tensor
        def _(pe):
            pe.wait_ge(m.s_wattn, 16)
            for t in range(TILES):
                ins = pe.matmul(ps_l[:, 1, t * RET_H:(t + 1) * RET_H], m.xnT[:, t * P:(t + 1) * P],
                                m.w_attn[:, 3 * HD:3 * HD + RET_H], start=True, stop=True)
            ins.then_inc(gates_ready, 1)

            def values(tiles):
                for t in tiles:
                    if t >= 2:
                        pe.wait_ge(v_done, t - 1)
                    pe.matmul(ps_v[:, t % 2, :], m.xnT[:, t * P:(t + 1) * P], m.w_attn[:, 2 * HD:3 * HD], start=True,
                              stop=True).then_inc(v_ready, 1)

            values(range(0, 4))
            pe.wait_ge(dve_step, 9)
            for t in range(TILES):
                ins = pe.transpose(ps_g[0:SPLIT, t // 4, (t % 4) * P:(t % 4 + 1) * P], spread[:, t, :], m.ident)
            ins.then_inc(gates_ready, 1)
            values(range(4, 9))
            pe.wait_ge(dve_step, 10)
            for t in range(TILES):
                ins = pe.transpose(ps_l[:, 0, t * RET_H:(t + 1) * RET_H], LT[0:RET_H, t * P:(t + 1) * P], m.ident[0:RET_H, 0:RET_H])
            ins.then_inc(pe_step, 1)
            values(range(9, 11))
            pe.wait_ge(dve_step, 11)
            pe.matmul(ps_l[:, 1, 0:TILES * RET_H], m.one[0:1, :], r.Lcol[0:1, :, :].rearrange("p t h -> p (t h)"),
                      start=True, stop=True).then_inc(pe_step, 1)
            values(range(11, TILES))

        @block.gpsimd
        def _(pool):
            pool.memset(r.v[:, :, :, RET_D:RET_D + 1], 1.0)
            pool.memset(spread[:, :, :], 0.0).then_inc(v_ones, 1)
            pool.memset(LT[:, :], 0.0).then_inc(v_ones, 1)
            pool.memset(r.Lsplit[:, :], 0.0).then_inc(v_ones, 1)
            pool.wait_ge(m.s_wattn, 16)
            pairs = m.w_attn[:, 0:2 * HD].rearrange("p (c two) -> p c two", two=2)
            swap = r.wswap[:, :].rearrange("p (c two) -> p c two", two=2)
            pool.tensor_scalar(swap[:, :, 0], pairs[:, :, 1], -1.0, None, ALU.mult).then_inc(swapped, 1)
            pool.tensor_copy(swap[:, :, 1], pairs[:, :, 0]).then_inc(swapped, 1)
            pool.tensor_tensor(rows[:, :], m.ident[:, 0:RET_H], m.ident[:, 32:32 + RET_H], ALU.add).then_inc(swapped, 1)
            pool.wait_ge(swapped, 3)
            pool.tensor_tensor(rows[:, :], rows[:, :], m.ident[:, 64:64 + RET_H], ALU.add).then_inc(swapped, 1)
            pool.wait_ge(swapped, 4)
            pool.tensor_copy(r.pick[:, :, :], rows[:, :].unsqueeze(2).broadcast_to([P, RET_H, P])).then_inc(swapped, 1)

        @block.scalar
        def _(act):
            act.wait_ge(dve_step, 2)
            act.activation(u[:, :], w1[:, :], ACT.Exp, scale=-1.0).then_inc(act_step, 1)
            act.wait_ge(dve_step, 3)
            act.activation(lw[:, :], w1[:, :], ACT.Ln).then_inc(act_step, 1)
            for t in range(TILES):
                act.wait_ge(v_ready, t + 1)
                act.activation(r.v[:, t, :, 0:RET_D], ps_v[:, t % 2, :].rearrange("p (h d) -> p h d", h=RET_H), ACT.Copy)\
                   .then_inc(v_done, 1)
                if t == TILES - 5:
                    act.wait_ge(split_step, 2)
                    act.activation(r.Lsplit[32:64, :], rest[32:64, :], ACT.Copy)
                if t == TILES - 3:
                    act.wait_ge(dve_step, 13)
                    act.activation(r.fade[:, :, :], gap[:, :, :], ACT.Exp).then_inc(act_step, 1)
            act.wait_ge(dve_step, 15)
            kf = r.keyfade[:, :, :, :, :].rearrange("p b j i h -> p (b j i h)")
            act.activation(kf, kf, ACT.Exp, scale=0.5).then_inc(act_step, 1)

        @block.vector
        def _(dve):
            steps = [0]

            def link(ins):
                steps[0] += 1
                ins.then_inc(dve_step, 1)
                dve.wait_ge(dve_step, steps[0])

            dve.wait_ge(gates_ready, 1)
            link(dve.tensor_scalar(x[:, :], ps_l[:, 1, 0:TILES * RET_H], GATE_BIAS, None, ALU.add))
            link(dve.scalar_tensor_tensor(w1[:, :], x[:, :], -1.0, x[:, :], ALU.mult, ALU.max))
            dve.wait_ge(act_step, 1)
            link(dve.tensor_scalar(w1[:, :], u[:, :], 1.0, None, ALU.add))
            dve.wait_ge(act_step, 2)
            link(dve.tensor_scalar(w1[:, :], w1[:, :], -1.0, 1e-30, ALU.add, ALU.max))
            link(dve.reciprocal(w1[:, :], w1[:, :]))
            link(dve.tensor_tensor(lw[:, :], lw[:, :], u[:, :], ALU.mult))
            link(dve.tensor_tensor(lw[:, :], lw[:, :], w1[:, :], ALU.mult))
            link(dve.scalar_tensor_tensor(x[:, :], x[:, :], 0.0, lw[:, :], ALU.min, ALU.subtract))
            dve.wait_ge(v_ones, 2)
            link(dve.tensor_copy(spread[:, :, :].rearrange("p t (k z) -> p t k z", k=3)[:, :, :, 0:RET_H],
                                 x[:, :].rearrange("p (t h) -> p t h", h=RET_H).unsqueeze(2).broadcast_to([P, TILES, 3, RET_H])))
            dve.wait_ge(gates_ready, 2)
            for b in range(B):
                lg = ps_g[0:SPLIT, 2 * b:2 * b + 2, :].rearrange("p g n -> p (g n)")
                to = LT[:, b * S:(b + 1) * S]
                ins = dve.tensor_tensor_scan(to, lg, to, 0.0, ALU.add, ALU.add)
            link(ins)
            dve.wait_ge(v_ones, 3)
            dve.tensor_copy(r.Lsplit[0:SPLIT, :], LT[:, :]).then_inc(split_step, 1)
            dve.wait_ge(split_step, 1)
            dve.tensor_tensor(rest[:, :], LT[:, :], r.Lsplit[0:SPLIT, :], ALU.subtract).then_inc(split_step, 1)
            dve.wait_ge(pe_step, 1)
            link(dve.tensor_copy(r.Lcol[:, :, :].rearrange("p t h -> p (t h)"), ps_l[:, 0, 0:TILES * RET_H]))
            dve.wait_ge(pe_step, 2)
            link(dve.tensor_copy(r.Lfirst[:, :, :].rearrange("p t h -> p (t h)"), ps_l[:, 1, 0:TILES * RET_H]))
            link(dve.tensor_tensor(gap[:, :, :], r.Lcol[:, :, :], r.Lfirst[:, :, :], ALU.subtract))
            for b in range(B):
                tiles = slice(b * CH, (b + 1) * CH)
                for j in range(CH):
                    ins = dve.tensor_tensor(r.keyfade[:, b, j, :, :], r.Lfirst[:, tiles, :],
                                            r.Lcol[:, b * CH + j, :].unsqueeze(1).broadcast_to([P, CH, RET_H]), ALU.subtract)
            link(ins)
            kf = r.keyfade[:, :, :, :, :].rearrange("p b j i h -> p (b j i h)")
            link(dve.tensor_scalar(kf, kf, 0.0, None, ALU.min))
            dve.wait_ge(split_step, 2)
            dve.tensor_copy(r.Lsplit[64:SPLIT, :], rest[64:SPLIT, :]).then_inc(split_step, 1)
            dve.wait_ge(split_step, 3)
            dve.tensor_tensor(rest[64:SPLIT, :], rest[64:SPLIT, :], r.Lsplit[64:SPLIT, :], ALU.subtract).then_inc(split_step, 1)
            dve.wait_ge(split_step, 4)
            dve.tensor_copy(r.Lsplit[64:SPLIT, :], rest[64:SPLIT, :])
            dve.wait_ge(act_step, 4)
            link(dve.tensor_scalar(kf, kf, float(RET_D) ** -0.5, None, ALU.mult))


def l1_heads(nc, m, r):
    WIDE = WIDE_PER_HEAD * RET_H + CH // 2
    YJOBS = 4 * RET_H + CH // 2
    ROPES = 16
    OFF = [sum(CH - 1 - k for k in range(j)) * P for j in range(CH)]
    with ExitStack() as ctx:
        def sb(name, shape, dt=F32):
            return ctx.enter_context(nc.sbuf_tensor(f"l1h_{name}", shape, dt))

        sem = signals(nc, m, "l1h_")

        qr = sb("qr", [P, 2, S])
        kz = sb("kz", [P, 2, 2, S])
        rc, rs = sb("rc", [P, 2, BANK]), sb("rs", [P, 2, BANK])
        sq = sb("sq", [P, 2, 28 * P])
        sqd = sb("sqd", [P, 2, S])
        decay = sb("decay", [P, 2, S])
        ty = sb("ty", [P, 2, RET_D + 1])
        yraw = sb("yraw", [P, CH, RET_H, RET_D + 1])
        rden = sb("rden", [P, CH, RET_H])
        yn = sq[:, :, :].rearrange("p a n -> p (a n)")[:, 0:CH * HD].rearrange("p (i n) -> p i n", i=CH)
        yT = decay[:, :, :].rearrange("p a (e n) -> p a e n", e=2)
        ab = ctx.enter_context(nc.psum_tensor("l1h_ab", [P, 2, BANK], F32))
        wide = ctx.enter_context(nc.psum_tensor("l1h_wide", [P, 2, 2 * BANK], F32))
        yps = ctx.enter_context(nc.psum_tensor("l1h_y", [P, 2, BANK], F32))
        a_filled, b_filled, a_used, b_used, q_ready, k_ready = (
            sem(x) for x in ("a_filled", "b_filled", "a_used", "b_used", "q_ready", "k_ready"))
        wide_filled, wide_free = sem("wide_filled"), [sem("wide_free0"), sem("wide_free1")]
        scaled, off_squared = sem("scaled"), sem("off_squared")
        gap_ready, exp_ready, decay_ready, diag_squared, diag_ready = (sem(x) for x in ("gap_ready", "exp_ready", "decay_ready", "diag_squared", "diag_ready"))
        y_filled, y_used, ty_ready = sem("y_filled"), sem("y_used"), sem("ty_ready")
        norm_step, yT_ready, kz_clear = sem("norm_step"), sem("yT_ready"), sem("kz_clear")
        block = ctx.enter_context(nc.Block())

        def order():
            for n in range(4):
                yield "rope", 0, n
            for h in range(RET_H + 1):
                parts = [("gap", h, 0), ("rope", h // 2 + 1, 2 * (h % 2)), ("diag", h, 0), ("values", h - 1, 0), ("off", h, 0),
                         ("off", h, 1), ("values", h - 1, 1), ("off", h, 2), ("off", h, 3), ("values", h - 1, 2), ("off", h, 4),
                         ("off", h, 5), ("rope", h // 2 + 1, 2 * (h % 2) + 1), ("off", h, 6), ("mask", h, 0),
                         ("values", h - 1, 3)]
                for kind, k, part in parts:
                    if kind == "values" and k >= 0 or kind == "rope" and k < RET_H // 2 and h < RET_H or \
                            kind in ("gap", "diag", "off", "mask") and k < RET_H:
                        yield kind, k, part

        @block.tensor
        def _(pe):
            pe.wait_ge(m.s_wproj1, 16)
            for signal in (y_filled, wide_filled):
                pe.sem_inc(signal, FROM)
            with pe.Fori(0, B) as b:
                def rope(hp, n):
                    job, kind, half = 4 * hp + n, n // 2, n % 2
                    cols = slice(kind * HD + hp * P, kind * HD + (hp + 1) * P)
                    x = m.xnT[:, bass.ds(b * S + half * BANK, BANK)]
                    pe.wait_ge(a_used, FROM + b * ROPES + job)
                    pe.matmul(ab[:, 0, :], m.w_attn[:, cols], x, start=True, stop=True).then_inc(a_filled, 1)
                    pe.wait_ge(b_used, FROM + b * ROPES + job)
                    pe.matmul(ab[:, 1, :], r.wswap[:, cols], x, start=True, stop=True).then_inc(b_filled, 1)

                def gap(h, _):
                    job = WIDE_PER_HEAD * h
                    slot = job % 2
                    pe.wait_ge(wide_free[slot], FROM + b * (WIDE // 2) + job // 2)
                    pe.nop(nofuse=True)
                    for half in range(2):
                        ins = pe.matmul(wide[:, slot, half * BANK:(half + 1) * BANK], r.pick[:, h, :],
                                        r.Lsplit[:, bass.ds(b * S + half * BANK, BANK)], start=True, stop=True)
                    ins.then_inc(wide_filled, 1)

                def rotated(h):
                    return qr[:, (h // 2) % 2, :], kz[:, (h // 2) % 2, h % 2, :]

                def diag(h, _):
                    if h == 0:
                        pe.wait_ge(kz_clear, 1)
                    if h % 2 == 0:
                        pe.wait_ge(q_ready, FROM + b * (ROPES // 2) + 2 * (h // 2 + 1))
                        pe.wait_ge(k_ready, FROM + b * (ROPES // 2) + 2 * (h // 2 + 1))
                    q, k = rotated(h)
                    job = WIDE_PER_HEAD * h + 1
                    slot = job % 2
                    pe.wait_ge(wide_free[slot], FROM + b * (WIDE // 2) + job // 2)
                    for i in range(CH):
                        t = slice(i * P, (i + 1) * P)
                        ins = pe.matmul(wide[:, slot, t], k[:, t], q[:, t], start=True, stop=True)
                    ins.then_inc(wide_filled, 1)

                def off(h, j):
                    q, k = rotated(h)
                    job = WIDE_PER_HEAD * h + 2 + j
                    slot = job % 2
                    pe.wait_ge(wide_free[slot], FROM + b * (WIDE // 2) + job // 2)
                    width = (CH - 1 - j) * P
                    for c in range(0, width, BANK):
                        n = min(BANK, width - c)
                        t0 = (j + 1) * P + c
                        ins = pe.matmul(wide[:, slot, c:c + n], k[:, j * P:(j + 1) * P], q[:, t0:t0 + n], start=True, stop=True)
                    ins.then_inc(wide_filled, 1)

                def values(h, g):
                    if g == 0:
                        pe.wait_ge(diag_ready, FROM + b * RET_H + h + 1)
                        pe.wait_ge(off_squared, b * 7 * RET_H + 7 * (h + 1))
                    y = yps[:, (4 * h + g) % 2, :]
                    pe.wait_ge(y_used, FROM + b * YJOBS + max(4 * h + g - 1, 0))
                    for e in range(2):
                        i = 2 * g + e
                        for j in range(i):
                            block_at = OFF[j] + (i - j - 1) * P
                            pe.matmul(y[:, e * 130:e * 130 + 65], sq[:, h % 2, block_at:block_at + P],
                                      r.v[:, bass.ds(b * CH + j, 1), h, :].rearrange("p a d -> p (a d)"), start=(j == 0), stop=(j == i - 1))
                        ins = pe.matmul(y[:, e * 130 + 65:e * 130 + 130], sqd[:, h % 2, i * P:(i + 1) * P],
                                        r.v[:, bass.ds(b * CH + i, 1), h, :].rearrange("p a d -> p (a d)"), start=True, stop=True)
                    ins.then_inc(y_filled, 1)

                work = {"rope": rope, "gap": gap, "diag": diag, "off": off, "values": values}
                for kind, k, part in order():
                    if kind in work:
                        work[kind](k, part)
                def turn_output(g):
                    job = WIDE_PER_HEAD * RET_H + g
                    slot = job % 2
                    pe.wait_ge(norm_step, b * 6 + 3 + g)
                    pe.wait_ge(wide_free[slot], FROM + b * (WIDE // 2) + job // 2)
                    for e in range(2):
                        for c in range(4):
                            ins = pe.transpose(wide[:, slot, e * BANK + c * P:e * BANK + (c + 1) * P],
                                               yn[:, 2 * g + e, c * P:(c + 1) * P], m.ident)
                    ins.then_inc(wide_filled, 1)

                def project_output(g):
                    pe.wait_ge(yT_ready, b * 4 + g + 1)
                    yjob = 4 * RET_H + g
                    pe.wait_ge(y_used, FROM + b * YJOBS + yjob - 1)
                    for e in range(2):
                        for c in range(4):
                            ins = pe.matmul(yps[:, yjob % 2, e * P:(e + 1) * P], yT[:, g % 2, e, c * P:(c + 1) * P],
                                            m.w_proj1[:, c, :], start=(c == 0), stop=(c == 3))
                    ins.then_inc(y_filled, 1)

                turn_output(0)
                for g in range(1, CH // 2):
                    turn_output(g)
                    project_output(g - 1)
                project_output(CH // 2 - 1)

        @block.vector
        def _(dve):
            dve.wait_ge(m.s_consts, 16)
            for signal in (a_used, b_used, k_ready, *wide_free, y_used, diag_ready):
                dve.sem_inc(signal, FROM)
            with dve.Fori(0, B) as b:
                def rope(hp, n):
                    job, half = 4 * hp + n, n % 2
                    t = slice(half * BANK, (half + 1) * BANK)
                    if n < 2:
                        dve.wait_ge(k_ready, FROM + b * (ROPES // 2) + max(2 * hp - 1 + n, 0))
                    else:
                        dve.wait_ge(q_ready, FROM + b * (ROPES // 2) + 2 * hp + n - 1)
                    dve.wait_ge(a_filled, b * ROPES + job + 1)
                    dve.tensor_tensor(rc[:, job % 2, :], ab[:, 0, :], m.ropecos[:, t], ALU.mult).then_inc(a_used, 1)
                    dve.wait_ge(b_filled, b * ROPES + job + 1)
                    dve.tensor_tensor(rs[:, job % 2, :], ab[:, 1, :], m.ropesin[:, t], ALU.mult).then_inc(b_used, 1)
                    if n >= 2:
                        dve.wait_ge(b_used, FROM + b * ROPES + job + 1)
                        dve.wait_ge(wide_filled, FROM + b * WIDE + WIDE_PER_HEAD * max(2 * hp - 2, 0))
                        for k in range(2):
                            c = slice(64 * k, 64 * k + 64)
                            ins = dve.tensor_tensor(kz[c, hp % 2, k, t], rc[c, job % 2, :], rs[c, job % 2, :], ALU.add)
                        ins.then_inc(k_ready, 1)

                def gap(h, _):
                    job = WIDE_PER_HEAD * h
                    dve.wait_ge(wide_filled, FROM + b * WIDE + job + 1)
                    dve.wait_ge(diag_ready, FROM + b * RET_H + max(h - 1, 0))
                    dve.tensor_tensor(decay[:, h % 2, :].rearrange("p (i t) -> p i t", i=CH),
                                      wide[:, job % 2, :].rearrange("p (i t) -> p i t", i=CH),
                                      r.Lcol[:, bass.ds(b * CH, CH), h].unsqueeze(2).broadcast_to([P, CH, P]),
                                      ALU.subtract).then_inc(gap_ready, 1)
                    dve.wait_ge(gap_ready, b * RET_H + h + 1)
                    dve.sem_inc(wide_free[job % 2], 1)

                def off(h, j):
                    if j == 0:
                        dve.wait_ge(y_filled, FROM + b * YJOBS + 4 * max(h - 1, 0))
                    job = WIDE_PER_HEAD * h + 2 + j
                    width = (CH - 1 - j) * P
                    dve.wait_ge(wide_filled, FROM + b * WIDE + job + 1)
                    dve.tensor_tensor(sq[:, h % 2, OFF[j]:OFF[j] + width].rearrange("p (i t) -> p i t", t=P),
                                      wide[:, job % 2, 0:width].rearrange("p (i t) -> p i t", t=P),
                                      r.keyfade[:, bass.ds(b, 1), j, j + 1:CH, h].rearrange("p a i -> p (a i)").unsqueeze(2)
                                      .broadcast_to([P, CH - 1 - j, P]), ALU.mult).then_inc(scaled, 1)
                    dve.wait_ge(scaled, b * 7 * RET_H + 7 * h + j + 1)
                    dve.sem_inc(wide_free[job % 2], 1)

                def mask(h, _):
                    dve.wait_ge(diag_squared, b * RET_H + h + 1)
                    dve.wait_ge(decay_ready, b * RET_H + h + 1)
                    dve.tensor_tensor(sqd[:, h % 2, :], sqd[:, h % 2, :], decay[:, h % 2, :], ALU.mult).then_inc(diag_ready, 1)

                def values(h, g):
                    y = yps[:, (4 * h + g) % 2, 0:260].rearrange("p (e k d) -> p e k d", e=2, k=2)
                    dve.wait_ge(y_filled, FROM + b * YJOBS + 4 * h + g + 1)
                    fade = r.fade[:, bass.ds(b * CH + 2 * g, 2), h]
                    out = yraw[:, 2 * g:2 * g + 2, h, :]
                    if g == 0:
                        dve.tensor_tensor(ty[:, 1:2, :], y[:, 1:2, 0, :], fade[:, 1:2].unsqueeze(2).broadcast_to([P, 1, RET_D + 1]),
                                          ALU.mult).then_inc(ty_ready, 1)
                        dve.wait_ge(ty_ready, b * 4 * RET_H + 4 * h + g + 1)
                        dve.tensor_copy(out[:, 0:1, :], y[:, 0:1, 1, :])
                        dve.tensor_tensor(out[:, 1:2, :], ty[:, 1:2, :], y[:, 1:2, 1, :], ALU.add).then_inc(y_used, 1)
                    else:
                        dve.tensor_tensor(ty[:, :, :], y[:, :, 0, :], fade.unsqueeze(2).broadcast_to([P, 2, RET_D + 1]),
                                          ALU.mult).then_inc(ty_ready, 1)
                        dve.wait_ge(ty_ready, b * 4 * RET_H + 4 * h + g + 1)
                        dve.tensor_tensor(out, ty[:, :, :], y[:, :, 1, :], ALU.add).then_inc(y_used, 1)
                    dve.wait_ge(y_used, FROM + b * YJOBS + 4 * h + g + 1)

                work = {"rope": rope, "gap": gap, "off": off, "mask": mask, "values": values}
                for kind, k, part in order():
                    if kind in work:
                        work[kind](k, part)
                dve.tensor_scalar(rden[:, :, :], yraw[:, :, :, RET_D], 1e-6, None, ALU.max).then_inc(norm_step, 1)
                dve.wait_ge(norm_step, b * 6 + 1)
                dve.reciprocal(rden[:, :, :], rden[:, :, :]).then_inc(norm_step, 1)
                dve.wait_ge(norm_step, b * 6 + 2)
                for i in range(CH):
                    ins = dve.tensor_tensor(yn[:, i, :].rearrange("p (h d) -> p h d", h=RET_H), yraw[:, i, :, 0:RET_D],
                                            rden[:, i, :].unsqueeze(2).broadcast_to([P, RET_H, RET_D]), ALU.mult)
                    if i % 2 == 1:
                        ins.then_inc(norm_step, 1)
                for g in range(CH // 2):
                    yjob = 4 * RET_H + g
                    dve.wait_ge(y_filled, FROM + b * YJOBS + yjob + 1)
                    hh = m.h[:, bass.ds(b * CH + 2 * g, 2), :]
                    dve.tensor_tensor(hh, hh, yps[:, yjob % 2, 0:2 * P].rearrange("p (e d) -> p e d", e=2), ALU.add).then_inc(y_used, 1)

        @block.scalar
        def _(act):
            with act.Fori(0, B) as b:
                def gap(h, _):
                    act.wait_ge(gap_ready, b * RET_H + h + 1)
                    act.activation(decay[:, h % 2, :], decay[:, h % 2, :], ACT.Exp).then_inc(exp_ready, 1)

                def diag(h, _):
                    job = WIDE_PER_HEAD * h + 1
                    act.wait_ge(wide_filled, FROM + b * WIDE + job + 1)
                    act.wait_ge(y_filled, FROM + b * YJOBS + 4 * max(h - 1, 0))
                    act.activation(sqd[:, h % 2, :], wide[:, job % 2, :], ACT.Square, scale=float(RET_D) ** -0.5).then_inc(diag_squared, 1)
                    act.wait_ge(diag_squared, b * RET_H + h + 1)
                    act.sem_inc(wide_free[job % 2], 1)

                def off(h, j):
                    act.wait_ge(scaled, b * 7 * RET_H + 7 * h + j + 1)
                    s = sq[:, h % 2, OFF[j]:OFF[j] + (CH - 1 - j) * P]
                    act.activation(s, s, ACT.Square).then_inc(off_squared, 1)

                work = {"gap": gap, "diag": diag, "off": off}
                for kind, k, part in order():
                    if kind in work:
                        work[kind](k, part)
                for g in range(CH // 2):
                    job = WIDE_PER_HEAD * RET_H + g
                    act.wait_ge(wide_filled, FROM + b * WIDE + job + 1)
                    act.wait_ge(y_filled, FROM + b * YJOBS + 4 * RET_H + max(g - 1, 0))
                    act.activation(yT[:, g % 2, :, :].rearrange("p e n -> p (e n)"), wide[:, job % 2, :], ACT.Copy).then_inc(yT_ready, 1)
                    act.wait_ge(yT_ready, b * 4 + g + 1)
                    act.sem_inc(wide_free[job % 2], 1)

        @block.gpsimd
        def _(pool):
            for k in range(2):
                ins = pool.memset(kz[64 * (1 - k):64 * (2 - k), :, k, :], 0.0)
            ins.then_inc(kz_clear, 1)
            pool.wait_ge(kz_clear, 1)
            pool.sem_inc(q_ready, FROM)
            with pool.Fori(0, B) as b:
                def rope(hp, half):
                    if half > 1:
                        return
                    pool.wait_ge(wide_filled, FROM + b * WIDE + WIDE_PER_HEAD * max(2 * hp - 2, 0))
                    job = 4 * hp + half
                    pool.wait_ge(b_used, FROM + b * ROPES + job + 1)
                    pool.wait_ge(a_used, FROM + b * ROPES + job + 1)
                    pool.tensor_tensor(qr[:, hp % 2, half * BANK:(half + 1) * BANK], rc[:, job % 2, :], rs[:, job % 2, :],
                                       ALU.add).then_inc(q_ready, 1)

                def gap(h, _):
                    pool.wait_ge(exp_ready, b * RET_H + h + 1)
                    pool.nop(nofuse=True)
                    g = decay[:, h % 2, :].rearrange("p (i t) -> p i t", i=CH)
                    pool.affine_select(out=g, in_=g, compare_op=ALU.is_ge, fill=0.0, base=0, pattern=[[0, CH], [1, P]],
                                       channel_multiplier=-1).then_inc(decay_ready, 1)

                work = {"rope": rope, "gap": gap}
                for kind, k, part in order():
                    if kind in work:
                        work[kind](k, part)


def router(nc, m, r, name, E, wrT, extra):
    G = E + extra
    with ExitStack() as ctx:
        def sb(x, shape, dt=F32):
            return ctx.enter_context(nc.sbuf_tensor(f"{name}_{x}", shape, dt))

        sem = signals(nc, m, f"{name}_")

        lg, left, pick, kept = (sb(x, [P, TILES, E]) for x in ("lg", "left", "pick", "kept"))
        mx = sb("mx", [P, 3, TILES])
        ps_l = ctx.enter_context(nc.psum_tensor(f"{name}_ps_l", [P, BANK], F32))
        logits, exps, dve_step = sem("logits"), sem("exps"), sem("dve_step")
        block = ctx.enter_context(nc.Block())

        @block.tensor
        def _(pe):
            pe.wait_ge(r.s_router, r.n_router)
            pe.matmul(ps_l[:, 0:TILES * E].rearrange("p (t e) -> p t e", e=E), m.one[0:1, :],
                      r.b_r[:, :].unsqueeze(1).broadcast_to([1, TILES, E]), start=True, stop=False)
            for t in range(TILES):
                ins = pe.matmul(ps_l[:, t * E:(t + 1) * E], r.hT[:, t * P:(t + 1) * P], wrT, start=False, stop=(t == TILES - 1))
            ins.then_inc(logits, 1)

        @block.scalar
        def _(act):
            act.wait_ge(dve_step, 7)
            act.activation(r.gates[:, :, 0:E], lg[:, :, :], ACT.Exp).then_inc(exps, 1)

        @block.vector
        def _(dve):
            steps = [0]

            def link(ins):
                steps[0] += 1
                ins.then_inc(dve_step, 1)
                dve.wait_ge(dve_step, steps[0])

            def wide(x):
                return x.unsqueeze(2).broadcast_to([P, TILES, E])

            def take(k):
                link(dve.tensor_reduce(mx[:, k, :], left[:, :, :], AX.X, ALU.max))
                link(dve.tensor_tensor(pick[:, :, :], left[:, :, :], wide(mx[:, k, :]), ALU.is_equal))
                link(dve.tensor_tensor(pick[:, :, :], pick[:, :, :], order, ALU.mult))
                link(dve.tensor_reduce(mx[:, 2, :], pick[:, :, :], AX.X, ALU.max))
                link(dve.tensor_tensor(pick[:, :, :], pick[:, :, :], wide(mx[:, 2, :]), ALU.is_equal))

            order = m.order[:, 16 - E:16].unsqueeze(1).broadcast_to([P, TILES, E])
            dve.wait_ge(logits, 1)
            link(dve.tensor_copy(left[:, :, :].rearrange("p t e -> p (t e)"), ps_l[:, 0:TILES * E]))
            take(0)
            link(dve.tensor_tensor(lg[:, :, :], left[:, :, :], wide(mx[:, 0, :]), ALU.subtract))
            dve.tensor_copy(kept[:, :, :], pick[:, :, :])
            link(dve.scalar_tensor_tensor(left[:, :, :], pick[:, :, :], -BIG, left[:, :, :], ALU.mult, ALU.add))
            take(1)
            link(dve.tensor_tensor(kept[:, :, :], kept[:, :, :], pick[:, :, :], ALU.add))
            dve.wait_ge(exps, 1)
            link(dve.tensor_tensor(r.gates[:, :, 0:E], r.gates[:, :, 0:E], kept[:, :, :], ALU.mult))
            link(dve.tensor_reduce(mx[:, 0, :], r.gates[:, :, 0:E], AX.X, ALU.add))
            link(dve.reciprocal(mx[:, 0, :], mx[:, 0, :]))
            link(dve.tensor_tensor(r.gates[:, :, 0:E], r.gates[:, :, 0:E], wide(mx[:, 0, :]), ALU.mult))
            if extra:
                dve.memset(r.gates[:, :, E:G], 1.0)


def l1_experts(nc, m, r):
    E, GROUPS = 8, 4
    UNITS = 2 * GROUPS
    LOOPS = E // 2
    with ExitStack() as ctx:
        def sb(name, shape, dt=F32):
            return ctx.enter_context(nc.sbuf_tensor(f"l1e_{name}", shape, dt))

        sem = signals(nc, m, "l1e_")

        w1, w2, b1 = sb("w1", [P, 2, 512]), sb("w2", [P, 2, 4, D]), sb("b1", [P, 2, 4])
        gT, b2 = sb("gT", [E, N]), sb("b2", [E, D])
        hid = sb("hid", [P, 2, 4, BANK])
        prime = sb("prime", [P, 1])
        ps_u = ctx.enter_context(nc.psum_tensor("l1e_ps_u", [P, 4, BANK], F32))
        ps_d = ctx.enter_context(nc.psum_tensor("l1e_ps_d", [P, 2, BANK], F32))
        w1_in, w2_in = [sem("w1_in0"), sem("w1_in1")], [sem("w2_in0"), sem("w2_in1")]
        up_ready, hid_ready, down_ready, down_free = sem("up_ready"), sem("hid_ready"), sem("down_ready"), sem("down_free")
        b2_in, gates_turned, gates_in, bias_ready, bias_added = (
            sem(x) for x in ("b2_in", "gates_turned", "gates_in", "bias_ready", "bias_added"))
        xn_added = sem("xn_added")
        block = ctx.enter_context(nc.Block())

        @block.sync
        def _(sp):
            def load(k, e, units):
                sp.wait_ge(up_ready, FROM + units * 4)
                sp.wait_ge(hid_ready, FROM + units * 4)
                sp.dma_start(w1[:, k, :], r.W1_dram[bass.ds(e, 1), :, :].rearrange("e p f -> p (e f)")).then_inc(w1_in[k], 16)
                sp.dma_start(b1[:, k, :], r.b1_dram[bass.ds(e, 1), :].rearrange("e (c p) -> p (e c)", p=P),
                             allow_slow_non_contiguous=True).then_inc(w1_in[k], 16)
                sp.wait_ge(down_ready, FROM + units)
                sp.dma_start(w2[:, k, :, :], r.W2_dram[bass.ds(e, 1), :, :].rearrange("e (c p) d -> p (e c) d", p=P)).then_inc(w2_in[k], 16)

            load(0, 0, 0)
            sp.dma_start(b2[:, :], r.b2_dram).then_inc(b2_in, 16)
            with sp.Fori(0, LOOPS - 1) as it:
                load(1, it * 2 + 1, it * UNITS)
                load(0, it * 2 + 2, it * UNITS + GROUPS)
            load(1, E - 1, (LOOPS - 1) * UNITS)

        @block.tensor
        def _(pe):
            def up(it, u):
                k, g, n = (u // GROUPS) % 2, u % GROUPS, it * UNITS + u
                if g == 0:
                    pe.wait_ge(w1_in[k], (it + u // UNITS) * 32 + 32)
                for c in range(4):
                    if isinstance(n, int) and n == 0:
                        pe.wait_ge(gates_in, c + 1)
                    pe.wait_ge(hid_ready, FROM + (it * (UNITS * 4) + (4 * u + c - 3)) if u >= 1 else FROM)
                    pe.matmul(ps_u[:, c, :], w1[:, k, c * P:(c + 1) * P], r.hT[:, g * BANK:(g + 1) * BANK], start=True,
                              stop=True).then_inc(up_ready, 1)

            def down(it, u):
                k, g, n = u // GROUPS, u % GROUPS, it * UNITS + u
                if g == 0:
                    pe.wait_ge(w2_in[k], it * 16 + 16)
                pe.wait_ge(hid_ready, FROM + (n * 4 + 4))
                pe.wait_ge(down_free, n + 1)
                for t in range(4):
                    for c in range(4):
                        ins = pe.matmul(ps_d[:, u % 2, t * P:(t + 1) * P], hid[:, u % 2, c, t * P:(t + 1) * P], w2[:, k, c, :],
                                        start=(c == 0), stop=(c == 3))
                ins.then_inc(down_ready, 1)

            for signal in (up_ready, down_ready):
                pe.sem_inc(signal, FROM)
            for t in range(TILES):
                ins = pe.transpose(ps_u[0:E, t // 4, (t % 4) * P:(t % 4 + 1) * P], r.gates[:, t, :], m.ident)
                if t % 4 == 3:
                    ins.then_inc(gates_turned, 1)
            up(0, 0)
            pe.wait_ge(b2_in, 16)
            for t in range(TILES):
                g = t // 4
                if g >= 2 and t % 4 == 0:
                    pe.wait_ge(bias_added, g - 1)
                ins = pe.matmul(ps_d[:, g % 2, (t % 4) * P:(t % 4 + 1) * P], gT[:, t * P:(t + 1) * P], b2[:, :], start=True, stop=True)
                if t % 4 == 3:
                    ins.then_inc(bias_ready, 1)
            with pe.Fori(0, LOOPS - 1) as it:
                for u in range(UNITS):
                    up(it, u + 1)
                    down(it, u)
            for u in range(UNITS):
                if u + 1 < UNITS:
                    up(LOOPS - 1, u + 1)
                down(LOOPS - 1, u)

        @block.scalar
        def _(act):
            act.activation(prime[:, :], m.pid, ACT.Gelu)
            act.sem_inc(hid_ready, FROM)
            for g in range(4):
                act.wait_ge(gates_turned, g + 1)
                act.activation(gT[:, g * BANK:(g + 1) * BANK], ps_u[0:E, g, :], ACT.Copy).then_inc(gates_in, 1)
            with act.Fori(0, LOOPS) as it:
                for u in range(UNITS):
                    act.wait_ge(down_ready, FROM + it * UNITS + max(u - 1, 0))
                    for c in range(4):
                        act.wait_ge(up_ready, FROM + (it * (UNITS * 4) + (4 * u + c + 1)))
                        act.activation(hid[:, u % 2, c, :], ps_u[:, c, :], ACT.Gelu, bias=b1[:, u // 4, c:c + 1]).then_inc(hid_ready, 1)

        @block.vector
        def _(dve):
            dve.tensor_tensor(m.h[:, :, :], m.h[:, :, :], m.xn[:, :, :], ALU.add).then_inc(xn_added, 1)
            dve.wait_ge(xn_added, 1)
            for g in range(4):
                dve.wait_ge(bias_ready, g + 1)
                hh = m.h[:, 4 * g:4 * g + 4, :]
                dve.tensor_tensor(hh, hh, ps_d[:, g % 2, :].rearrange("p (t d) -> p t d", t=4), ALU.add).then_inc(bias_added, 1)
            dve.wait_ge(bias_added, 4)
            dve.sem_inc(down_free, 2)
            with dve.Fori(0, LOOPS) as it:
                for u in range(UNITS):
                    k, g, n = u // GROUPS, u % GROUPS, it * UNITS + u
                    dve.wait_ge(down_free, n + 1)
                    dve.wait_ge(down_ready, FROM + (n + 1))
                    for t in range(4):
                        hh = m.h[:, 4 * g + t, :]
                        ins = dve.scalar_tensor_tensor(hh, ps_d[:, u % 2, t * P:(t + 1) * P],
                                                       r.gates[:, 4 * g + t, bass.ds(it * 2 + k, 1)], hh, ALU.mult, ALU.add)
                    ins.then_inc(down_free, 1)


def stage_l1_ffn(nc, m, w):
    with ExitStack() as ctx:
        def sb(name, shape, dt=F32):
            return ctx.enter_context(nc.sbuf_tensor(f"l1f_{name}", shape, dt))

        r = Core()
        r.hn, r.hT = sb("hn", [P, TILES, D]), sb("hT", [P, N])
        r.gates = sb("gates", [P, TILES, 8])
        r.b_r, r.ln_g, r.ln_b = sb("b_r", [1, 8]), sb("ln_g", [P, 1]), sb("ln_b", [P, 1])
        r.b2_dram, r.b1_dram, r.W1_dram, r.W2_dram = w["L1_ffn_b2"], w["L1_ffn_b1"], w["L1_ffn_W1"], w["L1_ffn_W2"]
        r.s_router, r.n_router = signals(nc, m, "l1f_")("router"), 48
        with nc.Block() as block:
            @block.sync
            def _(sp):
                sp.dma_start(r.b_r[:, :], row(w["L1_ffn_b_r"])).then_inc(r.s_router, 16)
                sp.dma_start(r.ln_g[:, :], col(w["L1_ffn_ln_g"]), allow_slow_non_contiguous=True).then_inc(r.s_router, 16)
                sp.dma_start(r.ln_b[:, :], col(w["L1_ffn_ln_b"]), allow_slow_non_contiguous=True).then_inc(r.s_router, 16)
                sp.wait_ge(r.s_router, 48)
        layernorm(nc, m, "ln_l1f", m.h, m.xn, None)
        layernorm(nc, m, "ln_l1g", m.xn, r.hn, r.hT, gain=r.ln_g[:, 0:1], shift=r.ln_b[:, 0:1])
        router(nc, m, r, "l1r", 8, m.wrT[:, :], 0)
        l1_experts(nc, m, r)


def stage_l2_attn(nc, m, w):
    H, HW, ROLL = 8, 16, 32
    GROUPS = TILES // 4
    with ExitStack() as ctx:
        def sb(name, shape, dt=F32):
            return ctx.enter_context(nc.sbuf_tensor(f"l2_{name}", shape, dt))

        sem = signals(nc, m, "l2_")

        b_proj = sb("b_proj", [1, D])
        bias_in = sem("bias_in")
        with nc.Block() as block:
            @block.sync
            def _(sp):
                sp.dma_start(b_proj[:, :], row(w["L2_attn_b_proj"])).then_inc(bias_in, 16)
        layernorm(nc, m, "ln_l2a", m.h, m.xn, m.xnT)
        qkv = sb("qkv", [P, 3, 4, 3 * D])
        qk, av = sb("qk", [P, 4, H, H, HW]), sb("av", [P, 4, H, HW, H])
        s, e = sb("s", [P, 4, H, H]), sb("e", [P, 4, H, H])
        mx = sb("mx", [P, 4, H])
        o = sb("o", [P, 2, 4, D])
        oT = sb("oT", [P, S])
        y = sb("y", [P, H, 8, HW])
        yT = sb("yT", [P, S + ROLL])
        prime = sb("prime", [P, 1])
        ps_q = ctx.enter_context(nc.psum_tensor("l2_ps_q", [P, 4, BANK], F32))
        ps_t = ctx.enter_context(nc.psum_tensor("l2_ps_t", [P, BANK], F32))
        ps_y = ctx.enter_context(nc.psum_tensor("l2_ps_y", [P, 2, BANK], F32))
        qkv_ready, qkv_in, qk_ready, qk_used, av_ready, dve_step, exps, normed, av_done = (
            sem(x) for x in ("qkv_ready", "qkv_in", "qk_ready", "qk_used", "av_ready", "dve_step", "exps", "normed", "av_done"))
        o_ready, o_turned, oT_in, spread, y_in, regrouped, yT_in, out_ready, out_used = (
            sem(x) for x in ("o_ready", "o_turned", "oT_in", "spread", "y_in", "regrouped", "yT_in", "out_ready", "out_used"))
        block = ctx.enter_context(nc.Block())

        def factors(g, t):
            a = e[:, t, :, :].unsqueeze(2).broadcast_to([P, H, HW, H])
            v = qkv[:, g % 3, t, 2 * D:3 * D].rearrange("p (g d) -> p d g", g=H).unsqueeze(1).broadcast_to([P, H, HW, H])
            return a, v

        @block.tensor
        def _(pe):
            def project_in(g):
                if g >= 1:
                    pe.wait_ge(qkv_in, g)
                for t in range(4):
                    n = 4 * g + t
                    ins = pe.matmul(ps_q[:, t, 0:3 * D], m.xnT[:, n * P:(n + 1) * P], m.wqkv2[:, :, :].rearrange("p c d -> p (c d)"),
                                    start=True, stop=True)
                ins.then_inc(qkv_ready, 1)

            project_in(0)
            project_in(1)
            project_in(2)
            pe.wait_ge(bias_in, 16)
            for g in range(GROUPS):
                b = g // 2
                pe.wait_ge(o_ready, g + 1)
                if g >= 1:
                    pe.wait_ge(oT_in, g)
                for t in range(4):
                    ins = pe.transpose(ps_t[:, t * P:(t + 1) * P], o[:, g % 2, t, :], m.ident)
                ins.then_inc(o_turned, 1)
                if g + 3 < GROUPS:
                    project_in(g + 3)
                if g % 2 == 0:
                    continue
                pe.wait_ge(oT_in, g + 1)
                if b >= 1:
                    pe.wait_ge(out_used, 2 * b)
                for l in range(8):
                    ins = pe.transpose(ps_y[:, l // 4, (l % 4) * P:(l % 4 + 1) * P], oT[:, l:S:8], m.ident)
                ins.then_inc(spread, 1)
                pe.wait_ge(y_in, b + 1)
                for h in range(H):
                    ins = pe.transpose(ps_y[:, h // 4, (h % 4) * P:(h % 4 + 1) * P], y[:, h, :, :].rearrange("p l d -> p (l d)"), m.ident)
                ins.then_inc(regrouped, 1)
                pe.wait_ge(yT_in, b + 1)
                for half in range(2):
                    for t in range(4):
                        n = 4 * half + t
                        pe.matmul(ps_y[:, half, t * P:(t + 1) * P], yT[:, n * P:(n + 1) * P], m.wproj2[:, :], start=True, stop=False)
                        ins = pe.matmul(ps_y[:, half, t * P:(t + 1) * P], m.one[0:1, :], b_proj[:, :], start=False, stop=True)
                    ins.then_inc(out_ready, 1)

        @block.scalar
        def _(act):
            def fetch_qkv(g):
                act.wait_ge(qkv_ready, g + 1)
                act.activation(qkv[:, g % 3, :, :], ps_q[:, :, 0:3 * D], ACT.Copy).then_inc(qkv_in, 1)

            act.activation(prime[:, :], m.pid, ACT.Exp, scale=-1.0)
            fetch_qkv(0)
            fetch_qkv(1)
            fetch_qkv(2)
            for g in range(GROUPS):
                b = g // 2
                act.wait_ge(normed, g + 1)
                act.activation(e[:, :, :, :], s[:, :, :, :], ACT.Exp, scale=float(HW) ** -0.5).then_inc(exps, 1)
                act.wait_ge(o_turned, g + 1)
                if g % 2 == 0:
                    if b >= 1:
                        act.wait_ge(spread, b)
                    act.activation(oT[:, S - ROLL:S], ps_t[:, 0:ROLL], ACT.Copy)
                    act.activation(oT[:, 0:BANK - ROLL], ps_t[:, ROLL:BANK], ACT.Copy).then_inc(oT_in, 1)
                else:
                    act.activation(oT[:, BANK - ROLL:S - ROLL], ps_t[:, :], ACT.Copy).then_inc(oT_in, 1)
                if g + 3 < GROUPS:
                    fetch_qkv(g + 3)
                if g % 2 == 0:
                    continue
                act.wait_ge(spread, b + 1)
                for k in range(2):
                    ins = act.activation(y[:, :, 4 * k:4 * k + 4, :], ps_y[:, k, :].rearrange("p (l h d) -> p h l d", l=4, h=H), ACT.Copy)
                ins.then_inc(y_in, 1)
                act.wait_ge(regrouped, b + 1)
                of = ps_y[:, :, :].rearrange("p q (a k r) -> p q k a r", a=4, r=8)
                to = yT[:, ROLL:ROLL + S].rearrange("p (k h r) -> p k h r", h=H, r=8)
                for half in range(2):
                    act.activation(to[:, 0:15, 4 * half:4 * half + 4, :], of[:, half, 0:15, :, :], ACT.Copy)
                    place = (to[:, 15, 0:4, :] if half == 0 else yT[:, 0:ROLL].rearrange("p (h r) -> p h r", r=8))
                    ins = act.activation(place, of[:, half, 15, :, :], ACT.Copy)
                ins.then_inc(yT_in, 1)

        @block.gpsimd
        def _(pool):
            def products(g):
                pool.wait_ge(qkv_in, g + 1)
                for t in range(4):
                    if g >= 1:
                        pool.wait_ge(qk_used, 4 * (g - 1) + t + 1)
                    q = qkv[:, g % 3, t, 0:D].rearrange("p (h d) -> p h d", h=H).unsqueeze(2).broadcast_to([P, H, H, HW])
                    k = qkv[:, g % 3, t, D:2 * D].rearrange("p (h d) -> p h d", h=H).unsqueeze(1).broadcast_to([P, H, H, HW])
                    pool.tensor_tensor(qk[:, t, :, :, :], q, k, ALU.mult).then_inc(qk_ready, 1)

            products(0)
            for g in range(GROUPS):
                if g + 1 < GROUPS:
                    products(g + 1)
                pool.wait_ge(dve_step, g * 4 + 4)
                if g >= 1:
                    pool.wait_ge(o_ready, g)
                a, v = factors(g, 3)
                pool.tensor_tensor(av[:, 3, :, :, :], a, v, ALU.mult).then_inc(av_ready, 1)

        @block.vector
        def _(dve):
            def add(b):
                for half in range(2):
                    dve.wait_ge(out_ready, 2 * b + half + 1)
                    hh = m.h[:, b * CH + 4 * half:b * CH + 4 * half + 4, :]
                    dve.tensor_tensor(hh, hh, ps_y[:, half, :].rearrange("p (t d) -> p t d", t=4), ALU.add).then_inc(out_used, 1)

            for g in range(GROUPS):
                for t in range(4):
                    dve.wait_ge(qk_ready, g * 4 + t + 1)
                    dve.tensor_reduce(s[:, t, :, :].rearrange("p h g -> p (h g)"), qk[:, t, :, :, :].rearrange("p h g d -> p (h g) d"),
                                      AX.X, ALU.add).then_inc(qk_used, 1)
                s2, e2 = (x.rearrange("p t h g -> p (t h) g") for x in (s[:, :, :, :], e[:, :, :, :]))
                mx1 = mx[:, :, :].rearrange("p t h -> p (t h)")
                wide_mx = mx1.unsqueeze(2).broadcast_to([P, 4 * H, H])
                dve.wait_ge(qk_used, g * 4 + 4)
                dve.tensor_reduce(mx1, s2, AX.X, ALU.max).then_inc(dve_step, 1)
                dve.wait_ge(dve_step, g * 4 + 1)
                dve.tensor_tensor(s2, s2, wide_mx, ALU.subtract).then_inc(normed, 1)
                if g % 2 == 0 and g >= 2:
                    add(g // 2 - 1)
                dve.wait_ge(exps, g + 1)
                dve.tensor_reduce(mx1, e2, AX.X, ALU.add).then_inc(dve_step, 1)
                dve.wait_ge(dve_step, g * 4 + 2)
                dve.reciprocal(mx1, mx1).then_inc(dve_step, 1)
                dve.wait_ge(dve_step, g * 4 + 3)
                dve.tensor_tensor(e2, e2, wide_mx, ALU.mult).then_inc(dve_step, 1)
                dve.wait_ge(dve_step, g * 4 + 4)
                for t in range(3):
                    a, v = factors(g, t)
                    ins = dve.tensor_tensor(av[:, t, :, :, :], a, v, ALU.mult)
                ins.then_inc(av_done, 1)
                dve.wait_ge(av_done, g + 1)
                if g >= 2:
                    dve.wait_ge(o_turned, g - 1)
                for t in range(4):
                    if t == 3:
                        dve.wait_ge(av_ready, g + 1)
                    ins = dve.tensor_reduce(o[:, g % 2, t, :], av[:, t, :, :, :].rearrange("p h d g -> p (h d) g"), AX.X, ALU.add)
                ins.then_inc(o_ready, 1)
                dve.wait_ge(o_ready, g + 1)
            add(B - 1)


TOPK = 16
TH, TW = 8, 16


def stage_l2_ffn(nc, m, w):
    layernorm(nc, m, "ln_l2f", m.h, m.xn, m.xnT)
    with ExitStack() as ctx:
        def sb(name, shape, dt=F32):
            return ctx.enter_context(nc.sbuf_tensor(f"t_{name}", shape, dt))

        r = Core()
        r.xc = sb("xc", [P, N])
        r.v = sb("v", [P, TILES, TH, TW + 1])
        r.wpad = sb("wpad", [P, 2, 2, P])
        r.bpad = sb("bpad", [P, 2, 2])
        r.wo_b, r.qkvb = sb("wo_b", [1, D]), sb("qkvb", [1, 3 * D])
        topk_prepare(nc, m, r, w)
        topk_attend(nc, m, r)


def topk_prepare(nc, m, r, w):
    with ExitStack() as ctx:
        def sb(name, shape, dt=F32):
            return ctx.enter_context(nc.sbuf_tensor(f"tp_{name}", shape, dt))

        sem = signals(nc, m, "tp_")

        posw, posb = sb("posw", [P, 3]), sb("posb", [P, 1])
        brow = sb("brow", [1, 2, 2, P])
        ps_v = ctx.enter_context(nc.psum_tensor("tp_ps_v", [P, 2, BANK], F32))
        ps_b = ctx.enter_context(nc.psum_tensor("tp_ps_b", [P, BANK], F32))
        loaded, dve_step, pool_step, v_ready, v_done, b_ready = (
            sem(x) for x in ("loaded", "dve_step", "pool_step", "v_ready", "v_done", "b_ready"))
        block = ctx.enter_context(nc.Block())

        @block.sync
        def _(sp):
            sp.dma_start(posw[:, :], w["L2_ffn_pos_w"].rearrange("d a k -> d (a k)")).then_inc(loaded, 16)
            sp.dma_start(posb[:, :], col(w["L2_ffn_pos_b"]), allow_slow_non_contiguous=True).then_inc(loaded, 16)
            sp.dma_start(r.qkvb[:, :], row(w["L2_ffn_qkv_b"])).then_inc(loaded, 16)
            sp.dma_start(r.wo_b[:, :], row(w["L2_ffn_wo_b"])).then_inc(loaded, 16)
            sp.wait_ge(loaded, 64)

        @block.gpsimd
        def _(pool):
            pool.memset(r.v[:, :, :, TW:TW + 1], 1.0)
            pool.memset(r.wpad[:, :, :, :], 0.0).then_inc(pool_step, 1)
            pool.memset(brow[:, :, :, :], 0.0).then_inc(pool_step, 1)
            pool.wait_ge(loaded, 64)
            pool.wait_ge(pool_step, 2)
            for kind in range(2):
                pool.tensor_copy(r.wpad[:, kind, :, :].rearrange("p g (h x) -> p (g h) x", x=32)[:, :, 0:TW],
                                 m.wqkv3[:, kind, :].rearrange("p (gh d) -> p gh d", d=TW)).then_inc(pool_step, 1)
                pool.tensor_copy(brow[:, kind, :, :].rearrange("p g (h x) -> p (g h) x", x=32)[:, :, 0:TW],
                                 r.qkvb[:, kind * D:(kind + 1) * D].rearrange("p (gh d) -> p gh d", d=TW)).then_inc(pool_step, 1)

        @block.tensor
        def _(pe):
            pe.wait_ge(pool_step, 6)
            for n in range(4):
                ins = pe.matmul(ps_b[:, n:n + 1], brow[0:1, n // 2, n % 2, :], m.one[0:1, 0:1], start=True, stop=True)
            ins.then_inc(b_ready, 1)
            pe.wait_ge(dve_step, 4)
            for t in range(CH):
                if t >= 2:
                    pe.wait_ge(v_done, t - 1)
                pe.matmul(ps_v[:, t % 2, 0:D], r.xc[:, t * P:(t + 1) * P], m.wqkv3[:, 2, :], start=True, stop=False)
                pe.matmul(ps_v[:, t % 2, 0:D], m.one[0:1, :], r.qkvb[:, 2 * D:3 * D], start=False, stop=True).then_inc(v_ready, 1)

        @block.scalar
        def _(act):
            for t in range(CH):
                act.wait_ge(v_ready, t + 1)
                act.activation(r.v[:, t, :, 0:TW], ps_v[:, t % 2, 0:D].rearrange("p (h d) -> p h d", h=TH), ACT.Copy).then_inc(v_done, 1)

        @block.vector
        def _(dve):
            steps = [0]

            def link(ins):
                steps[0] += 1
                ins.then_inc(dve_step, 1)
                dve.wait_ge(dve_step, steps[0])

            dve.wait_ge(loaded, 64)
            mid = posw[:, 1:2]
            link(dve.tensor_scalar(mid, mid, 1.0, None, ALU.add))
            for b in range(B):
                a, z = b * S, (b + 1) * S
                link(dve.tensor_scalar(r.xc[:, a:z], m.xnT[:, a:z], mid, posb[:, 0:1], ALU.mult, ALU.add))
                link(dve.scalar_tensor_tensor(r.xc[:, a + 1:z], m.xnT[:, a:z - 1], posw[:, 0:1], r.xc[:, a + 1:z], ALU.mult, ALU.add))
                link(dve.scalar_tensor_tensor(r.xc[:, a:z - 1], m.xnT[:, a + 1:z], posw[:, 2:3], r.xc[:, a:z - 1], ALU.mult, ALU.add))
            dve.wait_ge(b_ready, 1)
            dve.tensor_copy(r.bpad[:, :, :].rearrange("p a b -> p (a b)"), ps_b[:, 0:4])


def topk_attend(nc, m, r):
    SC = float(D) ** -0.5
    PAIR, FIRST, AHEAD = 2 * TH, 8, 4
    KEPT = 4
    nc.disable_value_cache = True
    with ExitStack() as ctx:
        def sb(name, shape, dt=F32):
            return ctx.enter_context(nc.sbuf_tensor(f"ta_{name}", shape, dt))

        sem = signals(nc, m, "ta_")
        qT, kT = sb("qT", [P, 2, N]), sb("kT", [P, 2, N])
        vseq = sb("vseq", [P, CH, TH, 2 * TW])
        qz = sb("qz", [P, 2, TH, P])
        top, ntop = sb("top", [P, 2, 2, 8]), sb("ntop", [P, 4])
        left = sb("left", [P, 4, S])
        ex = sb("ex", [P, 4, S])
        exT = sb("exT", [P, 2, CH, P])
        acc = sb("acc", [P, 2, P])
        rden, o, oT = sb("rden", [P, TH]), sb("o", [P, D]), sb("oT", [P, D])
        prime = sb("prime", [P, 1])
        ps_s = ctx.enter_context(nc.psum_tensor("ta_ps_s", [P, 2, S], F32))
        ps_t = ctx.enter_context(nc.psum_tensor("ta_ps_t", [P, S], F32))
        ps_o = ctx.enter_context(nc.psum_tensor("ta_ps_o", [P, BANK], F32))
        ps_p = ctx.enter_context(nc.psum_tensor("ta_ps_p", [P, BANK], F32))
        proj_ready, proj_done, q_in, v_in = sem("proj_ready"), sem("proj_done"), sem("q_in"), sem("v_in")
        late_ready, late_done, late_v_ready, late_v_done = sem("late_ready"), sem("late_done"), sem("late_v_ready"), sem("late_v_done")
        max_done = [sem("first_max"), sem("second_max")]
        s_ready, s_free, first_out, left_ready, left_exp, kept, turned, exT_in = (
            sem(x) for x in ("s_ready", "s_free", "first_out", "left_ready", "left_exp", "kept", "turned", "exT_in"))
        acc_out, acc_turned = sem("acc_out"), sem("acc_turned")
        values_done, rden_ready, o_ready, o_turned, oT_in, out_ready, out_used = (
            sem(x) for x in ("values_done", "rden_ready", "o_ready", "o_turned", "oT_in", "out_ready", "out_used"))
        block = ctx.enter_context(nc.Block())
        PAIRS = TILES // 2

        def place(eng, pair):
            at = Core()
            at.pair, at.item0, at.tile0 = pair, pair * PAIR, pair * 2
            at.key0 = [(pair + k) // (PAIRS // B) * S for k in range(2)]
            if not isinstance(pair, int):
                at.item0, at.tile0 = eng.snap(at.item0), eng.snap(at.tile0)
                if eng is nc.tensor:
                    at.key0 = [eng.snap(x) for x in at.key0]
            return at

        def steps(eng, step):
            for i in range(FIRST):
                step(place(eng, 0), i, False)
            with eng.Fori(0, PAIRS - 1) as pair:
                at = place(eng, pair)
                for i in range(FIRST, PAIR + FIRST):
                    step(at, i, False)
            for i in range(FIRST, PAIR + FIRST):
                step(place(eng, PAIRS - 1), i, True)

        def projected(seq, k):
            kind, grp, half = [(0, 0, 0), (0, 1, 0), (1, 0, 0), (1, 0, 1), (1, 1, 0), (1, 1, 1), (0, 0, 1), (0, 1, 1)][k]
            tokens = slice(seq * S + half * BANK, seq * S + (half + 1) * BANK)
            return kind, grp, tokens

        start_banks = [ps_t[:, 0:BANK], ps_t[:, BANK:2 * BANK], ps_o[:, :], ps_p[:, :]]

        @block.tensor
        def _(pe):
            def project(seq, k, bank):
                kind, grp, tokens = projected(seq, k)
                return pe.matmul(bank, r.wpad[:, kind, grp, :], r.xc[:, tokens], start=True, stop=True)

            def logits(at, i):
                h, odd, n = i % TH, (i // TH) % 2, at.item0 + i
                grp = h // 4
                if h == 0:
                    pe.wait_ge(q_in, at.tile0 + (i // TH + 1))
                pe.wait_ge(s_free, n + 1)
                for half in range(2):
                    ins = pe.matmul(ps_s[:, i % 2, half * BANK:(half + 1) * BANK], qz[:, odd, h, :],
                                    kT[:, grp, bass.ds(at.key0[i // PAIR] + half * BANK, BANK)], start=True, stop=True)
                ins.then_inc(s_ready, 1)

            def step(at, i, last):
                h, n = i % TH, at.item0 + i
                if i < FIRST:
                    if i >= 1:
                        pe.wait_ge(late_done, i)
                    project(1, i, ps_p[:, :]).then_inc(late_ready, 1)
                if i >= TH and h == 1:
                    tile = at.tile0 + (i // TH - 1)
                    pe.wait_ge(acc_out, tile + 2)
                    pe.wait_ge(out_used, tile + 1)
                    for grp in range(2):
                        ins = pe.transpose(ps_p[:, grp * P:(grp + 1) * P], acc[:, grp, :], m.ident)
                    ins.then_inc(acc_turned, 1)
                if i >= TH and h == 4:
                    tile = at.tile0 + (i // TH - 1)
                    pe.wait_ge(o_ready, tile + 1)
                    pe.transpose(ps_p[:, 0:P], o[:, :], m.ident).then_inc(o_turned, 1)
                if i >= TH and h == 5:
                    tile = at.tile0 + (i // TH - 1)
                    pe.wait_ge(oT_in, tile + 1)
                    pe.matmul(ps_p[:, 0:P], oT[:, :], m.wo[:, :], start=True, stop=False)
                    pe.matmul(ps_p[:, 0:P], m.one[0:1, :], r.wo_b[:, :], start=False, stop=True).then_inc(out_ready, 1)
                if i < PAIR or not last:
                    pe.wait_ge(kept, n + (KEPT + 1))
                    for j in range(CH):
                        ins = pe.transpose(ps_t[:, j * P:(j + 1) * P], ex[:, i % 4, j * P:(j + 1) * P], m.ident)
                    ins.then_inc(turned, 1)
                if i < FIRST and i % 2 == 0:
                    if i >= 2:
                        pe.wait_ge(late_v_done, i // 2)
                    for k in range(2):
                        t, out = slice(S + (i + k) * P, S + (i + k + 1) * P), ps_o[:, (2 + k) * P:(3 + k) * P]
                        pe.matmul(out, r.xc[:, t], m.wqkv3[:, 2, :], start=True, stop=False)
                        ins = pe.matmul(out, m.one[0:1, :], r.qkvb[:, 2 * D:3 * D], start=False, stop=True)
                    ins.then_inc(late_v_ready, 1)
                if i + AHEAD < PAIR or not last:
                    logits(at, i + AHEAD)
                if i < PAIR or not last:
                    pe.wait_ge(exT_in, n + 1)
                    if i % PAIR == 0:
                        pe.wait_ge(v_in, at.pair + (i // PAIR + 2))
                    if h == 0:
                        pe.wait_ge(acc_out, at.tile0 + (i // TH + 1))
                    a, grp = 32 * (h % 4), h // 4
                    for j in range(CH):
                        ins = pe.matmul(ps_o[a:a + 2 * TW, grp * P:(grp + 1) * P], vseq[:, j, h, :], exT[:, i % 2, j, :],
                                        start=(j == 0), stop=(j == CH - 1))
                    if h == TH - 1:
                        ins.then_inc(values_done, 1)
                if i == FIRST - 1:
                    pe.wait_ge(late_done, FIRST)

            for k in range(8):
                if k >= 4:
                    pe.wait_ge(proj_done, k - 3)
                project(0, k, start_banks[k % 4]).then_inc(proj_ready, 1)
            pe.wait_ge(proj_done, 8)
            for i in range(AHEAD):
                logits(place(pe, 0), i)
            steps(pe, step)

        @block.scalar
        def _(act):
            def fetch_values(tile):
                act.activation(vseq[:, :, :, 0:TW + 1], r.v[:, bass.ds(tile, CH), :, :], ACT.Copy).then_inc(v_in, 1)

            def copy_projection(seq, k, bank):
                kind, grp, tokens = projected(seq, k)
                return act.activation((qT, kT)[kind][:, grp, tokens], bank, ACT.Identity, bias=r.bpad[:, kind, grp:grp + 1])

            def all_exp(at, i):
                act.wait_ge(first_out, at.item0 + (i + 1))
                act.nop(nofuse=True)
                act.activation(ex[:, i % 4, :], ps_s[:, i % 2, :], ACT.Exp, bias=ntop[:, i % 4:i % 4 + 1], scale=SC).then_inc(s_free, 1)

            def turn(at, i):
                act.wait_ge(turned, at.item0 + (i + 1))
                act.activation(exT[:, i % 2, :, :].rearrange("p j q -> p (j q)"), ps_t[:, :], ACT.Copy).then_inc(exT_in, 1)

            def step(at, i, last):
                h, n = i % TH, at.item0 + i
                if i + 1 < PAIR or not last:
                    all_exp(at, i + 1)
                if i < PAIR or not last:
                    act.wait_ge(left_ready, n + 1)
                    act.activation(left[:, i % 4, :], left[:, i % 4, :], ACT.Exp, bias=ntop[:, i % 4:i % 4 + 1], scale=SC).then_inc(left_exp, 1)
                if i >= TH and h == 1:
                    act.wait_ge(values_done, at.tile0 + i // TH)
                    act.activation(acc[:, :, :].rearrange("p g q -> p (g q)"), ps_o[:, 0:2 * P], ACT.Copy).then_inc(acc_out, 1)
                if i >= TH and h == 5:
                    act.wait_ge(o_turned, at.tile0 + i // TH)
                    act.activation(oT[:, :], ps_p[:, 0:P], ACT.Copy).then_inc(oT_in, 1)
                if 1 <= i <= PAIR or (i > PAIR and not last):
                    turn(at, i - 1)
                if i < FIRST:
                    act.wait_ge(late_ready, i + 1)
                    copy_projection(1, i, ps_p[:, :]).then_inc(late_done, 1)
                if i < FIRST and i % 2 == 1:
                    act.wait_ge(late_v_ready, i // 2 + 1)
                    act.activation(r.v[:, CH + i - 1:CH + i + 1, :, 0:TW],
                                   ps_o[:, 2 * P:4 * P].rearrange("p (t h d) -> p t h d", t=2, h=TH), ACT.Copy).then_inc(late_v_done, 1)
                if i == FIRST - 1:
                    act.wait_ge(late_v_done, FIRST // 2)
                if i == PAIR and not last:
                    act.wait_ge(values_done, at.tile0 + 2)
                    act.nop(nofuse=True)
                    fetch_values((at.pair + 1) // (PAIRS // B) * CH)

            act.activation(prime[:, :], m.pid, ACT.Exp, scale=-1.0)
            act.sem_inc(s_free, 2)
            act.sem_inc(acc_out, 1)
            for k in range(8):
                act.wait_ge(proj_ready, k + 1)
                copy_projection(0, k, start_banks[k % 4]).then_inc(proj_done, 1)
            act.wait_ge(v_in, 1)
            fetch_values(0)
            all_exp(place(act, 0), 0)
            steps(act, step)

        @block.gpsimd
        def _(pool):
            def query(at, tile_rel):
                for grp in range(2):
                    ins = pool.tensor_tensor(qz[:, tile_rel % 2, 4 * grp:4 * grp + 4, :],
                                             qT[:, grp, bass.ds(at.pair * (2 * P) + tile_rel * P, P)].unsqueeze(1).broadcast_to([P, 4, P]),
                                             m.quarter.unsqueeze(2).broadcast_to([P, 4, P]), ALU.mult)
                ins.then_inc(q_in, 1)

            def step(at, i, last):
                if i < PAIR or not last:
                    pool.wait_ge(left_exp, at.item0 + (i + 1))
                    pool.tensor_tensor(ex[:, i % 4, :], ex[:, i % 4, :], left[:, i % 4, :], ALU.subtract).then_inc(kept, 1)
                if i % TH == 2 and (i < TH or not last):
                    query(at, i // TH + 1)
                if i == FIRST - 1:
                    pool.wait_ge(late_done, FIRST)

            pool.memset(vseq[:, :, :, :], 0.0).then_inc(v_in, 1)
            pool.sem_inc(kept, KEPT)
            pool.wait_ge(proj_done, 2)
            query(place(pool, 0), 0)
            pool.wait_ge(proj_done, 8)
            steps(pool, step)

        @block.vector
        def _(dve):
            def first_max(at, i):
                dve.wait_ge(s_ready, at.item0 + (i + 1))
                dve.nop(nofuse=True)
                dve.max(top[:, i % 2, 0, :], ps_s[:, i % 2, :]).then_inc(max_done[0], 1)

            def first_replace(at, i):
                dve.wait_ge(max_done[0], at.item0 + (i + 1))
                dve.tensor_scalar(ntop[:, i % 4:i % 4 + 1], top[:, i % 2, 0, 0:1], -SC, None, ALU.mult)
                dve.wait_ge(kept, at.item0 + (i + 1))
                dve.nop(nofuse=True)
                dve.match_replace(left[:, i % 4, :], top[:, i % 2, 0, :], ps_s[:, i % 2, :], -BIG).then_inc(first_out, 1)

            def second_max(at, i):
                dve.wait_ge(first_out, at.item0 + (i + 1))
                dve.nop(nofuse=True)
                dve.max(top[:, i % 2, 1, :], left[:, i % 4, :]).then_inc(max_done[1], 1)

            def second_replace(at, i):
                dve.wait_ge(max_done[1], at.item0 + (i + 1))
                dve.nop(nofuse=True)
                dve.match_replace(left[:, i % 4, :], top[:, i % 2, 1, :], left[:, i % 4, :], -BIG).then_inc(left_ready, 1)

            def step(at, i, last):
                h = i % TH
                more, here = i + 1 < PAIR or not last, i < PAIR or not last
                if more:
                    first_max(at, i + 1)
                if here:
                    second_max(at, i)
                if more:
                    first_replace(at, i + 1)
                if here:
                    second_replace(at, i)
                if i >= TH and h == 3:
                    tile = at.tile0 + (i // TH - 1)
                    out = ps_p[:, 0:2 * P].rearrange("p (h d) -> p h d", h=TH)
                    dve.wait_ge(acc_turned, tile + 1)
                    dve.reciprocal(rden[:, :], out[:, :, TW]).then_inc(rden_ready, 1)
                    dve.wait_ge(rden_ready, tile + 1)
                    dve.tensor_tensor(o[:, :].rearrange("p (h d) -> p h d", h=TH), out[:, :, 0:TW],
                                      rden[:, :].unsqueeze(2).broadcast_to([P, TH, TW]), ALU.mult).then_inc(o_ready, 1)
                if i >= TH and h == 7:
                    tile = at.tile0 + (i // TH - 1)
                    dve.wait_ge(out_ready, tile + 1)
                    hh = m.h[:, bass.ds(tile, 1), :]
                    dve.tensor_tensor(hh, hh, ps_p[:, 0:P].unsqueeze(1), ALU.add).then_inc(out_used, 1)

            dve.sem_inc(out_used, 1)
            first_max(place(dve, 0), 0)
            first_replace(place(dve, 0), 0)
            steps(dve, step)


SSM_ST = 64


def ssm_memory(nc, m, ctx):
    def sb(name, shape, dt=F32):
        return ctx.enter_context(nc.sbuf_tensor(f"l3_{name}", shape, dt))

    r = Core()
    r.w1, r.w2, r.v1, r.v2, r.dd = (sb(x, [P, P]) for x in ("w1", "w2", "v1", "v2", "dd"))
    r.cos, r.sin, r.fade = sb("cos", [P, S]), sb("sin", [P, S]), sb("fade", [P, 1])
    m.ssm = r


def stage_l3_attn(nc, m, w):
    layernorm(nc, m, "ln_l3a", m.h, m.xn, m.xnT)
    ssm_run(nc, m, m.ssm)


def ssm_prepare(nc, m, r, w, sp_loads, act_loads, w_first, w_turn):
    ST = SSM_ST
    with ExitStack() as ctx:
        def sb(name, shape, dt=F32):
            return ctx.enter_context(nc.sbuf_tensor(f"l3p_{name}", shape, dt))

        small = sb("small", [P, 32])
        r.B, r.C, r.D = sb("B", [ST, D, 2]), sb("C", [P, ST, 2]), sb("D", [P, 1])
        r.par = sb("par", [P, 3])
        names = ("step angle turns r half sh sr c s a b den t1 t2 gr gi magr pc ps").split()
        v = {name: small[:, i:i + 1] for i, name in enumerate(names)}
        power = sb("power", [P, 2, 12])
        tmp = sb("tmp", [P, 2, S // 2])
        bbar = sb("bbar", [ST, 2, D])
        tb = sb("tb", [ST, 2, D])
        x1, x2 = sb("x1", [P, 2, ST]), sb("x2", [P, 2, ST])
        ps_b = ctx.enter_context(nc.psum_tensor("l3p_ps_b", [P, BANK], F32))
        ps_c = ctx.enter_context(nc.psum_tensor("l3p_ps_c", [P, BANK], F32))
        sem = signals(nc, m, "l3p_")
        dve_step, act_step, outs, turned, x_ready = (sem(k) for k in ("dve_step", "act_step", "outs", "turned", "x_ready"))
        r.par_in, r.n_par = sem("par_in"), 9 * 16
        TWO_PI = 2.0 * np.pi
        TWO_PI_HI = 6.28125
        ROUND = 12582912.0
        PI_BELOW = 3.1415925
        block = ctx.enter_context(nc.Block())

        @block.sync
        def _(sp):
            for half in range(2):
                for i, name in enumerate(("Lambda_re", "Lambda_im", "log_step")):
                    sp.dma_start(r.par[half * ST:(half + 1) * ST, i:i + 1], col(w["L3_attn_" + name]),
                                 allow_slow_non_contiguous=True).then_inc(r.par_in, 16)
            sp.dma_start(r.B[:, :, :], w["L3_attn_B"]).then_inc(r.par_in, 16)
            sp.dma_start(r.C[:, :, :], w["L3_attn_C"]).then_inc(r.par_in, 16)
            sp.dma_start(r.D[:, :], col(w["L3_attn_D"]), allow_slow_non_contiguous=True).then_inc(r.par_in, 16)
            for dst, src in sp_loads:
                sp.dma_start(dst, src, allow_slow_non_contiguous=True).then_inc(w_first, 16)
            for dst, src, s in m.later_loads:
                sp.dma_start(dst, src, allow_slow_non_contiguous=True).then_inc(s, 16)

        @block.scalar
        def _(act):
            for dst, src in act_loads:
                act.dma_start(dst, src, allow_slow_non_contiguous=True).then_inc(w_turn, 16)
            act.wait_ge(r.par_in, r.n_par)
            act.activation(v["step"], r.par[:, 2:3], ACT.Exp).then_inc(act_step, 1)
            act.wait_ge(act_step, 1)
            act.activation(r.fade[:, :], r.par[:, 0:1], ACT.Exp, scale=v["step"]).then_inc(act_step, 1)
            act.wait_ge(dve_step, 7)
            act.activation(v["sr"], v["r"], ACT.Sin).then_inc(act_step, 1)
            act.activation(v["sh"], v["half"], ACT.Sin).then_inc(act_step, 1)
            act.wait_ge(turned, 1)
            act.activation(r.w1[:, :], ps_b[:, 0:P], ACT.Copy)
            act.activation(r.w2[:, 0:ST], ps_b[:, ST:2 * ST], ACT.Copy)
            act.activation(r.w2[:, ST:P], ps_b[:, 0:ST], ACT.Copy, scale=-1.0)
            act.activation(r.v1[:, :], ps_c[:, 0:P], ACT.Copy)
            act.activation(r.v2[:, :], ps_c[:, P:2 * P], ACT.Copy)

        @block.gpsimd
        def _(pool):
            pool.wait_ge(r.par_in, r.n_par)
            pool.tensor_scalar(x1[:, 0, :], r.C[:, :, 0], 2.0, None, ALU.mult)
            pool.tensor_scalar(x1[:, 1, :], r.C[:, :, 1], -2.0, None, ALU.mult)
            pool.tensor_scalar(x2[:, 0, :], r.C[:, :, 1], -2.0, None, ALU.mult)
            pool.tensor_scalar(x2[:, 1, :], r.C[:, :, 0], -2.0, None, ALU.mult)
            pool.wait_ge(w_first, 16 * len(sp_loads))
            pool.tensor_scalar(r.dd[:, :], m.ident, r.D[:, 0:1], None, ALU.mult).then_inc(x_ready, 1)

        @block.tensor
        def _(pe):
            pe.wait_ge(w_first, 16 * len(sp_loads))
            pe.wait_ge(x_ready, 1)
            pe.transpose(ps_c[:, 0:P], x1[:, :, :].rearrange("p a s -> p (a s)"), m.ident)
            pe.transpose(ps_c[:, P:2 * P], x2[:, :, :].rearrange("p a s -> p (a s)"), m.ident)
            pe.wait_ge(outs, 1)
            pe.transpose(ps_b[:, 0:ST], bbar[:, 0, :], m.ident[0:ST, 0:ST])
            pe.transpose(ps_b[:, ST:P], bbar[:, 1, :], m.ident[0:ST, 0:ST]).then_inc(turned, 1)

        @block.vector
        def _(dve):
            steps = [0]

            def link(ins):
                steps[0] += 1
                ins.then_inc(dve_step, 1)
                dve.wait_ge(dve_step, steps[0])

            re, im = r.par[:, 0:1], r.par[:, 1:2]
            dve.wait_ge(act_step, 1)
            link(dve.tensor_tensor(v["angle"], im, v["step"], ALU.mult))
            link(dve.tensor_scalar(v["turns"], v["angle"], 1.0 / TWO_PI, ROUND, ALU.mult, ALU.add))
            link(dve.tensor_scalar(v["turns"], v["turns"], ROUND, None, ALU.subtract))
            link(dve.scalar_tensor_tensor(v["r"], v["turns"], -TWO_PI_HI, v["angle"], ALU.mult, ALU.add))
            link(dve.scalar_tensor_tensor(v["r"], v["turns"], -(TWO_PI - TWO_PI_HI), v["r"], ALU.mult, ALU.add))
            link(dve.tensor_scalar(v["r"], v["r"], PI_BELOW, -PI_BELOW, ALU.min, ALU.max))
            link(dve.tensor_scalar(v["half"], v["r"], 0.5, None, ALU.mult))
            link(dve.tensor_tensor(v["t1"], re, re, ALU.mult))
            link(dve.scalar_tensor_tensor(v["den"], im, im, v["t1"], ALU.mult, ALU.add))
            link(dve.reciprocal(v["den"], v["den"]))
            dve.wait_ge(act_step, 4)
            link(dve.tensor_copy(power[:, 1, 0:1], v["sr"]))
            link(dve.tensor_tensor(v["t1"], v["sh"], v["sh"], ALU.mult))
            link(dve.tensor_scalar(power[:, 0, 0:1], v["t1"], -2.0, 1.0, ALU.mult, ALU.add))
            link(dve.tensor_scalar(v["a"], power[:, 0, 0:1], r.fade[:, 0:1], 1.0, ALU.mult, ALU.subtract))
            link(dve.tensor_tensor(v["b"], power[:, 1, 0:1], r.fade[:, 0:1], ALU.mult))
            link(dve.tensor_tensor(v["t1"], v["a"], re, ALU.mult))
            link(dve.scalar_tensor_tensor(v["gr"], v["b"], im, v["t1"], ALU.mult, ALU.add))
            link(dve.tensor_tensor(v["gr"], v["gr"], v["den"], ALU.mult))
            link(dve.tensor_tensor(v["t2"], v["a"], im, ALU.mult))
            link(dve.scalar_tensor_tensor(v["gi"], v["b"], re, v["t2"], ALU.mult, ALU.subtract))
            link(dve.tensor_tensor(v["gi"], v["gi"], v["den"], ALU.mult))
            gr, gi = small[0:ST, names.index("gr"):names.index("gr") + 1], small[0:ST, names.index("gi"):names.index("gi") + 1]
            link(dve.tensor_scalar(tb[:, 0, :], r.B[:, :, 1], gi, None, ALU.mult))
            link(dve.tensor_scalar(tb[:, 1, :], r.B[:, :, 0], gi, None, ALU.mult))
            link(dve.scalar_tensor_tensor(bbar[:, 0, :], r.B[:, :, 0], gr, tb[:, 0, :], ALU.mult, ALU.subtract))
            link(dve.scalar_tensor_tensor(bbar[:, 1, :], r.B[:, :, 1], gr, tb[:, 1, :], ALU.mult, ALU.add))
            dve.memset(r.cos[:, 0:1], 1.0).then_inc(outs, 1)
            link(dve.memset(r.sin[:, 0:1], 0.0))
            for i in range(10):
                n = 1 << i
                pc, ps = power[:, 0, i:i + 1], power[:, 1, i:i + 1]
                c0, s0, c1, s1 = r.cos[:, 0:n], r.sin[:, 0:n], r.cos[:, n:2 * n], r.sin[:, n:2 * n]
                dve.tensor_scalar(tmp[:, 0, 0:n], s0, ps, None, ALU.mult)
                dve.tensor_scalar(tmp[:, 1, 0:n], c0, ps, None, ALU.mult)
                link(dve.tensor_tensor(v["t1"], ps, ps, ALU.mult))
                dve.scalar_tensor_tensor(c1, c0, pc, tmp[:, 0, 0:n], ALU.mult, ALU.subtract)
                dve.scalar_tensor_tensor(s1, s0, pc, tmp[:, 1, 0:n], ALU.mult, ALU.add)
                dve.scalar_tensor_tensor(power[:, 0, i + 1:i + 2], pc, pc, v["t1"], ALU.mult, ALU.subtract)
                link(dve.scalar_tensor_tensor(power[:, 1, i + 1:i + 2], pc, 2.0, ps, ALU.mult, ALU.mult))


def ssm_run(nc, m, r):
    JOBS = N // BANK
    with ExitStack() as ctx:
        def sb(name, shape, dt=F32):
            return ctx.enter_context(nc.sbuf_tensor(f"l3r_{name}", shape, dt))

        sem = signals(nc, m, "l3r_")

        z1, z2, z = sb("z1", [P, 2, BANK]), sb("z2", [P, 2, BANK]), sb("z", [P, 2, BANK])
        y, u, v = sb("y", [P, JOBS, BANK]), sb("u", [P, 2, BANK]), sb("v", [P, 2, BANK])
        ps_1 = ctx.enter_context(nc.psum_tensor("l3r_ps_1", [P, 2, BANK], F32))
        ps_2 = ctx.enter_context(nc.psum_tensor("l3r_ps_2", [P, 2, BANK], F32))
        ps_o = ctx.enter_context(nc.psum_tensor("l3r_ps_o", [P, 2, BANK], F32))
        bu_ready, bu_used, z_ready, y_ready, u_ready, v_ready, out_ready, out_used = (
            sem(k) for k in ("bu_ready", "bu_used", "z_ready", "y_ready", "u_ready", "v_ready", "out_ready", "out_used"))
        block = ctx.enter_context(nc.Block())

        @block.tensor
        def _(pe):
            def drive(j):
                if j >= 2:
                    pe.wait_ge(bu_used, j - 1)
                pe.matmul(ps_1[:, j % 2, :], r.w1[:, :], m.xnT[:, j * BANK:(j + 1) * BANK], start=True, stop=True)
                pe.matmul(ps_2[:, j % 2, :], r.w2[:, :], m.xnT[:, j * BANK:(j + 1) * BANK], start=True, stop=True).then_inc(bu_ready, 1)

            drive(0)
            for j in range(JOBS):
                if j + 1 < JOBS:
                    drive(j + 1)
                pe.wait_ge(u_ready, j + 1)
                pe.wait_ge(v_ready, j + 1)
                if j >= 2:
                    pe.wait_ge(out_used, j - 1)
                for t in range(4):
                    c = slice(t * P, (t + 1) * P)
                    pe.matmul(ps_o[:, j % 2, c], u[:, j % 2, c], r.v1[:, :], start=True, stop=False)
                    pe.matmul(ps_o[:, j % 2, c], v[:, j % 2, c], r.v2[:, :], start=False, stop=False)
                    ins = pe.matmul(ps_o[:, j % 2, c], m.xnT[:, j * BANK + t * P:j * BANK + (t + 1) * P], r.dd[:, :], start=False, stop=True)
                ins.then_inc(out_ready, 1)

        @block.vector
        def _(dve):
            def add(j):
                dve.wait_ge(out_ready, j + 1)
                hh = m.h[:, 4 * j:4 * j + 4, :]
                dve.tensor_tensor(hh, hh, ps_o[:, j % 2, :].rearrange("p (t d) -> p t d", t=4), ALU.add).then_inc(out_used, 1)

            for j in range(JOBS):
                k, c = j % 2, slice((j % 2) * BANK, (j % 2 + 1) * BANK)
                dve.wait_ge(bu_ready, j + 1)
                dve.tensor_tensor(z1[:, k, :], ps_1[:, k, :], r.cos[:, c], ALU.mult)
                dve.tensor_tensor(z2[:, k, :], ps_2[:, k, :], r.sin[:, c], ALU.mult).then_inc(bu_used, 1)
                dve.wait_ge(bu_used, j + 1)
                dve.tensor_tensor(z[:, k, :], z1[:, k, :], z2[:, k, :], ALU.add).then_inc(z_ready, 1)
                dve.wait_ge(z_ready, j + 1)
                start = 0.0 if k == 0 else y[:, j - 1, BANK - 1:BANK]
                dve.tensor_tensor_scan(y[:, j, :], r.fade[:, 0:1].broadcast_to([P, BANK]), z[:, k, :], start, ALU.mult, ALU.add)\
                   .then_inc(y_ready, 1)
                dve.wait_ge(y_ready, j + 1)
                if j >= 2:
                    dve.wait_ge(out_ready, j - 1)
                dve.tensor_tensor(u[:, k, :], y[:, j, :], r.cos[:, c], ALU.mult).then_inc(u_ready, 1)
                if j >= 1:
                    add(j - 1)
            add(JOBS - 1)

        @block.gpsimd
        def _(pool):
            for j in range(JOBS):
                k, c = j % 2, slice((j % 2) * BANK, (j % 2 + 1) * BANK)
                pool.wait_ge(y_ready, j + 1)
                if j >= 2:
                    pool.wait_ge(out_ready, j - 1)
                pool.tensor_tensor(v[:, k, :], y[:, j, :], r.sin[:, c], ALU.mult).then_inc(v_ready, 1)


L3_E, L3_I = 16, 96


def stage_l3_ffn(nc, m, w):
    G = L3_E + 1
    with ExitStack() as ctx:
        def sb(name, shape, dt=F32):
            return ctx.enter_context(nc.sbuf_tensor(f"l3f_{name}", shape, dt))

        r = Core()
        r.hT, r.gates = m.xnT, sb("gates", [P, TILES, G])
        r.gate_w, r.b_r = sb("gate_w", [P, L3_E]), sb("b_r", [1, L3_E])
        r.raw_act, r.raw_b1 = sb("raw_act", [P, G, 5]), sb("raw_b1", [G, 2 * L3_I])
        r.bias = sb("bias", [L3_I, 2, G])
        r.clamp = sb("clamp", [P, G, 2])
        r.limit = sb("limit", [P, 2, 2, G])
        r.b2_dram, r.b2_shared = w["L3_ffn_expert_b2"], row(w["L3_ffn_shared_b2"])
        sem = signals(nc, m, "l3f_")
        r.s_router, r.n_router = sem("router"), 32
        r.s_par, r.n_par = sem("par"), 64
        with nc.Block() as block:
            @block.sync
            def _(sp):
                sp.dma_start(r.gate_w[:, :], w["L3_ffn_gate_w"]).then_inc(r.s_router, 16)
                sp.dma_start(r.b_r[:, :], row(w["L3_ffn_gate_b"])).then_inc(r.s_router, 16)
                sp.dma_start(r.raw_act[:, 0:L3_E, :], w["L3_ffn_expert_act"].rearrange("(o e) a -> o e a", o=1)
                             .broadcast_to([P, L3_E, 5])).then_inc(r.s_par, 16)
                sp.dma_start(r.raw_act[:, L3_E, :], row(w["L3_ffn_shared_act"]).broadcast_to([P, 5])).then_inc(r.s_par, 16)
                sp.dma_start(r.raw_b1[0:L3_E, :], w["L3_ffn_expert_b1"]).then_inc(r.s_par, 16)
                sp.dma_start(r.raw_b1[L3_E:G, :], row(w["L3_ffn_shared_b1"])).then_inc(r.s_par, 16)
        layernorm(nc, m, "ln_l3f", m.h, m.xn, m.xnT)
        router(nc, m, r, "l3r", L3_E, r.gate_w[:, :], 1)
        l3_expert_scalars(nc, m, r)
        l3_experts(nc, m, r, w)


def l3_expert_scalars(nc, m, r):
    G = L3_E + 1
    with ExitStack() as ctx:
        size, ex = (ctx.enter_context(nc.sbuf_tensor(f"l3s_{x}", [P, G, 2], F32)) for x in ("size", "ex"))
        ps = ctx.enter_context(nc.psum_tensor("l3s_ps", [P, BANK], F32))
        sem = signals(nc, m, "l3s_")
        turned, dve_step, act_step = (sem(x) for x in ("turned", "dve_step", "act_step"))
        block = ctx.enter_context(nc.Block())

        @block.tensor
        def _(pe):
            pe.wait_ge(r.s_par, r.n_par)
            pairs = r.raw_b1[:, :].rearrange("e (i two) -> e i two", two=2)
            for k in range(2):
                ins = pe.transpose(ps[0:L3_I, k * G:(k + 1) * G], pairs[:, :, k], m.ident[0:G, 0:G])
            ins.then_inc(turned, 1)

        @block.scalar
        def _(act):
            act.wait_ge(dve_step, 1)
            act.activation(ex[:, :, :], size[:, :, :], ACT.Exp, scale=-1.0).then_inc(act_step, 1)
            act.wait_ge(dve_step, 2)
            act.activation(ex[:, :, :], ex[:, :, :], ACT.Ln).then_inc(act_step, 1)

        @block.vector
        def _(dve):
            steps = [0]

            def link(ins):
                steps[0] += 1
                ins.then_inc(dve_step, 1)
                dve.wait_ge(dve_step, steps[0])

            raw = r.raw_act[:, :, 3:5]
            dve.wait_ge(r.s_par, r.n_par)
            link(dve.scalar_tensor_tensor(size[:, :, :], raw, -1.0, raw, ALU.mult, ALU.max))
            dve.wait_ge(act_step, 1)
            link(dve.tensor_scalar(ex[:, :, :], ex[:, :, :], 1.0, None, ALU.add))
            dve.wait_ge(act_step, 2)
            link(dve.scalar_tensor_tensor(r.clamp[:, :, :], raw, 0.0, ex[:, :, :], ALU.max, ALU.add))
            dve.wait_ge(turned, 1)
            shift = r.raw_act[:, :, 2]
            dve.tensor_copy(r.bias[:, 0, :], ps[0:L3_I, 0:G])
            dve.tensor_tensor(r.bias[:, 1, :], ps[0:L3_I, G:2 * G], shift[0:L3_I, :], ALU.add)
            dve.tensor_copy(r.limit[:, 0, 0, :], r.clamp[:, :, 0])
            dve.tensor_scalar(r.limit[:, 0, 1, :], r.clamp[:, :, 0], -1.0, None, ALU.mult)
            dve.tensor_tensor(r.limit[:, 1, 0, :], shift, r.clamp[:, :, 1], ALU.add)
            dve.tensor_tensor(r.limit[:, 1, 1, :], shift, r.clamp[:, :, 1], ALU.subtract)


def l3_experts(nc, m, r, w):
    G, GROUPS = L3_E + 1, 4
    UNITS = 2 * GROUPS
    LOOPS = L3_E // 2
    with ExitStack() as ctx:
        def sb(name, shape, dt=F32):
            return ctx.enter_context(nc.sbuf_tensor(f"l3e_{name}", shape, dt))

        sem = signals(nc, m, "l3e_")

        w1, w2 = sb("w1", [P, 2, 2 * L3_I]), sb("w2", [L3_I, 2, D])
        gate, sig, up_, te = (sb(x, [L3_I, GROUPS, BANK]) for x in ("gate", "sig", "up", "te"))
        gT, b2 = sb("gT", [G, N]), sb("b2", [G, D])
        prime = sb("prime", [P, 1])
        ps_g = ctx.enter_context(nc.psum_tensor("l3e_ps_g", [P, 2, BANK], F32))
        ps_u = ctx.enter_context(nc.psum_tensor("l3e_ps_u", [P, 2, BANK], F32))
        ps_d = ctx.enter_context(nc.psum_tensor("l3e_ps_d", [P, 2, BANK], F32))
        w1_in, w2_in = [sem("w1_in0"), sem("w1_in1")], [sem("w2_in0"), sem("w2_in1")]
        g_ready, u_ready, g_out, u_out, clipped, sig_ready, t1_ready, te_ready, down_ready, down_free = (
            sem(k) for k in ("g_ready", "u_ready", "g_out", "u_out", "clipped", "sig_ready", "t1_ready", "te_ready",
                             "down_ready", "down_free"))
        b2_in, gates_turned, gates_in, bias_ready, bias_added = (
            sem(x) for x in ("b2_in", "gates_turned", "gates_in", "bias_ready", "bias_added"))
        gates_scaled = sem("gates_scaled")
        gates_banks = [ps_g[0:G, 0, :], ps_g[0:G, 1, :], ps_u[0:G, 0, :], ps_u[0:G, 1, :]]
        block = ctx.enter_context(nc.Block())

        @block.sync
        def _(sp):
            def load(k, w1_src, w2_src, units):
                sp.wait_ge(u_ready, FROM + units)
                sp.dma_start(w1[:, k, :], w1_src).then_inc(w1_in[k], 16)
                sp.wait_ge(down_ready, FROM + units)
                sp.dma_start(w2[:, k, :], w2_src).then_inc(w2_in[k], 16)

            def expert(e):
                return (w["L3_ffn_expert_w1"][bass.ds(e, 1), :, :].rearrange("e p f -> p (e f)"),
                        w["L3_ffn_expert_w2"][bass.ds(e, 1), :, :].rearrange("e p f -> p (e f)"))

            load(0, *expert(0), 0)
            sp.dma_start(b2[0:L3_E, :], r.b2_dram).then_inc(b2_in, 16)
            sp.dma_start(b2[L3_E:G, :], r.b2_shared).then_inc(b2_in, 16)
            with sp.Fori(0, LOOPS - 1) as it:
                load(1, *expert(it * 2 + 1), it * UNITS)
                load(0, *expert(it * 2 + 2), it * UNITS + GROUPS)
            load(1, *expert(L3_E - 1), (LOOPS - 1) * UNITS)
            load(0, w["L3_ffn_shared_w1"], w["L3_ffn_shared_w2"], (LOOPS - 1) * UNITS + GROUPS)

        @block.tensor
        def _(pe):
            def up(it, u):
                k, g, n = (u // GROUPS) % 2, u % GROUPS, it * UNITS + u
                if g == 0:
                    pe.wait_ge(w1_in[k], (it + u // UNITS) * 16 + 16)
                if not (isinstance(n, int) and n < 2):
                    pe.wait_ge(g_out, n - 1)
                pe.matmul(ps_g[0:L3_I, u % 2, :], w1[:, k, 0::2], r.hT[:, g * BANK:(g + 1) * BANK], start=True, stop=True).then_inc(g_ready, 1)
                if not (isinstance(n, int) and n < 2):
                    pe.wait_ge(u_out, n - 1)
                pe.matmul(ps_u[0:L3_I, u % 2, :], w1[:, k, 1::2], r.hT[:, g * BANK:(g + 1) * BANK], start=True, stop=True).then_inc(u_ready, 1)

            def down(it, u):
                k, g, n = (u // GROUPS) % 2, u % GROUPS, it * UNITS + u
                if g == 0:
                    pe.wait_ge(w2_in[k], it * 16 + 16)
                pe.wait_ge(te_ready, n + 1)
                pe.wait_ge(down_free, n + 1)
                for t in range(4):
                    ins = pe.matmul(ps_d[:, u % 2, t * P:(t + 1) * P], te[:, g, t * P:(t + 1) * P], w2[:, k, :], start=True, stop=True)
                ins.then_inc(down_ready, 1)

            for signal in (u_ready, down_ready):
                pe.sem_inc(signal, FROM)
            for t in range(TILES):
                ins = pe.transpose(gates_banks[t // 4][:, (t % 4) * P:(t % 4 + 1) * P], r.gates[:, t, :], m.ident)
                if t % 4 == 3:
                    ins.then_inc(gates_turned, 1)
            pe.wait_ge(gates_in, 4)
            up(0, 0)
            pe.wait_ge(b2_in, 32)
            for t in range(TILES):
                g = t // 4
                if g >= 2 and t % 4 == 0:
                    pe.wait_ge(bias_added, g - 1)
                ins = pe.matmul(ps_d[:, g % 2, (t % 4) * P:(t % 4 + 1) * P], gT[:, t * P:(t + 1) * P], b2[:, :], start=True, stop=True)
                if t % 4 == 3:
                    ins.then_inc(bias_ready, 1)
            up(0, 1)
            up(0, 2)
            with pe.Fori(0, LOOPS) as it:
                for u in range(UNITS):
                    up(it, u + 3)
                    down(it, u)
            up(LOOPS, 3)
            for u in range(GROUPS):
                down(LOOPS, u)

        @block.scalar
        def _(act):
            def fetch(it, u):
                g, n, e = u % GROUPS, it * UNITS + u, it * 2 + u // GROUPS
                act.wait_ge(g_ready, n + 1)
                act.nop(nofuse=True)
                act.activation(gate[:, g, :], ps_g[0:L3_I, u % 2, :], ACT.Identity, bias=r.bias[:, 0, bass.ds(e, 1)]).then_inc(g_out, 1)
                act.wait_ge(u_ready, FROM + n + 1)
                act.nop(nofuse=True)
                act.activation(up_[:, g, :], ps_u[0:L3_I, u % 2, :], ACT.Identity, bias=r.bias[:, 1, bass.ds(e, 1)]).then_inc(u_out, 1)

            def sigmoid(it, u):
                g, n, e = u % GROUPS, it * UNITS + u, it * 2 + u // GROUPS
                act.wait_ge(clipped, n + 1)
                act.nop(nofuse=True)
                act.activation(sig[:, g, :], gate[:, g, :], ACT.Sigmoid, scale=r.raw_act[0:L3_I, bass.ds(e, 1), 0]).then_inc(sig_ready, 1)

            act.activation(prime[:, :], m.pid, ACT.Sigmoid)
            for g in range(4):
                act.wait_ge(gates_turned, g + 1)
                act.activation(gT[:, g * BANK:(g + 1) * BANK], gates_banks[g], ACT.Copy).then_inc(gates_in, 1)
            fetch(0, 0)
            with act.Fori(0, LOOPS) as it:
                for u in range(UNITS):
                    fetch(it, u + 1)
                    sigmoid(it, u)
            for u in range(GROUPS):
                if u + 1 < GROUPS:
                    fetch(LOOPS, u + 1)
                sigmoid(LOOPS, u)

        @block.gpsimd
        def _(pool):
            def hidden(it, u):
                g, n = u % GROUPS, it * UNITS + u
                pool.wait_ge(sig_ready, n + 1)
                pool.tensor_tensor(sig[:, g, :], gate[:, g, :], sig[:, g, :], ALU.mult).then_inc(t1_ready, 1)
                pool.wait_ge(t1_ready, n + 1)
                pool.tensor_tensor(te[:, g, :], up_[:, g, :], sig[:, g, :], ALU.mult).then_inc(te_ready, 1)

            with pool.Fori(0, LOOPS) as it:
                for u in range(UNITS):
                    hidden(it, u)
            for u in range(GROUPS):
                hidden(LOOPS, u)

        @block.vector
        def _(dve):
            def clip(it, u):
                g, n, e = u % GROUPS, it * UNITS + u, it * 2 + u // GROUPS
                dve.wait_ge(u_out, n + 1)
                for k, x in enumerate((up_, gate)):
                    ins = dve.tensor_scalar(x[:, g, :], x[:, g, :], r.limit[0:L3_I, 1 - k, 0, bass.ds(e, 1)],
                                            r.limit[0:L3_I, 1 - k, 1, bass.ds(e, 1)], ALU.min, ALU.max)
                ins.then_inc(clipped, 1)

            def add(it, u):
                g, n, e = u % GROUPS, it * UNITS + u, it * 2 + u // GROUPS
                dve.wait_ge(down_free, n + 1)
                dve.wait_ge(down_ready, FROM + n + 1)
                for t in range(4):
                    hh = m.h[:, 4 * g + t, :]
                    ins = dve.scalar_tensor_tensor(hh, ps_d[:, u % 2, t * P:(t + 1) * P], r.gates[:, 4 * g + t, bass.ds(e, 1)], hh,
                                                   ALU.mult, ALU.add)
                ins.then_inc(down_free, 1)

            dve.wait_ge(gates_turned, 4)
            dve.tensor_tensor(r.gates[:, :, :], r.gates[:, :, :], r.raw_act[:, :, 1].unsqueeze(1).broadcast_to([P, TILES, G]),
                              ALU.mult).then_inc(gates_scaled, 1)
            for g in range(4):
                dve.wait_ge(bias_ready, g + 1)
                hh = m.h[:, 4 * g:4 * g + 4, :]
                dve.tensor_tensor(hh, hh, ps_d[:, g % 2, :].rearrange("p (t d) -> p t d", t=4), ALU.add).then_inc(bias_added, 1)
            dve.wait_ge(gates_scaled, 1)
            dve.wait_ge(bias_added, 4)
            dve.sem_inc(down_free, 2)
            for u in range(3):
                clip(0, u)
            with dve.Fori(0, LOOPS) as it:
                for u in range(UNITS):
                    clip(it, u + 3)
                    add(it, u)
            clip(LOOPS, 3)
            for u in range(GROUPS):
                add(LOOPS, u)


def tower_memory(nc, m, ctx):
    def sb(name, shape, dt=F32):
        return ctx.enter_context(nc.sbuf_tensor(name, shape, dt))

    m.consts = sb("consts", [P, sum(CONST_COLS.values())])
    at, part = 0, {}
    for name, width in CONST_COLS.items():
        part[name] = m.consts[:, at:at + width]
        at += width
    m.ident, m.interp, m.pairmean, m.one = (part[x] for x in ("ident", "interp", "pairmean", "one"))
    m.ropecos, m.ropesin, m.expand, m.pid = (part[x] for x in ("ropecos", "ropesin", "expand", "pid"))
    m.quarter, m.order = part["quarter"], part["order"]
    m.h, m.xn, m.xnT = sb("h", [P, TILES, D]), sb("xn", [P, TILES, D]), sb("xnT", [P, N])
    m.neghalf = sb("neghalf", [P, TILES])
    m.wqkv0, m.fc1T, m.fc2T = sb("wqkv0", [P, 3, D]), sb("fc1T", [P, 4, D]), sb("fc2T", [P, 4, 64])
    m.w1f, m.fc1_b, m.fc2_b = sb("w1f", [P, 512]), sb("fc1_b", [P, 4]), sb("fc2_b", [1, 64])
    m.wqkv2, m.wproj2, m.wqkv3, m.wo = sb("wqkv2", [P, 3, D]), sb("wproj2", [P, D]), sb("wqkv3", [P, 3, D]), sb("wo", [P, D])
    m.wrT = sb("wrT", [P, 8])
    m.w_attn, m.w_proj1 = sb("w_attn", [P, 3 * HD + RET_H]), sb("w_proj1", [P, 4, D])
    m.s_wattn = ctx.enter_context(nc.semaphore("s_wattn"))
    m.s_wproj1 = ctx.enter_context(nc.semaphore("s_wproj1"))
    m.s_consts = ctx.enter_context(nc.semaphore("s_consts"))


def l0_memory(nc, m, ctx):
    def sb(name, shape, dt=F32):
        return ctx.enter_context(nc.sbuf_tensor(name, shape, dt))

    m.ids, m.onehot, m.pairhot = sb("ids", [P, N], I32), sb("onehot", [VOC, N]), sb("pairhot", [VOC, N // 2])
    m.feat, m.tok_w1, m.tok_w2 = sb("feat", [VOC, 37]), sb("tok_w1", [37, 64]), sb("tok_w2", [64, D])
    m.tok_b1, m.tok_b2 = sb("tok_b1", [64, 1]), sb("tok_b2", [1, D])
    m.bq, m.bk, m.bv = sb("bq", [P, 1]), sb("bk", [P, 1]), sb("bv", [1, D])
    m.table_x, m.table_tx = sb("table_x", [VOC, B, D]), sb("table_tx", [VOC, B, D])


def stage_l0(nc, m, w):
    stage_l0_tables(nc, m, w)
    stage_l0_ffn(nc, m, w)


def tower(nc, w, out, l0=stage_l0, stages=(stage_l1_attn, stage_l1_ffn, recycle, stage_l2_attn, stage_l2_ffn, recycle,
                                           stage_l3_attn, stage_l3_ffn)):
    with ExitStack() as ctx:
        m = Core()
        m.signals = []
        tower_memory(nc, m, ctx)
        m.later_loads = [
            (m.consts[:, FIRST_CONSTS:], w["consts"][:, FIRST_CONSTS:], m.s_consts),
            (m.w_attn[:, :], w["L1_attn_w_attn"], m.s_wattn),
            (m.w_proj1[:, :, :], w["L1_attn_w_proj"].rearrange("(c p) d -> p c d", p=P), m.s_wproj1),
        ]
        ssm_memory(nc, m, ctx)
        with ExitStack() as l0_ctx:
            l0_memory(nc, m, l0_ctx)
            with nc.Block() as block:
                @block.gpsimd
                def _(pool):
                    pool.memset(m.neghalf[:, :], -0.5)
            load_stage(nc, m, w)
            l0(nc, m, w)
        for stage in stages:
            stage(nc, m, w)
        with nc.semaphore("stored") as stored, nc.Block() as block:
            @block.sync
            def _(sp):
                sp.dma_start(out.rearrange("b (t p) d -> p (b t) d", p=P), m.h[:, :, :]).then_inc(stored, 16)
                sp.wait_ge(stored, 16)


def kernel(**inputs):
    import concourse.bacc as _bacc
    from concourse.bass_utils import run_bass_kernel_spmd as _run

    nc = _bacc.Bacc("TRN2", target_bir_lowering=False, num_devices=1)
    arrays, w = {}, {}
    for name, value in list(inputs.items()) + [("consts", constants())]:
        a = np.ascontiguousarray(value)
        arrays[f"in_{name}_dram"] = a
        w[name] = nc.dram_tensor(f"in_{name}_dram", a.shape, mybir.dt.from_np(a.dtype), kind="ExternalInput").ap()
    out = nc.dram_tensor("out_0_dram", (B, S, D), F32, kind="ExternalOutput").ap()
    tower(nc, w, out)
    r = _run(nc, [arrays], core_ids=[0])
    return r.results[0]["out_0_dram"]
```
